# Optimizing a Trainium2 kernel written in Bass

```python
import numpy as np
import jax
import jax.numpy as jnp

def _softmax(x, axis=-1):
    return jax.nn.softmax(x, axis=axis)

def _gelu(x):
    return jax.nn.gelu(x, approximate=True)

def _silu(x):
    return jax.nn.silu(x)

def _sigmoid(x):
    return jax.nn.sigmoid(x)

def _layernorm(x, axis=-1, eps=1e-05):
    m = jnp.mean(x, axis=axis, keepdims=True)
    v = jnp.var(x, axis=axis, keepdims=True)
    return (x - m) / jnp.sqrt(v + eps)

def _scatter_add(tgt, idx, src, axis=0):
    return tgt.at[idx].add(src)

def _segment_sum(src, seg, n):
    return jax.ops.segment_sum(src, seg, n)
kernel_name = 'mk_flamingo_gated_d4_seqx_r4_abd68f'

def setup_inputs(seed: int=0):
    np.random.seed(seed)
    _w = jnp.asarray

    def _rec_inputs():
        import jax
        import jax.numpy as jnp
        _rk = jax.random.key(seed)
        x = -0.0002928 + 1 * jax.random.normal(jax.random.fold_in(_rk, 1), (8, 256, 256), jnp.float32)
        _lenS = 256 - jax.random.randint(jax.random.fold_in(_rk, 7), (8,), 0, max(1, 256 // 4) + 1, jnp.int32)
        _lenS2 = 256 - jax.random.randint(jax.random.fold_in(_rk, 8), (8,), 0, max(1, 256 // 4) + 1, jnp.int32)
        _ctx_1024P = jax.random.normal(jax.random.fold_in(_rk, 11), (8, 16, 256), jnp.float32)
        _ctx_1024c = jax.random.dirichlet(jax.random.fold_in(_rk, 511), 0.3 * jnp.ones((16,), jnp.float32), (8, 256))
        _ctx_1024t = jnp.einsum('bsk,bkd->bsd', _ctx_1024c, _ctx_1024P)
        _ctx_1024t = _ctx_1024t * jax.lax.rsqrt(jnp.mean(jnp.square(_ctx_1024t)) + 1e-12) * 0.953939
        ctx_1024 = -1.39393e-06 + 0.999914 * (_ctx_1024t + 0.3 * jax.random.normal(jax.random.fold_in(_rk, 611), (8, 256, 256), jnp.float32))
        _validS = jnp.arange(256)[None, :] < _lenS[:, None]
        _validS2 = jnp.arange(256)[None, :] < _lenS2[:, None]
        _causal = jnp.tril(jnp.ones((256, 256), dtype=bool))
        mask_Bx1xSxS2_bf1 = jnp.ones((8, 1, 256, 256), dtype=bool)
        _g = jax.random.normal(jax.random.fold_in(_rk, 9001), (2, 4), jnp.float32)
        _g = jnp.sign(_g) * jnp.maximum(jnp.abs(_g), 1.0) + (_g == 0) * 1.0
        g_xattn = _g[0]
        g_ffn = _g[1]
        return (x, ctx_1024, mask_Bx1xSxS2_bf1, g_xattn, g_ffn)
    x, ctx_1024, mask_Bx1xSxS2_bf1, g_xattn, g_ffn = _rec_inputs()

    def _L0_xattn_setup():
        import jax, jax.numpy as jnp
        import numpy as np
        NUM_HEADS = 16
        LN_EPS = 1e-05

        def _layernorm(x, scale, bias):
            mu = jnp.mean(x, axis=-1, keepdims=True)
            var = jnp.mean((x - mu) ** 2, axis=-1, keepdims=True)
            return (x - mu) * jax.lax.rsqrt(var + LN_EPS) * scale + bias
        key = jax.random.key(seed)
        ks = jax.random.split(key, 10)
        B, S, D = (2, 512, 256)
        hd = D // NUM_HEADS
        w_scale = 1.0 / np.sqrt(D)
        return {'q': jax.random.normal(ks[0], (B, S, D), jnp.float32), 'k': jax.random.normal(ks[1], (B, S, D), jnp.float32), 'v': jax.random.normal(ks[2], (B, S, D), jnp.float32), 'Wq': jax.random.normal(ks[3], (D, D), jnp.float32) * w_scale, 'bq': jax.random.normal(ks[4], (D,), jnp.float32) * 0.02, 'Wk': jax.random.normal(ks[5], (D, D), jnp.float32) * w_scale, 'bk': jax.random.normal(ks[6], (D,), jnp.float32) * 0.02, 'Wv': jax.random.normal(ks[7], (D, D), jnp.float32) * w_scale, 'bv': jax.random.normal(ks[8], (D,), jnp.float32) * 0.02, 'q_scale': jnp.ones((hd,), jnp.float32), 'q_bias': jnp.zeros((hd,), jnp.float32), 'k_scale': jnp.ones((hd,), jnp.float32), 'k_bias': jnp.zeros((hd,), jnp.float32)}
    _L0_xattn_all = _L0_xattn_setup()
    _L0_xattn_in = {k: v for k, v in _L0_xattn_all.items() if k in ('Wq', 'bq', 'Wk', 'bk', 'Wv', 'bv', 'q_scale', 'q_bias', 'k_scale', 'k_bias')}
    del _L0_xattn_all

    def _L0_ffn_setup():
        import jax, jax.numpy as jnp
        import numpy as np

        def _ste(w, w_q):
            return w + jax.lax.stop_gradient(w_q - w)

        def quantize_w8_per(w, axis):
            amax = jnp.clip(jnp.max(jnp.abs(w), axis=axis, keepdims=True), 1e-08, None)
            scale = 127.0 / amax
            w_q = jnp.clip(jnp.round(w * scale), -128.0, 127.0) / scale
            return _ste(w, w_q)

        def quantize_a16(x):
            amax = jnp.clip(jnp.max(jnp.abs(x)), 1e-08, None)
            scale = 32767.0 / amax
            x_q = jnp.clip(jnp.round(x * scale), -32768.0, 32767.0) / scale
            return _ste(x, x_q)
        key = jax.random.key(seed)
        k1, k2, k3 = jax.random.split(key, 3)
        d_model, d_ff = (256, 1024)
        x = jax.random.normal(k1, (4, 512, d_model), dtype=jnp.float32)
        W_in = jax.random.normal(k2, (d_model, d_ff), dtype=jnp.float32) / np.sqrt(d_model)
        b_in = jnp.zeros((d_ff,), dtype=jnp.float32)
        W_out = jax.random.normal(k3, (d_ff, d_model), dtype=jnp.float32) / np.sqrt(d_ff)
        b_out = jnp.zeros((d_model,), dtype=jnp.float32)
        return {'x': x, 'W_in': W_in, 'b_in': b_in, 'W_out': W_out, 'b_out': b_out}
    _L0_ffn_all = _L0_ffn_setup()
    _L0_ffn_in = {k: v for k, v in _L0_ffn_all.items() if k in ('W_in', 'b_in', 'W_out', 'b_out')}
    del _L0_ffn_all

    def _L1_xattn_setup():
        import jax, jax.numpy as jnp
        import numpy as np
        key = jax.random.key(seed)
        ks = jax.random.split(key, 5)
        b, n_q, n_kv = (16, 128, 1024)
        query_dim, context_dim, heads, dim_head = (256, 256, 16, 64)
        inner = heads * dim_head
        x = jax.random.normal(ks[0], (b, n_q, query_dim), dtype=jnp.float32)
        context = jax.random.normal(ks[1], (b, n_kv, context_dim), dtype=jnp.float32)
        Wq = jax.random.normal(ks[2], (query_dim, inner), dtype=jnp.float32) * query_dim ** (-0.5)
        Wkv = jax.random.normal(ks[3], (context_dim, 2 * inner), dtype=jnp.float32) * context_dim ** (-0.5)
        Wout = jax.random.normal(ks[4], (inner, query_dim), dtype=jnp.float32) * inner ** (-0.5)
        bout = jnp.zeros((query_dim,), dtype=jnp.float32)
        return {'x': x, 'context': context, 'Wq': Wq, 'Wkv': Wkv, 'Wout': Wout, 'bout': bout}
    _L1_xattn_all = _L1_xattn_setup()
    _L1_xattn_in = {k: v for k, v in _L1_xattn_all.items() if k in ('Wq', 'Wkv', 'Wout', 'bout')}
    del _L1_xattn_all

    def _L1_ffn_setup():
        import jax, jax.numpy as jnp
        import numpy as np
        NUM_GEMMS = 8
        HIDDEN = 256
        INTER = 1024
        key = jax.random.key(seed)
        k_x, k_w1, k_b1, k_w2, k_b2 = jax.random.split(key, 5)
        x = jax.random.normal(k_x, (8, 512, HIDDEN), dtype=jnp.float32)
        s1 = 1.0 / np.sqrt(HIDDEN)
        s2 = 1.0 / np.sqrt(INTER)
        W1 = jax.random.uniform(k_w1, (NUM_GEMMS, INTER, HIDDEN), jnp.float32, -s1, s1)
        b1 = jax.random.uniform(k_b1, (NUM_GEMMS, INTER), jnp.float32, -s1, s1)
        W2 = jax.random.uniform(k_w2, (NUM_GEMMS, HIDDEN, INTER), jnp.float32, -s2, s2)
        b2 = jax.random.uniform(k_b2, (NUM_GEMMS, HIDDEN), jnp.float32, -s2, s2)
        return {'x': x, 'W1': W1, 'b1': b1, 'W2': W2, 'b2': b2}
    _L1_ffn_all = _L1_ffn_setup()
    _L1_ffn_in = {k: v for k, v in _L1_ffn_all.items() if k in ('W1', 'b1', 'W2', 'b2')}
    del _L1_ffn_all

    def _L2_xattn_setup():
        import jax, jax.numpy as jnp
        import numpy as np
        DIM = 256
        HEAD_NUM = 8
        D_HEAD = DIM // HEAD_NUM
        B, S = (4, 512)
        key = jax.random.key(seed)
        ks = jax.random.split(key, 7)
        scale = 0.02
        return {'Q': jax.random.normal(ks[0], (B, S, DIM), dtype=jnp.float32), 'K': jax.random.normal(ks[1], (B, S, DIM), dtype=jnp.float32), 'V': jax.random.normal(ks[2], (B, S, DIM), dtype=jnp.float32), 'W_Q': jax.random.normal(ks[3], (DIM, DIM), dtype=jnp.float32) * scale, 'W_K': jax.random.normal(ks[4], (DIM, DIM), dtype=jnp.float32) * scale, 'W_V': jax.random.normal(ks[5], (DIM, DIM), dtype=jnp.float32) * scale, 'W_O': jax.random.normal(ks[6], (DIM, DIM), dtype=jnp.float32) * scale}
    _L2_xattn_all = _L2_xattn_setup()
    _L2_xattn_in = {k: v for k, v in _L2_xattn_all.items() if k in ('W_Q', 'W_K', 'W_V', 'W_O')}
    del _L2_xattn_all

    def _L2_ffn_setup():
        import jax, jax.numpy as jnp
        import numpy as np
        from jax.scipy.linalg import expm
        D = 256
        E = 6
        K = 2
        H = 2 * D
        A4 = 4 * D
        NROT = 4
        LN_EPS = 1e-05

        def _xavier(key, shape):
            fan_in, fan_out = (shape[-2], shape[-1])
            lim = np.sqrt(6.0 / (fan_in + fan_out))
            return jax.random.uniform(key, shape, jnp.float32, -lim, lim)

        def _layernorm(x, g, b):
            mu = jnp.mean(x, axis=-1, keepdims=True)
            var = jnp.var(x, axis=-1, keepdims=True)
            return (x - mu) * jax.lax.rsqrt(var + LN_EPS) * g + b

        def _moe(xn, gate_w, gate_b, ew1, eb1, ew2, eb2):
            logits = xn @ gate_w + gate_b
            tw, ti = jax.lax.top_k(logits, K)
            tw = jax.nn.softmax(tw, axis=-1)
            w_full = jnp.sum(tw[..., None] * jax.nn.one_hot(ti, E, dtype=tw.dtype), axis=-2)
            h = jax.nn.gelu(jnp.einsum('bsd,edh->besh', xn, ew1) + eb1[None, :, None, :], approximate=False)
            eo = jnp.einsum('besh,ehd->besd', h, ew2) + eb2[None, :, None, :]
            return jnp.einsum('bse,besd->bsd', w_full, eo)

        def _rotate(x, gens):
            for i in range(NROT):
                x = x @ expm(gens[i])
            return x
        key = jax.random.key(seed)
        ks = jax.random.split(key, 16)
        x = jax.random.normal(ks[0], (4, 512, D), jnp.float32)
        gens_raw = _xavier(ks[1], (NROT, D, D))
        gens = 0.5 * (gens_raw - jnp.swapaxes(gens_raw, -1, -2))
        return {'x': x, 'ln_g': jnp.ones((D,), jnp.float32), 'ln_b': jnp.zeros((D,), jnp.float32), 'aw1': _xavier(ks[2], (D, A4)), 'ab1': jnp.zeros((A4,), jnp.float32), 'aw2': _xavier(ks[3], (A4, D)), 'ab2': jnp.zeros((D,), jnp.float32), 'gate_w': _xavier(ks[4], (D, E)), 'gate_b': jnp.zeros((E,), jnp.float32), 'ew1': _xavier(ks[5], (E, D, H)), 'eb1': jnp.zeros((E, H), jnp.float32), 'ew2': _xavier(ks[6], (E, H, D)), 'eb2': jnp.zeros((E, D), jnp.float32), 'gens': gens, 'gc_w': _xavier(ks[7], (2 * D, 1)), 'gc_b': jnp.zeros((1,), jnp.float32)}
    _L2_ffn_all = _L2_ffn_setup()
    _L2_ffn_in = {k: v for k, v in _L2_ffn_all.items() if k in ('ln_g', 'ln_b', 'aw1', 'ab1', 'aw2', 'ab2', 'gate_w', 'gate_b', 'ew1', 'eb1', 'ew2', 'eb2', 'gens', 'gc_w', 'gc_b')}
    del _L2_ffn_all

    def _L3_xattn_setup():
        import jax, jax.numpy as jnp
        import numpy as np
        D_MODEL = 256
        H = 16
        D_K = D_MODEL // H
        key = jax.random.key(seed)
        ks = jax.random.split(key, 12)
        B, S = (4, 512)
        scale = 1.0 / np.sqrt(D_MODEL)
        inp = {'q': jax.random.normal(ks[0], (B, S, D_MODEL), jnp.float32), 'k': jax.random.normal(ks[1], (B, S, D_MODEL), jnp.float32), 'v': jax.random.normal(ks[2], (B, S, D_MODEL), jnp.float32), 'mask': jnp.ones((B, 1, S, S), dtype=bool), 'Wq': jax.random.normal(ks[3], (D_MODEL, D_MODEL), jnp.float32) * scale, 'bq': jax.random.normal(ks[4], (D_MODEL,), jnp.float32) * 0.01, 'Wk': jax.random.normal(ks[5], (D_MODEL, D_MODEL), jnp.float32) * scale, 'bk': jax.random.normal(ks[6], (D_MODEL,), jnp.float32) * 0.01, 'Wv': jax.random.normal(ks[7], (D_MODEL, D_MODEL), jnp.float32) * scale, 'bv': jax.random.normal(ks[8], (D_MODEL,), jnp.float32) * 0.01, 'Wo': jax.random.normal(ks[9], (D_MODEL, D_MODEL), jnp.float32) * scale, 'bo': jax.random.normal(ks[10], (D_MODEL,), jnp.float32) * 0.01}
        return inp
    _L3_xattn_all = _L3_xattn_setup()
    _L3_xattn_in = {k: v for k, v in _L3_xattn_all.items() if k in ('Wq', 'bq', 'Wk', 'bk', 'Wv', 'bv', 'Wo', 'bo')}
    del _L3_xattn_all

    def _L3_ffn_setup():
        import jax, jax.numpy as jnp
        import numpy as np
        QMAX = 127.0

        def _ste_round(v):
            return v + jax.lax.stop_gradient(jnp.round(v) - v)

        def _act_fake_quant(x, clip_factor):
            scale = jax.nn.sigmoid(clip_factor) * jnp.max(jnp.abs(x)) / QMAX
            return jnp.clip(_ste_round(x / scale), -QMAX - 1.0, QMAX) * scale

        def _weight_fake_quant(w):
            scale = jnp.max(jnp.abs(w), axis=1, keepdims=True) / QMAX
            return jnp.clip(_ste_round(w / scale), -QMAX - 1.0, QMAX) * scale
        key = jax.random.key(seed)
        k1, k2, k3, k4 = jax.random.split(key, 4)
        B, S, H, I = (8, 2048, 256, 704)
        return {'x': jax.random.normal(k1, (B, S, H), dtype=jnp.float32), 'clip_x': jnp.full((1,), 4.0, dtype=jnp.float32), 'clip_down': jnp.full((1,), 4.0, dtype=jnp.float32), 'w_gate': jax.random.normal(k2, (I, H), dtype=jnp.float32) * 0.02, 'w_up': jax.random.normal(k3, (I, H), dtype=jnp.float32) * 0.02, 'w_down': jax.random.normal(k4, (H, I), dtype=jnp.float32) * 0.02}
    _L3_ffn_all = _L3_ffn_setup()
    _L3_ffn_in = {k: v for k, v in _L3_ffn_all.items() if k in ('clip_x', 'clip_down', 'w_gate', 'w_up', 'w_down')}
    del _L3_ffn_all
    return {'x': x, 'ctx_1024': ctx_1024, 'mask_Bx1xSxS2_bf1': mask_Bx1xSxS2_bf1, 'g_xattn': g_xattn, 'g_ffn': g_ffn, 'L0_xattn_Wq': _L0_xattn_in['Wq'], 'L0_xattn_bq': _L0_xattn_in['bq'], 'L0_xattn_Wk': _L0_xattn_in['Wk'], 'L0_xattn_bk': _L0_xattn_in['bk'], 'L0_xattn_Wv': _L0_xattn_in['Wv'], 'L0_xattn_bv': _L0_xattn_in['bv'], 'L0_xattn_q_scale': _L0_xattn_in['q_scale'], 'L0_xattn_q_bias': _L0_xattn_in['q_bias'], 'L0_xattn_k_scale': _L0_xattn_in['k_scale'], 'L0_xattn_k_bias': _L0_xattn_in['k_bias'], 'L0_ffn_W_in': _L0_ffn_in['W_in'], 'L0_ffn_b_in': _L0_ffn_in['b_in'], 'L0_ffn_W_out': _L0_ffn_in['W_out'], 'L0_ffn_b_out': _L0_ffn_in['b_out'], 'L1_xattn_Wq': _L1_xattn_in['Wq'], 'L1_xattn_Wkv': _L1_xattn_in['Wkv'], 'L1_xattn_Wout': _L1_xattn_in['Wout'], 'L1_xattn_bout': _L1_xattn_in['bout'], 'L1_ffn_W1': _L1_ffn_in['W1'], 'L1_ffn_b1': _L1_ffn_in['b1'], 'L1_ffn_W2': _L1_ffn_in['W2'], 'L1_ffn_b2': _L1_ffn_in['b2'], 'L2_xattn_W_Q': _L2_xattn_in['W_Q'], 'L2_xattn_W_K': _L2_xattn_in['W_K'], 'L2_xattn_W_V': _L2_xattn_in['W_V'], 'L2_xattn_W_O': _L2_xattn_in['W_O'], 'L2_ffn_ln_g': _L2_ffn_in['ln_g'], 'L2_ffn_ln_b': _L2_ffn_in['ln_b'], 'L2_ffn_aw1': _L2_ffn_in['aw1'], 'L2_ffn_ab1': _L2_ffn_in['ab1'], 'L2_ffn_aw2': _L2_ffn_in['aw2'], 'L2_ffn_ab2': _L2_ffn_in['ab2'], 'L2_ffn_gate_w': _L2_ffn_in['gate_w'], 'L2_ffn_gate_b': _L2_ffn_in['gate_b'], 'L2_ffn_ew1': _L2_ffn_in['ew1'], 'L2_ffn_eb1': _L2_ffn_in['eb1'], 'L2_ffn_ew2': _L2_ffn_in['ew2'], 'L2_ffn_eb2': _L2_ffn_in['eb2'], 'L2_ffn_gens': _L2_ffn_in['gens'], 'L2_ffn_gc_w': _L2_ffn_in['gc_w'], 'L2_ffn_gc_b': _L2_ffn_in['gc_b'], 'L3_xattn_Wq': _L3_xattn_in['Wq'], 'L3_xattn_bq': _L3_xattn_in['bq'], 'L3_xattn_Wk': _L3_xattn_in['Wk'], 'L3_xattn_bk': _L3_xattn_in['bk'], 'L3_xattn_Wv': _L3_xattn_in['Wv'], 'L3_xattn_bv': _L3_xattn_in['bv'], 'L3_xattn_Wo': _L3_xattn_in['Wo'], 'L3_xattn_bo': _L3_xattn_in['bo'], 'L3_ffn_clip_x': _L3_ffn_in['clip_x'], 'L3_ffn_clip_down': _L3_ffn_in['clip_down'], 'L3_ffn_w_gate': _L3_ffn_in['w_gate'], 'L3_ffn_w_up': _L3_ffn_in['w_up'], 'L3_ffn_w_down': _L3_ffn_in['w_down']}

def reference(x, ctx_1024, mask_Bx1xSxS2_bf1, g_xattn, g_ffn, L0_xattn_Wq, L0_xattn_bq, L0_xattn_Wk, L0_xattn_bk, L0_xattn_Wv, L0_xattn_bv, L0_xattn_q_scale, L0_xattn_q_bias, L0_xattn_k_scale, L0_xattn_k_bias, L0_ffn_W_in, L0_ffn_b_in, L0_ffn_W_out, L0_ffn_b_out, L1_xattn_Wq, L1_xattn_Wkv, L1_xattn_Wout, L1_xattn_bout, L1_ffn_W1, L1_ffn_b1, L1_ffn_W2, L1_ffn_b2, L2_xattn_W_Q, L2_xattn_W_K, L2_xattn_W_V, L2_xattn_W_O, L2_ffn_ln_g, L2_ffn_ln_b, L2_ffn_aw1, L2_ffn_ab1, L2_ffn_aw2, L2_ffn_ab2, L2_ffn_gate_w, L2_ffn_gate_b, L2_ffn_ew1, L2_ffn_eb1, L2_ffn_ew2, L2_ffn_eb2, L2_ffn_gens, L2_ffn_gc_w, L2_ffn_gc_b, L3_xattn_Wq, L3_xattn_bq, L3_xattn_Wk, L3_xattn_bk, L3_xattn_Wv, L3_xattn_bv, L3_xattn_Wo, L3_xattn_bo, L3_ffn_clip_x, L3_ffn_clip_down, L3_ffn_w_gate, L3_ffn_w_up, L3_ffn_w_down):
    import jax
    import jax.numpy as jnp

    def _L0_xattn_ref(q, k, v, Wq, bq, Wk, bk, Wv, bv, q_scale, q_bias, k_scale, k_bias):
        import jax, jax.numpy as jnp
        import numpy as np
        NUM_HEADS = 16
        LN_EPS = 1e-05

        def _layernorm(x, scale, bias):
            mu = jnp.mean(x, axis=-1, keepdims=True)
            var = jnp.mean((x - mu) ** 2, axis=-1, keepdims=True)
            return (x - mu) * jax.lax.rsqrt(var + LN_EPS) * scale + bias
        B, S, D = q.shape
        H = NUM_HEADS
        hd = D // H
        qp = q @ Wq.T + bq
        kp = k @ Wk.T + bk
        vp = v @ Wv.T + bv
        qp = qp.reshape(B, H, S, hd)
        kp = kp.reshape(B, H, S, hd)
        vp = vp.reshape(B, H, S, hd)
        qp = _layernorm(qp, q_scale, q_bias)
        kp = _layernorm(kp, k_scale, k_bias)
        scale = 1.0 / jnp.sqrt(jnp.asarray(hd, qp.dtype))
        scores = jnp.einsum('bhqd,bhkd->bhqk', qp, kp) * scale
        attn = jax.nn.softmax(scores, axis=-1)
        out = jnp.einsum('bhqk,bhkd->bhqd', attn, vp)
        return out.transpose(0, 2, 1, 3).reshape(B, S, D)

    def _L0_ffn_ref(x, W_in, b_in, W_out, b_out):
        import jax, jax.numpy as jnp
        import numpy as np

        def _ste(w, w_q):
            return w + jax.lax.stop_gradient(w_q - w)

        def quantize_w8_per(w, axis):
            amax = jnp.clip(jnp.max(jnp.abs(w), axis=axis, keepdims=True), 1e-08, None)
            scale = 127.0 / amax
            w_q = jnp.clip(jnp.round(w * scale), -128.0, 127.0) / scale
            return _ste(w, w_q)

        def quantize_a16(x):
            amax = jnp.clip(jnp.max(jnp.abs(x)), 1e-08, None)
            scale = 32767.0 / amax
            x_q = jnp.clip(jnp.round(x * scale), -32768.0, 32767.0) / scale
            return _ste(x, x_q)
        W_in_sim = quantize_w8_per(W_in, axis=0)
        W_out_sim = quantize_w8_per(W_out, axis=1)
        x_sim = quantize_a16(x)
        hidden = jax.nn.gelu(x_sim @ W_in_sim + b_in, approximate=False)
        hidden_sim = quantize_a16(hidden)
        out = hidden_sim @ W_out_sim + b_out
        return out

    def _L1_xattn_ref(x, context, Wq, Wkv, Wout, bout):
        import jax, jax.numpy as jnp
        import numpy as np
        heads, dim_head = (16, 64)
        b, n_q, _ = x.shape
        n_kv = context.shape[1]
        scale = dim_head ** (-0.5)
        q = x @ Wq
        kv = context @ Wkv
        k, v = jnp.split(kv, 2, axis=-1)

        def split_heads(t):
            bb, n, _ = t.shape
            return t.reshape(bb, n, heads, dim_head).transpose(0, 2, 1, 3)
        q, k, v = map(split_heads, (q, k, v))
        i_idx = jnp.arange(n_q)[:, None]
        j_idx = jnp.arange(n_kv)[None, :]
        mask = j_idx % n_q == i_idx
        sim = jnp.einsum('bhid,bhjd->bhij', q, k) * scale
        max_neg = -jnp.finfo(sim.dtype).max
        sim = jnp.where(mask[None, None, :, :], sim, max_neg)
        attn = jax.nn.softmax(sim, axis=-1)
        out = jnp.einsum('bhij,bhjd->bhid', attn, v)
        out = out.transpose(0, 2, 1, 3).reshape(b, n_q, heads * dim_head)
        return out @ Wout + bout

    def _L1_ffn_ref(x, W1, b1, W2, b2):
        import jax, jax.numpy as jnp
        import numpy as np
        NUM_GEMMS = 8
        HIDDEN = 256
        INTER = 1024
        orig_shape = x.shape
        token_num = int(np.prod(orig_shape[:-1]))
        m = token_num // NUM_GEMMS
        xg = x.reshape(NUM_GEMMS, m, HIDDEN)
        h1 = jnp.einsum('gmh,goh->gmo', xg, W1) + b1[:, None, :]
        h2 = jnp.einsum('gmo,gho->gmh', h1, W2) + b2[:, None, :]
        return h2.reshape(orig_shape)

    def _L2_xattn_ref(Q, K, V, W_Q, W_K, W_V, W_O):
        import jax, jax.numpy as jnp
        import numpy as np
        DIM = 256
        HEAD_NUM = 8
        D_HEAD = DIM // HEAD_NUM
        B, S = (4, 512)
        b, s, d = Q.shape
        h, dh = (HEAD_NUM, d // HEAD_NUM)

        def proj_split(x, W):
            y = jnp.einsum('bsd,ed->bse', x, W)
            return y.reshape(b, s, h, dh).transpose(0, 2, 1, 3)
        q = proj_split(Q, W_Q)
        k = proj_split(K, W_K)
        v = proj_split(V, W_V)
        scores = jnp.einsum('bhqd,bhkd->bhqk', q, k) / jnp.sqrt(jnp.float32(dh))
        attn = jax.nn.softmax(scores, axis=1)
        ctx = jnp.einsum('bhqk,bhkd->bhqd', attn, v)
        ctx = ctx.transpose(0, 2, 1, 3).reshape(b, s, d)
        return jnp.einsum('bsd,ed->bse', ctx, W_O)

    def _L2_ffn_ref(x, ln_g, ln_b, aw1, ab1, aw2, ab2, gate_w, gate_b, ew1, eb1, ew2, eb2, gens, gc_w, gc_b):
        import jax, jax.numpy as jnp
        import numpy as np
        from jax.scipy.linalg import expm
        D = 256
        E = 6
        K = 2
        H = 2 * D
        A4 = 4 * D
        NROT = 4
        LN_EPS = 1e-05

        def _xavier(key, shape):
            fan_in, fan_out = (shape[-2], shape[-1])
            lim = np.sqrt(6.0 / (fan_in + fan_out))
            return jax.random.uniform(key, shape, jnp.float32, -lim, lim)

        def _layernorm(x, g, b):
            mu = jnp.mean(x, axis=-1, keepdims=True)
            var = jnp.var(x, axis=-1, keepdims=True)
            return (x - mu) * jax.lax.rsqrt(var + LN_EPS) * g + b

        def _moe(xn, gate_w, gate_b, ew1, eb1, ew2, eb2):
            logits = xn @ gate_w + gate_b
            tw, ti = jax.lax.top_k(logits, K)
            tw = jax.nn.softmax(tw, axis=-1)
            w_full = jnp.sum(tw[..., None] * jax.nn.one_hot(ti, E, dtype=tw.dtype), axis=-2)
            h = jax.nn.gelu(jnp.einsum('bsd,edh->besh', xn, ew1) + eb1[None, :, None, :], approximate=False)
            eo = jnp.einsum('besh,ehd->besd', h, ew2) + eb2[None, :, None, :]
            return jnp.einsum('bse,besd->bsd', w_full, eo)

        def _rotate(x, gens):
            for i in range(NROT):
                x = x @ expm(gens[i])
            return x
        residual = x
        xn = _layernorm(x, ln_g, ln_b)
        abel = jax.nn.gelu(xn @ aw1 + ab1, approximate=False) @ aw2 + ab2
        nonabel = _rotate(_moe(xn, gate_w, gate_b, ew1, eb1, ew2, eb2), gens)
        combined = jnp.concatenate([abel, nonabel], axis=-1)
        gate = jax.nn.sigmoid(combined @ gc_w + gc_b)
        mixed = abel * (1.0 - gate) + nonabel * gate
        return residual + mixed

    def _L3_xattn_ref(q, k, v, mask, Wq, bq, Wk, bk, Wv, bv, Wo, bo):
        import jax, jax.numpy as jnp
        import numpy as np
        D_MODEL = 256
        H = 16
        D_K = D_MODEL // H
        B, S, _ = q.shape
        qh = (q @ Wq.T + bq).reshape(B, S, H, D_K).transpose(0, 2, 1, 3)
        kh = (k @ Wk.T + bk).reshape(B, -1, H, D_K).transpose(0, 2, 1, 3)
        vh = (v @ Wv.T + bv).reshape(B, -1, H, D_K).transpose(0, 2, 1, 3)
        scores = jnp.einsum('bhqd,bhkd->bhqk', qh, kh) / np.sqrt(D_K)
        scores = jnp.where(mask, scores, -1000000000.0)
        weights = jax.nn.softmax(scores, axis=-1)
        out = jnp.einsum('bhqk,bhkd->bhqd', weights, vh)
        out = out.transpose(0, 2, 1, 3).reshape(B, S, D_MODEL)
        return out @ Wo.T + bo

    def _L3_ffn_ref(x, clip_x, clip_down, w_gate, w_up, w_down):
        import jax, jax.numpy as jnp
        import numpy as np
        QMAX = 127.0

        def _ste_round(v):
            return v + jax.lax.stop_gradient(jnp.round(v) - v)

        def _act_fake_quant(x, clip_factor):
            scale = jax.nn.sigmoid(clip_factor) * jnp.max(jnp.abs(x)) / QMAX
            return jnp.clip(_ste_round(x / scale), -QMAX - 1.0, QMAX) * scale

        def _weight_fake_quant(w):
            scale = jnp.max(jnp.abs(w), axis=1, keepdims=True) / QMAX
            return jnp.clip(_ste_round(w / scale), -QMAX - 1.0, QMAX) * scale
        xq = _act_fake_quant(x, clip_x[0])
        gate = jnp.einsum('bsh,ih->bsi', xq, _weight_fake_quant(w_gate))
        up = jnp.einsum('bsh,ih->bsi', xq, _weight_fake_quant(w_up))
        h = _act_fake_quant(jax.nn.silu(gate) * up, clip_down[0])
        return jnp.einsum('bsi,hi->bsh', h, _weight_fake_quant(w_down))
    x = x + jnp.tanh(g_xattn[0]) * _L0_xattn_ref(_layernorm(x, axis=-1), ctx_1024, ctx_1024, L0_xattn_Wq, L0_xattn_bq, L0_xattn_Wk, L0_xattn_bk, L0_xattn_Wv, L0_xattn_bv, L0_xattn_q_scale, L0_xattn_q_bias, L0_xattn_k_scale, L0_xattn_k_bias)
    x = x + jnp.tanh(g_ffn[0]) * _L0_ffn_ref(_layernorm(x, axis=-1), L0_ffn_W_in, L0_ffn_b_in, L0_ffn_W_out, L0_ffn_b_out)
    x = x + jnp.tanh(g_xattn[1]) * _L1_xattn_ref(_layernorm(x, axis=-1), ctx_1024, L1_xattn_Wq, L1_xattn_Wkv, L1_xattn_Wout, L1_xattn_bout)
    x = x + jnp.tanh(g_ffn[1]) * _L1_ffn_ref(_layernorm(x, axis=-1), L1_ffn_W1, L1_ffn_b1, L1_ffn_W2, L1_ffn_b2)
    x = x + jnp.tanh(g_xattn[2]) * _L2_xattn_ref(_layernorm(x, axis=-1), ctx_1024, ctx_1024, L2_xattn_W_Q, L2_xattn_W_K, L2_xattn_W_V, L2_xattn_W_O)
    x = x + jnp.tanh(g_ffn[2]) * _L2_ffn_ref(_layernorm(x, axis=-1), L2_ffn_ln_g, L2_ffn_ln_b, L2_ffn_aw1, L2_ffn_ab1, L2_ffn_aw2, L2_ffn_ab2, L2_ffn_gate_w, L2_ffn_gate_b, L2_ffn_ew1, L2_ffn_eb1, L2_ffn_ew2, L2_ffn_eb2, L2_ffn_gens, L2_ffn_gc_w, L2_ffn_gc_b)
    x = x + jnp.tanh(g_xattn[3]) * _L3_xattn_ref(_layernorm(x, axis=-1), ctx_1024, ctx_1024, mask_Bx1xSxS2_bf1, L3_xattn_Wq, L3_xattn_bq, L3_xattn_Wk, L3_xattn_bk, L3_xattn_Wv, L3_xattn_bv, L3_xattn_Wo, L3_xattn_bo)
    x = x + jnp.tanh(g_ffn[3]) * _L3_ffn_ref(_layernorm(x, axis=-1), L3_ffn_clip_x, L3_ffn_clip_down, L3_ffn_w_gate, L3_ffn_w_up, L3_ffn_w_down)
    return x

_drawn_inputs = setup_inputs


def setup_inputs(seed=0):
    import zlib

    import numpy as np

    out = dict(_drawn_inputs(seed))
    spreads = {'L0_xattn_q_scale': (1.0, 0.6),
     'L0_xattn_q_bias': (0.0, 0.8),
     'L0_xattn_k_scale': (1.0, 0.6),
     'L0_xattn_k_bias': (0.0, 2.0),
     'L0_ffn_b_in': (0.0, 0.267),
     'L0_ffn_b_out': (0.0, 0.1),
     'L1_xattn_bout': (0.0, 0.1),
     'L2_ffn_ln_g': (1.0, 0.2),
     'L2_ffn_ln_b': (0.0, 0.1),
     'L2_ffn_ab1': (0.0, 0.334),
     'L2_ffn_ab2': (0.0, 0.1),
     'L2_ffn_gate_b': (0.0, 0.1),
     'L2_ffn_eb1': (0.0, 0.403),
     'L2_ffn_eb2': (0.0, 0.307)}
    factors = {'g_ffn': 46.792,
     'L0_xattn_bq': 8.0,
     'L0_xattn_bk': 8.0,
     'L0_xattn_bv': 8.0,
     'L1_ffn_b1': 4.146,
     'L1_ffn_b2': 4.637,
     'L3_xattn_bq': 8.0,
     'L3_xattn_bk': 64.0,
     'L3_xattn_bv': 8.0,
     'L3_xattn_bo': 8.0,
     'L3_ffn_w_gate': 2.964,
     'L3_ffn_w_up': 2.903,
     'L3_ffn_w_down': 2.905}
    for name, (base, spread) in spreads.items():
        noise = np.random.default_rng([zlib.crc32(name.encode()), seed]).standard_normal(out[name].shape)
        drawn = base * np.exp(spread * noise) if base else spread * noise
        out[name] = jnp.asarray(drawn.astype(out[name].dtype))
    for name, factor in factors.items():
        out[name] = (out[name] * factor).astype(out[name].dtype)
    return out
```

```python
import concourse.bass as bass
from concourse import mybir
from contextlib import ExitStack

F32 = mybir.dt.float32
BF16 = mybir.dt.bfloat16
I32 = mybir.dt.int32
U32 = mybir.dt.uint32
U8 = mybir.dt.uint8
ALU = mybir.AluOpType
ACT = mybir.ActivationFunctionType
AX = mybir.AxisListType.X
ds = bass.ds

P = 128
B, S, D = 8, 256, 256
U = S // P
KT = D // P
NT = B * U
NTD = NT + U
TD = NTD * P
LN_EPS = 1e-5
ROUND = 12582912.0
ROUND256 = 3221225472.0
MASKED = 4294967296.0
HD = 16
HP = 32
NH = D // HD
NG = 4


class Chain:

    def __init__(self, eng, sem, base=0):
        self.eng, self.sem, self.base, self.n = eng, sem, base, 0

    def __call__(self, ins):
        self.n += 1
        ins.then_inc(self.sem, 1)
        self.eng.wait_ge(self.sem, self.base + self.n)


def rsqrt(link, eng, v, y, t):
    link(eng.tensor_scalar(y.bitcast(I32), v.bitcast(I32), 1, None, ALU.logical_shift_right))
    link(eng.tensor_scalar(y.bitcast(I32), y.bitcast(I32), -1.0, float(0x5F3759DF), ALU.mult, ALU.add))
    for _ in range(3):
        link(eng.tensor_tensor(t, y, y, ALU.mult))
        link(eng.tensor_tensor(t, t, v, ALU.mult))
        link(eng.tensor_scalar(t, t, -0.5, 1.5, ALU.mult, ALU.add))
        link(eng.tensor_tensor(y, y, t, ALU.mult))


RSQRT_LINKS = 14


def moments(link, eng, st, mean, rstd, t):
    link(eng.tensor_tensor(mean, st[:, :, 1], st[:, :, 4], ALU.add))
    link(eng.tensor_scalar(mean, mean, 0.5, None, ALU.mult))
    link(eng.tensor_tensor(t, st[:, :, 1], st[:, :, 4], ALU.subtract))
    link(eng.tensor_tensor(t, t, t, ALU.mult))
    link(eng.tensor_tensor(rstd, st[:, :, 2], st[:, :, 5], ALU.add))
    link(eng.tensor_scalar(rstd, rstd, 1.0 / D, LN_EPS, ALU.mult, ALU.add))
    link(eng.scalar_tensor_tensor(t, t, 0.25, rstd, ALU.mult, ALU.add))


MOMENT_LINKS = 7


class Core:

    def semaphore(self, name):
        self.sems.append(self.nc.alloc_semaphore(name=name))
        return self.sems[-1]


def row(ap, parts=P):
    return ap.partition_broadcast(parts)


def col(ap):
    return ap.rearrange("(t p) -> p t", p=P)


def setup(nc, I, c):
    with ExitStack() as ctx:
        sem = lambda n: c.semaphore("setup_" + n)
        ctx_in = ctx.enter_context(nc.sbuf_tensor("ctx_in", [P, NT, D], F32))
        tr = ctx.enter_context(nc.psum_tensor("setup_tr", [P, 4, KT, S], F32))
        x_loaded, ctx_loaded, g_loaded = sem("x_loaded"), sem("ctx_loaded"), sem("g_loaded")
        zeroed, ident_made, tr_done, tr_out = sem("zeroed"), sem("ident"), sem("tr"), sem("tr_out")
        stats, tanhs, pool_chain = sem("stats"), sem("tanhs"), sem("pool_chain")
        block = ctx.enter_context(nc.Block())

        @block.sync
        def _(sp):
            for b in range(B):
                sp.dma_start(ctx_in[:, U * b:U * b + U, :],
                             I["ctx_1024"][b].rearrange("(u p) d -> p u d", p=P)).then_inc(ctx_loaded, 16)
            sp.dma_start(c.g[:, 0:4], row(I["g_xattn"])).then_inc(g_loaded, 16)
            sp.dma_start(c.g[:, 4:8], row(I["g_ffn"])).then_inc(g_loaded, 16)
            for b in range(B):
                sp.dma_start(c.x[:, U * b:U * b + U, :],
                             I["x"][b].rearrange("(u p) d -> p u d", p=P)).then_inc(x_loaded, 16)

        @block.gpsimd
        def _(pool):
            link = Chain(pool, pool_chain)
            link(pool.memset(c.ident[:], 0.0))
            link(pool.affine_select(out=c.ident[:], in_=c.ident[:], compare_op=ALU.not_equal, fill=1.0,
                                    base=0, pattern=[[-1, P]], channel_multiplier=1))
            pool.tensor_copy(c.identb[:], c.ident[:]).then_inc(ident_made, 1)
            pool.memset(c.ones[:], 1.0).then_inc(ident_made, 1)

        @block.scalar
        def _(act):
            act.wait_ge(g_loaded, 32)
            act.activation(c.tg[:], c.g[:], ACT.Tanh).then_inc(tanhs, 1)
            for b in range(B):
                act.wait_ge(tr_done, b + 1)
                act.activation(c.ctxT[:, :, S * b:S * b + S], tr[:, b % 4], ACT.Copy).then_inc(tr_out, 1)

        @block.vector
        def _(dve):
            dve.memset(c.x[:, NT:NTD, :], 0.0).then_inc(zeroed, 1)
            dve.memset(c.ctxT[:, :, B * S:], 0.0)
            dve.wait_ge(x_loaded, 16 * B)
            dve.wait_ge(zeroed, 1)
            for t in range(NTD):
                dve.bn_stats(c.st[:, t, :], c.x[:, t, :]).then_inc(stats, 1)
            dve.wait_ge(stats, NTD)

        @block.tensor
        def _(pe):
            pe.wait_ge(ident_made, 2)
            pe.wait_ge(ctx_loaded, 16 * B)
            for b in range(B):
                if b >= 4:
                    pe.wait_ge(tr_out, b - 3)
                for u in range(U):
                    for kt in range(KT):
                        last = pe.transpose(tr[:, b % 4, kt, P * u:P * u + P],
                                            ctx_in[:, U * b + u, P * kt:P * kt + P], c.ident[:])
                last.then_inc(tr_done, 1)


def attention_core_pe(pe, c, a, b, s, masked, mid):
    a.wait_qk(pe, b)

    def max_scores(n):
        g, r = n // 4, HP * (n % 4)
        pe.wait_ge(a.max_reduced, NH * b + max(n - 1, 0))
        for qt in range(U):
            last = pe.matmul(a.smax[n % 2][:, qt, :], a.qT[s][r:r + HD, g, P * qt:P * qt + P],
                             a.kT[s][r:r + HD, g, :], start=True, stop=not masked)
            if masked:
                last = pe.matmul(a.smax[n % 2][:, qt, :], c.identb[:], a.pen[s][:, qt, :], start=False, stop=True)
        last.then_inc(a.max_scored, 1)

    def turn_maxima(g):
        pe.wait_ge(a.max_reduced, NH * b + 4 * g + 4)
        pe.wait_ge(a.qa_ready, NG * b + max(g - 1, 0))
        for qt in range(U):
            last = pe.transpose(a.mrow[:, g % 2, P * qt:P * qt + P], a.mx[g % 2][:, qt, :], c.ident[:])
        last.then_inc(a.mrow_ready, 1)

    def scores(n):
        g, r = n // 4, HP * (n % 4)
        if n % 4 == 0:
            pe.wait_ge(a.qa_ready, NG * b + g + 1)
        pe.wait_ge(a.exp_done, NH * b + max(n - 1, 0))
        for kt in range(U):
            last = pe.matmul(a.sc[n % 2][:, kt, :], a.kT[s][r:r + HP, g, P * kt:P * kt + P],
                             a.qa[g % 2][r:r + HP, :], start=True, stop=not masked)
            if masked:
                last = pe.matmul(a.sc[n % 2][:, kt, :], c.identb[:], a.penT[s][:, kt, :], start=False, stop=True)
        last.then_inc(a.scored, 1)

    def values(n):
        h = a.head(n)
        pe.wait_ge(a.exp_done, NH * b + n + 1)
        if n == 0:
            pe.wait_ge(a.norm_done, U * b)
            pe.wait_ge(a.va_copied, a.va_per * (b + 1))
        for qt in range(U):
            for kt in range(U):
                last = pe.matmul(a.po[qt][:, h, :], a.pT[n % 2][:, kt, P * qt:P * qt + P],
                                 a.va[s][:, kt, n, 0:HD + 1], start=(kt == 0), stop=(kt == U - 1))
        last.then_inc(a.pv_done, 1)

    for n in range(4):
        max_scores(n)
    turn_maxima(0)
    for n in range(NH):
        if n + 4 < NH:
            max_scores(n + 4)
        scores(n)
        if n >= 1:
            values(n - 1)
        if n % 4 == 3 and n + 1 < NH:
            turn_maxima(n // 4 + 1)
        mid(n)
    values(NH - 1)


def attention_core_act(act, a, b, scale, mid):
    for n in range(NH):
        act.wait_ge(a.scored, NH * b + n + 1)
        act.activation(a.pT[n % 2][:], a.sc[n % 2][:], ACT.Exp, scale=scale).then_inc(a.exp_done, 1)
        mid(n)


def attention_core_dve(dve, a, b, s, mid):
    def reduce(n):
        g, r = n // 4, HP * (n % 4)
        dve.wait_ge(a.max_scored, NH * b + n + 1)
        dve.tensor_reduce(a.mx[g % 2][:, :, r + HD:r + HD + 1], a.smax[n % 2][:], AX, ALU.max,
                          negate=True).then_inc(a.max_reduced, 1)

    def add_maxima(g):
        dve.wait_ge(a.mrow_ready, NG * b + g + 1)
        dve.tensor_tensor(a.qa[g % 2][:], a.mrow[:, g % 2, :], a.qT[s][:, g, :], ALU.add).then_inc(a.qa_ready, 1)

    for n in range(4):
        reduce(n)
    add_maxima(0)
    for n in range(NH):
        if n + 4 < NH:
            reduce(n + 4)
        if n % 4 == 3 and n + 1 < NH:
            add_maxima(n // 4 + 1)
        mid(n)


def attention_tiles(nc, c, ctx, tag):
    a = Core()
    sb = lambda n, s, d=F32: ctx.enter_context(nc.sbuf_tensor(tag + n, s, d))
    ps = lambda n, s, d=F32: ctx.enter_context(nc.psum_tensor(tag + n, s, d))
    sem = lambda n: c.semaphore(tag + n)
    a.sb, a.ps, a.sem = sb, ps, sem
    a.qT = [sb(f"qT{i}", [P, NG, S]) for i in range(2)]
    a.kT = [sb(f"kT{i}", [P, NG, S]) for i in range(2)]
    a.va = [sb(f"va{i}", [P, U, NH, HP]) for i in range(2)]
    a.qa = [sb(f"qa{i}", [P, S]) for i in range(2)]
    a.pT = [sb(f"pT{i}", [P, U, S]) for i in range(2)]
    a.mx = [sb(f"mx{i}", [P, U, P]) for i in range(2)]
    a.xs = sb("xs", [P, U, D])
    a.xsT = sb("xsT", [P, KT, S])
    a.csT = sb("csT", [P, KT, S])
    a.on = [sb(f"on{u}", [P, NH, HD]) for u in range(U)]
    a.rden = [sb(f"rden{u}", [P, NH, 1]) for u in range(U)]
    a.mean, a.rstd, a.mt = sb("mean", [P, NTD]), sb("rstd", [P, NTD]), sb("mt", [P, NTD])
    a.smax = [ps(f"smax{i}", [P, U, S]) for i in range(2)]
    a.sc = [ps(f"sc{i}", [P, U, S]) for i in range(2)]
    a.mrow = ps("mrow", [P, 2, S])
    a.po = [ps(f"po{u}", [P, NH, HD + 1]) for u in range(U)]
    a.prep = ps("prep", [P, 2, 256])
    a.qk_ready, a.va_ready, a.max_scored = sem("qk_ready"), sem("va_ready"), sem("max_scored")
    a.max_reduced, a.mrow_ready, a.qa_ready = sem("max_reduced"), sem("mrow_ready"), sem("qa_ready")
    a.scored, a.exp_done, a.pv_done = sem("scored"), sem("exp_done"), sem("pv_done")
    a.norm_done, a.xs_ready, a.cs_ready = sem("norm_done"), sem("xs_ready"), sem("cs_ready")
    a.prep_filled, a.prep_act, a.prep_dve = sem("prep_filled"), sem("prep_act"), sem("prep_dve")
    a.dve_chain, a.w_loaded, a.w_turned = sem("dve_chain"), sem("w_loaded"), sem("w_turned")
    a.w_copied, a.act_chain, a.pool_chain = sem("w_copied"), sem("act_chain"), sem("pool_chain")
    a.prep_done = sem("prep_done")
    return a


def layer0_attention(nc, I, c):
    with ExitStack() as ctx:
        a = attention_tiles(nc, c, ctx, "l0a_")
        a.head = lambda n: 8 * (n // 8) + 2 * (n % 4) + (n // 4) % 2
        a.va_per, a.va_copied = 3, a.prep_act
        a.wait_qk = lambda eng, b: eng.wait_ge(a.qk_ready, b + 1)
        w_in = a.sb("w_in", [P, 3, KT, D])
        wT = a.sb("wT", [P, KT, 3, D])
        bias = a.sb("bias", [P, 3, D])
        gmean = a.sb("gmean", [P, 3, KT, 2 * NH])
        lnsc = a.sb("lnsc", [P, 2, HD])
        lnbi = a.sb("lnbi", [P, 2, HD])
        qkv = a.sb("qkv", [P, U, 3, NH, HP])
        sq = a.sb("sq", [P, U, 2 * NH, HD])
        ss = a.sb("ss", [P, U, 2 * NH])
        rs = a.sb("rs", [P, U, 2 * NH])
        rt = a.sb("rt", [P, U, 2 * NH])
        vT = a.sb("vT", [P, NG, S])
        squared, normed, scaled, v_turned = a.sem("squared"), a.sem("normed"), a.sem("scaled"), a.sem("v_turned")
        ready0 = a.sem("ready0")
        block = ctx.enter_context(nc.Block())
        PREP = 6

        @block.sync
        def _(sp):
            for k, n in enumerate("qkv"):
                sp.dma_start(w_in[:, k], I["L0_xattn_W" + n].rearrange("(t p) d -> p t d", p=P)).then_inc(a.w_loaded, 16)
                sp.dma_start(bias[:, k], row(I["L0_xattn_b" + n])).then_inc(a.w_loaded, 16)
            for k, n in enumerate("qk"):
                sp.dma_start(lnsc[:, k], row(I[f"L0_xattn_{n}_scale"])).then_inc(a.w_loaded, 16)
                sp.dma_start(lnbi[:, k], row(I[f"L0_xattn_{n}_bias"])).then_inc(a.w_loaded, 16)

        @block.tensor
        def _(pe):
            pe.wait_ge(a.w_loaded, 160)
            for k in range(3):
                pe.wait_ge(a.w_copied, k)
                bank = a.prep
                for ot in range(KT):
                    for kt in range(KT):
                        last = pe.transpose(bank[:, kt, P * ot:P * ot + P], w_in[:, k, ot, P * kt:P * kt + P], c.ident[:])
                last.then_inc(a.w_turned, 1)
            pe.wait_ge(ready0, 1)

            def prep(step, n, s):
                bank = a.prep
                if step == 0:
                    pe.wait_ge(a.xs_ready, n + 1)
                    pe.wait_ge(a.prep_act, 3 * n)
                    for u in range(U):
                        for kt in range(KT):
                            last = pe.transpose(bank[:, kt, P * u:P * u + P], a.xs[:, u, P * kt:P * kt + P], c.ident[:])
                if step == 1:
                    pe.wait_ge(a.prep_act, 3 * n + 1)
                    for u in range(U):
                        for kt in range(KT):
                            last = pe.matmul(bank[:, u, :], a.xsT[:, kt, P * u:P * u + P], wT[:, kt, 0, :],
                                             start=(kt == 0), stop=(kt == KT - 1))
                if step in (2, 3):
                    u = step - 2
                    pe.wait_ge(a.prep_dve, 3 * n + 1 + u)
                    pe.wait_ge(a.cs_ready, n + 1)
                    for kt in range(KT):
                        last = pe.matmul(bank[:], a.csT[:, kt, P * u:P * u + P], wT[:, kt, 1:3, :],
                                         start=(kt == 0), stop=(kt == KT - 1))
                if step in (4, 5):
                    kt = step - 4
                    if kt == 0:
                        pe.wait_ge(a.prep_dve, 3 * n + 3)
                        pe.wait_ge(v_turned, n + 1)
                    else:
                        pe.wait_ge(a.prep_act, 3 * n + 2)
                    for g in range(NG):
                        last = pe.transpose(bank[:, g // 2, P * (g % 2):P * (g % 2) + P],
                                            vT[:, g, P * kt:P * kt + P], c.ident[:])
                last.then_inc(a.prep_filled, 1)

            for step in range(PREP):
                prep(step, 0, 0)
            at = {1: 0, 2: 1, 3: 2, 4: 3, 12: 4, 13: 5}
            with pe.Fori(0, B // 2) as i:
                for s in range(2):
                    b = 2 * i + s
                    attention_core_pe(pe, c, a, b, s, False,
                                      lambda n: prep(at[n], b + 1, 1 - s) if n in at else None)

        @block.scalar
        def _(act):
            def prep(step, n, s):
                if step == 0:
                    act.wait_ge(a.prep_filled, PREP * n + 1)
                    act.activation(a.xsT[:], a.prep[:], ACT.Copy).then_inc(a.prep_act, 1)
                if step == 1:
                    for u in range(U):
                        act.wait_ge(a.prep_dve, 3 * n + 2 + u)
                        act.activation(sq[:, u].rearrange("p (a c) e -> p a c e", a=2), qkv[:, u, 0:2, :, 0:HD],
                                       ACT.Square).then_inc(squared, 1)
                if step in (2, 3):
                    act.wait_ge(a.prep_filled, PREP * n + 3 + step)
                    act.activation(a.va[s][:, step - 2].rearrange("p (a h) e -> p a (h e)", a=2), a.prep[:],
                                   ACT.Copy).then_inc(a.prep_act, 1)

            for k in range(4):
                prep(k, 0, 0)
            at = {1: 0, 5: 1, 12: 2, 13: 3}
            with act.Fori(0, B // 2) as i:
                for s in range(2):
                    b = 2 * i + s
                    attention_core_act(act, a, b, HD ** -0.5,
                                       lambda n: prep(at[n], b + 1, 1 - s) if n in at else None)

        @block.gpsimd
        def _(pool):
            def prep(n, base):
                if base is not None:
                    pool.wait_ge(a.prep_filled, PREP * n - 2)
                pool.tensor_copy(a.csT[:], c.ctxT[:, :, ds(n * S, S)]).then_inc(a.cs_ready, 1)
                link = Chain(pool, a.pool_chain, 2 * n)
                for u in range(U):
                    v = qkv[:, u, 0:2, :, 0:HD]
                    pool.wait_ge(normed, U * n + u + 1)
                    link(pool.tensor_tensor(v, v, lnsc[:].unsqueeze(2).to_broadcast([P, 2, NH, HD]), ALU.mult))
                    pool.tensor_tensor(v, v, lnbi[:].unsqueeze(2).to_broadcast([P, 2, NH, HD]),
                                       ALU.add).then_inc(scaled, 1)
            pool.wait_ge(a.w_loaded, 160)
            prep(0, None)
            with pool.Fori(1, B + 1) as n:
                prep(n, n)

        @block.vector
        def _(dve):
            link = Chain(dve, a.dve_chain)
            for t in (a.mx[0], a.mx[1]):
                link(dve.memset(t[:], 0.0))
            link(dve.memset(qkv[:], 0.0))
            link(dve.memset(qkv[:, :, 1:3, :, HD:HD + 1], 1.0))
            dve.wait_ge(a.w_loaded, 160)
            for k in range(3):
                dve.wait_ge(a.w_turned, k + 1)
                for kt in range(KT):
                    link(dve.tensor_copy(wT[:, kt, k, :], a.prep[:, kt, :]))
                if k < 2:
                    for kt in range(KT):
                        v = wT[:, kt, k, :].rearrange("p (c e) -> p c e", e=HD)
                        m = gmean[:, k, kt, 0:NH]
                        link(dve.tensor_reduce(m, v, AX, ALU.add))
                        link(dve.tensor_scalar(m, m, 1.0 / HD, None, ALU.mult))
                        link(dve.tensor_tensor(v, v, m.unsqueeze(2).to_broadcast([P, NH, HD]), ALU.subtract))
                    v = bias[:, k, :].rearrange("p (c e) -> p c e", e=HD)
                    m = gmean[:, 2, k, 0:NH]
                    link(dve.tensor_reduce(m, v, AX, ALU.add))
                    link(dve.tensor_scalar(m, m, 1.0 / HD, None, ALU.mult))
                    link(dve.tensor_tensor(v, v, m.unsqueeze(2).to_broadcast([P, NH, HD]), ALU.subtract))
                dve.sem_inc(a.w_copied, 1)
            moments(link, dve, c.st[:], a.mean[:], a.rstd[:], a.mt[:])
            rsqrt(link, dve, a.mt[:], a.rstd[:], a.xs[:, 0, 0:NTD])
            dve.sem_inc(ready0, 1)
            SETUP = link.n
            PER = 1 + 1 + 1 + 2 + 1 + RSQRT_LINKS + 6 + 6

            def prep(step, link, n, s):
                if step == 0:
                    for u in range(U):
                        t = U * n + u
                        last = dve.tensor_scalar(a.xs[:, u, :], c.x[:, t, :], a.mean[:, ds(t, 1)], a.rstd[:, ds(t, 1)],
                                                 ALU.subtract, ALU.mult)
                    last.then_inc(a.xs_ready, 1)
                if step == 1:
                    dve.wait_ge(a.prep_filled, PREP * n + 2)
                    ps = a.prep[:].rearrange("p u (c e) -> p u c e", e=HD)
                    bi = bias[:, 0, :].rearrange("p (c e) -> p c e", e=HD)
                    for u in range(U):
                        last = dve.tensor_tensor(qkv[:, u, 0, :, 0:HD], ps[:, u], bi, ALU.add)
                    last.then_inc(a.prep_dve, 1)
                if step in (2, 3):
                    dve.wait_ge(a.prep_filled, PREP * n + 1 + step)
                    dve.tensor_tensor(qkv[:, step - 2, 1:3, :, 0:HD], a.prep[:].rearrange("p a (c e) -> p a c e", e=HD),
                                      bias[:, 1:3, :].rearrange("p a (c e) -> p a c e", e=HD), ALU.add).then_inc(a.prep_dve, 1)
                if step == 4:
                    for u in range(U):
                        dve.wait_ge(squared, U * n + u + 1)
                        link(dve.tensor_reduce(ss[:, u, :], sq[:, u], AX, ALU.add))
                    link(dve.tensor_scalar(ss[:], ss[:], 1.0 / HD, LN_EPS, ALU.mult, ALU.add))
                    rsqrt(link, dve, ss[:], rs[:], rt[:])
                    for u in range(U):
                        v = qkv[:, u, 0:2, :, 0:HD].rearrange("p a c e -> p (a c) e")
                        dve.tensor_tensor(v, v, rs[:, u, :].unsqueeze(2).to_broadcast([P, 2 * NH, HD]),
                                          ALU.mult).then_inc(normed, 1)
                if step == 5:
                    dve.wait_ge(a.prep_filled, PREP * n)
                    for u in range(U):
                        dve.transpose(vT[:, 2 * u:2 * u + 2, :].rearrange("p a (t c) -> p c (a t)", c=HD),
                                      qkv[:, u, 2]).then_inc(v_turned if u else a.prep_done, 1)
                if step == 6:
                    for u in range(U):
                        dve.wait_ge(scaled, U * n + u + 1)
                        for k, dst in ((0, a.qT[s]), (1, a.kT[s])):
                            last = dve.transpose(dst[:, 2 * u:2 * u + 2, :].rearrange("p a (t c) -> p c (a t)", c=HD),
                                                 qkv[:, u, k])
                    last.then_inc(a.qk_ready, 1)

            def waits_own(step, n):
                if step == 4:
                    dve.wait_ge(a.prep_dve, 3 * n + 3)
                if step == 6:
                    dve.wait_ge(normed, U * n + 2)

            PREP_LINKS = 2 + 1 + RSQRT_LINKS
            for step in range(7):
                waits_own(step, 0)
                prep(step, link, 0, 0)
            base = link.n
            at = {0: 0, 2: 1, 3: 2, 4: 3, 6: 4, 8: 5, 11: 6}
            with dve.Fori(0, B // 2) as i:
                for s in range(2):
                    b = 2 * i + s
                    link = Chain(dve, a.dve_chain, base + b * (PREP_LINKS + 3 * U))

                    def mid(n):
                        if n in at:
                            if at[n] == 0:
                                dve.wait_ge(a.prep_filled, PREP * b + 1)
                            if at[n] == 1:
                                dve.wait_ge(a.qk_ready, b + 1)
                            waits_own(at[n], b + 1)
                            prep(at[n], link, b + 1, 1 - s)
                    dve.wait_ge(a.qk_ready, b + 1)
                    attention_core_dve(dve, a, b, s, mid)
                    dve.wait_ge(a.pv_done, NH * (b + 1))
                    for u in range(U):
                        t = U * b + u
                        link(dve.reciprocal(a.rden[u][:], a.po[u][:, :, HD:HD + 1]))
                        ins = dve.tensor_tensor(a.on[u][:], a.po[u][:, :, 0:HD], a.rden[u][:].to_broadcast([P, NH, HD]), ALU.mult)
                        ins.then_inc(a.norm_done, 1)
                        dve.wait_ge(a.norm_done, t + 1)
                        link(dve.scalar_tensor_tensor(c.x[:, t, :], a.on[u][:].rearrange("p h e -> p (h e)"),
                                                      c.tg[:, 0:1], c.x[:, t, :], ALU.mult, ALU.add))
                        link(dve.bn_stats(c.st[:, t, :], c.x[:, t, :]))
            dve.wait_ge(a.qk_ready, B + 1)


def layer3_attention(nc, I, c):
    with ExitStack() as ctx:
        a = attention_tiles(nc, c, ctx, "l3a_")
        a.head = lambda n: n
        w_in = a.sb("w_in", [P, 4, KT, D])
        wqk = a.sb("wqk", [P, KT, 2, NG * P])
        wvo = a.sb("wvo", [P, KT, 2, D])
        bqk = a.sb("bqk", [P, 2, NG])
        bvo = a.sb("bvo", [P, 2, D])
        row16 = a.sb("row16", [P, 1])
        mask = a.sb("mask", [P, NTD, S], U8)
        a.pen = [a.sb(f"pen{i}", [P, U, S], BF16) for i in range(2)]
        a.penT = [a.sb(f"penT{i}", [P, U, S], BF16) for i in range(2)]
        onT = a.sb("onT", [P, KT, S])
        mask_f = a.sb("mask_f", [P, U, S], BF16)
        y = [a.sb(f"y{u}", [P, D]) for u in range(U)]
        pen_ready, pool_setup, mask_loaded = a.sem("pen_ready"), a.sem("pool_setup"), a.sem("mask_loaded")
        on_turned, on_copied, projected, ready0 = a.sem("on_turned"), a.sem("on_copied"), a.sem("projected"), a.sem("ready0")
        a.va_copied, a.va_per = a.prep_dve, 1
        a.wait_qk = lambda eng, b: eng.wait_ge(a.prep_act, 6 * (b + 1))
        block = ctx.enter_context(nc.Block())
        PREP = 7
        ACTS = 6

        @block.sync
        def _(sp):
            for k, n in enumerate("qkvo"):
                sp.dma_start(w_in[:, k], I["L3_xattn_W" + n].rearrange("(t p) d -> p t d", p=P)).then_inc(a.w_loaded, 16)
            for k, n in enumerate("vo"):
                sp.dma_start(bvo[:, k], row(I["L3_xattn_b" + n])).then_inc(a.w_loaded, 16)
            sp.wait_ge(pool_setup, 1)
            for k, n in enumerate("qk"):
                v = I["L3_xattn_b" + n].rearrange("(g j e) -> j e g", g=NG, j=4)
                for j in range(4):
                    sp.dma_start(bqk[HP * j:HP * j + HD, k, :], v[j]).then_inc(a.w_loaded, 16)
            for b in range(B):
                sp.dma_start(mask[:, U * b:U * b + U, :],
                             I["mask_Bx1xSxS2_bf1"][b, 0].rearrange("(u p) k -> p u k", p=P)).then_inc(mask_loaded, 16)

        WLOADS = 16 * (4 + 2 + 8)

        @block.tensor
        def _(pe):
            pe.wait_ge(a.w_loaded, WLOADS)
            for k in range(4):
                pe.wait_ge(a.w_copied, k)
                for ot in range(KT):
                    for kt in range(KT):
                        last = pe.transpose(a.prep[:, kt, P * ot:P * ot + P], w_in[:, k, ot, P * kt:P * kt + P], c.ident[:])
                last.then_inc(a.w_turned, 1)
            pe.wait_ge(ready0, 1)

            def prep(step, n, s):
                if step == 0:
                    pe.wait_ge(a.xs_ready, n + 1)
                    pe.wait_ge(a.prep_dve, n)
                    for u in range(U):
                        for kt in range(KT):
                            last = pe.transpose(a.prep[:, kt, P * u:P * u + P], a.xs[:, u, P * kt:P * kt + P], c.ident[:])
                if 1 <= step <= NG:
                    g = step - 1
                    pe.wait_ge(a.prep_act, ACTS * n + step)
                    for kt in range(KT):
                        pe.matmul(a.prep[:, 0, :], wqk[:, kt, 0, P * g:P * g + P], a.xsT[:, kt, :],
                                  start=(kt == 0), stop=(kt == KT - 1))
                    for kt in range(KT):
                        last = pe.matmul(a.prep[:, 1, :], wqk[:, kt, 1, P * g:P * g + P], c.ctxT[:, kt, ds(n * S, S)],
                                         start=(kt == 0), stop=(kt == KT - 1))
                if step == 5:
                    pe.wait_ge(pen_ready, n + 1)
                    pe.wait_ge(a.prep_act, ACTS * n + 5)
                    for u in range(U):
                        for kt in range(U):
                            last = pe.matmul(a.prep[:, kt, P * u:P * u + P], a.pen[s][:, u, P * kt:P * kt + P],
                                             c.identb[:], start=True, stop=True)
                if step == 6:
                    pe.wait_ge(a.prep_act, ACTS * n + 6)
                    pe.wait_ge(a.cs_ready, n + 1)
                    for u in range(U):
                        for kt in range(KT):
                            last = pe.matmul(a.prep[:, u, :], a.csT[:, kt, P * u:P * u + P], wvo[:, kt, 0, :],
                                             start=(kt == 0), stop=(kt == KT - 1))
                last.then_inc(a.prep_filled, 1)

            for step in range(PREP):
                prep(step, 0, 0)
            at = {1: 0, 3: 1, 5: 2, 7: 3, 9: 4, 11: 5, 13: 6}
            with pe.Fori(0, B // 2) as i:
                for s in range(2):
                    b = 2 * i + s
                    attention_core_pe(pe, c, a, b, s, True,
                                      lambda n: prep(at[n], b + 1, 1 - s) if n in at else None)
                    pe.wait_ge(a.norm_done, U * b + U)
                    for u in range(U):
                        for kt in range(KT):
                            last = pe.transpose(a.mrow[:, kt, P * u:P * u + P],
                                                a.on[u][:, 8 * kt:8 * kt + 8, :].rearrange("p h e -> p (h e)"), c.ident[:])
                    last.then_inc(on_turned, 1)
                    pe.wait_ge(on_copied, b + 1)
                    for u in range(U):
                        for kt in range(KT):
                            last = pe.matmul(a.mrow[:, u, :], onT[:, kt, P * u:P * u + P], wvo[:, kt, 1, :],
                                             start=(kt == 0), stop=(kt == KT - 1))
                    last.then_inc(projected, 1)
                    pe.wait_ge(a.prep_done, b + 1)

        @block.scalar
        def _(act):
            def prep(step, n, s):
                if step == 0:
                    act.wait_ge(a.prep_filled, PREP * n + 1)
                    act.activation(a.xsT[:], a.prep[:], ACT.Copy).then_inc(a.prep_act, 1)
                if 1 <= step <= NG:
                    g = step - 1
                    act.wait_ge(a.prep_filled, PREP * n + 1 + step)
                    act.activation(a.qT[s][:, g, :], a.prep[:, 0, :], ACT.Identity, bias=bqk[:, 0, g:g + 1])
                    act.activation(a.kT[s][:, g, :], a.prep[:, 1, :], ACT.Identity,
                                   bias=bqk[:, 1, g:g + 1]).then_inc(a.prep_act, 1)
                if step == 5:
                    act.wait_ge(a.prep_filled, PREP * n + 6)
                    act.activation(a.penT[s][:], a.prep[:], ACT.Copy).then_inc(a.prep_act, 1)

            act.wait_ge(ready0, 1)
            for k in range(6):
                prep(k, 0, 0)
            at = {1: 0, 3: 1, 5: 2, 7: 3, 9: 4, 11: 5}
            with act.Fori(0, B // 2) as i:
                for s in range(2):
                    b = 2 * i + s
                    attention_core_act(act, a, b, HD ** -0.5,
                                       lambda n: prep(at[n], b + 1, 1 - s) if n in at else None)
                    act.wait_ge(on_turned, b + 1)
                    act.activation(onT[:], a.mrow[:], ACT.Copy).then_inc(on_copied, 1)

        @block.gpsimd
        def _(pool):
            pool.memset(bqk[:], 0.0).then_inc(pool_setup, 1)
            pool.wait_ge(mask_loaded, 16 * B)

            def prep(n, s):
                pool.tensor_copy(a.csT[:], c.ctxT[:, :, ds(n * S, S)]).then_inc(a.cs_ready, 1)
                pool.tensor_scalar(a.pen[s][:], mask_f[:], MASKED, -MASKED, ALU.mult, ALU.add).then_inc(pen_ready, 1)

            def mask_step(n):
                pool.tensor_copy(mask_f[:], mask[:, ds(n * U, U), :]).then_inc(a.pool_chain, 1)
                pool.wait_ge(a.pool_chain, n + 1)
            mask_step(0)
            prep(0, 0)
            with pool.Fori(0, B // 2) as i:
                for s in range(2):
                    n = 2 * i + s + 1
                    pool.wait_ge(a.prep_filled, PREP * n)
                    pool.wait_ge(a.max_scored, NH * (n - 1) + 1)
                    mask_step(n)
                    prep(n, 1 - s)

        @block.vector
        def _(dve):
            link = Chain(dve, a.dve_chain)
            link(dve.memset(a.mx[0][:], 0.0))
            link(dve.memset(a.mx[1][:], 0.0))
            link(dve.memset(wqk[:], 0.0))
            link(dve.memset(mask[:, NT:, :], 0))
            for s in range(2):
                link(dve.memset(a.va[s][:], 1.0))
            link(dve.tensor_reduce(row16[:], c.ident[:, HD:P:HP], AX, ALU.add))
            dve.wait_ge(a.w_loaded, WLOADS)
            for g in range(NG):
                link(dve.tensor_tensor(bqk[:, 1, g:g + 1], bqk[:, 1, g:g + 1], row16[:], ALU.add))
            for k in range(4):
                dve.wait_ge(a.w_turned, k + 1)
                for kt in range(KT):
                    if k < 2:
                        link(dve.tensor_copy(wqk[:, kt, k, :].rearrange("p (h e) -> p h e", e=HP)[:, :, 0:HD],
                                             a.prep[:, kt, :].rearrange("p (h e) -> p h e", e=HD)))
                    else:
                        link(dve.tensor_copy(wvo[:, kt, k - 2, :], a.prep[:, kt, :]))
                dve.sem_inc(a.w_copied, 1)
            moments(link, dve, c.st[:], a.mean[:], a.rstd[:], a.mt[:])
            rsqrt(link, dve, a.mt[:], a.rstd[:], a.xs[:, 0, 0:NTD])
            dve.sem_inc(ready0, 1)

            def prep(step, n, s):
                if step == 0:
                    for u in range(U):
                        t = U * n + u
                        last = dve.tensor_scalar(a.xs[:, u, :], c.x[:, t, :], a.mean[:, ds(t, 1)], a.rstd[:, ds(t, 1)],
                                                 ALU.subtract, ALU.mult)
                    last.then_inc(a.xs_ready, 1)
                if step == 1:
                    dve.wait_ge(a.prep_filled, PREP * n + 7)
                    for u in range(U):
                        last = dve.tensor_tensor(a.va[s][:, u, :, 0:HD], a.prep[:, u, :].rearrange("p (h e) -> p h e", e=HD),
                                                 bvo[:, 0, :].rearrange("p (h e) -> p h e", e=HD), ALU.add)
                    last.then_inc(a.prep_dve, 1)

            prep(0, 0, 0)
            prep(1, 0, 0)
            base = link.n
            at = {0: 0, 13: 1}
            with dve.Fori(0, B // 2) as i:
                for s in range(2):
                    b = 2 * i + s
                    link = Chain(dve, a.dve_chain, base + b * 4 * U)

                    def mid(n):
                        if n in at:
                            if at[n] == 0:
                                dve.wait_ge(a.prep_filled, PREP * b + 1)
                            prep(at[n], b + 1, 1 - s)
                    a.wait_qk(dve, b)
                    attention_core_dve(dve, a, b, s, mid)
                    dve.wait_ge(a.pv_done, NH * (b + 1))
                    for u in range(U):
                        link(dve.reciprocal(a.rden[u][:], a.po[u][:, :, HD:HD + 1]))
                        dve.tensor_tensor(a.on[u][:], a.po[u][:, :, 0:HD], a.rden[u][:].to_broadcast([P, NH, HD]),
                                          ALU.mult).then_inc(a.norm_done, 1)
                    dve.wait_ge(projected, b + 1)
                    for u in range(U):
                        t = U * b + u
                        link(dve.tensor_tensor(y[u][:], a.mrow[:, u, :], bvo[:, 1, :], ALU.add))
                        if u == U - 1:
                            dve.sem_inc(a.prep_done, 1)
                        link(dve.scalar_tensor_tensor(c.x[:, t, :], y[u][:], c.tg[:, 3:4], c.x[:, t, :], ALU.mult, ALU.add))
                        link(dve.bn_stats(c.st[:, t, :], c.x[:, t, :]))
            dve.wait_ge(a.prep_dve, B + 1)


QUADS = 4
NQ = NT // QUADS
QT = QUADS * P
FF0 = 1024 // P


def layer0_ffn(nc, I, c):
    with ExitStack() as ctx:
        sb = lambda n, s, d=F32: ctx.enter_context(nc.sbuf_tensor("l0f_" + n, s, d))
        ps = lambda n, s, d=F32: ctx.enter_context(nc.psum_tensor("l0f_" + n, s, d))
        sem = lambda n: c.semaphore("l0f_" + n)
        w_in, wq = sb("w_in", [P, KT, FF0 * P]), sb("wq", [P, KT, FF0 * P], BF16)
        wqT, wt = sb("wqT", [P, FF0, D], BF16), sb("wt", [P, D])
        wo, wot = sb("wo", [P, FF0, D]), sb("wot", [P, FF0, D])
        amax_in, mul_in, dq_in = sb("amax_in", [P, FF0]), sb("mul_in", [P, FF0]), sb("dq_in", [P, FF0])
        amax_out, mul_out = sb("amax_out", [P, FF0]), sb("mul_out", [P, FF0])
        b_in, b_out = sb("b_in", [P, FF0]), sb("b_out", [P, D])
        mean, rstd, mt, mt2 = sb("mean", [P, NTD]), sb("rstd", [P, NTD]), sb("mt", [P, NTD]), sb("mt2", [P, NTD])
        xn, xmax, xall = sb("xn", [P, NT, D]), sb("xmax", [P, NT]), sb("xall", [P, 4])
        xi, xh, xl = sb("xi", [P, QUADS, D]), sb("xh", [P, KT, QT], BF16), sb("xl", [P, KT, QT], BF16)
        hid, hmax, hall = sb("hid", [P, FF0, NT * P]), sb("hmax", [P, NQ * FF0]), sb("hall", [P, 4])
        hq, ht = [sb(f"hq{i}", [P, FF0, S]) for i in range(2)], sb("ht", [P, FF0, S])
        y = sb("y", [P, U, D])
        xt = ps("xt", [P, KT, QT])
        hb = [ps(f"hb{i}", [P, QT]) for i in range(3)]
        ob = [ps(f"ob{i}", [P, U, D]) for i in range(2)]
        wb = ps("wb", [P, 4, KT, P], BF16)
        w_loaded, wo_loaded, w_turned, w_int, w_back, w_ready = (sem(n) for n in ("w_loaded", "wo_loaded", "w_turned", "w_int", "w_back", "w_ready"))
        chain, pchain, wo_amax, wo_ready, x_amax, x_all = (sem(n) for n in ("chain", "pchain", "wo_amax", "wo_ready", "x_amax", "x_all"))
        xi_ready, x_turned, x_split, h_done, gelu_done, hmax_done = (sem(n) for n in ("xi_ready", "x_turned", "x_split", "h_done", "gelu_done", "hmax_done"))
        h_amax, h_all, hq_ready, out_done, out_added = (sem(n) for n in ("h_amax", "h_all", "hq_ready", "out_done", "out_added"))
        lnc = sem("lnc")
        block = ctx.enter_context(nc.Block())

        @block.sync
        def _(sp):
            sp.dma_start(w_in[:], I["L0_ffn_W_in"].rearrange("(t p) f -> p t f", p=P)).then_inc(w_loaded, 16)
            sp.dma_start(wo[:], I["L0_ffn_W_out"].rearrange("(t p) d -> p t d", p=P)).then_inc(wo_loaded, 16)
            sp.dma_start(b_in[:], col(I["L0_ffn_b_in"])).then_inc(w_loaded, 16)
            sp.dma_start(b_out[:], row(I["L0_ffn_b_out"])).then_inc(w_loaded, 16)

        @block.tensor
        def _(pe):
            pe.wait_ge(w_loaded, 48)
            for f in range(FF0):
                if f >= 2:
                    pe.wait_ge(w_int, f - 1)
                for kt in range(KT):
                    last = pe.transpose(hb[f % 2][:, P * kt:P * kt + P], w_in[:, kt, P * f:P * f + P], c.ident[:])
                last.then_inc(w_turned, 1)
            for half in range(FF0 // 4):
                pe.wait_ge(w_int, 4 * half + 4)
                pe.wait_ge(w_ready, half)
                for f in range(4):
                    for kt in range(KT):
                        last = pe.transpose(wb[:, f, kt, :], wqT[:, 4 * half + f, P * kt:P * kt + P], c.identb[:])
                last.then_inc(w_back, 1)
            pe.wait_ge(w_ready, FF0 // 4)
            with pe.Fori(0, NQ) as i:
                pe.wait_ge(xi_ready, i + 1)
                pe.wait_ge(x_split, i)
                for t in range(QUADS):
                    for kt in range(KT):
                        last = pe.transpose(xt[:, kt, P * t:P * t + P], xi[:, t, P * kt:P * kt + P], c.ident[:])
                last.then_inc(x_turned, 1)
                pe.wait_ge(x_split, i + 1)
                for f in range(FF0):
                    pe.wait_ge(gelu_done, FF0 * i + max(f - 2, 0))
                    for kt in range(KT):
                        for part in (xh, xl):
                            last = pe.matmul(hb[f % 3][:], wq[:, kt, P * f:P * f + P], part[:, kt, :],
                                             start=(kt == 0 and part is xh), stop=(kt == KT - 1 and part is xl))
                    last.then_inc(h_done, 1)
            pe.wait_ge(wo_ready, 1)
            with pe.Fori(0, B // 2) as i:
                for s in range(2):
                    b = 2 * i + s
                    pe.wait_ge(hq_ready, b + 1)
                    pe.wait_ge(out_added, 2 * i)
                    for u in range(U):
                        for f in range(FF0):
                            last = pe.matmul(ob[s][:, u, :], hq[s][:, f, P * u:P * u + P], wo[:, f, :],
                                             start=(f == 0), stop=(f == FF0 - 1))
                    last.then_inc(out_done, 1)

        @block.scalar
        def _(act):
            for half in range(FF0 // 4):
                act.wait_ge(w_back, half + 1)
                act.activation(wq[:, :, 4 * P * half:4 * P * half + 4 * P].rearrange("p k (f c) -> p f k c", c=P), wb[:],
                               ACT.Copy).then_inc(w_ready, 1)
            act.wait_ge(x_all, 2)
            act.wait_ge(w_loaded, 48)
            act.activation(xall[:, 3:4], xall[:, 0:1], ACT.Gelu)
            with act.Fori(0, NQ) as i:
                for f in range(FF0):
                    act.wait_ge(h_done, FF0 * i + f + 1)
                    act.activation(hid[:, f, ds(i * QT, QT)], hb[f % 3][:], ACT.Gelu,
                                   bias=b_in[:, f:f + 1], scale=dq_in[:, f:f + 1]).then_inc(gelu_done, 1)

        @block.gpsimd
        def _(pool):
            link = Chain(pool, pchain)
            pool.wait_ge(wo_loaded, 16)
            pool.wait_ge(wo_amax, 1)
            full = [P, FF0, D]
            link(pool.tensor_tensor(wot[:], wo[:], mul_out[:].unsqueeze(2).to_broadcast(full), ALU.mult))
            link(pool.tensor_scalar(wot[:], wot[:], ROUND, ROUND, ALU.add, ALU.subtract))
            link(pool.tensor_scalar(wot[:], wot[:], 127.0, -128.0, ALU.min, ALU.max))
            pool.tensor_tensor(wo[:], wot[:], amax_out[:].unsqueeze(2).to_broadcast(full), ALU.mult).then_inc(wo_ready, 1)
            pool.wait_ge(x_amax, 1)
            pool.partition_all_reduce(xall[:, 1:2], xall[:, 0:1], P, bass.bass_isa.ReduceOp.max).then_inc(x_all, 1)
            pool.wait_ge(h_amax, 1)
            pool.partition_all_reduce(hall[:, 1:2], hall[:, 0:1], P, bass.bass_isa.ReduceOp.max).then_inc(h_all, 1)

        @block.vector
        def _(dve):
            link = Chain(dve, chain)
            dve.wait_ge(wo_loaded, 16)
            link(dve.tensor_reduce(amax_out[:], wo[:], AX, ALU.max, apply_absolute_value=True))
            link(dve.tensor_scalar(amax_out[:], amax_out[:], 1e-8, None, ALU.max))
            link(dve.reciprocal(mul_out[:], amax_out[:]))
            link(dve.tensor_scalar(mul_out[:], mul_out[:], 127.0, None, ALU.mult))
            link(dve.tensor_scalar(amax_out[:], amax_out[:], 1.0 / 127.0, None, ALU.mult))
            dve.sem_inc(wo_amax, 1)
            for f in range(FF0):
                am, mul, tile = amax_in[:, f:f + 1], mul_in[:, f:f + 1], hb[f % 2][:, 0:D]
                dve.wait_ge(w_turned, f + 1)
                link(dve.tensor_reduce(am, tile, AX, ALU.max, apply_absolute_value=True))
                link(dve.tensor_scalar(am, am, 1e-8, None, ALU.max))
                link(dve.reciprocal(mul, am))
                link(dve.tensor_scalar(mul, mul, 127.0, None, ALU.mult))
                link(dve.tensor_scalar(wt[:], tile, mul, ROUND, ALU.mult, ALU.add))
                link(dve.tensor_scalar(wt[:], wt[:], ROUND, 127.0, ALU.subtract, ALU.min))
                dve.tensor_scalar(wqT[:, f, :], wt[:], -128.0, None, ALU.max).then_inc(w_int, 1)
                dve.wait_ge(w_int, f + 1)
            moments(link, dve, c.st[:], mean[:], rstd[:], mt[:])
            rsqrt(link, dve, mt[:], rstd[:], mt2[:])
            with dve.Fori(0, NT) as t:
                dve.tensor_scalar(xn[:, t, :], c.x[:, t, :], mean[:, ds(t, 1)], rstd[:, ds(t, 1)],
                                  ALU.subtract, ALU.mult).then_inc(lnc, 1)
                dve.wait_ge(lnc, 2 * t + 1)
                dve.tensor_reduce(xmax[:, ds(t, 1)], xn[:, t, :], AX, ALU.max, apply_absolute_value=True).then_inc(lnc, 1)
            dve.wait_ge(lnc, 2 * NT)
            link(dve.tensor_reduce(xall[:, 0:1], xmax[:], AX, ALU.max))
            dve.sem_inc(x_amax, 1)
            dve.wait_ge(x_all, 1)
            link(dve.tensor_scalar(xall[:, 1:2], xall[:, 1:2], 1e-8, None, ALU.max))
            link(dve.reciprocal(xall[:, 2:3], xall[:, 1:2]))
            link(dve.tensor_scalar(xall[:, 2:3], xall[:, 2:3], 32767.0, None, ALU.mult))
            link(dve.tensor_scalar(dq_in[:], amax_in[:], xall[:, 1:2], 1.0 / (127.0 * 32767.0), ALU.mult, ALU.mult))
            dve.sem_inc(x_all, 1)
            base = link.n
            with dve.Fori(0, NQ) as i:
                link = Chain(dve, chain, base + i * 3)
                dve.wait_ge(x_turned, i)
                link(dve.tensor_scalar(xi[:], xn[:, ds(i * QUADS, QUADS), :], xall[:, 2:3], ROUND, ALU.mult, ALU.add))
                link(dve.tensor_scalar(xi[:], xi[:], ROUND, 32767.0, ALU.subtract, ALU.min))
                dve.tensor_scalar(xi[:], xi[:], -32768.0, None, ALU.max).then_inc(xi_ready, 1)
                dve.wait_ge(x_turned, i + 1)
                dve.wait_ge(h_done, FF0 * i)
                link(dve.tensor_scalar(xh[:], xt[:], ROUND256, ROUND256, ALU.add, ALU.subtract))
                dve.tensor_tensor(xl[:], xt[:], xh[:], ALU.subtract).then_inc(x_split, 1)
                for f in range(FF0):
                    dve.wait_ge(gelu_done, FF0 * i + f + 1)
                    dve.tensor_reduce(hmax[:, ds(i * FF0 + f, 1)], hid[:, f, ds(i * QT, QT)], AX, ALU.max,
                                      apply_absolute_value=True).then_inc(hmax_done, 1)
            dve.wait_ge(hmax_done, NQ * FF0)
            link = Chain(dve, chain, base + NQ * 3)
            link(dve.tensor_reduce(hall[:, 0:1], hmax[:], AX, ALU.max))
            dve.sem_inc(h_amax, 1)
            dve.wait_ge(h_all, 1)
            link(dve.tensor_scalar(hall[:, 1:2], hall[:, 1:2], 1e-8, None, ALU.max))
            link(dve.reciprocal(hall[:, 2:3], hall[:, 1:2]))
            link(dve.tensor_scalar(hall[:, 2:3], hall[:, 2:3], 32767.0, None, ALU.mult))
            link(dve.tensor_scalar(hall[:, 3:4], hall[:, 1:2], 1.0 / 32767.0, None, ALU.mult))
            base = base + NQ * 3 + link.n

            def quantise(link, b, s):
                link(dve.tensor_scalar(ht[:], hid[:, :, ds(b * S, S)], hall[:, 2:3], ROUND, ALU.mult, ALU.add))
                link(dve.tensor_scalar(ht[:], ht[:], ROUND, 32767.0, ALU.subtract, ALU.min))
                dve.tensor_scalar(hq[s][:], ht[:], -32768.0, hall[:, 3:4], ALU.max, ALU.mult).then_inc(hq_ready, 1)
                dve.wait_ge(hq_ready, b + 1)

            def add_out(link, b, s):
                dve.wait_ge(out_done, b + 1)
                dve.tensor_tensor(y[:], ob[s][:], b_out[:].unsqueeze(1).to_broadcast([P, U, D]), ALU.add).then_inc(out_added, 1)
                dve.wait_ge(out_added, b + 1)
                v = c.x[:, ds(b * U, U), :].rearrange("p u d -> p (u d)")
                link(dve.scalar_tensor_tensor(v, y[:].rearrange("p u d -> p (u d)"), c.tg[:, 4:5], v, ALU.mult, ALU.add))
                for u in range(U):
                    link(dve.bn_stats(c.st[:, U * b + u, :], c.x[:, U * b + u, :]))

            with dve.Fori(0, B // 2) as i:
                link = Chain(dve, chain, base + i * 10)
                quantise(link, 2 * i, 0)
                quantise(link, 2 * i + 1, 1)
                add_out(link, 2 * i, 0)
                add_out(link, 2 * i + 1, 1)


FF3, FF3W = 6, 704
FF3R = FF3W - (FF3 - 1) * P


def layer3_ffn(nc, I, c):
    with ExitStack() as ctx:
        sb = lambda n, s, d=F32: ctx.enter_context(nc.sbuf_tensor("l3f_" + n, s, d))
        ps = lambda n, s, d=F32: ctx.enter_context(nc.psum_tensor("l3f_" + n, s, d))
        sem = lambda n: c.semaphore("l3f_" + n)
        w_up = sb("w_up", [P, 2, FF3, D])
        w_dn = sb("w_dn", [P, KT, FF3W])
        q_up, q_dn = sb("q_up", [P, 2, FF3, D], BF16), sb("q_dn", [P, KT, FF3W], BF16)
        upT, dnT = sb("upT", [P, KT, 2, FF3W], BF16), sb("dnT", [P, FF3, D], BF16)
        am_up, mul_up, dq_up = (sb(n, [P, 2, FF3]) for n in ("am_up", "mul_up", "dq_up"))
        am_dn, mul_dn = sb("am_dn", [P, KT]), sb("mul_dn", [P, KT])
        diag, dn_row = sb("diag", [P, KT, P]), sb("dn_row", [P, D])
        mean, rstd, mt, mt2 = sb("mean", [P, NTD]), sb("rstd", [P, NTD]), sb("mt", [P, NTD]), sb("mt2", [P, NTD])
        xn, xmax, xall = sb("xn", [P, NT, D]), sb("xmax", [P, NT]), sb("xall", [P, 4])
        clip = sb("clip", [P, 2])
        xt1, xq, xT = sb("xt1", [P, QUADS, D]), sb("xq", [P, QUADS, D], BF16), sb("xT", [P, KT, QT], BF16)
        sg = [sb(f"sg{i}", [P, QT]) for i in range(2)]
        hid, hmax, hall = sb("hid", [P, FF3, NT * P]), sb("hmax", [P, NQ * FF3]), sb("hall", [P, 4])
        ht, hq = sb("ht", [P, FF3, S]), [sb(f"hq{i}", [P, FF3, S], BF16) for i in range(2)]
        y = sb("y", [P, U, D])
        xb = ps("xb", [P, KT, QT], BF16)
        gb = [ps(f"gb{i}", [P, QT]) for i in range(2)]
        ub = [ps(f"ub{i}", [P, QT]) for i in range(2)]
        ob = [ps(f"ob{i}", [P, U, D]) for i in range(2)]
        wb = ps("wb", [P, 8 * P], BF16)
        names = ("w_loaded", "chain", "zeroed", "w_int", "w_back", "w_ready", "clip_ready", "x_amax", "x_all", "xq_ready",
                 "x_turned", "x_copied", "gate_done", "up_done", "silu_done", "h_ready", "hmax_done", "h_amax", "h_all",
                 "hq_ready", "out_done", "out_taken", "lnc", "row_done", "diag_ready", "scales_ready")
        (w_loaded, chain, zeroed, w_int, w_back, w_ready, clip_ready, x_amax, x_all, xq_ready, x_turned, x_copied,
         gate_done, up_done, silu_done, h_ready, hmax_done, h_amax, h_all, hq_ready, out_done, out_taken, lnc,
         row_done, diag_ready, scales_ready) = (sem(n) for n in names)
        block = ctx.enter_context(nc.Block())
        FULL = (FF3 - 1) * P
        rows = lambda t: P if t < FF3 - 1 else FF3R
        WLOADS = 16 * 8

        @block.sync
        def _(sp):
            for k, n in enumerate(("gate", "up")):
                w = I["L3_ffn_w_" + n]
                sp.dma_start(w_up[:, k, 0:FF3 - 1, :], w[0:FULL, :].rearrange("(t p) d -> p t d", p=P)).then_inc(w_loaded, 16)
                sp.dma_start(w_up[0:FF3R, k, FF3 - 1, :], w[FULL:, :]).then_inc(w_loaded, 16)
            for kt in range(KT):
                sp.dma_start(w_dn[:, kt, :], I["L3_ffn_w_down"][P * kt:P * kt + P, :]).then_inc(w_loaded, 16)
            sp.dma_start(clip[:, 0:1], row(I["L3_ffn_clip_x"])).then_inc(w_loaded, 16)
            sp.dma_start(clip[:, 1:2], row(I["L3_ffn_clip_down"])).then_inc(w_loaded, 16)

        UP_JOBS = [(k, kt) for k in range(2) for kt in range(KT)]
        DN_JOBS = [(0, 1, 2), (3, 4), (5,)]
        N_JOBS = len(UP_JOBS) + len(DN_JOBS)
        turn_bank = [wb, xb[:].rearrange("p k n -> p (k n)")]

        @block.tensor
        def _(pe):
            pe.wait_ge(w_int, 3)
            for n in range(N_JOBS):
                bank = turn_bank[n % 2]
                if n >= 2:
                    pe.wait_ge(w_ready, n - 1)
                if n < len(UP_JOBS):
                    k, kt = UP_JOBS[n]
                    for t in range(FF3):
                        r = rows(t)
                        last = pe.transpose(bank[:, P * t:P * t + r], q_up[0:r, k, t, P * kt:P * kt + P], c.identb[0:r, 0:r])
                else:
                    for m, t in enumerate(DN_JOBS[n - len(UP_JOBS)]):
                        r = rows(t)
                        for kt in range(KT):
                            last = pe.transpose(bank[0:r, D * m + P * kt:D * m + P * kt + P], q_dn[:, kt, P * t:P * t + r],
                                                c.identb[:])
                last.then_inc(w_back, 1)
            pe.wait_ge(diag_ready, 1)
            for kt in range(KT):
                last = pe.matmul(ob[0][:, 0, P * kt:P * kt + P], c.ones[:], diag[:, kt, :], start=True, stop=True)
            last.then_inc(row_done, 1)
            pe.wait_ge(w_ready, N_JOBS)
            with pe.Fori(0, NQ) as i:
                pe.wait_ge(xq_ready, i + 1)
                pe.wait_ge(x_copied, i)
                for t in range(QUADS):
                    for kt in range(KT):
                        last = pe.transpose(xb[:, kt, P * t:P * t + P], xq[:, t, P * kt:P * kt + P], c.identb[:])
                last.then_inc(x_turned, 1)
                pe.wait_ge(x_copied, i + 1)
                for t in range(FF3):
                    r = rows(t)
                    pe.wait_ge(h_ready, FF3 * i + max(t - 1, 0))
                    for k, bank, done in ((0, gb, gate_done), (1, ub, up_done)):
                        for kt in range(KT):
                            last = pe.matmul(bank[t % 2][0:r, :], upT[:, kt, k, P * t:P * t + r], xT[:, kt, :],
                                             start=(kt == 0), stop=(kt == KT - 1))
                        last.then_inc(done, 1)
            with pe.Fori(0, B // 2) as i:
                for s in range(2):
                    b = 2 * i + s
                    pe.wait_ge(hq_ready, b + 1)
                    pe.wait_ge(out_taken, 2 * i)
                    for u in range(U):
                        for t in range(FF3):
                            r = rows(t)
                            last = pe.matmul(ob[s][:, u, :], hq[s][0:r, t, P * u:P * u + P], dnT[0:r, t, :],
                                             start=(t == 0), stop=(t == FF3 - 1))
                    last.then_inc(out_done, 1)

        @block.scalar
        def _(act):
            act.wait_ge(w_loaded, WLOADS)
            act.activation(clip[:], clip[:], ACT.Sigmoid).then_inc(clip_ready, 1)
            for n in range(N_JOBS):
                act.wait_ge(w_back, n + 1)
                bank = turn_bank[n % 2]
                if n < len(UP_JOBS):
                    k, kt = UP_JOBS[n]
                    act.activation(upT[:, kt, k, :], bank[:, 0:FF3W], ACT.Copy).then_inc(w_ready, 1)
                else:
                    ts = DN_JOBS[n - len(UP_JOBS)]
                    r = rows(ts[-1])
                    act.activation(dnT[0:r, ts[0]:ts[-1] + 1, :], bank[0:r, 0:D * len(ts)], ACT.Copy).then_inc(w_ready, 1)
            act.wait_ge(scales_ready, 1)
            act.activation(xall[:, 3:4], xall[:, 0:1], ACT.Silu)
            with act.Fori(0, NQ) as i:
                act.wait_ge(x_turned, i + 1)
                act.activation(xT[:], xb[:], ACT.Copy).then_inc(x_copied, 1)
                for t in range(FF3):
                    r = rows(t)
                    act.wait_ge(gate_done, FF3 * i + t + 1)
                    act.wait_ge(h_ready, FF3 * i + max(t - 1, 0))
                    act.activation(sg[t % 2][0:r, :], gb[t % 2][0:r, :], ACT.Silu,
                                   scale=dq_up[0:r, 0, t:t + 1]).then_inc(silu_done, 1)

        @block.gpsimd
        def _(pool):
            pool.memset(hid[:, FF3 - 1, :], 0.0).then_inc(zeroed, 1)
            pool.memset(hmax[:], 0.0).then_inc(zeroed, 1)
            pool.wait_ge(x_amax, 1)
            pool.partition_all_reduce(xall[:, 1:2], xall[:, 0:1], P, bass.bass_isa.ReduceOp.max).then_inc(x_all, 1)
            pool.wait_ge(h_amax, 1)
            pool.partition_all_reduce(hall[:, 1:2], hall[:, 0:1], P, bass.bass_isa.ReduceOp.max).then_inc(h_all, 1)

        @block.vector
        def _(dve):
            link = Chain(dve, chain)
            link(dve.memset(w_up[FF3R:, :, FF3 - 1, :], 1.0))
            dve.wait_ge(w_loaded, WLOADS)
            link(dve.tensor_reduce(am_up[:], w_up[:], AX, ALU.max, apply_absolute_value=True))
            link(dve.tensor_reduce(am_dn[:], w_dn[:], AX, ALU.max, apply_absolute_value=True))
            for am, mul in ((am_up, mul_up), (am_dn, mul_dn)):
                link(dve.tensor_scalar(am[:], am[:], 1.0 / 127.0, None, ALU.mult))
                link(dve.reciprocal(mul[:], am[:]))
            for w, q, mul in ((w_up[:, 0], q_up[:, 0], mul_up[:, 0]), (w_up[:, 1], q_up[:, 1], mul_up[:, 1]),
                              (w_dn[:], q_dn[:], mul_dn[:])):
                full = list(w.shape)
                link(dve.tensor_tensor(w, w, mul.unsqueeze(2).to_broadcast(full), ALU.mult))
                link(dve.tensor_scalar(w, w, ROUND, ROUND, ALU.add, ALU.subtract))
                link(dve.tensor_scalar(q, w, 127.0, -128.0, ALU.min, ALU.max))
                dve.sem_inc(w_int, 1)
            for kt in range(KT):
                link(dve.tensor_scalar(diag[:, kt, :], c.ident[:], am_dn[:, kt:kt + 1], None, ALU.mult))
            dve.sem_inc(diag_ready, 1)
            moments(link, dve, c.st[:], mean[:], rstd[:], mt[:])
            rsqrt(link, dve, mt[:], rstd[:], mt2[:])
            with dve.Fori(0, NT) as t:
                dve.tensor_scalar(xn[:, t, :], c.x[:, t, :], mean[:, ds(t, 1)], rstd[:, ds(t, 1)],
                                  ALU.subtract, ALU.mult).then_inc(lnc, 1)
                dve.wait_ge(lnc, 2 * t + 1)
                dve.tensor_reduce(xmax[:, ds(t, 1)], xn[:, t, :], AX, ALU.max, apply_absolute_value=True).then_inc(lnc, 1)
            dve.wait_ge(lnc, 2 * NT)
            link(dve.tensor_reduce(xall[:, 0:1], xmax[:], AX, ALU.max))
            dve.sem_inc(x_amax, 1)
            dve.wait_ge(x_all, 1)
            dve.wait_ge(clip_ready, 1)
            link(dve.tensor_scalar(xall[:, 1:2], xall[:, 1:2], clip[:, 0:1], 1.0 / 127.0, ALU.mult, ALU.mult))
            link(dve.reciprocal(xall[:, 2:3], xall[:, 1:2]))
            link(dve.tensor_scalar(dq_up[:], am_up[:], xall[:, 1:2], None, ALU.mult))
            dve.sem_inc(scales_ready, 1)
            dve.wait_ge(row_done, 1)
            link(dve.tensor_copy(dn_row[:], ob[0][:, 0, :]))
            base = link.n
            dve.wait_ge(zeroed, 2)
            with dve.Fori(0, NQ) as i:
                link = Chain(dve, chain, base + i * 2)
                dve.wait_ge(x_turned, i)
                link(dve.tensor_scalar(xt1[:], xn[:, ds(i * QUADS, QUADS), :], xall[:, 2:3], ROUND, ALU.mult, ALU.add))
                link(dve.tensor_scalar(xt1[:], xt1[:], ROUND, 127.0, ALU.subtract, ALU.min))
                dve.tensor_scalar(xq[:], xt1[:], -128.0, None, ALU.max).then_inc(xq_ready, 1)
                for t in range(FF3):
                    r = rows(t)
                    dve.wait_ge(silu_done, FF3 * i + t + 1)
                    dve.wait_ge(up_done, FF3 * i + t + 1)
                    h = hid[0:r, t, ds(i * QT, QT)]
                    dve.scalar_tensor_tensor(h, ub[t % 2][0:r, :], dq_up[0:r, 1, t:t + 1], sg[t % 2][0:r, :],
                                             ALU.mult, ALU.mult).then_inc(h_ready, 1)
                    dve.wait_ge(h_ready, FF3 * i + t + 1)
                    dve.tensor_reduce(hmax[0:r, ds(i * FF3 + t, 1)], h, AX, ALU.max,
                                      apply_absolute_value=True).then_inc(hmax_done, 1)
            dve.wait_ge(hmax_done, NQ * FF3)
            link = Chain(dve, chain, base + NQ * 2)
            link(dve.tensor_reduce(hall[:, 0:1], hmax[:], AX, ALU.max))
            dve.sem_inc(h_amax, 1)
            dve.wait_ge(h_all, 1)
            link(dve.tensor_scalar(hall[:, 1:2], hall[:, 1:2], clip[:, 1:2], 1.0 / 127.0, ALU.mult, ALU.mult))
            link(dve.reciprocal(hall[:, 2:3], hall[:, 1:2]))
            link(dve.tensor_scalar(dn_row[:], dn_row[:], hall[:, 1:2], c.tg[:, 7:8], ALU.mult, ALU.mult))
            base = base + NQ * 2 + link.n

            def quantise(link, b, s):
                link(dve.tensor_scalar(ht[:], hid[:, :, ds(b * S, S)], hall[:, 2:3], ROUND, ALU.mult, ALU.add))
                link(dve.tensor_scalar(ht[:], ht[:], ROUND, 127.0, ALU.subtract, ALU.min))
                dve.tensor_scalar(hq[s][:], ht[:], -128.0, None, ALU.max).then_inc(hq_ready, 1)
                dve.wait_ge(hq_ready, b + 1)

            def add_out(link, b, s):
                dve.wait_ge(out_done, b + 1)
                dve.tensor_tensor(y[:], ob[s][:], dn_row[:].unsqueeze(1).to_broadcast([P, U, D]), ALU.mult).then_inc(out_taken, 1)
                dve.wait_ge(out_taken, b + 1)
                v = c.x[:, ds(b * U, U), :]
                link(dve.tensor_tensor(v, y[:], v, ALU.add))

            with dve.Fori(0, B // 2) as i:
                link = Chain(dve, chain, base + i * 6)
                quantise(link, 2 * i, 0)
                quantise(link, 2 * i + 1, 1)
                add_out(link, 2 * i, 0)
                add_out(link, 2 * i + 1, 1)


FF1 = 1024 // P


def layer1_attention(nc, I, c):
    with ExitStack() as ctx:
        sb = lambda n, s, d=F32: ctx.enter_context(nc.sbuf_tensor("l1a_" + n, s, d))
        ps = lambda n, s, d=F32: ctx.enter_context(nc.psum_tensor("l1a_" + n, s, d))
        sem = lambda n: c.semaphore("l1a_" + n)
        INNER = FF1 * P
        wv, wvT, wout = sb("wv", [P, KT, INNER]), sb("wvT", [P, FF1, D]), sb("wout", [P, FF1, D])
        wf, bout = sb("wf", [P, KT, D]), sb("bout", [P, D])
        csT = [sb(f"csT{i}", [P, KT, S]) for i in range(2)]
        y = sb("y", [P, U, D])
        tb = [ps(f"tb{i}", [P, 2, D]) for i in range(2)]
        fb = ps("fb", [P, KT, D])
        ob = [ps(f"ob{i}", [P, U, D]) for i in range(2)]
        w_loaded, turned, copied, fused, wf_ready, cs_ready, out_done, out_taken, chain = (
            sem(n) for n in ("w_loaded", "turned", "copied", "fused", "wf_ready", "cs_ready", "out_done", "out_taken", "chain"))
        block = ctx.enter_context(nc.Block())

        @block.sync
        def _(sp):
            sp.dma_start(wv[:], I["L1_xattn_Wkv"][:, INNER:].rearrange("(t p) f -> p t f", p=P)).then_inc(w_loaded, 16)
            sp.dma_start(wout[:], I["L1_xattn_Wout"].rearrange("(t p) d -> p t d", p=P)).then_inc(w_loaded, 16)
            sp.dma_start(bout[:], row(I["L1_xattn_bout"])).then_inc(w_loaded, 16)

        @block.tensor
        def _(pe):
            pe.wait_ge(w_loaded, 48)
            for n in range(FF1 // 2):
                if n >= 2:
                    pe.wait_ge(copied, n - 1)
                for m in range(2):
                    for kt in range(KT):
                        last = pe.transpose(tb[n % 2][:, m, P * kt:P * kt + P],
                                            wv[:, kt, P * (2 * n + m):P * (2 * n + m) + P], c.ident[:])
                last.then_inc(turned, 1)
            pe.wait_ge(copied, FF1 // 2)
            for kt in range(KT):
                for f in range(FF1):
                    last = pe.matmul(fb[:, kt, :], wvT[:, f, P * kt:P * kt + P], wout[:, f, :], start=(f == 0), stop=(f == FF1 - 1))
            last.then_inc(fused, 1)
            pe.wait_ge(wf_ready, 1)
            with pe.Fori(0, B // 2) as i:
                for s in range(2):
                    pe.wait_ge(cs_ready, 2 * i + s + 1)
                    pe.wait_ge(out_taken, 2 * i)
                    for u in range(U):
                        for kt in range(KT):
                            last = pe.matmul(ob[s][:, u, :], csT[s][:, kt, P * u:P * u + P], wf[:, kt, :],
                                             start=(kt == 0), stop=(kt == KT - 1))
                    last.then_inc(out_done, 1)

        @block.scalar
        def _(act):
            for n in range(FF1 // 2):
                act.wait_ge(turned, n + 1)
                act.activation(wvT[:, 2 * n:2 * n + 2, :], tb[n % 2][:], ACT.Copy).then_inc(copied, 1)
            act.wait_ge(fused, 1)
            act.activation(wf[:], fb[:], ACT.Copy).then_inc(wf_ready, 1)

        @block.gpsimd
        def _(pool):
            with pool.Fori(0, B // 2) as i:
                for s in range(2):
                    pool.wait_ge(out_done, 2 * i)
                    pool.tensor_copy(csT[s][:], c.ctxT[:, :, ds((2 * i + s) * S, S)]).then_inc(cs_ready, 1)

        @block.vector
        def _(dve):
            dve.wait_ge(w_loaded, 48)
            with dve.Fori(0, B // 2) as i:
                link = Chain(dve, chain, i * 6)
                for s in range(2):
                    b = 2 * i + s
                    dve.wait_ge(out_done, b + 1)
                    dve.tensor_tensor(y[:], ob[s][:], bout[:].unsqueeze(1).to_broadcast([P, U, D]), ALU.add).then_inc(out_taken, 1)
                    dve.wait_ge(out_taken, b + 1)
                    v = c.x[:, ds(b * U, U), :].rearrange("p u d -> p (u d)")
                    link(dve.scalar_tensor_tensor(v, y[:].rearrange("p u d -> p (u d)"), c.tg[:, 1:2], v, ALU.mult, ALU.add))
                    for u in range(U):
                        link(dve.bn_stats(c.st[:, U * b + u, :], c.x[:, U * b + u, :]))


def layer1_ffn(nc, I, c):
    with ExitStack() as ctx:
        sb = lambda n, s, d=F32: ctx.enter_context(nc.sbuf_tensor("l1f_" + n, s, d))
        ps = lambda n, s, d=F32: ctx.enter_context(nc.psum_tensor("l1f_" + n, s, d))
        sem = lambda n: c.semaphore("l1f_" + n)
        w1 = [sb(f"w1_{i}", [P, FF1, D]) for i in range(2)]
        w2 = [sb(f"w2_{i}", [P, KT, FF1 * P]) for i in range(2)]
        w2T = [sb(f"w2T{i}", [P, FF1, D]) for i in range(2)]
        b1_rows, b1_cols, b2 = sb("b1_rows", [B * FF1, P]), sb("b1_cols", [P, B * FF1]), sb("b2", [P, B, D])
        b1s = [sb(f"b1s{i}", [P, FF1, P]) for i in range(2)]
        wf, bf = sb("wf", [P, KT, D]), sb("bf", [P, D])
        xs, xsT, y = sb("xs", [P, U, D]), sb("xsT", [P, KT, S]), sb("y", [P, U, D])
        mean, rstd, mt, mt2 = sb("mean", [P, NTD]), sb("rstd", [P, NTD]), sb("mt", [P, NTD]), sb("mt2", [P, NTD])
        tb = [ps(f"tb{i}", [P, 2, D]) for i in range(2)]
        fb, bb, xb, ob = ps("fb", [P, KT, D]), ps("bb", [P, D]), ps("xb", [P, KT, S]), ps("ob", [P, U, D])
        w1_loaded, w2_loaded = [sem(f"w1_loaded{i}") for i in range(2)], [sem(f"w2_loaded{i}") for i in range(2)]
        names = ("b_loaded", "b1_turned", "b1_ready", "b1s_ready", "turned", "copied", "fused",
                 "wf_ready", "xs_ready", "x_turned", "x_copied", "out_done", "out_taken", "chain")
        (b_loaded, b1_turned, b1_ready, b1s_ready, turned, copied, fused,
         wf_ready, xs_ready, x_turned, x_copied, out_done, out_taken, chain) = (sem(n) for n in names)
        block = ctx.enter_context(nc.Block())
        J = FF1 // 2

        @block.sync
        def _(sp):
            sp.dma_start(b1_rows[:], I["L1_ffn_b1"].rearrange("g (t p) -> (g t) p", p=P)).then_inc(b_loaded, 16)
            sp.dma_start(b2[:], row(I["L1_ffn_b2"])).then_inc(b_loaded, 16)
            for b in range(B):
                if b >= 2:
                    sp.wait_ge(fused, b - 1)
                sp.dma_start(w2[b % 2][:], I["L1_ffn_W2"][b].rearrange("(t p) f -> p t f", p=P)).then_inc(w2_loaded[b % 2], 16)
                sp.dma_start(w1[b % 2][:], I["L1_ffn_W1"][b].rearrange("(t p) d -> p t d", p=P)).then_inc(w1_loaded[b % 2], 16)

        @block.tensor
        def _(pe):
            pe.wait_ge(b_loaded, 32)
            pe.transpose(xb[:, 0, 0:B * FF1], b1_rows[:], c.ident[0:B * FF1, 0:B * FF1]).then_inc(b1_turned, 1)
            pe.wait_ge(b1_ready, 1)
            with pe.Fori(0, B // 2) as i:
                for s in range(2):
                    b = 2 * i + s
                    pe.wait_ge(w2_loaded[s], 16 * i + 16)
                    for n in range(J):
                        pe.wait_ge(copied, J * b + max(n - 1, 0))
                        for m in range(2):
                            for kt in range(KT):
                                last = pe.transpose(tb[n % 2][:, m, P * kt:P * kt + P],
                                                    w2[s][:, kt, P * (2 * n + m):P * (2 * n + m) + P], c.ident[:])
                        last.then_inc(turned, 1)
                    pe.wait_ge(xs_ready, b + 1)
                    pe.wait_ge(x_copied, b)
                    for u in range(U):
                        for kt in range(KT):
                            last = pe.transpose(xb[:, kt, P * u:P * u + P], xs[:, u, P * kt:P * kt + P], c.ident[:])
                    last.then_inc(x_turned, 1)
                    pe.wait_ge(copied, J * b + J)
                    pe.wait_ge(w1_loaded[s], 16 * i + 16)
                    pe.wait_ge(b1s_ready, b + 1)
                    pe.wait_ge(wf_ready, 2 * b)
                    for f in range(FF1):
                        pe.matmul(bb[:], b1s[s][:, f, :], w2T[s][:, f, :], start=(f == 0), stop=(f == FF1 - 1))
                    for kt in range(KT):
                        for f in range(FF1):
                            last = pe.matmul(fb[:, kt, :], w1[s][:, f, P * kt:P * kt + P], w2T[s][:, f, :],
                                             start=(f == 0), stop=(f == FF1 - 1))
                    last.then_inc(fused, 1)
                    pe.wait_ge(wf_ready, 2 * b + 2)
                    pe.wait_ge(x_copied, b + 1)
                    pe.wait_ge(out_taken, b)
                    for u in range(U):
                        for kt in range(KT):
                            last = pe.matmul(ob[:, u, :], xsT[:, kt, P * u:P * u + P], wf[:, kt, :],
                                             start=(kt == 0), stop=(kt == KT - 1))
                    last.then_inc(out_done, 1)

        @block.scalar
        def _(act):
            act.wait_ge(b1_turned, 1)
            act.activation(b1_cols[:], xb[:, 0, 0:B * FF1], ACT.Copy).then_inc(b1_ready, 1)
            with act.Fori(0, B // 2) as i:
                for s in range(2):
                    b = 2 * i + s
                    for n in range(J):
                        act.wait_ge(turned, J * b + n + 1)
                        act.activation(w2T[s][:, 2 * n:2 * n + 2, :], tb[n % 2][:], ACT.Copy).then_inc(copied, 1)
                    act.wait_ge(x_turned, b + 1)
                    act.activation(xsT[:], xb[:], ACT.Copy).then_inc(x_copied, 1)
                    act.wait_ge(fused, b + 1)
                    act.wait_ge(out_done, b)
                    act.activation(wf[:], fb[:], ACT.Copy).then_inc(wf_ready, 1)

        @block.gpsimd
        def _(pool):
            pool.wait_ge(b1_ready, 1)
            with pool.Fori(0, B // 2) as i:
                for s in range(2):
                    b = 2 * i + s
                    pool.wait_ge(fused, 2 * i)
                    pool.tensor_copy(b1s[s][:], b1_cols[:, ds(b * FF1, FF1)].unsqueeze(2).to_broadcast([P, FF1, P])).then_inc(b1s_ready, 1)

        @block.vector
        def _(dve):
            link = Chain(dve, chain)
            moments(link, dve, c.st[:], mean[:], rstd[:], mt[:])
            rsqrt(link, dve, mt[:], rstd[:], mt2[:])
            dve.wait_ge(b_loaded, 32)
            base = link.n

            def rows_of(n):
                for u in range(U):
                    t = U * n + u
                    last = dve.tensor_scalar(xs[:, u, :], c.x[:, t, :], mean[:, ds(t, 1)], rstd[:, ds(t, 1)], ALU.subtract, ALU.mult)
                last.then_inc(xs_ready, 1)
            rows_of(0)
            with dve.Fori(0, B) as b:
                link = Chain(dve, chain, base + b * 3)
                dve.wait_ge(fused, b + 1)
                dve.tensor_tensor(bf[:], bb[:], b2[:, b, :], ALU.add).then_inc(wf_ready, 1)
                dve.wait_ge(wf_ready, 2 * b + 2)
                rows_of(b + 1)
                dve.wait_ge(out_done, b + 1)
                dve.tensor_tensor(y[:], ob[:], bf[:].unsqueeze(1).to_broadcast([P, U, D]), ALU.add).then_inc(out_taken, 1)
                dve.wait_ge(out_taken, b + 1)
                v = c.x[:, ds(b * U, U), :].rearrange("p u d -> p (u d)")
                link(dve.scalar_tensor_tensor(v, y[:].rearrange("p u d -> p (u d)"), c.tg[:, 5:6], v, ALU.mult, ALU.add))
                for u in range(U):
                    link(dve.bn_stats(c.st[:, U * b + u, :], c.x[:, U * b + u, :]))


H2, HD2 = 8, 32


def layer2_attention(nc, I, c):
    with ExitStack() as ctx:
        sb = lambda n, s, d=F32: ctx.enter_context(nc.sbuf_tensor("l2a_" + n, s, d))
        ps = lambda n, s, d=F32: ctx.enter_context(nc.psum_tensor("l2a_" + n, s, d))
        sem = lambda n: c.semaphore("l2a_" + n)
        w_in, wT = sb("w_in", [P, 4, KT, D]), sb("wT", [P, 4, KT, D])
        xs, xsT = sb("xs", [P, U, D]), sb("xsT", [P, KT, S])
        csT = sb("csT", [P, KT, S])
        qT, kT = [sb(f"qT{i}", [P, 2, S]) for i in range(2)], [sb(f"kT{i}", [P, 2, S]) for i in range(2)]
        vs = [sb(f"vs{i}", [P, U, D]) for i in range(2)]
        mx = [sb(f"mx{i}", [P, S]) for i in range(2)]
        low = [sb(f"low{i}", [P, 4, 2, S]) for i in range(2)]
        ex = [sb(f"ex{i}", [P, 4, 2, S]) for i in range(2)]
        den, rden = [sb(f"den{i}", [P, S]) for i in range(2)], [sb(f"rden{i}", [P, S]) for i in range(2)]
        oT = sb("oT", [P, 2, S])
        mean, rstd, mt, mt2 = sb("mean", [P, NTD]), sb("rstd", [P, NTD]), sb("mt", [P, NTD]), sb("mt2", [P, NTD])
        sc = ps("sc", [P, 4, 2, S])
        po = [ps(f"po{i}", [P, S]) for i in range(2)]
        pb = [ps(f"pb{i}", [P, 2, S]) for i in range(2)]
        names = ("w_loaded", "w_turned", "w_copied", "chain", "xs_ready", "cs_ready", "filled", "copied", "scored", "lowered",
                 "exp_done", "rden_ready", "weighted", "pv_done", "o_copied", "out_done", "out_taken", "ready0", "maxed")
        (w_loaded, w_turned, w_copied, chain, xs_ready, cs_ready, filled, copied, scored, lowered,
         exp_done, rden_ready, weighted, pv_done, o_copied, out_done, out_taken, ready0, maxed) = (sem(n) for n in names)
        block = ctx.enter_context(nc.Block())

        @block.sync
        def _(sp):
            for k, n in enumerate("QKVO"):
                sp.dma_start(w_in[:, k], I["L2_xattn_W_" + n].rearrange("(t p) d -> p t d", p=P)).then_inc(w_loaded, 16)

        @block.tensor
        def _(pe):
            pe.wait_ge(w_loaded, 64)
            for k in range(4):
                if k >= 2:
                    pe.wait_ge(w_copied, k - 1)
                for ot in range(KT):
                    for kt in range(KT):
                        last = pe.transpose(pb[k % 2][:, kt, P * ot:P * ot + P], w_in[:, k, ot, P * kt:P * kt + P], c.ident[:])
                last.then_inc(w_turned, 1)
            pe.wait_ge(w_copied, 4)
            pe.wait_ge(ready0, 1)

            def prep(step, n, s):
                if step == 0:
                    pe.wait_ge(xs_ready, n + 1)
                    for u in range(U):
                        for kt in range(KT):
                            last = pe.transpose(pb[0][:, kt, P * u:P * u + P], xs[:, u, P * kt:P * kt + P], c.ident[:])
                if step == 1:
                    pe.wait_ge(copied, 4 * n + 1)
                    for g in range(2):
                        for kt in range(KT):
                            last = pe.matmul(pb[1][:, g, :], wT[:, 0, kt, P * g:P * g + P], xsT[:, kt, :],
                                             start=(kt == 0), stop=(kt == KT - 1))
                if step == 2:
                    for g in range(2):
                        for kt in range(KT):
                            last = pe.matmul(pb[0][:, g, :], wT[:, 1, kt, P * g:P * g + P], c.ctxT[:, kt, ds(n * S, S)],
                                             start=(kt == 0), stop=(kt == KT - 1))
                if step == 3:
                    pe.wait_ge(cs_ready, n + 1)
                    pe.wait_ge(copied, 4 * n + 2)
                    for u in range(U):
                        for kt in range(KT):
                            last = pe.matmul(pb[1][:, u, :], csT[:, kt, P * u:P * u + P], wT[:, 2, kt, :],
                                             start=(kt == 0), stop=(kt == KT - 1))
                last.then_inc(filled, 1)

            def scores(b, s, kt):
                pe.wait_ge(copied, 4 * b + 3)
                pe.wait_ge(lowered, U * b + kt)
                for r in range(4):
                    for g in range(2):
                        last = pe.matmul(sc[:, r, g, :], kT[s][HD2 * r:HD2 * r + HD2, g, P * kt:P * kt + P],
                                         qT[s][HD2 * r:HD2 * r + HD2, g, :], start=True, stop=True)
                last.then_inc(scored, 1)

            def values(b, s, kt):
                pe.wait_ge(weighted, U * b + kt + 1)
                if kt == 0:
                    pe.wait_ge(copied, 4 * b + 4)
                    pe.wait_ge(o_copied, b)
                for g in range(2):
                    for r in range(4):
                        h = 4 * g + r
                        last = pe.matmul(po[g][HD2 * r:HD2 * r + HD2, :], vs[s][:, kt, HD2 * h:HD2 * h + HD2],
                                         ex[kt][:, r, g, :], start=(kt == 0), stop=(kt == U - 1))
                last.then_inc(pv_done, 1)

            for step in range(4):
                prep(step, 0, 0)
            scores(0, 0, 0)
            with pe.Fori(0, B // 2) as i:
                for s in range(2):
                    b = 2 * i + s
                    pe.wait_ge(out_taken, b)
                    prep(0, b + 1, 1 - s)
                    scores(b, s, 1)
                    pe.wait_ge(copied, 4 * b + 4)
                    prep(1, b + 1, 1 - s)
                    prep(2, b + 1, 1 - s)
                    values(b, s, 0)
                    prep(3, b + 1, 1 - s)
                    scores(b + 1, 1 - s, 0)
                    values(b, s, 1)
                    pe.wait_ge(o_copied, b + 1)
                    pe.wait_ge(copied, 4 * b + 7)
                    for u in range(U):
                        for g in range(2):
                            last = pe.matmul(pb[0][:, u, :], oT[:, g, P * u:P * u + P], wT[:, 3, g, :],
                                             start=(g == 0), stop=(g == 1))
                    last.then_inc(out_done, 1)

        @block.scalar
        def _(act):
            for k in range(4):
                act.wait_ge(w_turned, k + 1)
                act.activation(wT[:, k], pb[k % 2][:], ACT.Copy).then_inc(w_copied, 1)

            def prep(step, n, s):
                act.wait_ge(filled, 4 * n + step + 1)
                dst = (xsT, qT[s], kT[s], vs[s])[step]
                act.activation(dst[:], pb[step % 2][:], ACT.Copy).then_inc(copied, 1)

            for step in range(4):
                prep(step, 0, 0)

            def exps(b, kt):
                act.wait_ge(lowered, U * b + kt + 1)
                act.activation(ex[kt][:], low[kt][:], ACT.Exp, scale=HD2 ** -0.5).then_inc(exp_done, 1)

            with act.Fori(0, B // 2) as i:
                for s in range(2):
                    b = 2 * i + s
                    prep(0, b + 1, 1 - s)
                    act.wait_ge(pv_done, U * b)
                    exps(b, 0)
                    prep(1, b + 1, 1 - s)
                    prep(2, b + 1, 1 - s)
                    exps(b, 1)
                    prep(3, b + 1, 1 - s)
                    act.wait_ge(pv_done, U * b + U)
                    act.activation(oT[:, 0, :], po[0][:], ACT.Copy)
                    act.activation(oT[:, 1, :], po[1][:], ACT.Copy).then_inc(o_copied, 1)

        @block.gpsimd
        def _(pool):
            pool.tensor_copy(csT[:], c.ctxT[:, :, 0:S]).then_inc(cs_ready, 1)
            with pool.Fori(0, B) as b:
                for kt in range(U):
                    pool.wait_ge(rden_ready, U * b + kt + 1)
                    e = ex[kt][:].rearrange("p r g q -> p (r g) q")
                    pool.tensor_tensor(e, e, rden[kt][:].unsqueeze(1).to_broadcast([P, H2, S]), ALU.mult).then_inc(weighted, 1)
                    if kt == 0:
                        pool.wait_ge(filled, 4 * b + 4)
                        pool.tensor_copy(csT[:], c.ctxT[:, :, ds(b * S + S, S)]).then_inc(cs_ready, 1)

        @block.vector
        def _(dve):
            link = Chain(dve, chain)
            moments(link, dve, c.st[:], mean[:], rstd[:], mt[:])
            rsqrt(link, dve, mt[:], rstd[:], mt2[:])
            dve.sem_inc(ready0, 1)
            base = link.n

            def rows_of(n):
                for u in range(U):
                    t = U * n + u
                    last = dve.tensor_scalar(xs[:, u, :], c.x[:, t, :], mean[:, ds(t, 1)], rstd[:, ds(t, 1)], ALU.subtract, ALU.mult)
                last.then_inc(xs_ready, 1)

            def lower(b, kt):
                dve.wait_ge(scored, U * b + kt + 1)
                dve.tensor_reduce(mx[kt][:], sc[:].rearrange("p r g q -> p q (r g)"), AX, ALU.max).then_inc(maxed, 1)
                dve.wait_ge(maxed, U * b + kt + 1)
                dve.tensor_tensor(low[kt][:].rearrange("p r g q -> p (r g) q"), sc[:].rearrange("p r g q -> p (r g) q"),
                                  mx[kt][:].unsqueeze(1).to_broadcast([P, H2, S]), ALU.subtract).then_inc(lowered, 1)

            def divide(link, b, kt):
                dve.wait_ge(exp_done, U * b + kt + 1)
                link(dve.tensor_reduce(den[kt][:], ex[kt][:].rearrange("p r g q -> p q (r g)"), AX, ALU.add))
                dve.reciprocal(rden[kt][:], den[kt][:]).then_inc(rden_ready, 1)

            rows_of(0)
            lower(0, 0)
            with dve.Fori(0, B // 2) as i:
                for s in range(2):
                    b = 2 * i + s
                    link = Chain(dve, chain, base + b * 4)
                    dve.wait_ge(filled, 4 * b + 1)
                    rows_of(b + 1)
                    lower(b, 1)
                    divide(link, b, 0)
                    lower(b + 1, 0)
                    divide(link, b, 1)
                    dve.wait_ge(out_done, b + 1)
                    v = c.x[:, ds(b * U, U), :].rearrange("p u d -> p (u d)")
                    dve.scalar_tensor_tensor(v, pb[0][:].rearrange("p u d -> p (u d)"), c.tg[:, 2:3], v,
                                             ALU.mult, ALU.add).then_inc(out_taken, 1)
                    dve.wait_ge(out_taken, b + 1)
                    for u in range(U):
                        link(dve.bn_stats(c.st[:, U * b + u, :], c.x[:, U * b + u, :]))


NROT = 4
BASE_SQ = 5
LEVELS = 12
NORM0 = 16.0
TAYLOR0 = (1.0, 1.0, 1 / 2, 1 / 6)
TAYLOR1 = (1 / 24, 1 / 120, 1 / 720, 1 / 5040, 1 / 40320)


def rotation(nc, I, c):
    with ExitStack() as ctx:
        sb = lambda n, s, d=F32: ctx.enter_context(nc.sbuf_tensor("rot_" + n, s, d))
        sem = lambda n: c.semaphore("rot_" + n)
        mats = lambda n: [sb(f"{n}{m}", [P, KT, D]) for m in range(NROT)]
        A, L, A2, A3, A4, T0, T1, R = (mats(n) for n in ("A", "L", "A2_", "A3_", "A4_", "T0_", "T1_", "R"))
        rowsum, norm = sb("rowsum", [P, NROT, KT]), sb("norm", [P, 2, NROT])
        over, half, scale = sb("over", [P, LEVELS, NROT]), sb("half", [P, LEVELS, NROT]), sb("scale", [P, NROT])
        flag, take, aside = sb("flag", [P, 1], I32), sb("take", [P, NROT]), sb("aside", [P, NROT])
        bank = [ctx.enter_context(nc.psum_tensor(f"rot_bank{m}", [P, KT, D], F32)) for m in range(NROT)]
        names = ("loaded", "chain", "norm_ready", "norm_all", "scaled", "done", "copied", "poly", "summed", "flagged",
                 "x_done", "x_taken", "x_turned", "x_copied", "took", "f_done", "f_copied")
        (loaded, chain, norm_ready, norm_all, scaled, done, copied, poly, summed, flagged,
         x_done, x_taken, x_turned, x_copied, took, f_done, f_copied) = (sem(n) for n in names)

        def turn(pe, out, src):
            for ot in range(KT):
                for kt in range(KT):
                    last = pe.transpose(out[:, kt, P * ot:P * ot + P], src[:, ot, P * kt:P * kt + P], c.ident[:])
            return last

        def product(pe, out, leftT, right):
            for ot in range(KT):
                for kt in range(KT):
                    last = pe.matmul(out[:, ot, :], leftT[:, kt, P * ot:P * ot + P], right[:, kt, :],
                                     start=(kt == 0), stop=(kt == KT - 1))
            return last

        STEPS = [(A, None, L), (L, A, A2), (A2, None, L), (L, A, A3), (L, A2, A4), (A4, None, L), (L, T1, R)]
        POLY = len(STEPS) - 1
        STEPS += [(R, None, L), (L, R, R)] * BASE_SQ + [(R, None, L)]

        with nc.Block() as block:
            @block.sync
            def _(sp):
                for m in range(NROT):
                    sp.dma_start(A[m][:], I["L2_ffn_gens"][m].rearrange("(t p) d -> p t d", p=P)).then_inc(loaded, 16)

            @block.tensor
            def _(pe):
                for k, (left, right, dst) in enumerate(STEPS):
                    for m in range(NROT):
                        if k == 0:
                            pe.wait_ge(scaled, m + 1)
                        elif k == POLY + 1:
                            pe.wait_ge(summed, m + 1)
                        else:
                            pe.wait_ge(copied, NROT * (k - 1 if k <= POLY else k - 2) + m + 1)
                        if k == POLY:
                            pe.wait_ge(poly, m + 1)
                        last = turn(pe, bank[m], left[m]) if right is None else product(pe, bank[m], left[m], right[m])
                        last.then_inc(done, 1)

            @block.scalar
            def _(act):
                for k, (left, right, dst) in enumerate(STEPS):
                    if k == POLY:
                        continue
                    for m in range(NROT):
                        act.wait_ge(done, NROT * k + m + 1)
                        act.activation(dst[m][:], bank[m][:], ACT.Copy).then_inc(copied, 1)

            @block.gpsimd
            def _(pool):
                pool.wait_ge(norm_ready, 1)
                pool.partition_all_reduce(norm[:, 1, :], norm[:, 0, :], P, bass.bass_isa.ReduceOp.max).then_inc(norm_all, 1)

            @block.vector
            def _(dve):
                link = Chain(dve, chain)
                dve.wait_ge(loaded, 16 * NROT)
                for m in range(NROT):
                    link(dve.tensor_reduce(rowsum[:, m, :], A[m][:], AX, ALU.add, apply_absolute_value=True))
                link(dve.tensor_reduce(norm[:, 0, :], rowsum[:], AX, ALU.max))
                dve.sem_inc(norm_ready, 1)
                dve.wait_ge(norm_all, 1)
                for k in range(LEVELS):
                    link(dve.tensor_scalar(over[:, k, :], norm[:, 1, :], NORM0 * 2.0 ** k, None, ALU.is_gt))
                link(dve.tensor_scalar(half[:], over[:], -0.5, 1.0, ALU.mult, ALU.add))
                link(dve.tensor_reduce(scale[:], half[:].rearrange("p k m -> p m k"), AX, ALU.mult))
                link(dve.tensor_scalar(scale[:], scale[:], 2.0 ** -BASE_SQ, None, ALU.mult))
                link(dve.tensor_reduce(flag[:], over[:, 0, :], AX, ALU.max))
                for m in range(NROT):
                    dve.tensor_scalar(A[m][:], A[m][:], scale[:, m:m + 1], None, ALU.mult).then_inc(scaled, 1)
                dve.wait_ge(scaled, NROT)
                for m in range(NROT):
                    dve.wait_ge(copied, NROT * 4 + m + 1)
                    link(dve.tensor_scalar(T1[m][:], A4[m][:], TAYLOR1[4], None, ALU.mult))
                    for coef, mat in ((TAYLOR1[3], A3), (TAYLOR1[2], A2), (TAYLOR1[1], A)):
                        link(dve.scalar_tensor_tensor(T1[m][:], mat[m][:], coef, T1[m][:], ALU.mult, ALU.add))
                    for kt in range(KT):
                        v = T1[m][:, kt, P * kt:P * kt + P]
                        link(dve.scalar_tensor_tensor(v, c.ident[:], TAYLOR1[0], v, ALU.mult, ALU.add))
                    dve.sem_inc(poly, 1)
                    link(dve.scalar_tensor_tensor(T0[m][:], A2[m][:], TAYLOR0[2], A[m][:], ALU.mult, ALU.add))
                    link(dve.scalar_tensor_tensor(T0[m][:], A3[m][:], TAYLOR0[3], T0[m][:], ALU.mult, ALU.add))
                    for kt in range(KT):
                        v = T0[m][:, kt, P * kt:P * kt + P]
                        link(dve.tensor_tensor(v, v, c.ident[:], ALU.add))
                for m in range(NROT):
                    dve.wait_ge(done, NROT * POLY + m + 1)
                    dve.tensor_tensor(R[m][:], bank[m][:], T0[m][:], ALU.add).then_inc(summed, 1)
                dve.wait_ge(summed, NROT)

        with nc.Block() as block:
            @block.tensor
            def _(pe):
                with pe.If(pe.value_load(flag[0:1, 0:1], min_val=0, max_val=1) > 0):
                    with pe.Fori(0, LEVELS) as k:
                        for m in range(NROT):
                            pe.wait_ge(x_copied, NROT * k + m)
                            product(pe, bank[m], L[m], R[m]).then_inc(x_done, 1)
                            pe.wait_ge(x_taken, NROT * k + m + 1)
                            turn(pe, bank[m], R[m]).then_inc(x_turned, 1)

            @block.scalar
            def _(act):
                with act.If(act.value_load(flag[0:1, 0:1], min_val=0, max_val=1) > 0):
                    with act.Fori(0, LEVELS) as k:
                        for m in range(NROT):
                            act.wait_ge(x_turned, NROT * k + m + 1)
                            act.activation(L[m][:], bank[m][:], ACT.Copy).then_inc(x_copied, 1)

            @block.vector
            def _(dve):
                with dve.If(dve.value_load(flag[0:1, 0:1], min_val=0, max_val=1) > 0):
                    with dve.Fori(0, LEVELS) as k:
                        dve.tensor_copy(take[:], over[:, k, :]).then_inc(took, 1)
                        for m in range(NROT):
                            dve.wait_ge(x_done, NROT * k + m + 1)
                            dve.wait_ge(took, (NROT + 1) * k + m + 1)
                            dve.tensor_copy(aside[:, m:m + 1], take[:, m:m + 1]).then_inc(took, 1)
                            v = R[m][:].rearrange("p k d -> p (k d)")
                            dve.copy_predicated(v, take[:, m:m + 1].bitcast(I32).to_broadcast([P, KT * D]),
                                                bank[m][:].rearrange("p k d -> p (k d)")).then_inc(x_taken, 1)

        with nc.Block() as block:
            M = [R[0], A[1], A[2], c.rot]

            @block.tensor
            def _(pe):
                for m in range(1, NROT):
                    if m > 1:
                        pe.wait_ge(f_copied, 2 * m - 3)
                        turn(pe, bank[0], M[m - 1]).then_inc(f_done, 1)
                        pe.wait_ge(f_copied, 2 * m - 2)
                    product(pe, bank[1], L[0], R[m]).then_inc(f_done, 1)

            @block.scalar
            def _(act):
                for m in range(1, NROT):
                    if m > 1:
                        act.wait_ge(f_done, 2 * m - 2)
                        act.activation(L[0][:], bank[0][:], ACT.Copy).then_inc(f_copied, 1)
                    act.wait_ge(f_done, 2 * m - 1)
                    act.activation(M[m][:], bank[1][:], ACT.Copy).then_inc(f_copied, 1)
                act.wait_ge(f_copied, 2 * NROT - 3)


NE, TOPK = 6, 2
FE = 512 // P
UNITS = FF1 // FE + NE


def layer2_ffn(nc, I, c):
    with ExitStack() as ctx:
        sb = lambda n, s, d=F32: ctx.enter_context(nc.sbuf_tensor("l2f_" + n, s, d))
        sem = lambda n: c.semaphore("l2f_" + n)
        z, dense, moe = sb("z", [P, NT, D]), sb("dense", [P, NT, D]), sb("moe", [P, NT, D])
        znT = sb("znT", [P, KT, NT * P])
        logit, w6 = sb("logit", [P, NT, 8]), sb("w6", [P, NT, NE])
        mean, rstd, mt, mt2 = sb("mean", [P, NTD]), sb("rstd", [P, NTD]), sb("mt", [P, NTD]), sb("mt2", [P, NTD])

        with ExitStack() as first:
            fsb = lambda n, s, d=F32: first.enter_context(nc.sbuf_tensor("l2f_" + n, s, d))
            fps = lambda n, s, d=F32: first.enter_context(nc.psum_tensor("l2f_" + n, s, d))
            st2, zs, zsT = fsb("st2", [P, NT, 6]), fsb("zs", [P, U, D]), fsb("zsT", [P, KT, S])
            ln_g, ln_b, gate_w, gate_b = fsb("ln_g", [P, D]), fsb("ln_b", [P, D]), fsb("gate_w", [P, KT, NE]), fsb("gate_b", [P, NE])
            tb, lb = fps("tb", [P, KT, S]), fps("lb", [P, U, 8])
            names = ("loaded", "chain", "zst", "zs_ready", "turned", "copied", "logits_done", "logits_taken", "resident")
            loaded, chain, zst, zs_ready, turned, copied, logits_done, logits_taken, resident = (sem(n) for n in names)
            block = first.enter_context(nc.Block())

            @block.sync
            def _(sp):
                sp.dma_start(ln_g[:], row(I["L2_ffn_ln_g"])).then_inc(loaded, 16)
                sp.dma_start(ln_b[:], row(I["L2_ffn_ln_b"])).then_inc(loaded, 16)
                sp.dma_start(gate_w[:], I["L2_ffn_gate_w"].rearrange("(t p) e -> p t e", p=P)).then_inc(loaded, 16)
                sp.dma_start(gate_b[:], row(I["L2_ffn_gate_b"])).then_inc(loaded, 16)

            @block.vector
            def _(dve):
                link = Chain(dve, chain)
                moments(link, dve, c.st[:], mean[:], rstd[:], mt[:])
                rsqrt(link, dve, mt[:], rstd[:], mt2[:])
                link(dve.memset(logit[:], -3.0e38))
                with dve.Fori(0, NT) as t:
                    dve.tensor_scalar(z[:, t, :], c.x[:, t, :], mean[:, ds(t, 1)], rstd[:, ds(t, 1)],
                                      ALU.subtract, ALU.mult).then_inc(zst, 1)
                    dve.wait_ge(zst, 2 * t + 1)
                    dve.bn_stats(st2[:, t, :], z[:, t, :]).then_inc(zst, 1)
                dve.wait_ge(zst, 2 * NT)
                moments(link, dve, st2[:], mean[:, 0:NT], rstd[:, 0:NT], mt[:, 0:NT])
                rsqrt(link, dve, mt[:, 0:NT], rstd[:, 0:NT], mt2[:, 0:NT])
                dve.wait_ge(loaded, 64)
                base = link.n
                with dve.Fori(0, B) as b:
                    link = Chain(dve, chain, base + b * 2)
                    dve.wait_ge(turned, b)
                    for u in range(U):
                        t = U * b + u
                        ins = dve.tensor_scalar(zs[:, u, :], z[:, t, :], mean[:, ds(t, 1)], rstd[:, ds(t, 1)],
                                                ALU.subtract, ALU.mult)
                    link(ins)
                    link(dve.tensor_tensor(zs[:], zs[:], ln_g[:].unsqueeze(1).to_broadcast([P, U, D]), ALU.mult))
                    dve.tensor_tensor(zs[:], zs[:], ln_b[:].unsqueeze(1).to_broadcast([P, U, D]), ALU.add).then_inc(zs_ready, 1)
                    dve.wait_ge(logits_done, b + 1)
                    dve.tensor_tensor(logit[:, ds(b * U, U), 0:NE], lb[:, :, 0:NE], gate_b[:].unsqueeze(1).to_broadcast([P, U, NE]),
                                      ALU.add).then_inc(logits_taken, 1)

            @block.tensor
            def _(pe):
                pe.wait_ge(loaded, 64)
                with pe.Fori(0, B) as b:
                    pe.wait_ge(zs_ready, b + 1)
                    pe.wait_ge(copied, 2 * b)
                    for u in range(U):
                        for kt in range(KT):
                            last = pe.transpose(tb[:, kt, P * u:P * u + P], zs[:, u, P * kt:P * kt + P], c.ident[:])
                    last.then_inc(turned, 1)
                    pe.wait_ge(copied, 2 * b + 1)
                    pe.wait_ge(logits_taken, b)
                    for u in range(U):
                        for kt in range(KT):
                            last = pe.matmul(lb[:, u, 0:NE], zsT[:, kt, P * u:P * u + P], gate_w[:, kt, :],
                                             start=(kt == 0), stop=(kt == KT - 1))
                    last.then_inc(logits_done, 1)

            @block.scalar
            def _(act):
                with act.Fori(0, B) as b:
                    act.wait_ge(turned, b + 1)
                    act.wait_ge(logits_done, b)
                    act.activation(zsT[:], tb[:], ACT.Copy).then_inc(copied, 1)
                    act.activation(znT[:, :, ds(b * S, S)], tb[:], ACT.Copy).then_inc(copied, 1)

        with ExitStack() as second:
            fsb = lambda n, s, d=F32: second.enter_context(nc.sbuf_tensor("l2f_" + n, s, d))
            fps = lambda n, s, d=F32: second.enter_context(nc.psum_tensor("l2f_" + n, s, d))
            top, idx, idxf = fsb("top", [P, NT, 8]), fsb("idx", [P, NT, 8], U32), fsb("idxf", [P, NT, 8])
            iota, wk, sel = fsb("iota", [P, NE]), fsb("wk", [P, NT, 4]), fsb("sel", [P, NT, NE])
            w6T, eb2 = fsb("w6T", [NE, NT * P]), fsb("eb2", [NE, D])
            tb = fps("tb2", [NE, NT * P])
            bb = [fps(f"bb{i}", [P, 2, D]) for i in range(2)]
            names = ("loaded2", "chain2", "tops", "diff_ready", "exp_ready", "w6_ready", "w6_turned", "w6T_ready", "b_done", "b_copied")
            loaded, chain, tops, diff_ready, exp_ready, w6_ready, w6_turned, w6T_ready, b_done, b_copied = (sem(n) for n in names)
            block = second.enter_context(nc.Block())

            @block.sync
            def _(sp):
                sp.dma_start(eb2[:], I["L2_ffn_eb2"]).then_inc(loaded, 16)

            @block.vector
            def _(dve):
                link = Chain(dve, chain)
                for e in range(NE):
                    link(dve.memset(iota[:, e:e + 1], float(e)))
                for t in range(NT):
                    dve.max(top[:, t, :], logit[:, t, :]).then_inc(tops, 1)
                for t in range(NT):
                    dve.wait_ge(tops, t + 1)
                    last = dve.max_index(idx[:, t, :], top[:, t, :], logit[:, t, :])
                link(last)
                link(dve.tensor_copy(idxf[:], idx[:]))
                dve.tensor_tensor(wk[:, :, 0], top[:, :, 1], top[:, :, 0], ALU.subtract).then_inc(diff_ready, 1)
                dve.wait_ge(exp_ready, 1)
                link(dve.tensor_scalar(wk[:, :, 2], wk[:, :, 1], 1.0, None, ALU.add))
                link(dve.reciprocal(wk[:, :, 2], wk[:, :, 2]))
                link(dve.tensor_tensor(wk[:, :, 3], wk[:, :, 1], wk[:, :, 2], ALU.mult))
                full = [P, NT, NE]
                for k, out in ((0, w6), (1, sel)):
                    link(dve.tensor_tensor(out[:], iota[:].unsqueeze(1).to_broadcast(full),
                                           idxf[:, :, k:k + 1].to_broadcast(full), ALU.is_equal))
                    link(dve.tensor_tensor(out[:], out[:], wk[:, :, 2 + k:3 + k].to_broadcast(full), ALU.mult))
                dve.tensor_tensor(w6[:], w6[:], sel[:], ALU.add).then_inc(w6_ready, 1)
                dve.wait_ge(w6_ready, 1)

            @block.scalar
            def _(act):
                act.wait_ge(diff_ready, 1)
                act.activation(wk[:, :, 1], wk[:, :, 0], ACT.Exp).then_inc(exp_ready, 1)
                act.wait_ge(w6_turned, 1)
                act.activation(w6T[:], tb[:], ACT.Copy).then_inc(w6T_ready, 1)
                for n in range(NT // 2):
                    act.wait_ge(b_done, n + 1)
                    act.activation(moe[:, 2 * n:2 * n + 2, :], bb[n % 2][:], ACT.Copy).then_inc(b_copied, 1)

            @block.tensor
            def _(pe):
                pe.wait_ge(w6_ready, 1)
                for t in range(NT):
                    last = pe.transpose(tb[:, P * t:P * t + P], w6[:, t, :], c.ident[:])
                last.then_inc(w6_turned, 1)
                pe.wait_ge(w6T_ready, 1)
                pe.wait_ge(loaded, 16)
                for n in range(NT // 2):
                    if n >= 2:
                        pe.wait_ge(b_copied, n - 1)
                    for m in range(2):
                        t = 2 * n + m
                        last = pe.matmul(bb[n % 2][:, m, :], w6T[:, P * t:P * t + P], eb2[:], start=True, stop=True)
                    last.then_inc(b_done, 1)

        with ExitStack() as third:
            fsb = lambda n, s, d=F32: third.enter_context(nc.sbuf_tensor("l2f_" + n, s, d))
            fps = lambda n, s, d=F32: third.enter_context(nc.psum_tensor("l2f_" + n, s, d))
            aw1, aw2 = fsb("aw1", [P, KT, FF1 * P]), fsb("aw2", [P, FF1, D])
            ew1, ew2 = fsb("ew1", [P, NE, KT, FE * P]), fsb("ew2", [P, NE, FE, D])
            ab1, eb1, ab2 = fsb("ab1", [P, FF1]), fsb("eb1", [P, NE * FE]), fsb("ab2", [P, D])
            hs = [fsb(f"hs{i}", [P, FE, QT]) for i in range(2)]
            acc, accT = fsb("acc", [P, QUADS, D]), fsb("accT", [P, KT, QT])
            hb = [fps(f"hb{i}", [P, QT]) for i in range(2)]
            ob = [[fps(f"ob{i}{j}", [P, 2, D]) for j in range(2)] for i in range(2)]
            rb = [fps(f"rb{i}", [P, 2, D]) for i in range(2)]
            names = ("a_loaded", "e_loaded", "chain3", "h_done", "gelu_done", "o_done", "o_taken", "acc_turned", "accT_ready",
                     "rot_done", "rot_taken")
            a_loaded, e_loaded, chain, h_done, gelu_done, o_done, o_taken, acc_turned, accT_ready, rot_done, rot_taken = (sem(n) for n in names)
            block = third.enter_context(nc.Block())

            @block.sync
            def _(sp):
                sp.dma_start(aw1[:], I["L2_ffn_aw1"].rearrange("(t p) f -> p t f", p=P)).then_inc(a_loaded, 16)
                sp.dma_start(ab1[:], col(I["L2_ffn_ab1"])).then_inc(a_loaded, 16)
                sp.dma_start(eb1[:], col(I["L2_ffn_eb1"].rearrange("e f -> (e f)"))).then_inc(a_loaded, 16)
                sp.dma_start(aw2[:], I["L2_ffn_aw2"].rearrange("(t p) d -> p t d", p=P)).then_inc(a_loaded, 16)
                sp.dma_start(ab2[:], row(I["L2_ffn_ab2"])).then_inc(a_loaded, 16)
                for e in range(NE):
                    sp.dma_start(ew1[:, e], I["L2_ffn_ew1"][e].rearrange("(t p) f -> p t f", p=P)).then_inc(e_loaded, 16)
                    sp.dma_start(ew2[:, e], I["L2_ffn_ew2"][e].rearrange("(t p) d -> p t d", p=P)).then_inc(e_loaded, 16)

            DENSE = FF1 // FE

            @block.tensor
            def _(pe):
                pe.wait_ge(a_loaded, 80)
                pe.wait_ge(e_loaded, 32 * NE)
                with pe.Fori(0, NQ) as i:
                    def up(k):
                        for f in range(FE):
                            n = FE * k + f
                            pe.wait_ge(gelu_done, FE * UNITS * i + max(n - 1, 0))
                            for kt in range(KT):
                                w = aw1[:, kt, P * n:P * n + P] if k < DENSE else ew1[:, k - DENSE, kt, P * f:P * f + P]
                                last = pe.matmul(hb[n % 2][:], w, znT[:, kt, ds(i * QT, QT)], start=(kt == 0), stop=(kt == KT - 1))
                            last.then_inc(h_done, 1)

                    def down(k):
                        pe.wait_ge(gelu_done, FE * UNITS * i + FE * (k + 1))
                        pe.wait_ge(o_taken, UNITS * i + max(k - 1, 0))
                        for t in range(QUADS):
                            for f in range(FE):
                                w = aw2[:, FE * k + f, :] if k < DENSE else ew2[:, k - DENSE, f, :]
                                last = pe.matmul(ob[k % 2][t // 2][:, t % 2, :], hs[k % 2][:, f, P * t:P * t + P], w,
                                                 start=(f == 0), stop=(f == FE - 1))
                        last.then_inc(o_done, 1)

                    up(0)
                    for k in range(UNITS):
                        if k + 1 < UNITS:
                            up(k + 1)
                        down(k)
                    pe.wait_ge(o_taken, UNITS * (i + 1))
                    pe.wait_ge(rot_taken, i)
                    for t in range(QUADS):
                        for kt in range(KT):
                            last = pe.transpose(rb[kt][:, t // 2, P * (t % 2):P * (t % 2) + P],
                                                acc[:, t, P * kt:P * kt + P], c.ident[:])
                    last.then_inc(acc_turned, 1)
                    pe.wait_ge(accT_ready, i + 1)
                    for t in range(QUADS):
                        for kt in range(KT):
                            last = pe.matmul(rb[t // 2][:, t % 2, :], accT[:, kt, P * t:P * t + P], c.rot[:, kt, :],
                                             start=(kt == 0), stop=(kt == KT - 1))
                    last.then_inc(rot_done, 1)

            @block.scalar
            def _(act):
                act.wait_ge(a_loaded, 80)
                act.activation(mt[:, 0:1], ab1[:, 0:1], ACT.Gelu)
                with act.Fori(0, NQ) as i:
                    for k in range(UNITS):
                        act.wait_ge(o_done, UNITS * i + max(k - 1, 0))
                        for f in range(FE):
                            n = FE * k + f
                            bias = ab1[:, n:n + 1] if k < DENSE else eb1[:, n - FF1:n - FF1 + 1]
                            act.wait_ge(h_done, FE * UNITS * i + n + 1)
                            act.activation(hs[k % 2][:, f, :], hb[n % 2][:], ACT.Gelu, bias=bias).then_inc(gelu_done, 1)
                    act.wait_ge(acc_turned, i + 1)
                    for kt in range(KT):
                        ins = act.activation(accT[:, kt, :], rb[kt][:], ACT.Copy)
                    ins.then_inc(accT_ready, 1)
                    act.wait_ge(rot_done, i + 1)
                    for j in range(2):
                        ins = act.activation(moe[:, ds(i * QUADS + 2 * j, 2), :], rb[j][:], ACT.Copy)
                    ins.then_inc(rot_taken, 1)

            @block.vector
            def _(dve):
                dve.wait_ge(a_loaded, 80)
                with dve.Fori(0, NQ) as i:
                    for k in range(UNITS):
                        dve.wait_ge(o_done, UNITS * i + k + 1)
                        if k >= 1:
                            dve.wait_ge(o_taken, UNITS * i + k)
                        if k == DENSE:
                            dve.wait_ge(acc_turned, i)
                        for j in range(2):
                            if k < DENSE:
                                d = dense[:, ds(i * QUADS + 2 * j, 2), :]
                                other = ab2[:].unsqueeze(1).to_broadcast([P, 2, D]) if k == 0 else d
                                last = dve.tensor_tensor(d, ob[k % 2][j][:], other, ALU.add)
                            else:
                                for m in range(2):
                                    t = 2 * j + m
                                    old = moe[:, i * QUADS + t, :] if k == DENSE else acc[:, t, :]
                                    last = dve.scalar_tensor_tensor(acc[:, t, :], ob[k % 2][j][:, m, :],
                                                                    w6[:, i * QUADS + t, k - DENSE:k - DENSE + 1], old,
                                                                    ALU.mult, ALU.add)
                        last.then_inc(o_taken, 1)

        with ExitStack() as fourth:
            fsb = lambda n, s, d=F32: fourth.enter_context(nc.sbuf_tensor("l2f_" + n, s, d))
            gc_w, gc_b = fsb("gc_w", [P, 2, D]), fsb("gc_b", [P, 1])
            gate, gdot = fsb("gate", [P, NT]), fsb("gdot", [P, NT])
            ta, tc = [fsb(f"ta{i}", [P, U, D]) for i in range(2)], [fsb(f"tc{i}", [P, U, D]) for i in range(2)]
            names = ("loaded4", "chain4", "pa_ready", "gdots", "gates", "delta_ready")
            loaded, chain, pa_ready, gdots, gates, delta_ready = (sem(n) for n in names)
            block = fourth.enter_context(nc.Block())

            @block.sync
            def _(sp):
                v = I["L2_ffn_gc_w"].rearrange("(a d) o -> a (d o)", a=2)
                for k in range(2):
                    sp.dma_start(gc_w[:, k, :], row(v[k])).then_inc(loaded, 16)
                sp.dma_start(gc_b[:], row(I["L2_ffn_gc_b"])).then_inc(loaded, 16)

            wide = lambda k: gc_w[:, k, :].unsqueeze(1).to_broadcast([P, U, D])

            @block.gpsimd
            def _(pool):
                pool.wait_ge(loaded, 48)
                with pool.Fori(0, B // 2) as i:
                    for s in range(2):
                        b = 2 * i + s
                        pool.wait_ge(gdots, 2 * i)
                        pool.tensor_tensor(ta[s][:], dense[:, ds(b * U, U), :], wide(0), ALU.mult).then_inc(pa_ready, 1)
                with pool.Fori(0, B) as b:
                    v = moe[:, ds(b * U, U), :]
                    pool.wait_ge(gdots, B)
                    pool.tensor_tensor(v, v, dense[:, ds(b * U, U), :], ALU.subtract).then_inc(delta_ready, 1)

            @block.scalar
            def _(act):
                act.wait_ge(gdots, B)
                act.activation(gate[:], gdot[:], ACT.Sigmoid, bias=gc_b[:, 0:1]).then_inc(gates, 1)

            @block.vector
            def _(dve):
                dve.wait_ge(loaded, 48)
                with dve.Fori(0, B // 2) as i:
                    link = Chain(dve, chain, i * 4)
                    for s in range(2):
                        b = 2 * i + s
                        link(dve.tensor_tensor(tc[s][:], moe[:, ds(b * U, U), :], wide(1), ALU.mult))
                        dve.wait_ge(pa_ready, b + 1)
                        link(dve.tensor_tensor(tc[s][:], tc[s][:], ta[s][:], ALU.add))
                        dve.tensor_reduce(gdot[:, ds(b * U, U)], tc[s][:], AX, ALU.add).then_inc(gdots, 1)
                dve.wait_ge(gdots, B)
                dve.wait_ge(gates, 1)
                base = 4 * (B // 2)
                with dve.Fori(0, B) as b:
                    link = Chain(dve, chain, base + b * 5)
                    dve.wait_ge(delta_ready, b + 1)
                    for u in range(U):
                        t = U * b + u
                        last = dve.scalar_tensor_tensor(tc[0][:, u, :], moe[:, t, :], gate[:, ds(t, 1)], dense[:, t, :], ALU.mult, ALU.add)
                    link(last)
                    link(dve.tensor_tensor(tc[1][:], tc[0][:], z[:, ds(b * U, U), :], ALU.add))
                    v = c.x[:, ds(b * U, U), :]
                    link(dve.scalar_tensor_tensor(v.rearrange("p u d -> p (u d)"), tc[1][:].rearrange("p u d -> p (u d)"),
                                                  c.tg[:, 6:7], v.rearrange("p u d -> p (u d)"), ALU.mult, ALU.add))
                    for u in range(U):
                        link(dve.bn_stats(c.st[:, U * b + u, :], c.x[:, U * b + u, :]))


def store(nc, c, out):
    with ExitStack() as ctx:
        stored = c.semaphore("stored")
        block = ctx.enter_context(nc.Block())

        @block.sync
        def _(sp):
            for b in range(B):
                sp.dma_start(out[b].rearrange("(u p) d -> p u d", p=P), c.x[:, U * b:U * b + U, :]).then_inc(stored, 16)
            sp.wait_ge(stored, 16 * B)


STAGES = (layer0_attention, layer0_ffn, layer1_attention, layer1_ffn, layer2_attention, rotation, layer2_ffn,
          layer3_attention, layer3_ffn)


def program(nc, I, out, stages=STAGES):
    with ExitStack() as ctx:
        ctx.enter_context(nc.allow_non_contiguous_dma(reason="a few short bias columns"))
        c = Core()
        c.nc, c.sems = nc, []
        sb = lambda n, s, d=F32: ctx.enter_context(nc.sbuf_tensor(n, s, d))
        c.x = sb("x", [P, NTD, D])
        c.st = sb("st", [P, NTD, 6])
        c.ctxT = sb("ctxT", [P, KT, TD])
        c.ident = sb("ident", [P, P])
        c.identb = sb("identb", [P, P], BF16)
        c.ones = sb("ones", [P, P])
        c.g = sb("g", [P, 8])
        c.tg = sb("tg", [P, 8])
        c.rot = sb("rot", [P, KT, D])
        setup(nc, I, c)
        for n, s in enumerate(stages):
            s(nc, I, c)
            if n == 4:
                nc.clear_and_free_semaphores(c.sems)
                c.sems = []
                nc.all_engine_barrier()
        store(nc, c, out)


_INS = [
    "x", "ctx_1024", "mask_Bx1xSxS2_bf1", "g_xattn", "g_ffn", "L0_xattn_Wq", "L0_xattn_bq", "L0_xattn_Wk",
    "L0_xattn_bk", "L0_xattn_Wv", "L0_xattn_bv", "L0_xattn_q_scale", "L0_xattn_q_bias", "L0_xattn_k_scale",
    "L0_xattn_k_bias", "L0_ffn_W_in", "L0_ffn_b_in", "L0_ffn_W_out", "L0_ffn_b_out", "L1_xattn_Wq", "L1_xattn_Wkv",
    "L1_xattn_Wout", "L1_xattn_bout", "L1_ffn_W1", "L1_ffn_b1", "L1_ffn_W2", "L1_ffn_b2", "L2_xattn_W_Q",
    "L2_xattn_W_K", "L2_xattn_W_V", "L2_xattn_W_O", "L2_ffn_ln_g", "L2_ffn_ln_b", "L2_ffn_aw1", "L2_ffn_ab1",
    "L2_ffn_aw2", "L2_ffn_ab2", "L2_ffn_gate_w", "L2_ffn_gate_b", "L2_ffn_ew1", "L2_ffn_eb1", "L2_ffn_ew2",
    "L2_ffn_eb2", "L2_ffn_gens", "L2_ffn_gc_w", "L2_ffn_gc_b", "L3_xattn_Wq", "L3_xattn_bq", "L3_xattn_Wk",
    "L3_xattn_bk", "L3_xattn_Wv", "L3_xattn_bv", "L3_xattn_Wo", "L3_xattn_bo", "L3_ffn_clip_x", "L3_ffn_clip_down",
    "L3_ffn_w_gate", "L3_ffn_w_up", "L3_ffn_w_down",
]


def kernel(**inputs):
    import numpy as np
    import concourse.bacc as bacc
    from concourse.bass_utils import run_bass_kernel_spmd

    nc = bacc.Bacc("TRN2", target_bir_lowering=False, num_devices=1)
    arrays, drams = {}, {}
    for name in _INS:
        a = np.ascontiguousarray(inputs[name])
        if a.dtype == np.bool_:
            a = a.view(np.uint8)
        arrays["in_" + name] = a
        drams[name] = nc.dram_tensor("in_" + name, a.shape, mybir.dt.from_np(a.dtype), kind="ExternalInput").ap()
    out = nc.dram_tensor("out_0", (B, S, D), F32, kind="ExternalOutput").ap()
    program(nc, drams, out)
    r = run_bass_kernel_spmd(nc, [arrays], core_ids=[0])
    return r.results[0]["out_0"]
```

```python
import concourse.bass as bass
from concourse import mybir
from contextlib import ExitStack

F32 = mybir.dt.float32
BF16 = mybir.dt.bfloat16
I32 = mybir.dt.int32
U32 = mybir.dt.uint32
U8 = mybir.dt.uint8
ALU = mybir.AluOpType
ACT = mybir.ActivationFunctionType
AX = mybir.AxisListType.X
ds = bass.ds

P = 128
B, S, D = 8, 256, 256
U = S // P
KT = D // P
NT = B * U
NTD = NT + 2 * U
TD = NTD * P
LN_EPS = 1e-5
ROUND = 12582912.0
ROUND256 = 3221225472.0
MASKED = 4294967296.0
HD = 16
HP = 32
NH = D // HD
NG = 4


class Chain:

    def __init__(self, eng, sem, base=0):
        self.eng, self.sem, self.base, self.n = eng, sem, base, 0

    def __call__(self, ins):
        self.n += 1
        ins.then_inc(self.sem, 1)
        self.eng.wait_ge(self.sem, self.base + self.n)


def rsqrt(link, eng, v, y, t):
    rsqrt_seed(link, eng, v, y)
    for _ in range(3):
        newton(link, eng, v, y, t)


def rsqrt_seed(link, eng, v, y):
    link(eng.tensor_scalar(y.bitcast(I32), v.bitcast(I32), 1, None, ALU.logical_shift_right))
    link(eng.tensor_scalar(y.bitcast(I32), y.bitcast(I32), -1.0, float(0x5F3759DF), ALU.mult, ALU.add))


def newton(link, eng, v, y, t):
    link(eng.tensor_tensor(t, y, y, ALU.mult))
    link(eng.tensor_tensor(t, t, v, ALU.mult))
    link(eng.tensor_scalar(t, t, -0.5, 1.5, ALU.mult, ALU.add))
    link(eng.tensor_tensor(y, y, t, ALU.mult))


RSQRT_LINKS = 14


def moments(link, eng, st, mean, rstd, t):
    link(eng.tensor_tensor(mean, st[:, :, 1], st[:, :, 4], ALU.add))
    link(eng.tensor_scalar(mean, mean, 0.5, None, ALU.mult))
    link(eng.tensor_tensor(t, st[:, :, 1], st[:, :, 4], ALU.subtract))
    link(eng.tensor_tensor(t, t, t, ALU.mult))
    link(eng.tensor_tensor(rstd, st[:, :, 2], st[:, :, 5], ALU.add))
    link(eng.tensor_scalar(rstd, rstd, 1.0 / D, LN_EPS, ALU.mult, ALU.add))
    link(eng.scalar_tensor_tensor(t, t, 0.25, rstd, ALU.mult, ALU.add))


MOMENT_LINKS = 7


class Core:

    def semaphore(self, name):
        self.sems.append(self.nc.alloc_semaphore(name=name))
        return self.sems[-1]


def row(ap, parts=P):
    return ap.partition_broadcast(parts)


def col(ap):
    return ap.rearrange("(t p) -> p t", p=P)


def setup(nc, I, c):
    with ExitStack() as ctx:
        sem = lambda n: c.semaphore("setup_" + n)
        ctx_in = ctx.enter_context(nc.sbuf_tensor("ctx_in", [P, NT, D], F32))
        tr = ctx.enter_context(nc.psum_tensor("setup_tr", [P, 4, KT, S], F32))
        x_loaded, ctx_loaded, g_loaded = sem("x_loaded"), sem("ctx_loaded"), sem("g_loaded")
        zeroed, ident_made, tr_done, tr_out = sem("zeroed"), sem("ident"), sem("tr"), sem("tr_out")
        stats, tanhs, pool_chain = sem("stats"), sem("tanhs"), sem("pool_chain")
        block = ctx.enter_context(nc.Block())

        @block.sync
        def _(sp):
            for b in range(B):
                sp.dma_start(ctx_in[:, U * b:U * b + U, :],
                             I["ctx_1024"][b].rearrange("(u p) d -> p u d", p=P)).then_inc(ctx_loaded, 16)
            sp.dma_start(c.g[:, 0:4], row(I["g_xattn"])).then_inc(g_loaded, 16)
            sp.dma_start(c.g[:, 4:8], row(I["g_ffn"])).then_inc(g_loaded, 16)
            for b in range(B):
                sp.dma_start(c.x[:, U * b:U * b + U, :],
                             I["x"][b].rearrange("(u p) d -> p u d", p=P)).then_inc(x_loaded, 16)

        @block.gpsimd
        def _(pool):
            link = Chain(pool, pool_chain)
            link(pool.memset(c.ident[:], 0.0))
            link(pool.affine_select(out=c.ident[:], in_=c.ident[:], compare_op=ALU.not_equal, fill=1.0,
                                    base=0, pattern=[[-1, P]], channel_multiplier=1))
            pool.tensor_copy(c.identb[:], c.ident[:]).then_inc(ident_made, 1)
            pool.memset(c.ones[:], 1.0).then_inc(ident_made, 1)

        @block.scalar
        def _(act):
            act.wait_ge(g_loaded, 32)
            act.activation(c.tg[:], c.g[:], ACT.Tanh).then_inc(tanhs, 1)
            for b in range(B):
                act.wait_ge(tr_done, b + 1)
                act.activation(c.ctxT[:, :, S * b:S * b + S], tr[:, b % 4], ACT.Copy).then_inc(tr_out, 1)

        @block.vector
        def _(dve):
            dve.memset(c.x[:, NT:NTD, :], 0.0).then_inc(zeroed, 1)
            dve.memset(c.ctxT[:, :, B * S:], 0.0)
            dve.wait_ge(x_loaded, 16 * B)
            dve.wait_ge(zeroed, 1)
            for t in range(NTD):
                dve.bn_stats(c.st[:, t, :], c.x[:, t, :]).then_inc(stats, 1)
            dve.wait_ge(stats, NTD)

        @block.tensor
        def _(pe):
            pe.wait_ge(ident_made, 2)
            pe.wait_ge(ctx_loaded, 16 * B)
            for b in range(B):
                if b >= 4:
                    pe.wait_ge(tr_out, b - 3)
                for u in range(U):
                    for kt in range(KT):
                        last = pe.transpose(tr[:, b % 4, kt, P * u:P * u + P],
                                            ctx_in[:, U * b + u, P * kt:P * kt + P], c.ident[:])
                last.then_inc(tr_done, 1)


PARTS = 6
Q_PARTS = ((0, 3, 4), (1, 5), (2,))
K_PARTS = ((0, 2, 5), (1, 4), (3,))
SR = PARTS * HD
AHEAD = 6
STACKS = 8


class Fillings:

    def __init__(self, a, first, each):
        self.a, self.first, self.each = a, first, each

    def place(self, key, b):
        if b is None:
            f = self.first.index(key)
            return f % 2, f // 2
        f = len(self.first) + self.each.index(key)
        return f % 2, f // 2 + b * (len(self.each) // 2)

    def claim(self, pe, key, b):
        bank, before = self.place(key, b)
        pe.wait_ge(self.a.taken[bank], before)
        return self.a.bank[bank]

    def filled(self, key, b):
        return self.a.filled[self.place(key, b)[0]]

    def await_filled(self, eng, key, b):
        bank, before = self.place(key, b)
        eng.wait_ge(self.a.filled[bank], before + 1)
        return self.a.bank[bank]

    def taken(self, key, b):
        return self.a.taken[self.place(key, b)[0]]

    def await_taken(self, eng, key, b):
        bank, before = self.place(key, b)
        eng.wait_ge(self.a.taken[bank], before + 1)

    def await_before(self, eng, key, b):
        bank, before = self.place(key, b)
        eng.wait_ge(self.a.filled[bank], before)


def halves(bank):
    return bank[:].rearrange("p a n -> p (a n)").bitcast(BF16)


def core_pe(pe, c, a, fills, b, s, masked, mid):

    def scores(n):
        g, j = n // 4, n % 4
        if j == 0:
            fills.await_taken(pe, ("m", g), b if g else b - 1)
            if masked and g == 0:
                fills.await_taken(pe, ("pen", 0), b - 1)
        pe.wait_ge(a.exp_done, NH * b + max(n - 1, 0))
        for kt in range(U):
            pe.matmul(a.sc[n % 2][:, kt, :], a.qk[s][:, 1, n, P * kt:P * kt + P], a.qk[s][:, 0, n, :],
                      start=True, stop=False)
            if masked:
                pe.matmul(a.sc[n % 2][:, kt, :], c.identb[:], a.penT[s][:, kt, :], start=False, stop=False)
            last = pe.matmul(a.sc[n % 2][:, kt, :], a.pick[:, j, :], a.mT[g % 2][:], start=False, stop=True)
        last.then_inc(a.scored, 1)

    def values(n):
        pe.wait_ge(a.exp_done, NH * b + n + 1)
        if n == 0:
            pe.wait_ge(a.norm_done, U * b)
            a.await_values(pe, b)
        for qt in range(U):
            for kt in range(U):
                last = pe.matmul(a.po[qt][:, n, :], a.pT[n % 2][:, kt, P * qt:P * qt + P],
                                 a.va[s][:, kt, a.value_slot(n), 0:HD + 1], start=(kt == 0), stop=(kt == U - 1))
        last.then_inc(a.pv_done, 1)

    for n in range(NH):
        if n + AHEAD < NH:
            max_scores_pe(pe, c, a, fills, b, n + AHEAD, s, masked, b)
        else:
            max_scores_pe(pe, c, a, fills, b + 1, n + AHEAD - NH, 1 - s, masked, b)
        scores(n)
        if n >= 1:
            values(n - 1)
        mid(n)
    values(NH - 1)


def max_scores_pe(pe, c, a, fills, b, n, s, masked, turn):
    if n == 0:
        for m in range(STACKS - 3, STACKS):
            fills.await_taken(pe, ("s", m), turn)
        if masked:
            pe.wait_ge(a.pen_ready, b + 1)
    if turn is not None or n >= 2:
        pe.wait_ge(a.max_reduced, NH * b + n - 1)
    for qt in range(U):
        last = pe.matmul(a.smax[n % 2][:, qt, :], a.qk[s][:, 0, n, P * qt:P * qt + P], a.qk[s][:, 1, n, :],
                         start=True, stop=not masked)
        if masked:
            last = pe.matmul(a.smax[n % 2][:, qt, :], c.identb[:], a.pen[s][:, qt, :], start=False, stop=True)
    last.then_inc(a.max_scored, 1)


def turn_maxima_pe(pe, c, a, fills, key, b, group):
    bank = halves(fills.claim(pe, key, b))
    pe.wait_ge(a.maxima_split, group + 1)
    for qt in range(U):
        last = pe.transpose(bank[0:12, P * qt:P * qt + P], a.mparts[:, qt, :, :].rearrange("p k j -> p (k j)"),
                            c.identb[:])
    last.then_inc(fills.filled(key, b), 1)


def take_maxima_act(act, a, fills, key, b, group, slot):
    bank = halves(fills.await_filled(act, key, b))
    if b is not None:
        act.wait_ge(a.scored, 4 * group - 4)
    act.activation(a.mT[slot][:], bank[0:12, 0:S], ACT.Copy).then_inc(fills.taken(key, b), 1)


def turn_stacks_pe(pe, c, a, fills, key, b, n):
    bank = halves(fills.claim(pe, key, b))
    if key[1] == 0:
        pe.wait_ge(a.stacked, n + 1)
    for k in range(2):
        for h in range(2):
            for u in range(U):
                at = ((k * 2 + h) * U + u) * P
                last = pe.transpose(bank[0:SR, at:at + P], a.stack[:, u, k, 2 * key[1] + h, :, :].rearrange("p s e -> p (s e)"),
                                    c.identb[:])
    last.then_inc(fills.filled(key, b), 1)


def take_stacks(eng, a, fills, key, b, dst, copy):
    bank = halves(fills.await_filled(eng, key, b))
    copy(a.stack_out(dst, key[1]), a.stack_in(bank[0:SR])).then_inc(fills.taken(key, b), 1)


def reduce_dve(dve, a, b, n):
    dve.wait_ge(a.max_scored, NH * b + n + 1)
    dve.tensor_reduce(a.mneg[(n // 4) % 2][:, :, n % 4:n % 4 + 1], a.smax[n % 2][:], AX, ALU.max,
                      negate=True).then_inc(a.max_reduced, 1)


def split_maxima_dve(dve, link, a, b, g, turned):
    m = a.mneg[g % 2][:]
    if turned is not None:
        turned()
    dve.wait_ge(a.max_reduced, NH * b + 4 * g + 4)
    link(dve.tensor_copy(a.mparts[:, :, 0, :], m))
    link(dve.tensor_tensor(a.mrest[:], m, a.mparts[:, :, 0, :], ALU.subtract))
    link(dve.tensor_copy(a.mparts[:, :, 1, :], a.mrest[:]))
    dve.tensor_tensor(a.mparts[:, :, 2, :], a.mrest[:], a.mparts[:, :, 1, :], ALU.subtract).then_inc(a.maxima_split, 1)


SPLIT_LINKS = 3


def first_parts_act(act, a, n):
    for u in range(U):
        a.tm_ready(act, n, u)
        act.activation(a.stack[:, u, :, :, 0, :].rearrange("p k h e -> p (k h) e"), a.tm(u), ACT.Copy).then_inc(a.part1, 1)


def second_parts_act(act, a, n):
    for u in range(U):
        act.wait_ge(a.rest1, U * n + u + 1)
        act.activation(a.stack[:, u, :, :, 1, :].rearrange("p k h e -> p (k h) e"),
                       a.rest[:, u].rearrange("p k h e -> p (k h) e"), ACT.Copy).then_inc(a.part2, 1)


def parts_dve(dve, a, n, half):
    wide = lambda v, r: v.to_broadcast([P, NH, r, HD])
    for u in range(U):
        st = a.stack[:, u]
        if half == 0:
            dve.wait_ge(a.part1, U * n + u + 1)
            dve.tensor_tensor(a.rest[:, u].rearrange("p k h e -> p (k h) e"), a.tm(u),
                              st[:, :, :, 0, :].rearrange("p k h e -> p (k h) e"), ALU.subtract).then_inc(a.rest1, 1)
            dve.tensor_copy(st[:, 0, :, 3:5, :], wide(st[:, 0, :, 0:1, :], 2))
            dve.tensor_copy(st[:, 1, :, 2:6:3, :], wide(st[:, 1, :, 0:1, :], 2))
        else:
            dve.wait_ge(a.part2, U * n + u + 1)
            dve.tensor_tensor(st[:, 0, :, 2, :], a.rest[:, u, 0], st[:, 0, :, 1, :], ALU.subtract)
            dve.tensor_tensor(st[:, 1, :, 3, :], a.rest[:, u, 1], st[:, 1, :, 1, :], ALU.subtract)
            dve.tensor_copy(st[:, 0, :, 5, :], st[:, 0, :, 1, :])
            last = dve.tensor_copy(st[:, 1, :, 4, :], st[:, 1, :, 1, :])
    if half == 1:
        last.then_inc(a.stacked, 1)


def attention_tiles(nc, c, ctx, tag):
    a = Core()
    sb = lambda n, s, d=F32: ctx.enter_context(nc.sbuf_tensor(tag + n, s, d))
    ps = lambda n, s, d=F32: ctx.enter_context(nc.psum_tensor(tag + n, s, d))
    sem = lambda n: c.semaphore(tag + n)
    a.sb, a.ps, a.sem = sb, ps, sem
    a.stack = sb("stack", [P, U, 2, NH, PARTS, HD], BF16)
    a.rest = sb("rest", [P, U, 2, NH, HD])
    a.qk = [sb(f"qk{i}", [SR, 2, NH, S], BF16) for i in range(2)]
    a.va = [sb(f"va{i}", [P, U, NH, HP]) for i in range(2)]
    a.pT = [sb(f"pT{i}", [P, U, S]) for i in range(2)]
    a.mneg = [sb(f"mneg{i}", [P, U, 4]) for i in range(2)]
    a.mrest = sb("mrest", [P, U, 4])
    a.mparts = sb("mparts", [P, U, 3, 4], BF16)
    a.mT = [sb(f"mT{i}", [12, S], BF16) for i in range(2)]
    a.pick = sb("pick", [12, 4, P], BF16)
    a.pick4 = sb("pick4", [12, 4])
    a.xs = sb("xs", [P, U, D])
    a.xsT = sb("xsT", [P, KT, S])
    a.csT = sb("csT", [P, KT, S])
    a.on = [sb(f"on{u}", [P, NH, HD]) for u in range(U)]
    a.rden = [sb(f"rden{u}", [P, NH, 1]) for u in range(U)]
    a.mean, a.rstd, a.mt = sb("mean", [P, NTD]), sb("rstd", [P, NTD]), sb("mt", [P, NTD])
    a.smax = [ps(f"smax{i}", [P, U, S]) for i in range(2)]
    a.sc = [ps(f"sc{i}", [P, U, S]) for i in range(2)]
    a.po = [ps(f"po{u}", [P, NH, HD + 1]) for u in range(U)]
    a.bank = [ps(f"bank{i}", [P, 2, 256]) for i in range(2)]
    a.filled, a.taken = [sem(f"filled{i}") for i in range(2)], [sem(f"taken{i}") for i in range(2)]
    a.stacked = sem("stacked")
    a.part1, a.rest1, a.part2 = sem("part1"), sem("rest1"), sem("part2")
    a.max_scored, a.max_reduced, a.maxima_split = sem("max_scored"), sem("max_reduced"), sem("maxima_split")
    a.scored, a.exp_done = sem("scored"), sem("exp_done")
    a.pv_done, a.norm_done = sem("pv_done"), sem("norm_done")
    a.xs_ready, a.cs_ready, a.dve_chain = sem("xs_ready"), sem("cs_ready"), sem("dve_chain")
    a.w_loaded, a.w_turned, a.w_copied = sem("w_loaded"), sem("w_turned"), sem("w_copied")
    return a


def make_pick(dve, link, c, a):
    link(dve.tensor_reduce(a.pick4[:], c.ident[0:12, 0:12].rearrange("p (k j) -> p j k", j=4), AX, ALU.add))
    link(dve.tensor_copy(a.pick[:], a.pick4[:].unsqueeze(2).to_broadcast([12, 4, P])))


def layer0_attention(nc, I, c):
    with ExitStack() as ctx:
        a = attention_tiles(nc, c, ctx, "l0a_")
        a.value_slot = lambda h: 4 * (2 * (h // 8) + h % 2) + (h % 8) // 2
        a.stack_out = lambda dst, m: dst[:].rearrange("p k h (t c) -> p k (h t) c", c=HD)[:, :, :, 2 * m:2 * m + 2]
        a.stack_in = lambda bank: bank.rearrange("p (k c t) -> p k t c", k=2, c=2)
        w_in = a.sb("w_in", [P, 3, KT, D])
        wT = a.sb("wT", [P, KT, 3, D])
        bias = a.sb("bias", [P, 3, D])
        gmean = a.sb("gmean", [P, 3, KT, 2 * NH])
        lnsc = a.sb("lnsc", [P, 2, HD])
        lnbi = a.sb("lnbi", [P, 2, HD])
        qkv = a.sb("qkv", [P, U, 3, NH, HP])
        sq = a.sb("sq", [P, U, 2 * NH, HD])
        ss = a.sb("ss", [P, U, 2 * NH])
        rs = a.sb("rs", [P, U, 2 * NH])
        rt = a.sb("rt", [P, U, 2 * NH])
        vT = a.sb("vT", [P, NG, S])
        squared, normed, scaled, v_turned = a.sem("squared"), a.sem("normed"), a.sem("scaled"), a.sem("v_turned")
        ready0, pool_chain = a.sem("ready0"), a.sem("pool_chain")
        a.tm = lambda u: qkv[:, u, 0:2, :, 0:HD].rearrange("p k h e -> p (k h) e")
        a.tm_ready = lambda eng, n, u: eng.wait_ge(scaled, U * n + u + 1)
        block = ctx.enter_context(nc.Block())

        def token_steps(n):
            return [("x", n), ("q", n), ("kv0", n), ("kv1", n)]
        FIRST = token_steps(0) + [("s", m) for m in range(STACKS)] + token_steps(1) + [("v", 0), ("v", 1), ("m", 0)]
        AT = {1: [("s", 0)], 2: [("x", 2), ("s", 1), ("m", 1)], 3: [("q", 2), ("s", 2)], 4: [("kv0", 2), ("s", 3)],
              5: [("kv1", 2), ("s", 4)], 6: [("s", 5), ("m", 2)], 7: [("s", 6)], 8: [("s", 7)],
              10: [("m", 3)], 11: [("v", 0)], 12: [("v", 1)], 14: [("m", 0)]}
        LOOP = [k for n in range(NH) for k in AT.get(n, [])]
        fills = Fillings(a, FIRST, LOOP)
        a.await_values = lambda eng, b: [fills.await_taken(eng, ("v", k), b - 1) for k in range(U)]

        @block.sync
        def _(sp):
            for k, n in enumerate("qkv"):
                sp.dma_start(w_in[:, k], I["L0_xattn_W" + n].rearrange("(t p) d -> p t d", p=P)).then_inc(a.w_loaded, 16)
                sp.dma_start(bias[:, k], row(I["L0_xattn_b" + n])).then_inc(a.w_loaded, 16)
            for k, n in enumerate("qk"):
                sp.dma_start(lnsc[:, k], row(I[f"L0_xattn_{n}_scale"])).then_inc(a.w_loaded, 16)
                sp.dma_start(lnbi[:, k], row(I[f"L0_xattn_{n}_bias"])).then_inc(a.w_loaded, 16)

        @block.tensor
        def _(pe):
            pe.wait_ge(a.w_loaded, 160)
            for k in range(3):
                pe.wait_ge(a.w_copied, k)
                for ot in range(KT):
                    for kt in range(KT):
                        last = pe.transpose(a.sc[0][:, kt, P * ot:P * ot + P], w_in[:, k, ot, P * kt:P * kt + P], c.ident[:])
                last.then_inc(a.w_turned, 1)
            pe.wait_ge(ready0, 1)

            def fill(key, n, b):
                kind = key[0]
                if kind == "s":
                    turn_stacks_pe(pe, c, a, fills, key, b, n)
                    return
                bank = fills.claim(pe, key, b)
                if kind == "x":
                    pe.wait_ge(a.xs_ready, n + 1)
                    for u in range(U):
                        for kt in range(KT):
                            last = pe.transpose(bank[:, kt, P * u:P * u + P], a.xs[:, u, P * kt:P * kt + P], c.ident[:])
                if kind == "q":
                    fills.await_taken(pe, ("x", key[1]), b)
                    for u in range(U):
                        for kt in range(KT):
                            last = pe.matmul(bank[:, u, :], a.xsT[:, kt, P * u:P * u + P], wT[:, kt, 0, :],
                                             start=(kt == 0), stop=(kt == KT - 1))
                if kind in ("kv0", "kv1"):
                    u = int(kind[2])
                    pe.wait_ge(a.cs_ready, n + 1)
                    for kt in range(KT):
                        last = pe.matmul(bank[:], a.csT[:, kt, P * u:P * u + P], wT[:, kt, 1:3, :],
                                         start=(kt == 0), stop=(kt == KT - 1))
                if kind == "v":
                    pe.wait_ge(v_turned, U * n + U)
                    for g in range(NG):
                        last = pe.transpose(bank[:, g // 2, P * (g % 2):P * (g % 2) + P],
                                            vT[:, g, P * key[1]:P * key[1] + P], c.ident[:])
                last.then_inc(fills.filled(key, b), 1)

            for key in FIRST[:-1]:
                fill(key, key[1] if key in token_steps(1) else 0, None)
            for n in range(AHEAD):
                max_scores_pe(pe, c, a, fills, 0, n, 0, False, None)
            turn_maxima_pe(pe, c, a, fills, FIRST[-1], None, 0)
            with pe.Fori(0, B // 2) as i:
                for s in range(2):
                    b = 2 * i + s

                    def mid(n):
                        for key in AT.get(n, []):
                            if key[0] == "m":
                                turn_maxima_pe(pe, c, a, fills, key, b, 4 * b + n // 4 + 1)
                            else:
                                fill(key, b + 1 if key[0] in "sv" else b + 2, b)
                    core_pe(pe, c, a, fills, b, s, False, mid)

        @block.scalar
        def _(act):
            def take_x(key, n, b):
                bank = fills.await_filled(act, key, b)
                act.activation(a.xsT[:], bank[:], ACT.Copy).then_inc(fills.taken(key, b), 1)

            def squares(k, b):
                fills.await_taken(act, ("q", k), b)
                for u in range(U):
                    fills.await_taken(act, (f"kv{u}", k), b)
                    act.activation(sq[:, u].rearrange("p (a c) e -> p a c e", a=2), qkv[:, u, 0:2, :, 0:HD],
                                   ACT.Square).then_inc(squared, 1)

            def take_v(key, b, s):
                bank = fills.await_filled(act, key, b)
                act.activation(a.va[s][:, key[1]].rearrange("p (a h) e -> p a (h e)", a=2), bank[:],
                               ACT.Copy).then_inc(fills.taken(key, b), 1)

            copy = lambda out, in_: act.activation(out, in_, ACT.Copy)
            take_x(("x", 0), 0, None)
            squares(0, None)
            first_parts_act(act, a, 0)
            second_parts_act(act, a, 0)
            for m in range(0, STACKS, 2):
                take_stacks(act, a, fills, ("s", m), None, a.qk[0], copy)
            take_x(("x", 1), 1, None)
            squares(1, None)
            first_parts_act(act, a, 1)
            second_parts_act(act, a, 1)
            take_v(("v", 0), None, 0)
            take_v(("v", 1), None, 0)
            take_maxima_act(act, a, fills, ("m", 0), None, 0, 0)
            with act.Fori(0, B // 2) as i:
                for s in range(2):
                    b = 2 * i + s
                    for n in range(NH):
                        act.wait_ge(a.scored, NH * b + n + 1)
                        act.activation(a.pT[n % 2][:], a.sc[n % 2][:], ACT.Exp, scale=HD ** -0.5).then_inc(a.exp_done, 1)
                        for key in AT.get(n, []):
                            if key[0] == "m":
                                take_maxima_act(act, a, fills, key, b, 4 * b + n // 4 + 1, (n // 4 + 1) % 2)
                            if key[0] == "x":
                                take_x(key, b + 2, b)
                            if key[0] == "v":
                                take_v(key, b, 1 - s)
                            if key[0] == "s" and key[1] % 2 == 0:
                                take_stacks(act, a, fills, key, b, a.qk[1 - s], copy)
                        if n == 6:
                            squares(2, b)
                        if n == 12:
                            first_parts_act(act, a, b + 2)
                        if n == 14:
                            second_parts_act(act, a, b + 2)

        @block.gpsimd
        def _(pool):
            def prep(n):
                link = Chain(pool, pool_chain, 2 * n)
                for u in range(U):
                    v = qkv[:, u, 0:2, :, 0:HD]
                    pool.wait_ge(normed, U * n + u + 1)
                    link(pool.tensor_tensor(v, v, lnsc[:].unsqueeze(2).to_broadcast([P, 2, NH, HD]), ALU.mult))
                    pool.tensor_tensor(v, v, lnbi[:].unsqueeze(2).to_broadcast([P, 2, NH, HD]),
                                       ALU.add).then_inc(scaled, 1)
            pool.wait_ge(a.w_loaded, 160)
            def context(n):
                pool.tensor_copy(a.csT[:], c.ctxT[:, :, ds(n * S, S)]).then_inc(a.cs_ready, 1)
            context(0)
            prep(0)
            fills.await_filled(pool, ("kv1", 0), None)
            context(1)
            prep(1)
            with pool.Fori(0, B) as b:
                fills.await_before(pool, ("x", 2), b)
                context(b + 2)
                prep(b + 2)

        @block.vector
        def _(dve):
            link = Chain(dve, a.dve_chain)
            link(dve.memset(qkv[:], 0.0))
            link(dve.memset(qkv[:, :, 2, :, HD:HD + 1], 1.0))
            make_pick(dve, link, c, a)
            dve.wait_ge(a.w_loaded, 160)
            for k in range(3):
                dve.wait_ge(a.w_turned, k + 1)
                for kt in range(KT):
                    link(dve.tensor_copy(wT[:, kt, k, :], a.sc[0][:, kt, :]))
                if k < 2:
                    for kt in range(KT):
                        v = wT[:, kt, k, :].rearrange("p (c e) -> p c e", e=HD)
                        m = gmean[:, k, kt, 0:NH]
                        link(dve.tensor_reduce(m, v, AX, ALU.add))
                        link(dve.tensor_scalar(m, m, 1.0 / HD, None, ALU.mult))
                        link(dve.tensor_tensor(v, v, m.unsqueeze(2).to_broadcast([P, NH, HD]), ALU.subtract))
                    v = bias[:, k, :].rearrange("p (c e) -> p c e", e=HD)
                    m = gmean[:, 2, k, 0:NH]
                    link(dve.tensor_reduce(m, v, AX, ALU.add))
                    link(dve.tensor_scalar(m, m, 1.0 / HD, None, ALU.mult))
                    link(dve.tensor_tensor(v, v, m.unsqueeze(2).to_broadcast([P, NH, HD]), ALU.subtract))
                dve.sem_inc(a.w_copied, 1)
            moments(link, dve, c.st[:], a.mean[:], a.rstd[:], a.mt[:])
            rsqrt(link, dve, a.mt[:], a.rstd[:], a.xs[:, 0, 0:NTD])
            dve.sem_inc(ready0, 1)

            def rows_of(n):
                for u in range(U):
                    t = U * n + u
                    last = dve.tensor_scalar(a.xs[:, u, :], c.x[:, t, :], a.mean[:, ds(t, 1)], a.rstd[:, ds(t, 1)],
                                             ALU.subtract, ALU.mult)
                last.then_inc(a.xs_ready, 1)

            def take_q(key, n, b):
                bank = fills.await_filled(dve, key, b)
                if b is not None or n > 0:
                    dve.wait_ge(a.rest1, U * n)
                bi = bias[:, 0, :].rearrange("p (c e) -> p c e", e=HD)
                for u in range(U):
                    last = dve.tensor_tensor(qkv[:, u, 0, :, 0:HD], bank[:, u, :].rearrange("p (c e) -> p c e", e=HD), bi, ALU.add)
                last.then_inc(fills.taken(key, b), 1)

            def take_kv(key, n, b):
                u = int(key[0][2])
                bank = fills.await_filled(dve, key, b)
                if b is not None or n > 0:
                    dve.wait_ge(v_turned, U * n)
                dve.tensor_tensor(qkv[:, u, 1:3, :, 0:HD], bank[:].rearrange("p a (c e) -> p a c e", e=HD),
                                  bias[:, 1:3, :].rearrange("p a (c e) -> p a c e", e=HD), ALU.add).then_inc(fills.taken(key, b), 1)

            def norms(link, n, steps):
                if 0 in steps:
                    for u in range(U):
                        dve.wait_ge(squared, U * n + u + 1)
                        last = dve.tensor_reduce(ss[:, u, :], sq[:, u], AX, ALU.add)
                    link(last)
                    link(dve.tensor_scalar(ss[:], ss[:], 1.0 / HD, LN_EPS, ALU.mult, ALU.add))
                    rsqrt_seed(link, dve, ss[:], rs[:])
                    newton(link, dve, ss[:], rs[:], rt[:])
                if 1 in steps:
                    newton(link, dve, ss[:], rs[:], rt[:])
                    newton(link, dve, ss[:], rs[:], rt[:])
                for u in range(U if 2 in steps else 0):
                    v = qkv[:, u, 0:2, :, 0:HD].rearrange("p a c e -> p (a c) e")
                    dve.tensor_tensor(v, v, rs[:, u, :].unsqueeze(2).to_broadcast([P, 2 * NH, HD]),
                                      ALU.mult).then_inc(normed, 1)

            def turn_values(n):
                for u in range(U):
                    dve.transpose(vT[:, 2 * u:2 * u + 2, :].rearrange("p a (t c) -> p c (a t)", c=HD),
                                  qkv[:, u, 2]).then_inc(v_turned, 1)

            NORM_LINKS = 1 + 1 + RSQRT_LINKS
            rows_of(0)
            take_q(("q", 0), 0, None)
            take_kv(("kv0", 0), 0, None)
            take_kv(("kv1", 0), 0, None)
            fills.await_taken(dve, ("kv0", 0), None)
            fills.await_taken(dve, ("kv1", 0), None)
            turn_values(0)
            norms(link, 0, (0, 1, 2))
            parts_dve(dve, a, 0, 0)
            parts_dve(dve, a, 0, 1)
            fills.await_filled(dve, ("x", 0), None)
            rows_of(1)
            for m in range(1, STACKS, 2):
                take_stacks(dve, a, fills, ("s", m), None, a.qk[0], dve.tensor_copy)
            take_q(("q", 1), 1, None)
            take_kv(("kv0", 1), 1, None)
            take_kv(("kv1", 1), 1, None)
            norms(link, 1, (0, 1, 2))
            fills.await_filled(dve, ("s", STACKS - 1), None)
            parts_dve(dve, a, 1, 0)
            parts_dve(dve, a, 1, 1)
            for n in range(AHEAD):
                reduce_dve(dve, a, 0, n)
                if n == 3:
                    split_maxima_dve(dve, link, a, 0, 0, None)
            fills.await_filled(dve, ("v", 1), None)
            turn_values(1)
            base = link.n
            with dve.Fori(0, B // 2) as i:
                for s in range(2):
                    b = 2 * i + s
                    link = Chain(dve, a.dve_chain, base + b * (4 * SPLIT_LINKS + NORM_LINKS + 1 + 2 * U))
                    for n in range(NH):
                        if n + AHEAD < NH:
                            reduce_dve(dve, a, b, n + AHEAD)
                        else:
                            reduce_dve(dve, a, b + 1, n + AHEAD - NH)
                        if n % 4 == 1:
                            g = n // 4 + 1
                            split_maxima_dve(dve, link, a, b + g // 4, g % 4, lambda: fills.await_filled(dve, ("m", g - 1), b if g > 1 else b - 1))
                        if n == 0:
                            fills.await_before(dve, ("x", 2), b)
                            rows_of(b + 2)
                        for key in AT.get(n, []):
                            if key[0] == "q":
                                take_q(key, b + 2, b)
                            if key[0][0:2] == "kv":
                                take_kv(key, b + 2, b)
                            if key[0] == "s" and key[1] % 2:
                                take_stacks(dve, a, fills, key, b, a.qk[1 - s], dve.tensor_copy)
                        if n in (7, 8, 9):
                            norms(link, b + 2, (n - 7,))
                        if n == 12:
                            parts_dve(dve, a, b + 2, 0)
                        if n == 14:
                            parts_dve(dve, a, b + 2, 1)
                        if n == 14:
                            fills.await_filled(dve, ("v", 1), b)
                            turn_values(b + 2)
                    dve.wait_ge(a.pv_done, NH * (b + 1))
                    for u in range(U):
                        last = dve.reciprocal(a.rden[u][:], a.po[u][:, :, HD:HD + 1])
                    link(last)
                    for u in range(U):
                        dve.tensor_tensor(a.on[u][:], a.po[u][:, :, 0:HD], a.rden[u][:].to_broadcast([P, NH, HD]),
                                          ALU.mult).then_inc(a.norm_done, 1)
                    for u in range(U):
                        t = U * b + u
                        dve.wait_ge(a.norm_done, t + 1)
                        link(dve.scalar_tensor_tensor(c.x[:, t, :], a.on[u][:].rearrange("p h e -> p (h e)"),
                                                      c.tg[:, 0:1], c.x[:, t, :], ALU.mult, ALU.add))
                        link(dve.bn_stats(c.st[:, t, :], c.x[:, t, :]))


def layer3_attention(nc, I, c):
    with ExitStack() as ctx:
        a = attention_tiles(nc, c, ctx, "l3a_")
        a.value_slot = lambda h: h
        a.stack_out = lambda dst, m: dst[:, :, 2 * m:2 * m + 2, :].rearrange("p k h s -> p k (h s)")
        a.stack_in = lambda bank: bank.rearrange("p (k n) -> p k n", k=2)
        w_in = a.sb("w_in", [P, 4, KT, D])
        wT = a.sb("wT", [P, KT, 4, D])
        bias = a.sb("bias", [P, 4, D])
        mask = a.sb("mask", [P, NTD, S], U8)
        a.pen = [a.sb(f"pen{i}", [P, U, S], BF16) for i in range(2)]
        a.penT = [a.sb(f"penT{i}", [P, U, S], BF16) for i in range(2)]
        mask_f = a.sb("mask_f", [P, U, S], BF16)
        tm = a.sb("tm", [P, U, 3, NH, HD])
        onT = a.sb("onT", [P, KT, S])
        y = a.sb("y", [P, U, D])
        a.pen_ready, mask_loaded, mask_wide, va_ready = a.sem("pen_ready"), a.sem("mask_loaded"), a.sem("mask_wide"), a.sem("va_ready")
        on_turned, on_copied, ready0, y_ready, va_ones = a.sem("on_turned"), a.sem("on_copied"), a.sem("ready0"), a.sem("y_ready"), a.sem("va_ones")
        a.await_values = lambda eng, b: eng.wait_ge(va_ready, b + 1)
        a.tm = lambda u: tm[:, u, 0:2].rearrange("p k h e -> p (k h) e")
        block = ctx.enter_context(nc.Block())

        token_steps = lambda n: [("x", n), ("qkv0", n), ("qkv1", n), ("qkv2", n)]
        FIRST = token_steps(0) + [("s", m) for m in range(STACKS)] + token_steps(1)[:3] + [("m", 0), ("pen", 0), ("qkv2", 1)]
        AT = {1: [("s", 0)], 2: [("x", 2), ("s", 1), ("m", 1)], 3: [("qkv0", 2), ("s", 2)], 4: [("qkv1", 2), ("s", 3)],
              5: [("qkv2", 2), ("s", 4)], 6: [("s", 5), ("m", 2)], 7: [("s", 6)], 8: [("s", 7)],
              10: [("m", 3)], 14: [("m", 0)]}
        LOOP = [k for n in range(NH) for k in AT.get(n, [])] + [("pen", 0), ("out", 0)]
        fills = Fillings(a, FIRST, LOOP)

        def tm_ready(eng, n, u):
            for k in range(2):
                fills.await_taken(eng, (f"qkv{k}", n if isinstance(n, int) else 2), None if isinstance(n, int) else n - 2)
        a.tm_ready = tm_ready

        @block.sync
        def _(sp):
            for k, n in enumerate("qkvo"):
                sp.dma_start(w_in[:, k], I["L3_xattn_W" + n].rearrange("(t p) d -> p t d", p=P)).then_inc(a.w_loaded, 16)
                sp.dma_start(bias[:, k], row(I["L3_xattn_b" + n])).then_inc(a.w_loaded, 16)
            for b in range(B):
                sp.dma_start(mask[:, U * b:U * b + U, :],
                             I["mask_Bx1xSxS2_bf1"][b, 0].rearrange("(u p) k -> p u k", p=P)).then_inc(mask_loaded, 16)

        WLOADS = 16 * 8

        @block.tensor
        def _(pe):
            pe.wait_ge(a.w_loaded, WLOADS)
            for k in range(4):
                if k >= 2:
                    pe.wait_ge(a.w_copied, k - 1)
                for ot in range(KT):
                    for kt in range(KT):
                        last = pe.transpose(a.sc[k % 2][:, kt, P * ot:P * ot + P], w_in[:, k, ot, P * kt:P * kt + P], c.ident[:])
                last.then_inc(a.w_turned, 1)
            pe.wait_ge(ready0, 1)

            def fill(key, n, s, b):
                kind = key[0]
                if kind == "s":
                    turn_stacks_pe(pe, c, a, fills, key, b, n)
                    return
                bank = fills.claim(pe, key, b)
                if kind == "x":
                    pe.wait_ge(a.xs_ready, n + 1)
                    for u in range(U):
                        for kt in range(KT):
                            last = pe.transpose(bank[:, kt, P * u:P * u + P], a.xs[:, u, P * kt:P * kt + P], c.ident[:])
                if kind[0:3] == "qkv":
                    k = int(kind[3])
                    if k == 0:
                        fills.await_taken(pe, ("x", key[1]), b)
                    else:
                        pe.wait_ge(a.cs_ready, n + 1)
                    src = a.csT if k else a.xsT
                    for u in range(U):
                        for kt in range(KT):
                            last = pe.matmul(bank[:, u, :], src[:, kt, P * u:P * u + P], wT[:, kt, k, :],
                                             start=(kt == 0), stop=(kt == KT - 1))
                if kind == "pen":
                    pe.wait_ge(a.pen_ready, n + 1)
                    for u in range(U):
                        for kt in range(U):
                            last = pe.matmul(bank[:, kt, P * u:P * u + P], a.pen[s][:, u, P * kt:P * kt + P],
                                             c.identb[:], start=True, stop=True)
                last.then_inc(fills.filled(key, b), 1)

            for key in FIRST:
                if key[0] == "m":
                    for n in range(AHEAD):
                        max_scores_pe(pe, c, a, fills, 0, n, 0, True, None)
                    turn_maxima_pe(pe, c, a, fills, key, None, 0)
                else:
                    fill(key, 0 if key[0] == "s" else key[1], 0, None)
            with pe.Fori(0, B // 2) as i:
                for s in range(2):
                    b = 2 * i + s

                    def mid(n):
                        for key in AT.get(n, []):
                            if key[0] == "m":
                                turn_maxima_pe(pe, c, a, fills, key, b, 4 * b + n // 4 + 1)
                            else:
                                fill(key, b + 1 if key[0] == "s" else b + 2, s, b)
                    core_pe(pe, c, a, fills, b, s, True, mid)
                    fill(("pen", 0), b + 1, 1 - s, b)
                    pe.wait_ge(a.norm_done, U * b + U)
                    for u in range(U):
                        for kt in range(KT):
                            last = pe.transpose(a.sc[0][:, kt, P * u:P * u + P],
                                                a.on[u][:, 8 * kt:8 * kt + 8, :].rearrange("p h e -> p (h e)"), c.ident[:])
                    last.then_inc(on_turned, 1)
                    bank = fills.claim(pe, ("out", 0), b)
                    pe.wait_ge(on_copied, b + 1)
                    for u in range(U):
                        for kt in range(KT):
                            last = pe.matmul(bank[:, u, :], onT[:, kt, P * u:P * u + P], wT[:, kt, 3, :],
                                             start=(kt == 0), stop=(kt == KT - 1))
                    last.then_inc(fills.filled(("out", 0), b), 1)

        @block.scalar
        def _(act):
            def take_x(key, b):
                bank = fills.await_filled(act, key, b)
                act.activation(a.xsT[:], bank[:], ACT.Copy).then_inc(fills.taken(key, b), 1)

            def take_pen(key, s, b):
                bank = fills.await_filled(act, key, b)
                act.activation(a.penT[s][:], bank[:], ACT.Copy).then_inc(fills.taken(key, b), 1)

            copy = lambda out, in_: act.activation(out, in_, ACT.Copy)
            act.wait_ge(ready0, 1)
            take_x(("x", 0), None)
            first_parts_act(act, a, 0)
            second_parts_act(act, a, 0)
            for m in range(0, STACKS, 2):
                take_stacks(act, a, fills, ("s", m), None, a.qk[0], copy)
            take_x(("x", 1), None)
            first_parts_act(act, a, 1)
            second_parts_act(act, a, 1)
            take_maxima_act(act, a, fills, ("m", 0), None, 0, 0)
            take_pen(("pen", 0), 0, None)
            with act.Fori(0, B // 2) as i:
                for s in range(2):
                    b = 2 * i + s
                    for n in range(NH):
                        act.wait_ge(a.scored, NH * b + n + 1)
                        act.activation(a.pT[n % 2][:], a.sc[n % 2][:], ACT.Exp, scale=HD ** -0.5).then_inc(a.exp_done, 1)
                        for key in AT.get(n, []):
                            if key[0] == "m":
                                take_maxima_act(act, a, fills, key, b, 4 * b + n // 4 + 1, (n // 4 + 1) % 2)
                            if key[0] == "x":
                                take_x(key, b)
                            if key[0] == "s" and key[1] % 2 == 0:
                                take_stacks(act, a, fills, key, b, a.qk[1 - s], copy)
                        if n == 9:
                            first_parts_act(act, a, b + 2)
                        if n == 11:
                            second_parts_act(act, a, b + 2)
                    take_pen(("pen", 0), 1 - s, b)
                    act.wait_ge(on_turned, b + 1)
                    act.activation(onT[:], a.sc[0][:], ACT.Copy).then_inc(on_copied, 1)

        @block.gpsimd
        def _(pool):
            def context(n):
                pool.tensor_copy(a.csT[:], c.ctxT[:, :, ds(n * S, S)]).then_inc(a.cs_ready, 1)

            def values_and_penalties(n, s):
                pool.tensor_copy(mask_f[:], mask[:, ds(n * U, U), :]).then_inc(mask_wide, 1)
                pool.wait_ge(mask_wide, n + 1)
                pool.tensor_tensor(a.va[s][:, :, :, 0:HD], tm[:, :, 2, :, :],
                                   c.ones[:, 0:1].unsqueeze(2).unsqueeze(3).to_broadcast([P, U, NH, HD]), ALU.mult).then_inc(va_ready, 1)
                pool.tensor_scalar(a.pen[s][:], mask_f[:], MASKED, -MASKED, ALU.mult, ALU.add).then_inc(a.pen_ready, 1)

            context(0)
            pool.wait_ge(mask_loaded, 16 * B)
            pool.wait_ge(va_ones, 1)
            fills.await_taken(pool, ("qkv2", 0), None)
            values_and_penalties(0, 0)
            fills.await_filled(pool, ("qkv2", 0), None)
            context(1)
            fills.await_taken(pool, ("qkv2", 1), None)
            with pool.Fori(0, B // 2) as i:
                for s in range(2):
                    b = 2 * i + s
                    fills.await_before(pool, ("qkv0", 2), b)
                    pool.wait_ge(a.norm_done, U * b)
                    pool.wait_ge(a.pen_ready, b + 1)
                    context(b + 2)
                    values_and_penalties(b + 1, 1 - s)
                    fills.await_taken(pool, ("qkv2", 2), b)

        @block.vector
        def _(dve):
            link = Chain(dve, a.dve_chain)
            link(dve.memset(mask[:, NT:, :], 0))
            for s in range(2):
                link(dve.memset(a.va[s][:], 1.0))
            dve.sem_inc(va_ones, 1)
            make_pick(dve, link, c, a)
            dve.wait_ge(a.w_loaded, WLOADS)
            for k in range(4):
                dve.wait_ge(a.w_turned, k + 1)
                for kt in range(KT):
                    last = dve.tensor_copy(wT[:, kt, k, :], a.sc[k % 2][:, kt, :])
                last.then_inc(a.w_copied, 1)
            dve.wait_ge(a.w_copied, 4)
            moments(link, dve, c.st[:], a.mean[:], a.rstd[:], a.mt[:])
            rsqrt(link, dve, a.mt[:], a.rstd[:], a.xs[:, 0, 0:NTD])
            dve.sem_inc(ready0, 1)

            def rows_of(n):
                for u in range(U):
                    t = U * n + u
                    last = dve.tensor_scalar(a.xs[:, u, :], c.x[:, t, :], a.mean[:, ds(t, 1)], a.rstd[:, ds(t, 1)],
                                             ALU.subtract, ALU.mult)
                last.then_inc(a.xs_ready, 1)

            def take_qkv(key, n, b):
                k = int(key[0][3])
                bank = fills.await_filled(dve, key, b)
                if b is not None or n > 0:
                    dve.wait_ge(*((va_ready, n) if k == 2 else (a.rest1, U * n)))
                dve.tensor_tensor(tm[:, :, k, :, :].rearrange("p u h e -> p u (h e)"), bank[:],
                                  bias[:, k:k + 1, :].to_broadcast([P, U, D]), ALU.add).then_inc(fills.taken(key, b), 1)

            rows_of(0)
            for k in range(3):
                take_qkv((f"qkv{k}", 0), 0, None)
            parts_dve(dve, a, 0, 0)
            parts_dve(dve, a, 0, 1)
            fills.await_filled(dve, ("x", 0), None)
            rows_of(1)
            for m in range(1, STACKS, 2):
                take_stacks(dve, a, fills, ("s", m), None, a.qk[0], dve.tensor_copy)
            take_qkv(("qkv0", 1), 1, None)
            take_qkv(("qkv1", 1), 1, None)
            parts_dve(dve, a, 1, 0)
            parts_dve(dve, a, 1, 1)
            for n in range(AHEAD):
                reduce_dve(dve, a, 0, n)
                if n == 3:
                    split_maxima_dve(dve, link, a, 0, 0, None)
            take_qkv(("qkv2", 1), 1, None)
            base = link.n
            with dve.Fori(0, B // 2) as i:
                for s in range(2):
                    b = 2 * i + s
                    link = Chain(dve, a.dve_chain, base + b * (4 * SPLIT_LINKS + U + 1 + U))
                    for n in range(NH):
                        if n + AHEAD < NH:
                            reduce_dve(dve, a, b, n + AHEAD)
                        else:
                            reduce_dve(dve, a, b + 1, n + AHEAD - NH)
                        if n % 4 == 1:
                            g = n // 4 + 1
                            split_maxima_dve(dve, link, a, b + g // 4, g % 4,
                                             lambda: fills.await_filled(dve, ("m", g - 1), b if g > 1 else b - 1))
                        if n == 0:
                            fills.await_before(dve, ("x", 2), b)
                            rows_of(b + 2)
                        for key in AT.get(n, []):
                            if key[0][0:3] == "qkv":
                                take_qkv(key, b + 2, b)
                            if key[0] == "s" and key[1] % 2:
                                take_stacks(dve, a, fills, key, b, a.qk[1 - s], dve.tensor_copy)
                        if n == 9:
                            parts_dve(dve, a, b + 2, 0)
                        if n == 11:
                            parts_dve(dve, a, b + 2, 1)
                    dve.wait_ge(a.pv_done, NH * (b + 1))
                    for u in range(U):
                        link(dve.reciprocal(a.rden[u][:], a.po[u][:, :, HD:HD + 1]))
                        dve.tensor_tensor(a.on[u][:], a.po[u][:, :, 0:HD], a.rden[u][:].to_broadcast([P, NH, HD]),
                                          ALU.mult).then_inc(a.norm_done, 1)
                    bank = fills.await_filled(dve, ("out", 0), b)
                    dve.tensor_tensor(y[:], bank[:], bias[:, 3:4, :].to_broadcast([P, U, D]), ALU.add).then_inc(fills.taken(("out", 0), b), 1)
                    fills.await_taken(dve, ("out", 0), b)
                    v = c.x[:, ds(b * U, U), :].rearrange("p u d -> p (u d)")
                    link(dve.scalar_tensor_tensor(v, y[:].rearrange("p u d -> p (u d)"), c.tg[:, 3:4], v, ALU.mult, ALU.add))
                    for u in range(U):
                        link(dve.bn_stats(c.st[:, U * b + u, :], c.x[:, U * b + u, :]))


QUADS = 4
NQ = NT // QUADS
QT = QUADS * P
FF0 = 1024 // P


def layer0_ffn(nc, I, c):
    with ExitStack() as ctx:
        sb = lambda n, s, d=F32: ctx.enter_context(nc.sbuf_tensor("l0f_" + n, s, d))
        ps = lambda n, s, d=F32: ctx.enter_context(nc.psum_tensor("l0f_" + n, s, d))
        sem = lambda n: c.semaphore("l0f_" + n)
        w_in, wq = sb("w_in", [P, KT, FF0 * P]), sb("wq", [P, KT, FF0 * P], BF16)
        wqT, wt = sb("wqT", [P, FF0, D], BF16), sb("wt", [P, D])
        wo, wot = sb("wo", [P, FF0, D]), sb("wot", [P, FF0, D])
        amax_in, mul_in, dq_in = sb("amax_in", [P, FF0]), sb("mul_in", [P, FF0]), sb("dq_in", [P, FF0])
        amax_out, mul_out = sb("amax_out", [P, FF0]), sb("mul_out", [P, FF0])
        b_in, b_out = sb("b_in", [P, FF0]), sb("b_out", [P, D])
        mean, rstd, mt, mt2 = sb("mean", [P, NTD]), sb("rstd", [P, NTD]), sb("mt", [P, NTD]), sb("mt2", [P, NTD])
        xn, xmax, xall = sb("xn", [P, NT, D]), sb("xmax", [P, NT]), sb("xall", [P, 4])
        xi, xh, xl = sb("xi", [P, QUADS, D]), sb("xh", [P, KT, QT], BF16), sb("xl", [P, KT, QT], BF16)
        hid, hmax, hall = sb("hid", [P, FF0, NT * P]), sb("hmax", [P, NQ * FF0]), sb("hall", [P, 4])
        hq, ht = [sb(f"hq{i}", [P, FF0, S]) for i in range(2)], sb("ht", [P, FF0, S])
        y = sb("y", [P, U, D])
        xt = ps("xt", [P, KT, QT])
        hb = [ps(f"hb{i}", [P, QT]) for i in range(3)]
        ob = [ps(f"ob{i}", [P, U, D]) for i in range(2)]
        wb = ps("wb", [P, 4, KT, P], BF16)
        w_loaded, wo_loaded, w_turned, w_int, w_back, w_ready = (sem(n) for n in ("w_loaded", "wo_loaded", "w_turned", "w_int", "w_back", "w_ready"))
        chain, pchain, wo_amax, wo_ready, x_amax, x_all = (sem(n) for n in ("chain", "pchain", "wo_amax", "wo_ready", "x_amax", "x_all"))
        xi_ready, x_turned, x_split, h_done, gelu_done, hmax_done = (sem(n) for n in ("xi_ready", "x_turned", "x_split", "h_done", "gelu_done", "hmax_done"))
        h_amax, h_all, hq_ready, out_done, out_added = (sem(n) for n in ("h_amax", "h_all", "hq_ready", "out_done", "out_added"))
        lnc = sem("lnc")
        block = ctx.enter_context(nc.Block())

        @block.sync
        def _(sp):
            sp.dma_start(w_in[:], I["L0_ffn_W_in"].rearrange("(t p) f -> p t f", p=P)).then_inc(w_loaded, 16)
            sp.dma_start(wo[:], I["L0_ffn_W_out"].rearrange("(t p) d -> p t d", p=P)).then_inc(wo_loaded, 16)
            sp.dma_start(b_in[:], col(I["L0_ffn_b_in"])).then_inc(w_loaded, 16)
            sp.dma_start(b_out[:], row(I["L0_ffn_b_out"])).then_inc(w_loaded, 16)

        @block.tensor
        def _(pe):
            pe.wait_ge(w_loaded, 48)
            for f in range(FF0):
                if f >= 2:
                    pe.wait_ge(w_int, f - 1)
                for kt in range(KT):
                    last = pe.transpose(hb[f % 2][:, P * kt:P * kt + P], w_in[:, kt, P * f:P * f + P], c.ident[:])
                last.then_inc(w_turned, 1)
            for half in range(FF0 // 4):
                pe.wait_ge(w_int, 4 * half + 4)
                pe.wait_ge(w_ready, half)
                for f in range(4):
                    for kt in range(KT):
                        last = pe.transpose(wb[:, f, kt, :], wqT[:, 4 * half + f, P * kt:P * kt + P], c.identb[:])
                last.then_inc(w_back, 1)
            pe.wait_ge(w_ready, FF0 // 4)
            with pe.Fori(0, NQ) as i:
                pe.wait_ge(xi_ready, i + 1)
                pe.wait_ge(x_split, i)
                for t in range(QUADS):
                    for kt in range(KT):
                        last = pe.transpose(xt[:, kt, P * t:P * t + P], xi[:, t, P * kt:P * kt + P], c.ident[:])
                last.then_inc(x_turned, 1)
                pe.wait_ge(x_split, i + 1)
                for f in range(FF0):
                    pe.wait_ge(gelu_done, FF0 * i + max(f - 2, 0))
                    for kt in range(KT):
                        for part in (xh, xl):
                            last = pe.matmul(hb[f % 3][:], wq[:, kt, P * f:P * f + P], part[:, kt, :],
                                             start=(kt == 0 and part is xh), stop=(kt == KT - 1 and part is xl))
                    last.then_inc(h_done, 1)
            pe.wait_ge(wo_ready, 1)
            with pe.Fori(0, B // 2) as i:
                for s in range(2):
                    b = 2 * i + s
                    pe.wait_ge(hq_ready, b + 1)
                    pe.wait_ge(out_added, 2 * i)
                    for u in range(U):
                        for f in range(FF0):
                            last = pe.matmul(ob[s][:, u, :], hq[s][:, f, P * u:P * u + P], wo[:, f, :],
                                             start=(f == 0), stop=(f == FF0 - 1))
                    last.then_inc(out_done, 1)

        @block.scalar
        def _(act):
            for half in range(FF0 // 4):
                act.wait_ge(w_back, half + 1)
                act.activation(wq[:, :, 4 * P * half:4 * P * half + 4 * P].rearrange("p k (f c) -> p f k c", c=P), wb[:],
                               ACT.Copy).then_inc(w_ready, 1)
            act.wait_ge(x_all, 2)
            act.wait_ge(w_loaded, 48)
            act.activation(xall[:, 3:4], xall[:, 0:1], ACT.Gelu)
            with act.Fori(0, NQ) as i:
                for f in range(FF0):
                    act.wait_ge(h_done, FF0 * i + f + 1)
                    act.activation(hid[:, f, ds(i * QT, QT)], hb[f % 3][:], ACT.Gelu,
                                   bias=b_in[:, f:f + 1], scale=dq_in[:, f:f + 1]).then_inc(gelu_done, 1)

        @block.gpsimd
        def _(pool):
            link = Chain(pool, pchain)
            pool.wait_ge(wo_loaded, 16)
            pool.wait_ge(wo_amax, 1)
            full = [P, FF0, D]
            link(pool.tensor_tensor(wot[:], wo[:], mul_out[:].unsqueeze(2).to_broadcast(full), ALU.mult))
            link(pool.tensor_scalar(wot[:], wot[:], ROUND, ROUND, ALU.add, ALU.subtract))
            link(pool.tensor_scalar(wot[:], wot[:], 127.0, -128.0, ALU.min, ALU.max))
            pool.tensor_tensor(wo[:], wot[:], amax_out[:].unsqueeze(2).to_broadcast(full), ALU.mult).then_inc(wo_ready, 1)
            pool.wait_ge(x_amax, 1)
            pool.partition_all_reduce(xall[:, 1:2], xall[:, 0:1], P, bass.bass_isa.ReduceOp.max).then_inc(x_all, 1)
            pool.wait_ge(h_amax, 1)
            pool.partition_all_reduce(hall[:, 1:2], hall[:, 0:1], P, bass.bass_isa.ReduceOp.max).then_inc(h_all, 1)

        @block.vector
        def _(dve):
            link = Chain(dve, chain)
            dve.wait_ge(wo_loaded, 16)
            link(dve.tensor_reduce(amax_out[:], wo[:], AX, ALU.max, apply_absolute_value=True))
            link(dve.tensor_scalar(amax_out[:], amax_out[:], 1e-8, None, ALU.max))
            link(dve.reciprocal(mul_out[:], amax_out[:]))
            link(dve.tensor_scalar(mul_out[:], mul_out[:], 127.0, None, ALU.mult))
            link(dve.tensor_scalar(amax_out[:], amax_out[:], 1.0 / 127.0, None, ALU.mult))
            dve.sem_inc(wo_amax, 1)
            for f in range(FF0):
                am, mul, tile = amax_in[:, f:f + 1], mul_in[:, f:f + 1], hb[f % 2][:, 0:D]
                dve.wait_ge(w_turned, f + 1)
                link(dve.tensor_reduce(am, tile, AX, ALU.max, apply_absolute_value=True))
                link(dve.tensor_scalar(am, am, 1e-8, None, ALU.max))
                link(dve.reciprocal(mul, am))
                link(dve.tensor_scalar(mul, mul, 127.0, None, ALU.mult))
                link(dve.tensor_scalar(wt[:], tile, mul, ROUND, ALU.mult, ALU.add))
                link(dve.tensor_scalar(wt[:], wt[:], ROUND, 127.0, ALU.subtract, ALU.min))
                dve.tensor_scalar(wqT[:, f, :], wt[:], -128.0, None, ALU.max).then_inc(w_int, 1)
                dve.wait_ge(w_int, f + 1)
            moments(link, dve, c.st[:], mean[:], rstd[:], mt[:])
            rsqrt(link, dve, mt[:], rstd[:], mt2[:])
            with dve.Fori(0, NT) as t:
                dve.tensor_scalar(xn[:, t, :], c.x[:, t, :], mean[:, ds(t, 1)], rstd[:, ds(t, 1)],
                                  ALU.subtract, ALU.mult).then_inc(lnc, 1)
                dve.wait_ge(lnc, 2 * t + 1)
                dve.tensor_reduce(xmax[:, ds(t, 1)], xn[:, t, :], AX, ALU.max, apply_absolute_value=True).then_inc(lnc, 1)
            dve.wait_ge(lnc, 2 * NT)
            link(dve.tensor_reduce(xall[:, 0:1], xmax[:], AX, ALU.max))
            dve.sem_inc(x_amax, 1)
            dve.wait_ge(x_all, 1)
            link(dve.tensor_scalar(xall[:, 1:2], xall[:, 1:2], 1e-8, None, ALU.max))
            link(dve.reciprocal(xall[:, 2:3], xall[:, 1:2]))
            link(dve.tensor_scalar(xall[:, 2:3], xall[:, 2:3], 32767.0, None, ALU.mult))
            link(dve.tensor_scalar(dq_in[:], amax_in[:], xall[:, 1:2], 1.0 / (127.0 * 32767.0), ALU.mult, ALU.mult))
            dve.sem_inc(x_all, 1)
            base = link.n
            with dve.Fori(0, NQ) as i:
                link = Chain(dve, chain, base + i * 3)
                dve.wait_ge(x_turned, i)
                link(dve.tensor_scalar(xi[:], xn[:, ds(i * QUADS, QUADS), :], xall[:, 2:3], ROUND, ALU.mult, ALU.add))
                link(dve.tensor_scalar(xi[:], xi[:], ROUND, 32767.0, ALU.subtract, ALU.min))
                dve.tensor_scalar(xi[:], xi[:], -32768.0, None, ALU.max).then_inc(xi_ready, 1)
                dve.wait_ge(x_turned, i + 1)
                dve.wait_ge(h_done, FF0 * i)
                link(dve.tensor_scalar(xh[:], xt[:], ROUND256, ROUND256, ALU.add, ALU.subtract))
                dve.tensor_tensor(xl[:], xt[:], xh[:], ALU.subtract).then_inc(x_split, 1)
                for f in range(FF0):
                    dve.wait_ge(gelu_done, FF0 * i + f + 1)
                    dve.tensor_reduce(hmax[:, ds(i * FF0 + f, 1)], hid[:, f, ds(i * QT, QT)], AX, ALU.max,
                                      apply_absolute_value=True).then_inc(hmax_done, 1)
            dve.wait_ge(hmax_done, NQ * FF0)
            link = Chain(dve, chain, base + NQ * 3)
            link(dve.tensor_reduce(hall[:, 0:1], hmax[:], AX, ALU.max))
            dve.sem_inc(h_amax, 1)
            dve.wait_ge(h_all, 1)
            link(dve.tensor_scalar(hall[:, 1:2], hall[:, 1:2], 1e-8, None, ALU.max))
            link(dve.reciprocal(hall[:, 2:3], hall[:, 1:2]))
            link(dve.tensor_scalar(hall[:, 2:3], hall[:, 2:3], 32767.0, None, ALU.mult))
            link(dve.tensor_scalar(hall[:, 3:4], hall[:, 1:2], 1.0 / 32767.0, None, ALU.mult))
            base = base + NQ * 3 + link.n

            def quantise(link, b, s):
                link(dve.tensor_scalar(ht[:], hid[:, :, ds(b * S, S)], hall[:, 2:3], ROUND, ALU.mult, ALU.add))
                link(dve.tensor_scalar(ht[:], ht[:], ROUND, 32767.0, ALU.subtract, ALU.min))
                dve.tensor_scalar(hq[s][:], ht[:], -32768.0, hall[:, 3:4], ALU.max, ALU.mult).then_inc(hq_ready, 1)
                dve.wait_ge(hq_ready, b + 1)

            def add_out(link, b, s):
                dve.wait_ge(out_done, b + 1)
                dve.tensor_tensor(y[:], ob[s][:], b_out[:].unsqueeze(1).to_broadcast([P, U, D]), ALU.add).then_inc(out_added, 1)
                dve.wait_ge(out_added, b + 1)
                v = c.x[:, ds(b * U, U), :].rearrange("p u d -> p (u d)")
                link(dve.scalar_tensor_tensor(v, y[:].rearrange("p u d -> p (u d)"), c.tg[:, 4:5], v, ALU.mult, ALU.add))
                for u in range(U):
                    link(dve.bn_stats(c.st[:, U * b + u, :], c.x[:, U * b + u, :]))

            with dve.Fori(0, B // 2) as i:
                link = Chain(dve, chain, base + i * 10)
                quantise(link, 2 * i, 0)
                quantise(link, 2 * i + 1, 1)
                add_out(link, 2 * i, 0)
                add_out(link, 2 * i + 1, 1)


FF3, FF3W = 6, 704
FF3R = FF3W - (FF3 - 1) * P


def layer3_ffn(nc, I, c):
    with ExitStack() as ctx:
        sb = lambda n, s, d=F32: ctx.enter_context(nc.sbuf_tensor("l3f_" + n, s, d))
        ps = lambda n, s, d=F32: ctx.enter_context(nc.psum_tensor("l3f_" + n, s, d))
        sem = lambda n: c.semaphore("l3f_" + n)
        w_up = sb("w_up", [P, 2, FF3, D])
        w_dn = sb("w_dn", [P, KT, FF3W])
        q_up, q_dn = sb("q_up", [P, 2, FF3, D], BF16), sb("q_dn", [P, KT, FF3W], BF16)
        upT, dnT = sb("upT", [P, KT, 2, FF3W], BF16), sb("dnT", [P, FF3, D], BF16)
        am_up, mul_up, dq_up = (sb(n, [P, 2, FF3]) for n in ("am_up", "mul_up", "dq_up"))
        am_dn, mul_dn = sb("am_dn", [P, KT]), sb("mul_dn", [P, KT])
        diag, dn_row = sb("diag", [P, KT, P]), sb("dn_row", [P, D])
        mean, rstd, mt, mt2 = sb("mean", [P, NTD]), sb("rstd", [P, NTD]), sb("mt", [P, NTD]), sb("mt2", [P, NTD])
        xn, xmax, xall = sb("xn", [P, NT, D]), sb("xmax", [P, NT]), sb("xall", [P, 4])
        clip = sb("clip", [P, 2])
        xt1, xq, xT = sb("xt1", [P, QUADS, D]), sb("xq", [P, QUADS, D], BF16), sb("xT", [P, KT, QT], BF16)
        sg = [sb(f"sg{i}", [P, QT]) for i in range(2)]
        hid, hmax, hall = sb("hid", [P, FF3, NT * P]), sb("hmax", [P, NQ * FF3]), sb("hall", [P, 4])
        ht, hq = sb("ht", [P, FF3, S]), [sb(f"hq{i}", [P, FF3, S], BF16) for i in range(2)]
        y = sb("y", [P, U, D])
        xb = ps("xb", [P, KT, QT], BF16)
        gb = [ps(f"gb{i}", [P, QT]) for i in range(2)]
        ub = [ps(f"ub{i}", [P, QT]) for i in range(2)]
        ob = [ps(f"ob{i}", [P, U, D]) for i in range(2)]
        wb = ps("wb", [P, 8 * P], BF16)
        names = ("w_loaded", "chain", "zeroed", "w_int", "w_back", "w_ready", "clip_ready", "x_amax", "x_all", "xq_ready",
                 "x_turned", "x_copied", "gate_done", "up_done", "silu_done", "h_ready", "hmax_done", "h_amax", "h_all",
                 "hq_ready", "out_done", "out_taken", "lnc", "row_done", "diag_ready", "scales_ready")
        (w_loaded, chain, zeroed, w_int, w_back, w_ready, clip_ready, x_amax, x_all, xq_ready, x_turned, x_copied,
         gate_done, up_done, silu_done, h_ready, hmax_done, h_amax, h_all, hq_ready, out_done, out_taken, lnc,
         row_done, diag_ready, scales_ready) = (sem(n) for n in names)
        block = ctx.enter_context(nc.Block())
        FULL = (FF3 - 1) * P
        rows = lambda t: P if t < FF3 - 1 else FF3R
        WLOADS = 16 * 8

        @block.sync
        def _(sp):
            for k, n in enumerate(("gate", "up")):
                w = I["L3_ffn_w_" + n]
                sp.dma_start(w_up[:, k, 0:FF3 - 1, :], w[0:FULL, :].rearrange("(t p) d -> p t d", p=P)).then_inc(w_loaded, 16)
                sp.dma_start(w_up[0:FF3R, k, FF3 - 1, :], w[FULL:, :]).then_inc(w_loaded, 16)
            for kt in range(KT):
                sp.dma_start(w_dn[:, kt, :], I["L3_ffn_w_down"][P * kt:P * kt + P, :]).then_inc(w_loaded, 16)
            sp.dma_start(clip[:, 0:1], row(I["L3_ffn_clip_x"])).then_inc(w_loaded, 16)
            sp.dma_start(clip[:, 1:2], row(I["L3_ffn_clip_down"])).then_inc(w_loaded, 16)

        UP_JOBS = [(k, kt) for k in range(2) for kt in range(KT)]
        DN_JOBS = [(0, 1, 2), (3, 4), (5,)]
        N_JOBS = len(UP_JOBS) + len(DN_JOBS)
        turn_bank = [wb, xb[:].rearrange("p k n -> p (k n)")]

        @block.tensor
        def _(pe):
            pe.wait_ge(w_int, 3)
            for n in range(N_JOBS):
                bank = turn_bank[n % 2]
                if n >= 2:
                    pe.wait_ge(w_ready, n - 1)
                if n < len(UP_JOBS):
                    k, kt = UP_JOBS[n]
                    for t in range(FF3):
                        r = rows(t)
                        last = pe.transpose(bank[:, P * t:P * t + r], q_up[0:r, k, t, P * kt:P * kt + P], c.identb[0:r, 0:r])
                else:
                    for m, t in enumerate(DN_JOBS[n - len(UP_JOBS)]):
                        r = rows(t)
                        for kt in range(KT):
                            last = pe.transpose(bank[0:r, D * m + P * kt:D * m + P * kt + P], q_dn[:, kt, P * t:P * t + r],
                                                c.identb[:])
                last.then_inc(w_back, 1)
            pe.wait_ge(diag_ready, 1)
            for kt in range(KT):
                last = pe.matmul(ob[0][:, 0, P * kt:P * kt + P], c.ones[:], diag[:, kt, :], start=True, stop=True)
            last.then_inc(row_done, 1)
            pe.wait_ge(w_ready, N_JOBS)
            with pe.Fori(0, NQ) as i:
                pe.wait_ge(xq_ready, i + 1)
                pe.wait_ge(x_copied, i)
                for t in range(QUADS):
                    for kt in range(KT):
                        last = pe.transpose(xb[:, kt, P * t:P * t + P], xq[:, t, P * kt:P * kt + P], c.identb[:])
                last.then_inc(x_turned, 1)
                pe.wait_ge(x_copied, i + 1)
                for t in range(FF3):
                    r = rows(t)
                    pe.wait_ge(h_ready, FF3 * i + max(t - 1, 0))
                    for k, bank, done in ((0, gb, gate_done), (1, ub, up_done)):
                        for kt in range(KT):
                            last = pe.matmul(bank[t % 2][0:r, :], upT[:, kt, k, P * t:P * t + r], xT[:, kt, :],
                                             start=(kt == 0), stop=(kt == KT - 1))
                        last.then_inc(done, 1)
            with pe.Fori(0, B // 2) as i:
                for s in range(2):
                    b = 2 * i + s
                    pe.wait_ge(hq_ready, b + 1)
                    pe.wait_ge(out_taken, 2 * i)
                    for u in range(U):
                        for t in range(FF3):
                            r = rows(t)
                            last = pe.matmul(ob[s][:, u, :], hq[s][0:r, t, P * u:P * u + P], dnT[0:r, t, :],
                                             start=(t == 0), stop=(t == FF3 - 1))
                    last.then_inc(out_done, 1)

        @block.scalar
        def _(act):
            act.wait_ge(w_loaded, WLOADS)
            act.activation(clip[:], clip[:], ACT.Sigmoid).then_inc(clip_ready, 1)
            for n in range(N_JOBS):
                act.wait_ge(w_back, n + 1)
                bank = turn_bank[n % 2]
                if n < len(UP_JOBS):
                    k, kt = UP_JOBS[n]
                    act.activation(upT[:, kt, k, :], bank[:, 0:FF3W], ACT.Copy).then_inc(w_ready, 1)
                else:
                    ts = DN_JOBS[n - len(UP_JOBS)]
                    r = rows(ts[-1])
                    act.activation(dnT[0:r, ts[0]:ts[-1] + 1, :], bank[0:r, 0:D * len(ts)], ACT.Copy).then_inc(w_ready, 1)
            act.wait_ge(scales_ready, 1)
            act.activation(xall[:, 3:4], xall[:, 0:1], ACT.Silu)
            with act.Fori(0, NQ) as i:
                act.wait_ge(x_turned, i + 1)
                act.activation(xT[:], xb[:], ACT.Copy).then_inc(x_copied, 1)
                for t in range(FF3):
                    r = rows(t)
                    act.wait_ge(gate_done, FF3 * i + t + 1)
                    act.wait_ge(h_ready, FF3 * i + max(t - 1, 0))
                    act.activation(sg[t % 2][0:r, :], gb[t % 2][0:r, :], ACT.Silu,
                                   scale=dq_up[0:r, 0, t:t + 1]).then_inc(silu_done, 1)

        @block.gpsimd
        def _(pool):
            pool.memset(hid[:, FF3 - 1, :], 0.0).then_inc(zeroed, 1)
            pool.memset(hmax[:], 0.0).then_inc(zeroed, 1)
            pool.wait_ge(x_amax, 1)
            pool.partition_all_reduce(xall[:, 1:2], xall[:, 0:1], P, bass.bass_isa.ReduceOp.max).then_inc(x_all, 1)
            pool.wait_ge(h_amax, 1)
            pool.partition_all_reduce(hall[:, 1:2], hall[:, 0:1], P, bass.bass_isa.ReduceOp.max).then_inc(h_all, 1)

        @block.vector
        def _(dve):
            link = Chain(dve, chain)
            link(dve.memset(w_up[FF3R:, :, FF3 - 1, :], 1.0))
            dve.wait_ge(w_loaded, WLOADS)
            link(dve.tensor_reduce(am_up[:], w_up[:], AX, ALU.max, apply_absolute_value=True))
            link(dve.tensor_reduce(am_dn[:], w_dn[:], AX, ALU.max, apply_absolute_value=True))
            for am, mul in ((am_up, mul_up), (am_dn, mul_dn)):
                link(dve.tensor_scalar(am[:], am[:], 1.0 / 127.0, None, ALU.mult))
                link(dve.reciprocal(mul[:], am[:]))
            for w, q, mul in ((w_up[:, 0], q_up[:, 0], mul_up[:, 0]), (w_up[:, 1], q_up[:, 1], mul_up[:, 1]),
                              (w_dn[:], q_dn[:], mul_dn[:])):
                full = list(w.shape)
                link(dve.tensor_tensor(w, w, mul.unsqueeze(2).to_broadcast(full), ALU.mult))
                link(dve.tensor_scalar(w, w, ROUND, ROUND, ALU.add, ALU.subtract))
                link(dve.tensor_scalar(q, w, 127.0, -128.0, ALU.min, ALU.max))
                dve.sem_inc(w_int, 1)
            for kt in range(KT):
                link(dve.tensor_scalar(diag[:, kt, :], c.ident[:], am_dn[:, kt:kt + 1], None, ALU.mult))
            dve.sem_inc(diag_ready, 1)
            moments(link, dve, c.st[:], mean[:], rstd[:], mt[:])
            rsqrt(link, dve, mt[:], rstd[:], mt2[:])
            with dve.Fori(0, NT) as t:
                dve.tensor_scalar(xn[:, t, :], c.x[:, t, :], mean[:, ds(t, 1)], rstd[:, ds(t, 1)],
                                  ALU.subtract, ALU.mult).then_inc(lnc, 1)
                dve.wait_ge(lnc, 2 * t + 1)
                dve.tensor_reduce(xmax[:, ds(t, 1)], xn[:, t, :], AX, ALU.max, apply_absolute_value=True).then_inc(lnc, 1)
            dve.wait_ge(lnc, 2 * NT)
            link(dve.tensor_reduce(xall[:, 0:1], xmax[:], AX, ALU.max))
            dve.sem_inc(x_amax, 1)
            dve.wait_ge(x_all, 1)
            dve.wait_ge(clip_ready, 1)
            link(dve.tensor_scalar(xall[:, 1:2], xall[:, 1:2], clip[:, 0:1], 1.0 / 127.0, ALU.mult, ALU.mult))
            link(dve.reciprocal(xall[:, 2:3], xall[:, 1:2]))
            link(dve.tensor_scalar(dq_up[:], am_up[:], xall[:, 1:2], None, ALU.mult))
            dve.sem_inc(scales_ready, 1)
            dve.wait_ge(row_done, 1)
            link(dve.tensor_copy(dn_row[:], ob[0][:, 0, :]))
            base = link.n
            dve.wait_ge(zeroed, 2)
            with dve.Fori(0, NQ) as i:
                link = Chain(dve, chain, base + i * 2)
                dve.wait_ge(x_turned, i)
                link(dve.tensor_scalar(xt1[:], xn[:, ds(i * QUADS, QUADS), :], xall[:, 2:3], ROUND, ALU.mult, ALU.add))
                link(dve.tensor_scalar(xt1[:], xt1[:], ROUND, 127.0, ALU.subtract, ALU.min))
                dve.tensor_scalar(xq[:], xt1[:], -128.0, None, ALU.max).then_inc(xq_ready, 1)
                for t in range(FF3):
                    r = rows(t)
                    dve.wait_ge(silu_done, FF3 * i + t + 1)
                    dve.wait_ge(up_done, FF3 * i + t + 1)
                    h = hid[0:r, t, ds(i * QT, QT)]
                    dve.scalar_tensor_tensor(h, ub[t % 2][0:r, :], dq_up[0:r, 1, t:t + 1], sg[t % 2][0:r, :],
                                             ALU.mult, ALU.mult).then_inc(h_ready, 1)
                    dve.wait_ge(h_ready, FF3 * i + t + 1)
                    dve.tensor_reduce(hmax[0:r, ds(i * FF3 + t, 1)], h, AX, ALU.max,
                                      apply_absolute_value=True).then_inc(hmax_done, 1)
            dve.wait_ge(hmax_done, NQ * FF3)
            link = Chain(dve, chain, base + NQ * 2)
            link(dve.tensor_reduce(hall[:, 0:1], hmax[:], AX, ALU.max))
            dve.sem_inc(h_amax, 1)
            dve.wait_ge(h_all, 1)
            link(dve.tensor_scalar(hall[:, 1:2], hall[:, 1:2], clip[:, 1:2], 1.0 / 127.0, ALU.mult, ALU.mult))
            link(dve.reciprocal(hall[:, 2:3], hall[:, 1:2]))
            link(dve.tensor_scalar(dn_row[:], dn_row[:], hall[:, 1:2], c.tg[:, 7:8], ALU.mult, ALU.mult))
            base = base + NQ * 2 + link.n

            def quantise(link, b, s):
                link(dve.tensor_scalar(ht[:], hid[:, :, ds(b * S, S)], hall[:, 2:3], ROUND, ALU.mult, ALU.add))
                link(dve.tensor_scalar(ht[:], ht[:], ROUND, 127.0, ALU.subtract, ALU.min))
                dve.tensor_scalar(hq[s][:], ht[:], -128.0, None, ALU.max).then_inc(hq_ready, 1)
                dve.wait_ge(hq_ready, b + 1)

            def add_out(link, b, s):
                dve.wait_ge(out_done, b + 1)
                dve.tensor_tensor(y[:], ob[s][:], dn_row[:].unsqueeze(1).to_broadcast([P, U, D]), ALU.mult).then_inc(out_taken, 1)
                dve.wait_ge(out_taken, b + 1)
                v = c.x[:, ds(b * U, U), :]
                link(dve.tensor_tensor(v, y[:], v, ALU.add))

            with dve.Fori(0, B // 2) as i:
                link = Chain(dve, chain, base + i * 6)
                quantise(link, 2 * i, 0)
                quantise(link, 2 * i + 1, 1)
                add_out(link, 2 * i, 0)
                add_out(link, 2 * i + 1, 1)


FF1 = 1024 // P


def layer1_attention(nc, I, c):
    with ExitStack() as ctx:
        sb = lambda n, s, d=F32: ctx.enter_context(nc.sbuf_tensor("l1a_" + n, s, d))
        ps = lambda n, s, d=F32: ctx.enter_context(nc.psum_tensor("l1a_" + n, s, d))
        sem = lambda n: c.semaphore("l1a_" + n)
        INNER = FF1 * P
        wv, wvT, wout = sb("wv", [P, KT, INNER]), sb("wvT", [P, FF1, D]), sb("wout", [P, FF1, D])
        wf, bout = sb("wf", [P, KT, D]), sb("bout", [P, D])
        csT = [sb(f"csT{i}", [P, KT, S]) for i in range(2)]
        y = sb("y", [P, U, D])
        tb = [ps(f"tb{i}", [P, 2, D]) for i in range(2)]
        fb = ps("fb", [P, KT, D])
        ob = [ps(f"ob{i}", [P, U, D]) for i in range(2)]
        w_loaded, turned, copied, fused, wf_ready, cs_ready, out_done, out_taken, chain = (
            sem(n) for n in ("w_loaded", "turned", "copied", "fused", "wf_ready", "cs_ready", "out_done", "out_taken", "chain"))
        block = ctx.enter_context(nc.Block())

        @block.sync
        def _(sp):
            sp.dma_start(wv[:], I["L1_xattn_Wkv"][:, INNER:].rearrange("(t p) f -> p t f", p=P)).then_inc(w_loaded, 16)
            sp.dma_start(wout[:], I["L1_xattn_Wout"].rearrange("(t p) d -> p t d", p=P)).then_inc(w_loaded, 16)
            sp.dma_start(bout[:], row(I["L1_xattn_bout"])).then_inc(w_loaded, 16)

        @block.tensor
        def _(pe):
            pe.wait_ge(w_loaded, 48)
            for n in range(FF1 // 2):
                if n >= 2:
                    pe.wait_ge(copied, n - 1)
                for m in range(2):
                    for kt in range(KT):
                        last = pe.transpose(tb[n % 2][:, m, P * kt:P * kt + P],
                                            wv[:, kt, P * (2 * n + m):P * (2 * n + m) + P], c.ident[:])
                last.then_inc(turned, 1)
            pe.wait_ge(copied, FF1 // 2)
            for kt in range(KT):
                for f in range(FF1):
                    last = pe.matmul(fb[:, kt, :], wvT[:, f, P * kt:P * kt + P], wout[:, f, :], start=(f == 0), stop=(f == FF1 - 1))
            last.then_inc(fused, 1)
            pe.wait_ge(wf_ready, 1)
            with pe.Fori(0, B // 2) as i:
                for s in range(2):
                    pe.wait_ge(cs_ready, 2 * i + s + 1)
                    pe.wait_ge(out_taken, 2 * i)
                    for u in range(U):
                        for kt in range(KT):
                            last = pe.matmul(ob[s][:, u, :], csT[s][:, kt, P * u:P * u + P], wf[:, kt, :],
                                             start=(kt == 0), stop=(kt == KT - 1))
                    last.then_inc(out_done, 1)

        @block.scalar
        def _(act):
            for n in range(FF1 // 2):
                act.wait_ge(turned, n + 1)
                act.activation(wvT[:, 2 * n:2 * n + 2, :], tb[n % 2][:], ACT.Copy).then_inc(copied, 1)
            act.wait_ge(fused, 1)
            act.activation(wf[:], fb[:], ACT.Copy).then_inc(wf_ready, 1)

        @block.gpsimd
        def _(pool):
            with pool.Fori(0, B // 2) as i:
                for s in range(2):
                    pool.wait_ge(out_done, 2 * i)
                    pool.tensor_copy(csT[s][:], c.ctxT[:, :, ds((2 * i + s) * S, S)]).then_inc(cs_ready, 1)

        @block.vector
        def _(dve):
            dve.wait_ge(w_loaded, 48)
            with dve.Fori(0, B // 2) as i:
                link = Chain(dve, chain, i * 6)
                for s in range(2):
                    b = 2 * i + s
                    dve.wait_ge(out_done, b + 1)
                    dve.tensor_tensor(y[:], ob[s][:], bout[:].unsqueeze(1).to_broadcast([P, U, D]), ALU.add).then_inc(out_taken, 1)
                    dve.wait_ge(out_taken, b + 1)
                    v = c.x[:, ds(b * U, U), :].rearrange("p u d -> p (u d)")
                    link(dve.scalar_tensor_tensor(v, y[:].rearrange("p u d -> p (u d)"), c.tg[:, 1:2], v, ALU.mult, ALU.add))
                    for u in range(U):
                        link(dve.bn_stats(c.st[:, U * b + u, :], c.x[:, U * b + u, :]))


def layer1_ffn(nc, I, c):
    with ExitStack() as ctx:
        sb = lambda n, s, d=F32: ctx.enter_context(nc.sbuf_tensor("l1f_" + n, s, d))
        ps = lambda n, s, d=F32: ctx.enter_context(nc.psum_tensor("l1f_" + n, s, d))
        sem = lambda n: c.semaphore("l1f_" + n)
        w1 = [sb(f"w1_{i}", [P, FF1, D]) for i in range(2)]
        w2 = [sb(f"w2_{i}", [P, KT, FF1 * P]) for i in range(2)]
        w2T = [sb(f"w2T{i}", [P, FF1, D]) for i in range(2)]
        b1_rows, b1_cols, b2 = sb("b1_rows", [B * FF1, P]), sb("b1_cols", [P, B * FF1]), sb("b2", [P, B, D])
        b1s = [sb(f"b1s{i}", [P, FF1, P]) for i in range(2)]
        wf, bf = sb("wf", [P, KT, D]), sb("bf", [P, D])
        xs, xsT, y = sb("xs", [P, U, D]), sb("xsT", [P, KT, S]), sb("y", [P, U, D])
        mean, rstd, mt, mt2 = sb("mean", [P, NTD]), sb("rstd", [P, NTD]), sb("mt", [P, NTD]), sb("mt2", [P, NTD])
        tb = [ps(f"tb{i}", [P, 2, D]) for i in range(2)]
        fb, bb, xb, ob = ps("fb", [P, KT, D]), ps("bb", [P, D]), ps("xb", [P, KT, S]), ps("ob", [P, U, D])
        w1_loaded, w2_loaded = [sem(f"w1_loaded{i}") for i in range(2)], [sem(f"w2_loaded{i}") for i in range(2)]
        names = ("b_loaded", "b1_turned", "b1_ready", "b1s_ready", "turned", "copied", "fused",
                 "wf_ready", "xs_ready", "x_turned", "x_copied", "out_done", "out_taken", "chain")
        (b_loaded, b1_turned, b1_ready, b1s_ready, turned, copied, fused,
         wf_ready, xs_ready, x_turned, x_copied, out_done, out_taken, chain) = (sem(n) for n in names)
        block = ctx.enter_context(nc.Block())
        J = FF1 // 2

        @block.sync
        def _(sp):
            sp.dma_start(b1_rows[:], I["L1_ffn_b1"].rearrange("g (t p) -> (g t) p", p=P)).then_inc(b_loaded, 16)
            sp.dma_start(b2[:], row(I["L1_ffn_b2"])).then_inc(b_loaded, 16)
            for b in range(B):
                if b >= 2:
                    sp.wait_ge(fused, b - 1)
                sp.dma_start(w2[b % 2][:], I["L1_ffn_W2"][b].rearrange("(t p) f -> p t f", p=P)).then_inc(w2_loaded[b % 2], 16)
                sp.dma_start(w1[b % 2][:], I["L1_ffn_W1"][b].rearrange("(t p) d -> p t d", p=P)).then_inc(w1_loaded[b % 2], 16)

        @block.tensor
        def _(pe):
            pe.wait_ge(b_loaded, 32)
            pe.transpose(xb[:, 0, 0:B * FF1], b1_rows[:], c.ident[0:B * FF1, 0:B * FF1]).then_inc(b1_turned, 1)
            pe.wait_ge(b1_ready, 1)
            with pe.Fori(0, B // 2) as i:
                for s in range(2):
                    b = 2 * i + s
                    pe.wait_ge(w2_loaded[s], 16 * i + 16)
                    for n in range(J):
                        pe.wait_ge(copied, J * b + max(n - 1, 0))
                        for m in range(2):
                            for kt in range(KT):
                                last = pe.transpose(tb[n % 2][:, m, P * kt:P * kt + P],
                                                    w2[s][:, kt, P * (2 * n + m):P * (2 * n + m) + P], c.ident[:])
                        last.then_inc(turned, 1)
                    pe.wait_ge(xs_ready, b + 1)
                    pe.wait_ge(x_copied, b)
                    for u in range(U):
                        for kt in range(KT):
                            last = pe.transpose(xb[:, kt, P * u:P * u + P], xs[:, u, P * kt:P * kt + P], c.ident[:])
                    last.then_inc(x_turned, 1)
                    pe.wait_ge(copied, J * b + J)
                    pe.wait_ge(w1_loaded[s], 16 * i + 16)
                    pe.wait_ge(b1s_ready, b + 1)
                    pe.wait_ge(wf_ready, 2 * b)
                    for f in range(FF1):
                        pe.matmul(bb[:], b1s[s][:, f, :], w2T[s][:, f, :], start=(f == 0), stop=(f == FF1 - 1))
                    for kt in range(KT):
                        for f in range(FF1):
                            last = pe.matmul(fb[:, kt, :], w1[s][:, f, P * kt:P * kt + P], w2T[s][:, f, :],
                                             start=(f == 0), stop=(f == FF1 - 1))
                    last.then_inc(fused, 1)
                    pe.wait_ge(wf_ready, 2 * b + 2)
                    pe.wait_ge(x_copied, b + 1)
                    pe.wait_ge(out_taken, b)
                    for u in range(U):
                        for kt in range(KT):
                            last = pe.matmul(ob[:, u, :], xsT[:, kt, P * u:P * u + P], wf[:, kt, :],
                                             start=(kt == 0), stop=(kt == KT - 1))
                    last.then_inc(out_done, 1)

        @block.scalar
        def _(act):
            act.wait_ge(b1_turned, 1)
            act.activation(b1_cols[:], xb[:, 0, 0:B * FF1], ACT.Copy).then_inc(b1_ready, 1)
            with act.Fori(0, B // 2) as i:
                for s in range(2):
                    b = 2 * i + s
                    for n in range(J):
                        act.wait_ge(turned, J * b + n + 1)
                        act.activation(w2T[s][:, 2 * n:2 * n + 2, :], tb[n % 2][:], ACT.Copy).then_inc(copied, 1)
                    act.wait_ge(x_turned, b + 1)
                    act.activation(xsT[:], xb[:], ACT.Copy).then_inc(x_copied, 1)
                    act.wait_ge(fused, b + 1)
                    act.wait_ge(out_done, b)
                    act.activation(wf[:], fb[:], ACT.Copy).then_inc(wf_ready, 1)

        @block.gpsimd
        def _(pool):
            pool.wait_ge(b1_ready, 1)
            with pool.Fori(0, B // 2) as i:
                for s in range(2):
                    b = 2 * i + s
                    pool.wait_ge(fused, 2 * i)
                    pool.tensor_copy(b1s[s][:], b1_cols[:, ds(b * FF1, FF1)].unsqueeze(2).to_broadcast([P, FF1, P])).then_inc(b1s_ready, 1)

        @block.vector
        def _(dve):
            link = Chain(dve, chain)
            moments(link, dve, c.st[:], mean[:], rstd[:], mt[:])
            rsqrt(link, dve, mt[:], rstd[:], mt2[:])
            dve.wait_ge(b_loaded, 32)
            base = link.n

            def rows_of(n):
                for u in range(U):
                    t = U * n + u
                    last = dve.tensor_scalar(xs[:, u, :], c.x[:, t, :], mean[:, ds(t, 1)], rstd[:, ds(t, 1)], ALU.subtract, ALU.mult)
                last.then_inc(xs_ready, 1)
            rows_of(0)
            with dve.Fori(0, B) as b:
                link = Chain(dve, chain, base + b * 3)
                dve.wait_ge(fused, b + 1)
                dve.tensor_tensor(bf[:], bb[:], b2[:, b, :], ALU.add).then_inc(wf_ready, 1)
                dve.wait_ge(wf_ready, 2 * b + 2)
                rows_of(b + 1)
                dve.wait_ge(out_done, b + 1)
                dve.tensor_tensor(y[:], ob[:], bf[:].unsqueeze(1).to_broadcast([P, U, D]), ALU.add).then_inc(out_taken, 1)
                dve.wait_ge(out_taken, b + 1)
                v = c.x[:, ds(b * U, U), :].rearrange("p u d -> p (u d)")
                link(dve.scalar_tensor_tensor(v, y[:].rearrange("p u d -> p (u d)"), c.tg[:, 5:6], v, ALU.mult, ALU.add))
                for u in range(U):
                    link(dve.bn_stats(c.st[:, U * b + u, :], c.x[:, U * b + u, :]))


H2, HD2 = 8, 32


def layer2_attention(nc, I, c):
    with ExitStack() as ctx:
        sb = lambda n, s, d=F32: ctx.enter_context(nc.sbuf_tensor("l2a_" + n, s, d))
        ps = lambda n, s, d=F32: ctx.enter_context(nc.psum_tensor("l2a_" + n, s, d))
        sem = lambda n: c.semaphore("l2a_" + n)
        w_in, wT = sb("w_in", [P, 4, KT, D]), sb("wT", [P, 4, KT, D])
        xs, xsT = sb("xs", [P, U, D]), sb("xsT", [P, KT, S])
        csT = sb("csT", [P, KT, S])
        qT, kT = [sb(f"qT{i}", [P, 2, S]) for i in range(2)], [sb(f"kT{i}", [P, 2, S]) for i in range(2)]
        vs = [sb(f"vs{i}", [P, U, D]) for i in range(2)]
        mx = [sb(f"mx{i}", [P, S]) for i in range(2)]
        low = [sb(f"low{i}", [P, 4, 2, S]) for i in range(2)]
        ex = [sb(f"ex{i}", [P, 4, 2, S]) for i in range(2)]
        den, rden = [sb(f"den{i}", [P, S]) for i in range(2)], [sb(f"rden{i}", [P, S]) for i in range(2)]
        oT = sb("oT", [P, 2, S])
        mean, rstd, mt, mt2 = sb("mean", [P, NTD]), sb("rstd", [P, NTD]), sb("mt", [P, NTD]), sb("mt2", [P, NTD])
        sc = ps("sc", [P, 4, 2, S])
        po = [ps(f"po{i}", [P, S]) for i in range(2)]
        pb = [ps(f"pb{i}", [P, 2, S]) for i in range(2)]
        names = ("w_loaded", "w_turned", "w_copied", "chain", "xs_ready", "cs_ready", "filled", "copied", "scored", "lowered",
                 "exp_done", "rden_ready", "weighted", "pv_done", "o_copied", "out_done", "out_taken", "ready0", "maxed")
        (w_loaded, w_turned, w_copied, chain, xs_ready, cs_ready, filled, copied, scored, lowered,
         exp_done, rden_ready, weighted, pv_done, o_copied, out_done, out_taken, ready0, maxed) = (sem(n) for n in names)
        block = ctx.enter_context(nc.Block())

        @block.sync
        def _(sp):
            for k, n in enumerate("QKVO"):
                sp.dma_start(w_in[:, k], I["L2_xattn_W_" + n].rearrange("(t p) d -> p t d", p=P)).then_inc(w_loaded, 16)

        @block.tensor
        def _(pe):
            pe.wait_ge(w_loaded, 64)
            for k in range(4):
                if k >= 2:
                    pe.wait_ge(w_copied, k - 1)
                for ot in range(KT):
                    for kt in range(KT):
                        last = pe.transpose(pb[k % 2][:, kt, P * ot:P * ot + P], w_in[:, k, ot, P * kt:P * kt + P], c.ident[:])
                last.then_inc(w_turned, 1)
            pe.wait_ge(w_copied, 4)
            pe.wait_ge(ready0, 1)

            def prep(step, n, s):
                if step == 0:
                    pe.wait_ge(xs_ready, n + 1)
                    for u in range(U):
                        for kt in range(KT):
                            last = pe.transpose(pb[0][:, kt, P * u:P * u + P], xs[:, u, P * kt:P * kt + P], c.ident[:])
                if step == 1:
                    pe.wait_ge(copied, 4 * n + 1)
                    for g in range(2):
                        for kt in range(KT):
                            last = pe.matmul(pb[1][:, g, :], wT[:, 0, kt, P * g:P * g + P], xsT[:, kt, :],
                                             start=(kt == 0), stop=(kt == KT - 1))
                if step == 2:
                    for g in range(2):
                        for kt in range(KT):
                            last = pe.matmul(pb[0][:, g, :], wT[:, 1, kt, P * g:P * g + P], c.ctxT[:, kt, ds(n * S, S)],
                                             start=(kt == 0), stop=(kt == KT - 1))
                if step == 3:
                    pe.wait_ge(cs_ready, n + 1)
                    pe.wait_ge(copied, 4 * n + 2)
                    for u in range(U):
                        for kt in range(KT):
                            last = pe.matmul(pb[1][:, u, :], csT[:, kt, P * u:P * u + P], wT[:, 2, kt, :],
                                             start=(kt == 0), stop=(kt == KT - 1))
                last.then_inc(filled, 1)

            def scores(b, s, kt):
                pe.wait_ge(copied, 4 * b + 3)
                pe.wait_ge(lowered, U * b + kt)
                for r in range(4):
                    for g in range(2):
                        last = pe.matmul(sc[:, r, g, :], kT[s][HD2 * r:HD2 * r + HD2, g, P * kt:P * kt + P],
                                         qT[s][HD2 * r:HD2 * r + HD2, g, :], start=True, stop=True)
                last.then_inc(scored, 1)

            def values(b, s, kt):
                pe.wait_ge(weighted, U * b + kt + 1)
                if kt == 0:
                    pe.wait_ge(copied, 4 * b + 4)
                    pe.wait_ge(o_copied, b)
                for g in range(2):
                    for r in range(4):
                        h = 4 * g + r
                        last = pe.matmul(po[g][HD2 * r:HD2 * r + HD2, :], vs[s][:, kt, HD2 * h:HD2 * h + HD2],
                                         ex[kt][:, r, g, :], start=(kt == 0), stop=(kt == U - 1))
                last.then_inc(pv_done, 1)

            for step in range(4):
                prep(step, 0, 0)
            scores(0, 0, 0)
            with pe.Fori(0, B // 2) as i:
                for s in range(2):
                    b = 2 * i + s
                    pe.wait_ge(out_taken, b)
                    prep(0, b + 1, 1 - s)
                    scores(b, s, 1)
                    pe.wait_ge(copied, 4 * b + 4)
                    prep(1, b + 1, 1 - s)
                    prep(2, b + 1, 1 - s)
                    values(b, s, 0)
                    prep(3, b + 1, 1 - s)
                    scores(b + 1, 1 - s, 0)
                    values(b, s, 1)
                    pe.wait_ge(o_copied, b + 1)
                    pe.wait_ge(copied, 4 * b + 7)
                    for u in range(U):
                        for g in range(2):
                            last = pe.matmul(pb[0][:, u, :], oT[:, g, P * u:P * u + P], wT[:, 3, g, :],
                                             start=(g == 0), stop=(g == 1))
                    last.then_inc(out_done, 1)

        @block.scalar
        def _(act):
            for k in range(4):
                act.wait_ge(w_turned, k + 1)
                act.activation(wT[:, k], pb[k % 2][:], ACT.Copy).then_inc(w_copied, 1)

            def prep(step, n, s):
                act.wait_ge(filled, 4 * n + step + 1)
                dst = (xsT, qT[s], kT[s], vs[s])[step]
                act.activation(dst[:], pb[step % 2][:], ACT.Copy).then_inc(copied, 1)

            for step in range(4):
                prep(step, 0, 0)

            def exps(b, kt):
                act.wait_ge(lowered, U * b + kt + 1)
                act.activation(ex[kt][:], low[kt][:], ACT.Exp, scale=HD2 ** -0.5).then_inc(exp_done, 1)

            with act.Fori(0, B // 2) as i:
                for s in range(2):
                    b = 2 * i + s
                    prep(0, b + 1, 1 - s)
                    act.wait_ge(pv_done, U * b)
                    exps(b, 0)
                    prep(1, b + 1, 1 - s)
                    prep(2, b + 1, 1 - s)
                    exps(b, 1)
                    prep(3, b + 1, 1 - s)
                    act.wait_ge(pv_done, U * b + U)
                    act.activation(oT[:, 0, :], po[0][:], ACT.Copy)
                    act.activation(oT[:, 1, :], po[1][:], ACT.Copy).then_inc(o_copied, 1)

        @block.gpsimd
        def _(pool):
            pool.tensor_copy(csT[:], c.ctxT[:, :, 0:S]).then_inc(cs_ready, 1)
            with pool.Fori(0, B) as b:
                for kt in range(U):
                    pool.wait_ge(rden_ready, U * b + kt + 1)
                    e = ex[kt][:].rearrange("p r g q -> p (r g) q")
                    pool.tensor_tensor(e, e, rden[kt][:].unsqueeze(1).to_broadcast([P, H2, S]), ALU.mult).then_inc(weighted, 1)
                    if kt == 0:
                        pool.wait_ge(filled, 4 * b + 4)
                        pool.tensor_copy(csT[:], c.ctxT[:, :, ds(b * S + S, S)]).then_inc(cs_ready, 1)

        @block.vector
        def _(dve):
            link = Chain(dve, chain)
            moments(link, dve, c.st[:], mean[:], rstd[:], mt[:])
            rsqrt(link, dve, mt[:], rstd[:], mt2[:])
            dve.sem_inc(ready0, 1)
            base = link.n

            def rows_of(n):
                for u in range(U):
                    t = U * n + u
                    last = dve.tensor_scalar(xs[:, u, :], c.x[:, t, :], mean[:, ds(t, 1)], rstd[:, ds(t, 1)], ALU.subtract, ALU.mult)
                last.then_inc(xs_ready, 1)

            def lower(b, kt):
                dve.wait_ge(scored, U * b + kt + 1)
                dve.tensor_reduce(mx[kt][:], sc[:].rearrange("p r g q -> p q (r g)"), AX, ALU.max).then_inc(maxed, 1)
                dve.wait_ge(maxed, U * b + kt + 1)
                dve.tensor_tensor(low[kt][:].rearrange("p r g q -> p (r g) q"), sc[:].rearrange("p r g q -> p (r g) q"),
                                  mx[kt][:].unsqueeze(1).to_broadcast([P, H2, S]), ALU.subtract).then_inc(lowered, 1)

            def divide(link, b, kt):
                dve.wait_ge(exp_done, U * b + kt + 1)
                link(dve.tensor_reduce(den[kt][:], ex[kt][:].rearrange("p r g q -> p q (r g)"), AX, ALU.add))
                dve.reciprocal(rden[kt][:], den[kt][:]).then_inc(rden_ready, 1)

            rows_of(0)
            lower(0, 0)
            with dve.Fori(0, B // 2) as i:
                for s in range(2):
                    b = 2 * i + s
                    link = Chain(dve, chain, base + b * 4)
                    dve.wait_ge(filled, 4 * b + 1)
                    rows_of(b + 1)
                    lower(b, 1)
                    divide(link, b, 0)
                    lower(b + 1, 0)
                    divide(link, b, 1)
                    dve.wait_ge(out_done, b + 1)
                    v = c.x[:, ds(b * U, U), :].rearrange("p u d -> p (u d)")
                    dve.scalar_tensor_tensor(v, pb[0][:].rearrange("p u d -> p (u d)"), c.tg[:, 2:3], v,
                                             ALU.mult, ALU.add).then_inc(out_taken, 1)
                    dve.wait_ge(out_taken, b + 1)
                    for u in range(U):
                        link(dve.bn_stats(c.st[:, U * b + u, :], c.x[:, U * b + u, :]))


NROT = 4
BASE_SQ = 5
LEVELS = 12
NORM0 = 16.0
TAYLOR0 = (1.0, 1.0, 1 / 2, 1 / 6)
TAYLOR1 = (1 / 24, 1 / 120, 1 / 720, 1 / 5040, 1 / 40320)


def rotation(nc, I, c):
    with ExitStack() as ctx:
        sb = lambda n, s, d=F32: ctx.enter_context(nc.sbuf_tensor("rot_" + n, s, d))
        sem = lambda n: c.semaphore("rot_" + n)
        mats = lambda n: [sb(f"{n}{m}", [P, KT, D]) for m in range(NROT)]
        A, L, A2, A3, A4, T0, T1, R = (mats(n) for n in ("A", "L", "A2_", "A3_", "A4_", "T0_", "T1_", "R"))
        rowsum, norm = sb("rowsum", [P, NROT, KT]), sb("norm", [P, 2, NROT])
        over, half, scale = sb("over", [P, LEVELS, NROT]), sb("half", [P, LEVELS, NROT]), sb("scale", [P, NROT])
        flag, take, aside = sb("flag", [P, 1], I32), sb("take", [P, NROT]), sb("aside", [P, NROT])
        bank = [ctx.enter_context(nc.psum_tensor(f"rot_bank{m}", [P, KT, D], F32)) for m in range(NROT)]
        names = ("loaded", "chain", "norm_ready", "norm_all", "scaled", "done", "copied", "poly", "summed", "flagged",
                 "x_done", "x_taken", "x_turned", "x_copied", "took", "f_done", "f_copied")
        (loaded, chain, norm_ready, norm_all, scaled, done, copied, poly, summed, flagged,
         x_done, x_taken, x_turned, x_copied, took, f_done, f_copied) = (sem(n) for n in names)

        def turn(pe, out, src):
            for ot in range(KT):
                for kt in range(KT):
                    last = pe.transpose(out[:, kt, P * ot:P * ot + P], src[:, ot, P * kt:P * kt + P], c.ident[:])
            return last

        def product(pe, out, leftT, right):
            for ot in range(KT):
                for kt in range(KT):
                    last = pe.matmul(out[:, ot, :], leftT[:, kt, P * ot:P * ot + P], right[:, kt, :],
                                     start=(kt == 0), stop=(kt == KT - 1))
            return last

        STEPS = [(A, None, L), (L, A, A2), (A2, None, L), (L, A, A3), (L, A2, A4), (A4, None, L), (L, T1, R)]
        POLY = len(STEPS) - 1
        STEPS += [(R, None, L), (L, R, R)] * BASE_SQ + [(R, None, L)]

        with nc.Block() as block:
            @block.sync
            def _(sp):
                for m in range(NROT):
                    sp.dma_start(A[m][:], I["L2_ffn_gens"][m].rearrange("(t p) d -> p t d", p=P)).then_inc(loaded, 16)

            @block.tensor
            def _(pe):
                for k, (left, right, dst) in enumerate(STEPS):
                    for m in range(NROT):
                        if k == 0:
                            pe.wait_ge(scaled, m + 1)
                        elif k == POLY + 1:
                            pe.wait_ge(summed, m + 1)
                        else:
                            pe.wait_ge(copied, NROT * (k - 1 if k <= POLY else k - 2) + m + 1)
                        if k == POLY:
                            pe.wait_ge(poly, m + 1)
                        last = turn(pe, bank[m], left[m]) if right is None else product(pe, bank[m], left[m], right[m])
                        last.then_inc(done, 1)

            @block.scalar
            def _(act):
                for k, (left, right, dst) in enumerate(STEPS):
                    if k == POLY:
                        continue
                    for m in range(NROT):
                        act.wait_ge(done, NROT * k + m + 1)
                        act.activation(dst[m][:], bank[m][:], ACT.Copy).then_inc(copied, 1)

            @block.gpsimd
            def _(pool):
                pool.wait_ge(norm_ready, 1)
                pool.partition_all_reduce(norm[:, 1, :], norm[:, 0, :], P, bass.bass_isa.ReduceOp.max).then_inc(norm_all, 1)

            @block.vector
            def _(dve):
                link = Chain(dve, chain)
                dve.wait_ge(loaded, 16 * NROT)
                for m in range(NROT):
                    link(dve.tensor_reduce(rowsum[:, m, :], A[m][:], AX, ALU.add, apply_absolute_value=True))
                link(dve.tensor_reduce(norm[:, 0, :], rowsum[:], AX, ALU.max))
                dve.sem_inc(norm_ready, 1)
                dve.wait_ge(norm_all, 1)
                for k in range(LEVELS):
                    link(dve.tensor_scalar(over[:, k, :], norm[:, 1, :], NORM0 * 2.0 ** k, None, ALU.is_gt))
                link(dve.tensor_scalar(half[:], over[:], -0.5, 1.0, ALU.mult, ALU.add))
                link(dve.tensor_reduce(scale[:], half[:].rearrange("p k m -> p m k"), AX, ALU.mult))
                link(dve.tensor_scalar(scale[:], scale[:], 2.0 ** -BASE_SQ, None, ALU.mult))
                link(dve.tensor_reduce(flag[:], over[:, 0, :], AX, ALU.max))
                for m in range(NROT):
                    dve.tensor_scalar(A[m][:], A[m][:], scale[:, m:m + 1], None, ALU.mult).then_inc(scaled, 1)
                dve.wait_ge(scaled, NROT)
                for m in range(NROT):
                    dve.wait_ge(copied, NROT * 4 + m + 1)
                    link(dve.tensor_scalar(T1[m][:], A4[m][:], TAYLOR1[4], None, ALU.mult))
                    for coef, mat in ((TAYLOR1[3], A3), (TAYLOR1[2], A2), (TAYLOR1[1], A)):
                        link(dve.scalar_tensor_tensor(T1[m][:], mat[m][:], coef, T1[m][:], ALU.mult, ALU.add))
                    for kt in range(KT):
                        v = T1[m][:, kt, P * kt:P * kt + P]
                        link(dve.scalar_tensor_tensor(v, c.ident[:], TAYLOR1[0], v, ALU.mult, ALU.add))
                    dve.sem_inc(poly, 1)
                    link(dve.scalar_tensor_tensor(T0[m][:], A2[m][:], TAYLOR0[2], A[m][:], ALU.mult, ALU.add))
                    link(dve.scalar_tensor_tensor(T0[m][:], A3[m][:], TAYLOR0[3], T0[m][:], ALU.mult, ALU.add))
                    for kt in range(KT):
                        v = T0[m][:, kt, P * kt:P * kt + P]
                        link(dve.tensor_tensor(v, v, c.ident[:], ALU.add))
                for m in range(NROT):
                    dve.wait_ge(done, NROT * POLY + m + 1)
                    dve.tensor_tensor(R[m][:], bank[m][:], T0[m][:], ALU.add).then_inc(summed, 1)
                dve.wait_ge(summed, NROT)

        with nc.Block() as block:
            @block.tensor
            def _(pe):
                with pe.If(pe.value_load(flag[0:1, 0:1], min_val=0, max_val=1) > 0):
                    with pe.Fori(0, LEVELS) as k:
                        for m in range(NROT):
                            pe.wait_ge(x_copied, NROT * k + m)
                            product(pe, bank[m], L[m], R[m]).then_inc(x_done, 1)
                            pe.wait_ge(x_taken, NROT * k + m + 1)
                            turn(pe, bank[m], R[m]).then_inc(x_turned, 1)

            @block.scalar
            def _(act):
                with act.If(act.value_load(flag[0:1, 0:1], min_val=0, max_val=1) > 0):
                    with act.Fori(0, LEVELS) as k:
                        for m in range(NROT):
                            act.wait_ge(x_turned, NROT * k + m + 1)
                            act.activation(L[m][:], bank[m][:], ACT.Copy).then_inc(x_copied, 1)

            @block.vector
            def _(dve):
                with dve.If(dve.value_load(flag[0:1, 0:1], min_val=0, max_val=1) > 0):
                    with dve.Fori(0, LEVELS) as k:
                        dve.tensor_copy(take[:], over[:, k, :]).then_inc(took, 1)
                        for m in range(NROT):
                            dve.wait_ge(x_done, NROT * k + m + 1)
                            dve.wait_ge(took, (NROT + 1) * k + m + 1)
                            dve.tensor_copy(aside[:, m:m + 1], take[:, m:m + 1]).then_inc(took, 1)
                            v = R[m][:].rearrange("p k d -> p (k d)")
                            dve.copy_predicated(v, take[:, m:m + 1].bitcast(I32).to_broadcast([P, KT * D]),
                                                bank[m][:].rearrange("p k d -> p (k d)")).then_inc(x_taken, 1)

        with nc.Block() as block:
            M = [R[0], A[1], A[2], c.rot]

            @block.tensor
            def _(pe):
                for m in range(1, NROT):
                    if m > 1:
                        pe.wait_ge(f_copied, 2 * m - 3)
                        turn(pe, bank[0], M[m - 1]).then_inc(f_done, 1)
                        pe.wait_ge(f_copied, 2 * m - 2)
                    product(pe, bank[1], L[0], R[m]).then_inc(f_done, 1)

            @block.scalar
            def _(act):
                for m in range(1, NROT):
                    if m > 1:
                        act.wait_ge(f_done, 2 * m - 2)
                        act.activation(L[0][:], bank[0][:], ACT.Copy).then_inc(f_copied, 1)
                    act.wait_ge(f_done, 2 * m - 1)
                    act.activation(M[m][:], bank[1][:], ACT.Copy).then_inc(f_copied, 1)
                act.wait_ge(f_copied, 2 * NROT - 3)


NE, TOPK = 6, 2
FE = 512 // P
UNITS = FF1 // FE + NE


def layer2_ffn(nc, I, c):
    with ExitStack() as ctx:
        sb = lambda n, s, d=F32: ctx.enter_context(nc.sbuf_tensor("l2f_" + n, s, d))
        sem = lambda n: c.semaphore("l2f_" + n)
        z, dense, moe = sb("z", [P, NT, D]), sb("dense", [P, NT, D]), sb("moe", [P, NT, D])
        znT = sb("znT", [P, KT, NT * P])
        logit, w6 = sb("logit", [P, NT, 8]), sb("w6", [P, NT, NE])
        mean, rstd, mt, mt2 = sb("mean", [P, NTD]), sb("rstd", [P, NTD]), sb("mt", [P, NTD]), sb("mt2", [P, NTD])

        with ExitStack() as first:
            fsb = lambda n, s, d=F32: first.enter_context(nc.sbuf_tensor("l2f_" + n, s, d))
            fps = lambda n, s, d=F32: first.enter_context(nc.psum_tensor("l2f_" + n, s, d))
            st2, zs, zsT = fsb("st2", [P, NT, 6]), fsb("zs", [P, U, D]), fsb("zsT", [P, KT, S])
            ln_g, ln_b, gate_w, gate_b = fsb("ln_g", [P, D]), fsb("ln_b", [P, D]), fsb("gate_w", [P, KT, NE]), fsb("gate_b", [P, NE])
            tb, lb = fps("tb", [P, KT, S]), fps("lb", [P, U, 8])
            names = ("loaded", "chain", "zst", "zs_ready", "turned", "copied", "logits_done", "logits_taken", "resident")
            loaded, chain, zst, zs_ready, turned, copied, logits_done, logits_taken, resident = (sem(n) for n in names)
            block = first.enter_context(nc.Block())

            @block.sync
            def _(sp):
                sp.dma_start(ln_g[:], row(I["L2_ffn_ln_g"])).then_inc(loaded, 16)
                sp.dma_start(ln_b[:], row(I["L2_ffn_ln_b"])).then_inc(loaded, 16)
                sp.dma_start(gate_w[:], I["L2_ffn_gate_w"].rearrange("(t p) e -> p t e", p=P)).then_inc(loaded, 16)
                sp.dma_start(gate_b[:], row(I["L2_ffn_gate_b"])).then_inc(loaded, 16)

            @block.vector
            def _(dve):
                link = Chain(dve, chain)
                moments(link, dve, c.st[:], mean[:], rstd[:], mt[:])
                rsqrt(link, dve, mt[:], rstd[:], mt2[:])
                link(dve.memset(logit[:], -3.0e38))
                with dve.Fori(0, NT) as t:
                    dve.tensor_scalar(z[:, t, :], c.x[:, t, :], mean[:, ds(t, 1)], rstd[:, ds(t, 1)],
                                      ALU.subtract, ALU.mult).then_inc(zst, 1)
                    dve.wait_ge(zst, 2 * t + 1)
                    dve.bn_stats(st2[:, t, :], z[:, t, :]).then_inc(zst, 1)
                dve.wait_ge(zst, 2 * NT)
                moments(link, dve, st2[:], mean[:, 0:NT], rstd[:, 0:NT], mt[:, 0:NT])
                rsqrt(link, dve, mt[:, 0:NT], rstd[:, 0:NT], mt2[:, 0:NT])
                dve.wait_ge(loaded, 64)
                base = link.n
                with dve.Fori(0, B) as b:
                    link = Chain(dve, chain, base + b * 2)
                    dve.wait_ge(turned, b)
                    for u in range(U):
                        t = U * b + u
                        ins = dve.tensor_scalar(zs[:, u, :], z[:, t, :], mean[:, ds(t, 1)], rstd[:, ds(t, 1)],
                                                ALU.subtract, ALU.mult)
                    link(ins)
                    link(dve.tensor_tensor(zs[:], zs[:], ln_g[:].unsqueeze(1).to_broadcast([P, U, D]), ALU.mult))
                    dve.tensor_tensor(zs[:], zs[:], ln_b[:].unsqueeze(1).to_broadcast([P, U, D]), ALU.add).then_inc(zs_ready, 1)
                    dve.wait_ge(logits_done, b + 1)
                    dve.tensor_tensor(logit[:, ds(b * U, U), 0:NE], lb[:, :, 0:NE], gate_b[:].unsqueeze(1).to_broadcast([P, U, NE]),
                                      ALU.add).then_inc(logits_taken, 1)

            @block.tensor
            def _(pe):
                pe.wait_ge(loaded, 64)
                with pe.Fori(0, B) as b:
                    pe.wait_ge(zs_ready, b + 1)
                    pe.wait_ge(copied, 2 * b)
                    for u in range(U):
                        for kt in range(KT):
                            last = pe.transpose(tb[:, kt, P * u:P * u + P], zs[:, u, P * kt:P * kt + P], c.ident[:])
                    last.then_inc(turned, 1)
                    pe.wait_ge(copied, 2 * b + 1)
                    pe.wait_ge(logits_taken, b)
                    for u in range(U):
                        for kt in range(KT):
                            last = pe.matmul(lb[:, u, 0:NE], zsT[:, kt, P * u:P * u + P], gate_w[:, kt, :],
                                             start=(kt == 0), stop=(kt == KT - 1))
                    last.then_inc(logits_done, 1)

            @block.scalar
            def _(act):
                with act.Fori(0, B) as b:
                    act.wait_ge(turned, b + 1)
                    act.wait_ge(logits_done, b)
                    act.activation(zsT[:], tb[:], ACT.Copy).then_inc(copied, 1)
                    act.activation(znT[:, :, ds(b * S, S)], tb[:], ACT.Copy).then_inc(copied, 1)

        with ExitStack() as second:
            fsb = lambda n, s, d=F32: second.enter_context(nc.sbuf_tensor("l2f_" + n, s, d))
            fps = lambda n, s, d=F32: second.enter_context(nc.psum_tensor("l2f_" + n, s, d))
            top, idx, idxf = fsb("top", [P, NT, 8]), fsb("idx", [P, NT, 8], U32), fsb("idxf", [P, NT, 8])
            iota, wk, sel = fsb("iota", [P, NE]), fsb("wk", [P, NT, 4]), fsb("sel", [P, NT, NE])
            w6T, eb2 = fsb("w6T", [NE, NT * P]), fsb("eb2", [NE, D])
            tb = fps("tb2", [NE, NT * P])
            bb = [fps(f"bb{i}", [P, 2, D]) for i in range(2)]
            names = ("loaded2", "chain2", "tops", "diff_ready", "exp_ready", "w6_ready", "w6_turned", "w6T_ready", "b_done", "b_copied")
            loaded, chain, tops, diff_ready, exp_ready, w6_ready, w6_turned, w6T_ready, b_done, b_copied = (sem(n) for n in names)
            block = second.enter_context(nc.Block())

            @block.sync
            def _(sp):
                sp.dma_start(eb2[:], I["L2_ffn_eb2"]).then_inc(loaded, 16)

            @block.vector
            def _(dve):
                link = Chain(dve, chain)
                for e in range(NE):
                    link(dve.memset(iota[:, e:e + 1], float(e)))
                for t in range(NT):
                    dve.max(top[:, t, :], logit[:, t, :]).then_inc(tops, 1)
                for t in range(NT):
                    dve.wait_ge(tops, t + 1)
                    last = dve.max_index(idx[:, t, :], top[:, t, :], logit[:, t, :])
                link(last)
                link(dve.tensor_copy(idxf[:], idx[:]))
                dve.tensor_tensor(wk[:, :, 0], top[:, :, 1], top[:, :, 0], ALU.subtract).then_inc(diff_ready, 1)
                dve.wait_ge(exp_ready, 1)
                link(dve.tensor_scalar(wk[:, :, 2], wk[:, :, 1], 1.0, None, ALU.add))
                link(dve.reciprocal(wk[:, :, 2], wk[:, :, 2]))
                link(dve.tensor_tensor(wk[:, :, 3], wk[:, :, 1], wk[:, :, 2], ALU.mult))
                full = [P, NT, NE]
                for k, out in ((0, w6), (1, sel)):
                    link(dve.tensor_tensor(out[:], iota[:].unsqueeze(1).to_broadcast(full),
                                           idxf[:, :, k:k + 1].to_broadcast(full), ALU.is_equal))
                    link(dve.tensor_tensor(out[:], out[:], wk[:, :, 2 + k:3 + k].to_broadcast(full), ALU.mult))
                dve.tensor_tensor(w6[:], w6[:], sel[:], ALU.add).then_inc(w6_ready, 1)
                dve.wait_ge(w6_ready, 1)

            @block.scalar
            def _(act):
                act.wait_ge(diff_ready, 1)
                act.activation(wk[:, :, 1], wk[:, :, 0], ACT.Exp).then_inc(exp_ready, 1)
                act.wait_ge(w6_turned, 1)
                act.activation(w6T[:], tb[:], ACT.Copy).then_inc(w6T_ready, 1)
                for n in range(NT // 2):
                    act.wait_ge(b_done, n + 1)
                    act.activation(moe[:, 2 * n:2 * n + 2, :], bb[n % 2][:], ACT.Copy).then_inc(b_copied, 1)

            @block.tensor
            def _(pe):
                pe.wait_ge(w6_ready, 1)
                for t in range(NT):
                    last = pe.transpose(tb[:, P * t:P * t + P], w6[:, t, :], c.ident[:])
                last.then_inc(w6_turned, 1)
                pe.wait_ge(w6T_ready, 1)
                pe.wait_ge(loaded, 16)
                for n in range(NT // 2):
                    if n >= 2:
                        pe.wait_ge(b_copied, n - 1)
                    for m in range(2):
                        t = 2 * n + m
                        last = pe.matmul(bb[n % 2][:, m, :], w6T[:, P * t:P * t + P], eb2[:], start=True, stop=True)
                    last.then_inc(b_done, 1)

        with ExitStack() as third:
            fsb = lambda n, s, d=F32: third.enter_context(nc.sbuf_tensor("l2f_" + n, s, d))
            fps = lambda n, s, d=F32: third.enter_context(nc.psum_tensor("l2f_" + n, s, d))
            aw1, aw2 = fsb("aw1", [P, KT, FF1 * P]), fsb("aw2", [P, FF1, D])
            ew1, ew2 = fsb("ew1", [P, NE, KT, FE * P]), fsb("ew2", [P, NE, FE, D])
            ab1, eb1, ab2 = fsb("ab1", [P, FF1]), fsb("eb1", [P, NE * FE]), fsb("ab2", [P, D])
            hs = [fsb(f"hs{i}", [P, FE, QT]) for i in range(2)]
            acc, accT = fsb("acc", [P, QUADS, D]), fsb("accT", [P, KT, QT])
            hb = [fps(f"hb{i}", [P, QT]) for i in range(2)]
            ob = [[fps(f"ob{i}{j}", [P, 2, D]) for j in range(2)] for i in range(2)]
            rb = [fps(f"rb{i}", [P, 2, D]) for i in range(2)]
            names = ("a_loaded", "e_loaded", "chain3", "h_done", "gelu_done", "o_done", "o_taken", "acc_turned", "accT_ready",
                     "rot_done", "rot_taken")
            a_loaded, e_loaded, chain, h_done, gelu_done, o_done, o_taken, acc_turned, accT_ready, rot_done, rot_taken = (sem(n) for n in names)
            block = third.enter_context(nc.Block())

            @block.sync
            def _(sp):
                sp.dma_start(aw1[:], I["L2_ffn_aw1"].rearrange("(t p) f -> p t f", p=P)).then_inc(a_loaded, 16)
                sp.dma_start(ab1[:], col(I["L2_ffn_ab1"])).then_inc(a_loaded, 16)
                sp.dma_start(eb1[:], col(I["L2_ffn_eb1"].rearrange("e f -> (e f)"))).then_inc(a_loaded, 16)
                sp.dma_start(aw2[:], I["L2_ffn_aw2"].rearrange("(t p) d -> p t d", p=P)).then_inc(a_loaded, 16)
                sp.dma_start(ab2[:], row(I["L2_ffn_ab2"])).then_inc(a_loaded, 16)
                for e in range(NE):
                    sp.dma_start(ew1[:, e], I["L2_ffn_ew1"][e].rearrange("(t p) f -> p t f", p=P)).then_inc(e_loaded, 16)
                    sp.dma_start(ew2[:, e], I["L2_ffn_ew2"][e].rearrange("(t p) d -> p t d", p=P)).then_inc(e_loaded, 16)

            DENSE = FF1 // FE

            @block.tensor
            def _(pe):
                pe.wait_ge(a_loaded, 80)
                pe.wait_ge(e_loaded, 32 * NE)
                with pe.Fori(0, NQ) as i:
                    def up(k):
                        for f in range(FE):
                            n = FE * k + f
                            pe.wait_ge(gelu_done, FE * UNITS * i + max(n - 1, 0))
                            for kt in range(KT):
                                w = aw1[:, kt, P * n:P * n + P] if k < DENSE else ew1[:, k - DENSE, kt, P * f:P * f + P]
                                last = pe.matmul(hb[n % 2][:], w, znT[:, kt, ds(i * QT, QT)], start=(kt == 0), stop=(kt == KT - 1))
                            last.then_inc(h_done, 1)

                    def down(k):
                        pe.wait_ge(gelu_done, FE * UNITS * i + FE * (k + 1))
                        pe.wait_ge(o_taken, UNITS * i + max(k - 1, 0))
                        for t in range(QUADS):
                            for f in range(FE):
                                w = aw2[:, FE * k + f, :] if k < DENSE else ew2[:, k - DENSE, f, :]
                                last = pe.matmul(ob[k % 2][t // 2][:, t % 2, :], hs[k % 2][:, f, P * t:P * t + P], w,
                                                 start=(f == 0), stop=(f == FE - 1))
                        last.then_inc(o_done, 1)

                    up(0)
                    for k in range(UNITS):
                        if k + 1 < UNITS:
                            up(k + 1)
                        down(k)
                    pe.wait_ge(o_taken, UNITS * (i + 1))
                    pe.wait_ge(rot_taken, i)
                    for t in range(QUADS):
                        for kt in range(KT):
                            last = pe.transpose(rb[kt][:, t // 2, P * (t % 2):P * (t % 2) + P],
                                                acc[:, t, P * kt:P * kt + P], c.ident[:])
                    last.then_inc(acc_turned, 1)
                    pe.wait_ge(accT_ready, i + 1)
                    for t in range(QUADS):
                        for kt in range(KT):
                            last = pe.matmul(rb[t // 2][:, t % 2, :], accT[:, kt, P * t:P * t + P], c.rot[:, kt, :],
                                             start=(kt == 0), stop=(kt == KT - 1))
                    last.then_inc(rot_done, 1)

            @block.scalar
            def _(act):
                act.wait_ge(a_loaded, 80)
                act.activation(mt[:, 0:1], ab1[:, 0:1], ACT.Gelu)
                with act.Fori(0, NQ) as i:
                    for k in range(UNITS):
                        act.wait_ge(o_done, UNITS * i + max(k - 1, 0))
                        for f in range(FE):
                            n = FE * k + f
                            bias = ab1[:, n:n + 1] if k < DENSE else eb1[:, n - FF1:n - FF1 + 1]
                            act.wait_ge(h_done, FE * UNITS * i + n + 1)
                            act.activation(hs[k % 2][:, f, :], hb[n % 2][:], ACT.Gelu, bias=bias).then_inc(gelu_done, 1)
                    act.wait_ge(acc_turned, i + 1)
                    for kt in range(KT):
                        ins = act.activation(accT[:, kt, :], rb[kt][:], ACT.Copy)
                    ins.then_inc(accT_ready, 1)
                    act.wait_ge(rot_done, i + 1)
                    for j in range(2):
                        ins = act.activation(moe[:, ds(i * QUADS + 2 * j, 2), :], rb[j][:], ACT.Copy)
                    ins.then_inc(rot_taken, 1)

            @block.vector
            def _(dve):
                dve.wait_ge(a_loaded, 80)
                with dve.Fori(0, NQ) as i:
                    for k in range(UNITS):
                        dve.wait_ge(o_done, UNITS * i + k + 1)
                        if k >= 1:
                            dve.wait_ge(o_taken, UNITS * i + k)
                        if k == DENSE:
                            dve.wait_ge(acc_turned, i)
                        for j in range(2):
                            if k < DENSE:
                                d = dense[:, ds(i * QUADS + 2 * j, 2), :]
                                other = ab2[:].unsqueeze(1).to_broadcast([P, 2, D]) if k == 0 else d
                                last = dve.tensor_tensor(d, ob[k % 2][j][:], other, ALU.add)
                            else:
                                for m in range(2):
                                    t = 2 * j + m
                                    old = moe[:, i * QUADS + t, :] if k == DENSE else acc[:, t, :]
                                    last = dve.scalar_tensor_tensor(acc[:, t, :], ob[k % 2][j][:, m, :],
                                                                    w6[:, i * QUADS + t, k - DENSE:k - DENSE + 1], old,
                                                                    ALU.mult, ALU.add)
                        last.then_inc(o_taken, 1)

        with ExitStack() as fourth:
            fsb = lambda n, s, d=F32: fourth.enter_context(nc.sbuf_tensor("l2f_" + n, s, d))
            gc_w, gc_b = fsb("gc_w", [P, 2, D]), fsb("gc_b", [P, 1])
            gate, gdot = fsb("gate", [P, NT]), fsb("gdot", [P, NT])
            ta, tc = [fsb(f"ta{i}", [P, U, D]) for i in range(2)], [fsb(f"tc{i}", [P, U, D]) for i in range(2)]
            names = ("loaded4", "chain4", "pa_ready", "gdots", "gates", "delta_ready")
            loaded, chain, pa_ready, gdots, gates, delta_ready = (sem(n) for n in names)
            block = fourth.enter_context(nc.Block())

            @block.sync
            def _(sp):
                v = I["L2_ffn_gc_w"].rearrange("(a d) o -> a (d o)", a=2)
                for k in range(2):
                    sp.dma_start(gc_w[:, k, :], row(v[k])).then_inc(loaded, 16)
                sp.dma_start(gc_b[:], row(I["L2_ffn_gc_b"])).then_inc(loaded, 16)

            wide = lambda k: gc_w[:, k, :].unsqueeze(1).to_broadcast([P, U, D])

            @block.gpsimd
            def _(pool):
                pool.wait_ge(loaded, 48)
                with pool.Fori(0, B // 2) as i:
                    for s in range(2):
                        b = 2 * i + s
                        pool.wait_ge(gdots, 2 * i)
                        pool.tensor_tensor(ta[s][:], dense[:, ds(b * U, U), :], wide(0), ALU.mult).then_inc(pa_ready, 1)
                with pool.Fori(0, B) as b:
                    v = moe[:, ds(b * U, U), :]
                    pool.wait_ge(gdots, B)
                    pool.tensor_tensor(v, v, dense[:, ds(b * U, U), :], ALU.subtract).then_inc(delta_ready, 1)

            @block.scalar
            def _(act):
                act.wait_ge(gdots, B)
                act.activation(gate[:], gdot[:], ACT.Sigmoid, bias=gc_b[:, 0:1]).then_inc(gates, 1)

            @block.vector
            def _(dve):
                dve.wait_ge(loaded, 48)
                with dve.Fori(0, B // 2) as i:
                    link = Chain(dve, chain, i * 4)
                    for s in range(2):
                        b = 2 * i + s
                        link(dve.tensor_tensor(tc[s][:], moe[:, ds(b * U, U), :], wide(1), ALU.mult))
                        dve.wait_ge(pa_ready, b + 1)
                        link(dve.tensor_tensor(tc[s][:], tc[s][:], ta[s][:], ALU.add))
                        dve.tensor_reduce(gdot[:, ds(b * U, U)], tc[s][:], AX, ALU.add).then_inc(gdots, 1)
                dve.wait_ge(gdots, B)
                dve.wait_ge(gates, 1)
                base = 4 * (B // 2)
                with dve.Fori(0, B) as b:
                    link = Chain(dve, chain, base + b * 5)
                    dve.wait_ge(delta_ready, b + 1)
                    for u in range(U):
                        t = U * b + u
                        last = dve.scalar_tensor_tensor(tc[0][:, u, :], moe[:, t, :], gate[:, ds(t, 1)], dense[:, t, :], ALU.mult, ALU.add)
                    link(last)
                    link(dve.tensor_tensor(tc[1][:], tc[0][:], z[:, ds(b * U, U), :], ALU.add))
                    v = c.x[:, ds(b * U, U), :]
                    link(dve.scalar_tensor_tensor(v.rearrange("p u d -> p (u d)"), tc[1][:].rearrange("p u d -> p (u d)"),
                                                  c.tg[:, 6:7], v.rearrange("p u d -> p (u d)"), ALU.mult, ALU.add))
                    for u in range(U):
                        link(dve.bn_stats(c.st[:, U * b + u, :], c.x[:, U * b + u, :]))


def store(nc, c, out):
    with ExitStack() as ctx:
        stored = c.semaphore("stored")
        block = ctx.enter_context(nc.Block())

        @block.sync
        def _(sp):
            for b in range(B):
                sp.dma_start(out[b].rearrange("(u p) d -> p u d", p=P), c.x[:, U * b:U * b + U, :]).then_inc(stored, 16)
            sp.wait_ge(stored, 16 * B)


STAGES = (layer0_attention, layer0_ffn, layer1_attention, layer1_ffn, layer2_attention, rotation, layer2_ffn,
          layer3_attention, layer3_ffn)


def program(nc, I, out, stages=STAGES):
    with ExitStack() as ctx:
        ctx.enter_context(nc.allow_non_contiguous_dma(reason="a few short bias columns"))
        c = Core()
        c.nc, c.sems = nc, []
        sb = lambda n, s, d=F32: ctx.enter_context(nc.sbuf_tensor(n, s, d))
        c.x = sb("x", [P, NTD, D])
        c.st = sb("st", [P, NTD, 6])
        c.ctxT = sb("ctxT", [P, KT, TD])
        c.ident = sb("ident", [P, P])
        c.identb = sb("identb", [P, P], BF16)
        c.ones = sb("ones", [P, P])
        c.g = sb("g", [P, 8])
        c.tg = sb("tg", [P, 8])
        c.rot = sb("rot", [P, KT, D])
        setup(nc, I, c)
        for n, s in enumerate(stages):
            s(nc, I, c)
            if n == 4:
                nc.clear_and_free_semaphores(c.sems)
                c.sems = []
                nc.all_engine_barrier()
        store(nc, c, out)


_INS = [
    "x", "ctx_1024", "mask_Bx1xSxS2_bf1", "g_xattn", "g_ffn", "L0_xattn_Wq", "L0_xattn_bq", "L0_xattn_Wk",
    "L0_xattn_bk", "L0_xattn_Wv", "L0_xattn_bv", "L0_xattn_q_scale", "L0_xattn_q_bias", "L0_xattn_k_scale",
    "L0_xattn_k_bias", "L0_ffn_W_in", "L0_ffn_b_in", "L0_ffn_W_out", "L0_ffn_b_out", "L1_xattn_Wq", "L1_xattn_Wkv",
    "L1_xattn_Wout", "L1_xattn_bout", "L1_ffn_W1", "L1_ffn_b1", "L1_ffn_W2", "L1_ffn_b2", "L2_xattn_W_Q",
    "L2_xattn_W_K", "L2_xattn_W_V", "L2_xattn_W_O", "L2_ffn_ln_g", "L2_ffn_ln_b", "L2_ffn_aw1", "L2_ffn_ab1",
    "L2_ffn_aw2", "L2_ffn_ab2", "L2_ffn_gate_w", "L2_ffn_gate_b", "L2_ffn_ew1", "L2_ffn_eb1", "L2_ffn_ew2",
    "L2_ffn_eb2", "L2_ffn_gens", "L2_ffn_gc_w", "L2_ffn_gc_b", "L3_xattn_Wq", "L3_xattn_bq", "L3_xattn_Wk",
    "L3_xattn_bk", "L3_xattn_Wv", "L3_xattn_bv", "L3_xattn_Wo", "L3_xattn_bo", "L3_ffn_clip_x", "L3_ffn_clip_down",
    "L3_ffn_w_gate", "L3_ffn_w_up", "L3_ffn_w_down",
]


def kernel(**inputs):
    import numpy as np
    import concourse.bacc as bacc
    from concourse.bass_utils import run_bass_kernel_spmd

    nc = bacc.Bacc("TRN2", target_bir_lowering=False, num_devices=1)
    arrays, drams = {}, {}
    for name in _INS:
        a = np.ascontiguousarray(inputs[name])
        if a.dtype == np.bool_:
            a = a.view(np.uint8)
        arrays["in_" + name] = a
        drams[name] = nc.dram_tensor("in_" + name, a.shape, mybir.dt.from_np(a.dtype), kind="ExternalInput").ap()
    out = nc.dram_tensor("out_0", (B, S, D), F32, kind="ExternalOutput").ap()
    program(nc, drams, out)
    r = run_bass_kernel_spmd(nc, [arrays], core_ids=[0])
    return r.results[0]["out_0"]
```

```python
import concourse.bass as bass
from concourse import mybir
from contextlib import ExitStack

F32 = mybir.dt.float32
BF16 = mybir.dt.bfloat16
I32 = mybir.dt.int32
U32 = mybir.dt.uint32
U8 = mybir.dt.uint8
ALU = mybir.AluOpType
ACT = mybir.ActivationFunctionType
AX = mybir.AxisListType.X
ds = bass.ds

P = 128
B, S, D = 8, 256, 256
U = S // P
KT = D // P
NT = B * U
NTD = NT + 2 * U
TD = NTD * P
LN_EPS = 1e-5
ROUND = 12582912.0
ROUND256 = 3221225472.0
MASKED = 4294967296.0
HD = 16
HP = 32
NH = D // HD
NG = 4


class Chain:

    def __init__(self, eng, sem, base=0):
        self.eng, self.sem, self.base, self.n = eng, sem, base, 0

    def __call__(self, ins):
        self.n += 1
        ins.then_inc(self.sem, 1)
        self.eng.wait_ge(self.sem, self.base + self.n)


def rsqrt(link, eng, v, y, t):
    rsqrt_seed(link, eng, v, y)
    for _ in range(3):
        newton(link, eng, v, y, t)


def rsqrt_seed(link, eng, v, y):
    link(eng.tensor_scalar(y.bitcast(I32), v.bitcast(I32), 1, None, ALU.logical_shift_right))
    link(eng.tensor_scalar(y.bitcast(I32), y.bitcast(I32), -1.0, float(0x5F3759DF), ALU.mult, ALU.add))


def newton(link, eng, v, y, t):
    link(eng.tensor_tensor(t, y, y, ALU.mult))
    link(eng.tensor_tensor(t, t, v, ALU.mult))
    link(eng.tensor_scalar(t, t, -0.5, 1.5, ALU.mult, ALU.add))
    link(eng.tensor_tensor(y, y, t, ALU.mult))



def moments(link, eng, st, mean, rstd, t):
    link(eng.tensor_tensor(mean, st[:, :, 1], st[:, :, 4], ALU.add))
    link(eng.tensor_scalar(mean, mean, 0.5, None, ALU.mult))
    link(eng.tensor_tensor(t, st[:, :, 1], st[:, :, 4], ALU.subtract))
    link(eng.tensor_tensor(t, t, t, ALU.mult))
    link(eng.tensor_tensor(rstd, st[:, :, 2], st[:, :, 5], ALU.add))
    link(eng.tensor_scalar(rstd, rstd, 1.0 / D, LN_EPS, ALU.mult, ALU.add))
    link(eng.scalar_tensor_tensor(t, t, 0.25, rstd, ALU.mult, ALU.add))



class Core:

    def semaphore(self, name):
        self.sems.append(self.nc.alloc_semaphore(name=name))
        return self.sems[-1]


def row(ap, parts=P):
    return ap.partition_broadcast(parts)


def col(ap):
    return ap.rearrange("(t p) -> p t", p=P)


def setup(nc, I, c):
    with ExitStack() as ctx:
        sem = lambda n: c.semaphore("setup_" + n)
        ctx_in = ctx.enter_context(nc.sbuf_tensor("ctx_in", [P, NT, D], F32))
        tr = ctx.enter_context(nc.psum_tensor("setup_tr", [P, 4, KT, S], F32))
        x_loaded, ctx_loaded = ([sem(f"{n}_loaded{b}") for b in range(B)] for n in ("x", "ctx"))
        g_loaded = sem("g_loaded")
        zeroed, ident_made, tr_done, tr_out = sem("zeroed"), sem("ident"), sem("tr"), sem("tr_out")
        stats, tanhs, pool_chain = sem("stats"), sem("tanhs"), sem("pool_chain")
        block = ctx.enter_context(nc.Block())

        @block.sync
        def _(sp):
            for b in range(B):
                sp.dma_start(ctx_in[:, U * b:U * b + U, :],
                             I["ctx_1024"][b].rearrange("(u p) d -> p u d", p=P)).then_inc(ctx_loaded[b], 16)
                sp.dma_start(c.x[:, U * b:U * b + U, :],
                             I["x"][b].rearrange("(u p) d -> p u d", p=P)).then_inc(x_loaded[b], 16)
            sp.dma_start(c.g[:, 0:4], row(I["g_xattn"])).then_inc(g_loaded, 16)
            sp.dma_start(c.g[:, 4:8], row(I["g_ffn"])).then_inc(g_loaded, 16)

        @block.gpsimd
        def _(pool):
            link = Chain(pool, pool_chain)
            link(pool.memset(c.ident[:], 0.0))
            link(pool.affine_select(out=c.ident[:], in_=c.ident[:], compare_op=ALU.not_equal, fill=1.0,
                                    base=0, pattern=[[-1, P]], channel_multiplier=1))
            pool.tensor_copy(c.identb[:], c.ident[:]).then_inc(ident_made, 1)
            pool.memset(c.ones[:], 1.0).then_inc(ident_made, 1)

        @block.scalar
        def _(act):
            for b in range(B):
                act.wait_ge(tr_done, b + 1)
                act.activation(c.ctxT[:, :, S * b:S * b + S], tr[:, b % 4], ACT.Copy).then_inc(tr_out, 1)
            act.wait_ge(g_loaded, 32)
            act.activation(c.tg[:], c.g[:], ACT.Tanh).then_inc(tanhs, 1)

        @block.vector
        def _(dve):
            dve.memset(c.x[:, NT:NTD, :], 0.0).then_inc(zeroed, 1)
            dve.memset(c.ctxT[:, :, B * S:], 0.0)
            dve.wait_ge(zeroed, 1)
            for t in [*range(NT, NTD), *range(NT)]:
                if t < NT and t % U == 0:
                    dve.wait_ge(x_loaded[t // U], 16)
                dve.bn_stats(c.st[:, t, :], c.x[:, t, :]).then_inc(stats, 1)
            dve.wait_ge(stats, NTD)

        @block.tensor
        def _(pe):
            pe.wait_ge(ident_made, 2)
            for b in range(B):
                pe.wait_ge(ctx_loaded[b], 16)
                if b >= 4:
                    pe.wait_ge(tr_out, b - 3)
                for u in range(U):
                    for kt in range(KT):
                        last = pe.transpose(tr[:, b % 4, kt, P * u:P * u + P],
                                            ctx_in[:, U * b + u, P * kt:P * kt + P], c.ident[:])
                last.then_inc(tr_done, 1)


PARTS = 6
Q_PARTS = ((0, 3, 4), (1, 5), (2,))
K_PARTS = ((0, 2, 5), (1, 4), (3,))
SR = PARTS * HD
AHEAD = 6
STACKS = 8


class Fillings:

    def __init__(self, a, first, each):
        self.a, self.first, self.each = a, first, each

    def place(self, key, b):
        if b is None:
            f = self.first.index(key)
            return f % 2, f // 2
        f = len(self.first) + self.each.index(key)
        return f % 2, f // 2 + b * (len(self.each) // 2)

    def claim(self, pe, key, b):
        bank, before = self.place(key, b)
        pe.wait_ge(self.a.taken[bank], before)
        return self.a.bank[bank]

    def filled(self, key, b):
        return self.a.filled[self.place(key, b)[0]]

    def await_filled(self, eng, key, b):
        bank, before = self.place(key, b)
        eng.wait_ge(self.a.filled[bank], before + 1)
        return self.a.bank[bank]

    def taken(self, key, b):
        return self.a.taken[self.place(key, b)[0]]

    def await_taken(self, eng, key, b):
        bank, before = self.place(key, b)
        eng.wait_ge(self.a.taken[bank], before + 1)

    def await_before(self, eng, key, b):
        bank, before = self.place(key, b)
        eng.wait_ge(self.a.filled[bank], before)


def halves(bank):
    return bank[:].rearrange("p a n -> p (a n)").bitcast(BF16)


def values_pe(pe, a, b, n, s):
    g, r = n // 4, HP * (n % 4)
    pe.wait_ge(a.exp_done, NH * b + n + 1)
    if n == 0:
        a.await_values(pe, b)
        pe.wait_ge(a.o_copied, 2 * b)
    for kt in range(U):
        last = pe.matmul(a.po[g // 2][r:r + HP, g % 2, :], a.va[s][:, kt, a.value_slot(n), :],
                         a.pT[n % 2][:, kt, :], start=(kt == 0), stop=(kt == U - 1))
    last.then_inc(a.pv_done, 1)


def core_pe(pe, c, a, fills, b, s, masked, mid):

    def scores(n):
        g, j = n // 4, n % 4
        if j == 0:
            fills.await_taken(pe, ("m", g), b if g else b - 1)
            if masked and g == 0:
                fills.await_taken(pe, ("pen", 0), b - 1)
        pe.wait_ge(a.exp_done, NH * b + max(n - 1, 0))
        for kt in range(U):
            pe.matmul(a.sc[n % 2][:, kt, :], a.qk[s][:, 1, n, P * kt:P * kt + P], a.qk[s][:, 0, n, :],
                      start=True, stop=False)
            if masked:
                pe.matmul(a.sc[n % 2][:, kt, :], c.identb[:], a.penT[s][:, kt, :], start=False, stop=False)
            last = pe.matmul(a.sc[n % 2][:, kt, :], a.pick[:, j, :], a.mT[g % 2][:], start=False, stop=True)
        last.then_inc(a.scored, 1)

    for n in range(NH):
        if n + AHEAD < NH:
            max_scores_pe(pe, c, a, fills, b, n + AHEAD, s, masked, b)
        else:
            max_scores_pe(pe, c, a, fills, b + 1, n + AHEAD - NH, 1 - s, masked, b)
        scores(n)
        if n >= 1:
            values_pe(pe, a, b, n - 1, s)
        mid(n)
    values_pe(pe, a, b, NH - 1, s)


def max_scores_pe(pe, c, a, fills, b, n, s, masked, turn):
    if n == 0:
        for m in range(STACKS - 3, STACKS):
            fills.await_taken(pe, ("s", m), turn)
        if masked:
            pe.wait_ge(a.pen_ready, b + 1)
    if turn is not None or n >= 2:
        pe.wait_ge(a.max_reduced, NH * b + n - 1)
    for qt in range(U):
        last = pe.matmul(a.smax[n % 2][:, qt, :], a.qk[s][:, 0, n, P * qt:P * qt + P], a.qk[s][:, 1, n, :],
                         start=True, stop=not masked)
        if masked:
            last = pe.matmul(a.smax[n % 2][:, qt, :], c.identb[:], a.pen[s][:, qt, :], start=False, stop=True)
    last.then_inc(a.max_scored, 1)


def turn_maxima_pe(pe, c, a, fills, key, b, group):
    bank = halves(fills.claim(pe, key, b))
    pe.wait_ge(a.maxima_split, group + 1)
    for qt in range(U):
        last = pe.transpose(bank[0:12, P * qt:P * qt + P], a.mparts[:, qt, :, :].rearrange("p k j -> p (k j)"),
                            c.identb[:])
    last.then_inc(fills.filled(key, b), 1)


def take_maxima_act(act, a, fills, key, b, group, slot):
    bank = halves(fills.await_filled(act, key, b))
    if b is not None:
        act.wait_ge(a.scored, 4 * group - 4)
    act.activation(a.mT[slot][:], bank[0:12, 0:S], ACT.Copy).then_inc(fills.taken(key, b), 1)


def idle_fill_pe(pe, c, a, fills):
    bank = fills.claim(pe, ("idle", 0), None)
    pe.transpose(bank[:, 0, 0:P], c.ident[:], c.ident[:]).then_inc(fills.filled(("idle", 0), None), 1)


def idle_take_act(act, a, fills):
    bank = fills.await_filled(act, ("idle", 0), None)
    act.activation(a.spare[:], bank[:, 0, 0:1], ACT.Copy).then_inc(fills.taken(("idle", 0), None), 1)


def turn_stacks_pe(pe, c, a, fills, key, b, n):
    bank = halves(fills.claim(pe, key, b))
    if key[1] == 0:
        pe.wait_ge(a.stacked, n + 1)
    for k in range(2):
        for h in range(2):
            for u in range(U):
                at = ((k * 2 + h) * U + u) * P
                last = pe.transpose(bank[0:SR, at:at + P], a.stack[:, u, k, 2 * key[1] + h, :, :].rearrange("p s e -> p (s e)"),
                                    c.identb[:])
    last.then_inc(fills.filled(key, b), 1)


def take_stacks(eng, a, fills, key, b, dst, copy):
    bank = halves(fills.await_filled(eng, key, b))
    copy(a.stack_out(dst, key[1]), a.stack_in(bank[0:SR])).then_inc(fills.taken(key, b), 1)


def turn_outputs_pe(pe, c, a, fills, half, b):
    key = ("o", half)
    bank = fills.claim(pe, key, b)
    pe.wait_ge(a.o_copied, 2 * b + half + 1)
    for qt in range(U):
        for g in range(2):
            last = pe.transpose(bank[:, qt, P * g:P * g + P], a.oS[:, 2 * half + g, P * qt:P * qt + P], c.ident[:])
    last.then_inc(fills.filled(key, b), 1)


def normalise_dve(dve, link, a, fills, half, b):
    key = ("o", half)
    bank = fills.await_filled(dve, key, b)
    o = bank[:].rearrange("p q (h e) -> p q h e", e=HP)
    link(dve.reciprocal(a.rden[:], o[:, :, :, HD:HD + 1]))
    dve.tensor_tensor(a.on[:, half], o[:, :, :, 0:HD], a.rden[:].to_broadcast([P, U, 8, HD]),
                      ALU.mult).then_inc(fills.taken(key, b), 1)


def copy_outputs_act(act, a, b, half):
    act.wait_ge(a.pv_done, NH * b + 8 * half + 8)
    a.await_outputs_used(act, b)
    act.activation(a.oS[:, 2 * half:2 * half + 2, :], a.po[half][:], ACT.Copy).then_inc(a.o_copied, 1)


def reduce_dve(dve, a, b, n):
    dve.wait_ge(a.max_scored, NH * b + n + 1)
    dve.tensor_reduce(a.mneg[(n // 4) % 2][:, :, n % 4:n % 4 + 1], a.smax[n % 2][:], AX, ALU.max,
                      negate=True).then_inc(a.max_reduced, 1)


def split_maxima_dve(dve, link, a, b, g, turned):
    m = a.mneg[g % 2][:]
    if turned is not None:
        turned()
    dve.wait_ge(a.max_reduced, NH * b + 4 * g + 4)
    link(dve.tensor_copy(a.mparts[:, :, 0, :], m))
    link(dve.tensor_tensor(a.mrest[:], m, a.mparts[:, :, 0, :], ALU.subtract))
    link(dve.tensor_copy(a.mparts[:, :, 1, :], a.mrest[:]))
    dve.tensor_tensor(a.mparts[:, :, 2, :], a.mrest[:], a.mparts[:, :, 1, :], ALU.subtract).then_inc(a.maxima_split, 1)


SPLIT_LINKS = 3


def first_parts_act(act, a, n):
    for u in range(U):
        a.tm_ready(act, n, u)
        act.activation(a.stack[:, u, :, :, 0, :].rearrange("p k h e -> p (k h) e"), a.tm(u), ACT.Copy).then_inc(a.part1, 1)


def second_parts_act(act, a, n):
    for u in range(U):
        act.wait_ge(a.rest1, U * n + u + 1)
        act.activation(a.stack[:, u, :, :, 1, :].rearrange("p k h e -> p (k h) e"),
                       a.rest[:, u].rearrange("p k h e -> p (k h) e"), ACT.Copy).then_inc(a.part2, 1)


def parts_dve(dve, a, n, half):
    wide = lambda v, r: v.to_broadcast([P, NH, r, HD])
    for u in range(U):
        st = a.stack[:, u]
        if half == 0:
            dve.wait_ge(a.part1, U * n + u + 1)
            dve.tensor_tensor(a.rest[:, u].rearrange("p k h e -> p (k h) e"), a.tm(u),
                              st[:, :, :, 0, :].rearrange("p k h e -> p (k h) e"), ALU.subtract).then_inc(a.rest1, 1)
            dve.tensor_copy(st[:, 0, :, 3:5, :], wide(st[:, 0, :, 0:1, :], 2))
            dve.tensor_copy(st[:, 1, :, 2:6:3, :], wide(st[:, 1, :, 0:1, :], 2))
        else:
            dve.wait_ge(a.part2, U * n + u + 1)
            dve.tensor_tensor(st[:, 0, :, 2, :], a.rest[:, u, 0], st[:, 0, :, 1, :], ALU.subtract)
            dve.tensor_tensor(st[:, 1, :, 3, :], a.rest[:, u, 1], st[:, 1, :, 1, :], ALU.subtract)
            dve.tensor_copy(st[:, 0, :, 5, :], st[:, 0, :, 1, :])
            last = dve.tensor_copy(st[:, 1, :, 4, :], st[:, 1, :, 1, :])
    if half == 1:
        last.then_inc(a.stacked, 1)


def attention_tiles(nc, c, ctx, tag):
    a = Core()
    sb = lambda n, s, d=F32: ctx.enter_context(nc.sbuf_tensor(tag + n, s, d))
    ps = lambda n, s, d=F32: ctx.enter_context(nc.psum_tensor(tag + n, s, d))
    sem = lambda n: c.semaphore(tag + n)
    a.sb, a.ps, a.sem = sb, ps, sem
    a.stack = sb("stack", [P, U, 2, NH, PARTS, HD], BF16)
    a.rest = sb("rest", [P, U, 2, NH, HD])
    a.qk = [sb(f"qk{i}", [SR, 2, NH, S], BF16) for i in range(2)]
    a.va = [sb(f"va{i}", [P, U, NH, HP]) for i in range(2)]
    a.pT = [sb(f"pT{i}", [P, U, S]) for i in range(2)]
    a.mneg = [sb(f"mneg{i}", [P, U, 4]) for i in range(2)]
    a.mrest = sb("mrest", [P, U, 4])
    a.mparts = sb("mparts", [P, U, 3, 4], BF16)
    a.mT = [sb(f"mT{i}", [12, S], BF16) for i in range(2)]
    a.pick = sb("pick", [12, 4, P], BF16)
    a.pick4 = sb("pick4", [12, 4])
    a.xs = sb("xs", [P, U, D])
    a.xsT = sb("xsT", [P, KT, S])
    a.csT = sb("csT", [P, KT, S])
    a.mean, a.rstd, a.mt = sb("mean", [P, NTD]), sb("rstd", [P, NTD]), sb("mt", [P, NTD])
    a.oS = sb("oS", [P, NG, S])
    a.on, a.rden = sb("on", [P, 2, U, 8, HD]), sb("rden", [P, U, 8, 1])
    a.spare = sb("spare", [P, 1])
    a.smax = [ps(f"smax{i}", [P, U, S]) for i in range(2)]
    a.sc = [ps(f"sc{i}", [P, U, S]) for i in range(2)]
    a.po = [ps(f"po{i}", [P, 2, S]) for i in range(2)]
    a.bank = [ps(f"bank{i}", [P, 2, 256]) for i in range(2)]
    a.filled, a.taken = [sem(f"filled{i}") for i in range(2)], [sem(f"taken{i}") for i in range(2)]
    a.stacked = sem("stacked")
    a.part1, a.rest1, a.part2 = sem("part1"), sem("rest1"), sem("part2")
    a.max_scored, a.max_reduced, a.maxima_split = sem("max_scored"), sem("max_reduced"), sem("maxima_split")
    a.scored, a.exp_done = sem("scored"), sem("exp_done")
    a.pv_done, a.o_copied = sem("pv_done"), sem("o_copied")
    a.xs_ready, a.cs_ready, a.dve_chain = sem("xs_ready"), sem("cs_ready"), sem("dve_chain")
    a.w_loaded, a.w_turned, a.w_copied = sem("w_loaded"), sem("w_turned"), sem("w_copied")
    return a


def make_pick(dve, link, c, a):
    link(dve.tensor_reduce(a.pick4[:], c.ident[0:12, 0:12].rearrange("p (k j) -> p j k", j=4), AX, ALU.add))
    link(dve.tensor_copy(a.pick[:], a.pick4[:].unsqueeze(2).to_broadcast([12, 4, P])))


def layer0_attention(nc, I, c):
    with ExitStack() as ctx:
        a = attention_tiles(nc, c, ctx, "l0a_")
        a.value_slot = lambda h: 4 * (2 * (h // 8) + h % 2) + (h % 8) // 2
        a.stack_out = lambda dst, m: dst[:].rearrange("p k h (t c) -> p k (h t) c", c=HD)[:, :, :, 2 * m:2 * m + 2]
        a.stack_in = lambda bank: bank.rearrange("p (k c t) -> p k t c", k=2, c=2)
        w_in = a.sb("w_in", [P, 3, KT, D])
        wT = a.sb("wT", [P, KT, 3, D])
        bias = a.sb("bias", [P, 3, D])
        gmean = a.sb("gmean", [P, 3, KT, 2 * NH])
        lnsc = a.sb("lnsc", [P, 2, HD])
        lnbi = a.sb("lnbi", [P, 2, HD])
        qkv = a.sb("qkv", [P, U, 3, NH, HP])
        sq = a.sb("sq", [P, U, 2 * NH, HD])
        ss = a.sb("ss", [P, U, 2 * NH])
        rs = a.sb("rs", [P, U, 2 * NH])
        rt = a.sb("rt", [P, U, 2 * NH])
        vT = a.sb("vT", [P, NG, S])
        a.norm_done = a.sem("norm_done")
        a.await_outputs_used = lambda eng, b: eng.wait_ge(a.norm_done, 2 * b)
        squared, scaled, v_turned = a.sem("squared"), a.sem("scaled"), a.sem("v_turned")
        ready0, pool_chain, seeded, ones15 = a.sem("ready0"), a.sem("pool_chain"), a.sem("seeded"), a.sem("ones15")
        halves3 = a.sb("halves3", [P, 1, 1])
        NEWTONS = 3
        a.tm = lambda u: qkv[:, u, 0:2, :, 0:HD].rearrange("p k h e -> p (k h) e")
        a.tm_ready = lambda eng, n, u: eng.wait_ge(scaled, U * n + u + 1)
        block = ctx.enter_context(nc.Block())

        def token_steps(n):
            return [("x", n), ("q", n), ("kv0", n), ("kv1", n)]
        FIRST = token_steps(0) + token_steps(1) + [("s", m) for m in range(STACKS)] + [("v", 0), ("v", 1), ("m", 0), ("idle", 0)]
        AT = {1: [("s", 0)], 2: [("x", 2), ("s", 1), ("m", 1)], 3: [("q", 2), ("s", 2)], 4: [("kv0", 2), ("s", 3)],
              5: [("kv1", 2), ("s", 4)], 6: [("s", 5), ("m", 2)], 7: [("s", 6)], 8: [("s", 7)],
              10: [("m", 3), ("o", 0)], 11: [("v", 0)], 12: [("v", 1)], 14: [("m", 0)]}
        LOOP = [k for n in range(NH) for k in AT.get(n, [])] + [("o", 1)]
        fills = Fillings(a, FIRST, LOOP)
        a.await_values = lambda eng, b: [fills.await_taken(eng, ("v", k), b - 1) for k in range(U)]

        @block.sync
        def _(sp):
            for k, n in enumerate("qkv"):
                sp.dma_start(w_in[:, k], I["L0_xattn_W" + n].rearrange("(t p) d -> p t d", p=P)).then_inc(a.w_loaded, 16)
                sp.dma_start(bias[:, k], row(I["L0_xattn_b" + n])).then_inc(a.w_loaded, 16)
            for k, n in enumerate("qk"):
                sp.dma_start(lnsc[:, k], row(I[f"L0_xattn_{n}_scale"])).then_inc(a.w_loaded, 16)
                sp.dma_start(lnbi[:, k], row(I[f"L0_xattn_{n}_bias"])).then_inc(a.w_loaded, 16)
            if c.load_ahead:
                c.load_ahead(sp)

        @block.tensor
        def _(pe):
            pe.wait_ge(a.w_loaded, 160)
            for k in range(3):
                if k >= 2:
                    pe.wait_ge(a.w_copied, k - 1)
                for ot in range(KT):
                    for kt in range(KT):
                        last = pe.transpose(a.sc[k % 2][:, kt, P * ot:P * ot + P], w_in[:, k, ot, P * kt:P * kt + P], c.ident[:])
                last.then_inc(a.w_turned, 1)
            pe.wait_ge(ready0, 1)

            def fill(key, n, b):
                kind = key[0]
                if kind == "s":
                    turn_stacks_pe(pe, c, a, fills, key, b, n)
                    return
                bank = fills.claim(pe, key, b)
                if kind == "x":
                    pe.wait_ge(a.xs_ready, n + 1)
                    for u in range(U):
                        for kt in range(KT):
                            last = pe.transpose(bank[:, kt, P * u:P * u + P], a.xs[:, u, P * kt:P * kt + P], c.ident[:])
                if kind == "q":
                    fills.await_taken(pe, ("x", key[1]), b)
                    for u in range(U):
                        for kt in range(KT):
                            last = pe.matmul(bank[:, u, :], a.xsT[:, kt, P * u:P * u + P], wT[:, kt, 0, :],
                                             start=(kt == 0), stop=(kt == KT - 1))
                if kind in ("kv0", "kv1"):
                    u = int(kind[2])
                    pe.wait_ge(a.cs_ready, n + 1)
                    for kt in range(KT):
                        last = pe.matmul(bank[:], a.csT[:, kt, P * u:P * u + P], wT[:, kt, 1:3, :],
                                         start=(kt == 0), stop=(kt == KT - 1))
                if kind == "v":
                    pe.wait_ge(v_turned, U * n + U)
                    for g in range(NG):
                        last = pe.transpose(bank[:, g // 2, P * (g % 2):P * (g % 2) + P],
                                            vT[:, g, P * key[1]:P * key[1] + P], c.ident[:])
                last.then_inc(fills.filled(key, b), 1)

            for key in FIRST[:-2]:
                fill(key, key[1] if key in token_steps(1) else 0, None)
            for n in range(AHEAD):
                max_scores_pe(pe, c, a, fills, 0, n, 0, False, None)
            turn_maxima_pe(pe, c, a, fills, ("m", 0), None, 0)
            idle_fill_pe(pe, c, a, fills)
            with pe.Fori(0, B // 2) as i:
                for s in range(2):
                    b = 2 * i + s

                    def mid(n):
                        for key in AT.get(n, []):
                            if key[0] == "m":
                                turn_maxima_pe(pe, c, a, fills, key, b, 4 * b + n // 4 + 1)
                            elif key[0] == "o":
                                turn_outputs_pe(pe, c, a, fills, 0, b)
                            else:
                                fill(key, b + 1 if key[0] in "sv" else b + 2, b)
                    core_pe(pe, c, a, fills, b, s, False, mid)
                    turn_outputs_pe(pe, c, a, fills, 1, b)

        @block.scalar
        def _(act):
            def take_x(key, n, b):
                bank = fills.await_filled(act, key, b)
                act.activation(a.xsT[:], bank[:], ACT.Copy).then_inc(fills.taken(key, b), 1)

            def squares(k, b):
                fills.await_taken(act, ("q", k), b)
                for u in range(U):
                    fills.await_taken(act, (f"kv{u}", k), b)
                    act.activation(sq[:, u].rearrange("p (a c) e -> p a c e", a=2), qkv[:, u, 0:2, :, 0:HD],
                                   ACT.Square).then_inc(squared, 1)

            def take_v(key, b, s):
                bank = fills.await_filled(act, key, b)
                act.activation(a.va[s][:, key[1]].rearrange("p (a h) e -> p a (h e)", a=2), bank[:],
                               ACT.Copy).then_inc(fills.taken(key, b), 1)

            copy = lambda out, in_: act.activation(out, in_, ACT.Copy)
            for k in range(3):
                act.wait_ge(a.w_turned, k + 1)
                act.activation(wT[:, :, k, :], a.sc[k % 2][:], ACT.Copy).then_inc(a.w_copied, 1)
            take_x(("x", 0), 0, None)
            squares(0, None)
            take_x(("x", 1), 1, None)
            first_parts_act(act, a, 0)
            second_parts_act(act, a, 0)
            squares(1, None)
            for m in range(0, STACKS, 2):
                take_stacks(act, a, fills, ("s", m), None, a.qk[0], copy)
            fills.await_filled(act, ("s", STACKS - 1), None)
            first_parts_act(act, a, 1)
            second_parts_act(act, a, 1)
            take_v(("v", 0), None, 0)
            take_v(("v", 1), None, 0)
            take_maxima_act(act, a, fills, ("m", 0), None, 0, 0)
            idle_take_act(act, a, fills)
            with act.Fori(0, B // 2) as i:
                for s in range(2):
                    b = 2 * i + s
                    for n in range(NH):
                        act.wait_ge(a.scored, NH * b + n + 1)
                        act.activation(a.pT[n % 2][:], a.sc[n % 2][:], ACT.Exp, scale=HD ** -0.5).then_inc(a.exp_done, 1)
                        for key in AT.get(n, []):
                            if key[0] == "m":
                                take_maxima_act(act, a, fills, key, b, 4 * b + n // 4 + 1, (n // 4 + 1) % 2)
                            if key[0] == "x":
                                take_x(key, b + 2, b)
                            if key[0] == "v":
                                take_v(key, b, 1 - s)
                            if key[0] == "s" and key[1] % 2 == 0:
                                take_stacks(act, a, fills, key, b, a.qk[1 - s], copy)
                        if n == 5:
                            squares(2, b)
                        if n == 14:
                            fills.await_filled(act, ("s", STACKS - 1), b)
                            first_parts_act(act, a, b + 2)
                        if n == 9:
                            copy_outputs_act(act, a, b, 0)
                        if n == 15:
                            second_parts_act(act, a, b + 2)
                    copy_outputs_act(act, a, b, 1)

        @block.gpsimd
        def _(pool):
            def prep(n):
                link = Chain(pool, pool_chain, (4 * NEWTONS + 2 * U) * n)
                pool.wait_ge(seeded, n + 1)
                for _ in range(NEWTONS):
                    link(pool.tensor_tensor(rt[:], rs[:], rs[:], ALU.mult))
                    link(pool.tensor_tensor(rt[:], rt[:], ss[:], ALU.mult))
                    link(pool.tensor_tensor(rt[:], halves3[:].to_broadcast([P, U, 2 * NH]), rt[:], ALU.subtract))
                    link(pool.tensor_tensor(rs[:], rs[:], rt[:], ALU.mult))
                for u in range(U):
                    v = qkv[:, u, 0:2, :, 0:HD]
                    link(pool.tensor_tensor(v, v, rs[:, u, :].rearrange("p (a c) -> p a c", a=2).unsqueeze(3)
                                            .to_broadcast([P, 2, NH, HD]), ALU.mult))
                    link(pool.tensor_tensor(v, v, lnsc[:].unsqueeze(2).to_broadcast([P, 2, NH, HD]), ALU.mult))
                    pool.tensor_tensor(v, v, lnbi[:].unsqueeze(2).to_broadcast([P, 2, NH, HD]),
                                       ALU.add).then_inc(scaled, 1)
            pool.wait_ge(a.w_loaded, 160)
            def context(n):
                pool.tensor_copy(a.csT[:], c.ctxT[:, :, ds(n * S, S)]).then_inc(a.cs_ready, 1)
            pool.memset(halves3[:], 1.5).then_inc(ones15, 1)
            pool.wait_ge(ones15, 1)
            context(0)
            fills.await_filled(pool, ("kv1", 0), None)
            context(1)
            prep(0)
            prep(1)
            with pool.Fori(0, B) as b:
                fills.await_before(pool, ("x", 2), b)
                context(b + 2)
                prep(b + 2)

        @block.vector
        def _(dve):
            link = Chain(dve, a.dve_chain)
            link(dve.memset(qkv[:], 0.0))
            link(dve.memset(qkv[:, :, 2, :, HD:HD + 1], 1.0))
            make_pick(dve, link, c, a)
            dve.wait_ge(a.w_loaded, 160)
            moments(link, dve, c.st[:], a.mean[:], a.rstd[:], a.mt[:])
            rsqrt(link, dve, a.mt[:], a.rstd[:], a.xs[:, 0, 0:NTD])
            dve.wait_ge(a.w_copied, 3)
            for v, m in ((wT[:, :, 0:2, :].rearrange("p t k (c e) -> p t (k c) e", e=HD), gmean[:, 0]),
                         (bias[:, 0:2, :].rearrange("p k (c e) -> p k c e", e=HD), gmean[:, 1].rearrange("p t (k c) -> p (t k) c", k=2)[:, 0:2])):
                link(dve.tensor_reduce(m, v, AX, ALU.add))
                link(dve.tensor_scalar(m, m, 1.0 / HD, None, ALU.mult))
                link(dve.tensor_tensor(v, v, m.unsqueeze(3).to_broadcast(list(m.shape) + [HD]), ALU.subtract))
            dve.sem_inc(ready0, 1)

            def rows_of(n):
                for u in range(U):
                    t = U * n + u
                    last = dve.tensor_scalar(a.xs[:, u, :], c.x[:, t, :], a.mean[:, ds(t, 1)], a.rstd[:, ds(t, 1)],
                                             ALU.subtract, ALU.mult)
                last.then_inc(a.xs_ready, 1)

            def take_q(key, n, b):
                bank = fills.await_filled(dve, key, b)
                if b is not None or n > 0:
                    dve.wait_ge(a.rest1, U * n)
                bi = bias[:, 0, :].rearrange("p (c e) -> p c e", e=HD)
                for u in range(U):
                    last = dve.tensor_tensor(qkv[:, u, 0, :, 0:HD], bank[:, u, :].rearrange("p (c e) -> p c e", e=HD), bi, ALU.add)
                last.then_inc(fills.taken(key, b), 1)

            def take_kv(key, n, b):
                u = int(key[0][2])
                bank = fills.await_filled(dve, key, b)
                if b is not None or n > 0:
                    dve.wait_ge(v_turned, U * n)
                dve.tensor_tensor(qkv[:, u, 1:3, :, 0:HD], bank[:].rearrange("p a (c e) -> p a c e", e=HD),
                                  bias[:, 1:3, :].rearrange("p a (c e) -> p a c e", e=HD), ALU.add).then_inc(fills.taken(key, b), 1)

            def seeds(link, n):
                for u in range(U):
                    dve.wait_ge(squared, U * n + u + 1)
                    last = dve.tensor_reduce(ss[:, u, :], sq[:, u], AX, ALU.add)
                link(last)
                link(dve.tensor_scalar(ss[:], ss[:], 0.5 / HD, 0.5 * LN_EPS, ALU.mult, ALU.add))
                link(dve.tensor_scalar(rs[:].bitcast(I32), ss[:].bitcast(I32), 1, None, ALU.logical_shift_right))
                dve.tensor_scalar(rs[:].bitcast(I32), rs[:].bitcast(I32), -1.0, float(0x5F3759DF - (1 << 22)),
                                  ALU.mult, ALU.add).then_inc(seeded, 1)

            def turn_values(n):
                for u in range(U):
                    dve.transpose(vT[:, 2 * u:2 * u + 2, :].rearrange("p a (t c) -> p c (a t)", c=HD),
                                  qkv[:, u, 2]).then_inc(v_turned, 1)

            SEED_LINKS = 3
            rows_of(0)
            take_q(("q", 0), 0, None)
            take_kv(("kv0", 0), 0, None)
            take_kv(("kv1", 0), 0, None)
            fills.await_taken(dve, ("kv0", 0), None)
            fills.await_taken(dve, ("kv1", 0), None)
            turn_values(0)
            fills.await_filled(dve, ("x", 0), None)
            rows_of(1)
            seeds(link, 0)
            parts_dve(dve, a, 0, 0)
            take_q(("q", 1), 1, None)
            parts_dve(dve, a, 0, 1)
            take_kv(("kv0", 1), 1, None)
            take_kv(("kv1", 1), 1, None)
            seeds(link, 1)
            for m in range(1, STACKS, 2):
                take_stacks(dve, a, fills, ("s", m), None, a.qk[0], dve.tensor_copy)
            fills.await_filled(dve, ("s", STACKS - 1), None)
            parts_dve(dve, a, 1, 0)
            parts_dve(dve, a, 1, 1)
            for n in range(AHEAD):
                reduce_dve(dve, a, 0, n)
                if n == 3:
                    split_maxima_dve(dve, link, a, 0, 0, None)
            fills.await_filled(dve, ("v", 1), None)
            turn_values(1)
            base = link.n
            with dve.Fori(0, B // 2) as i:
                for s in range(2):
                    b = 2 * i + s
                    link = Chain(dve, a.dve_chain, base + b * (4 * SPLIT_LINKS + SEED_LINKS + 2))

                    def write_back(link, half):
                        key = ("o", half)
                        normalise_dve(dve, link, a, fills, half, b)
                        fills.await_taken(dve, key, b)
                        for u in range(U):
                            v = c.x[:, U * b + u, P * half:P * half + P]
                            last = dve.scalar_tensor_tensor(v, a.on[:, half, u].rearrange("p h e -> p (h e)"), c.tg[:, 0:1], v,
                                                            ALU.mult, ALU.add)
                        last.then_inc(a.norm_done, 1)

                    for n in range(NH):
                        if n + AHEAD < NH:
                            reduce_dve(dve, a, b, n + AHEAD)
                        else:
                            reduce_dve(dve, a, b + 1, n + AHEAD - NH)
                        if n % 4 == 1:
                            g = n // 4 + 1
                            split_maxima_dve(dve, link, a, b + g // 4, g % 4, lambda: fills.await_filled(dve, ("m", g - 1), b if g > 1 else b - 1))
                        if n == 0:
                            fills.await_before(dve, ("x", 2), b)
                            rows_of(b + 2)
                        for key in AT.get(n, []):
                            if key[0] == "q":
                                take_q(key, b + 2, b)
                            if key[0][0:2] == "kv":
                                take_kv(key, b + 2, b)
                            if key[0] == "s" and key[1] % 2:
                                take_stacks(dve, a, fills, key, b, a.qk[1 - s], dve.tensor_copy)
                        if n == 6:
                            seeds(link, b + 2)
                        if n == 11:
                            write_back(link, 0)
                        if n == 14:
                            parts_dve(dve, a, b + 2, 0)
                        if n == 15:
                            parts_dve(dve, a, b + 2, 1)
                        if n == 13:
                            fills.await_filled(dve, ("v", 1), b)
                            turn_values(b + 2)
                    write_back(link, 1)
                    dve.wait_ge(a.norm_done, 2 * b + 2)
                    for u in range(U):
                        dve.bn_stats(c.st[:, U * b + u, :], c.x[:, U * b + u, :])


def layer3_attention(nc, I, c):
    with ExitStack() as ctx:
        a = attention_tiles(nc, c, ctx, "l3a_")
        a.await_outputs_used = lambda eng, b: eng.wait_ge(on_turned, b)
        a.value_slot = lambda h: h
        a.stack_out = lambda dst, m: dst[:, :, 2 * m:2 * m + 2, :].rearrange("p k h s -> p k (h s)")
        a.stack_in = lambda bank: bank.rearrange("p (k n) -> p k n", k=2)
        w_in = a.sb("w_in", [P, 4, KT, D])
        wT = a.sb("wT", [P, KT, 4, D])
        bias = a.sb("bias", [P, 4, D])
        mask = a.sb("mask", [P, NTD, S], U8)
        a.pen = [a.sb(f"pen{i}", [P, U, S], BF16) for i in range(2)]
        a.penT = [a.sb(f"penT{i}", [P, U, S], BF16) for i in range(2)]
        mask_f = a.sb("mask_f", [P, U, S], BF16)
        tm = a.sb("tm", [P, U, 3, NH, HD])
        onT = a.sb("onT", [P, KT, S])
        y = a.sb("y", [P, U, D])
        a.pen_ready, mask_loaded, mask_wide, va_ready = a.sem("pen_ready"), a.sem("mask_loaded"), a.sem("mask_wide"), a.sem("va_ready")
        on_turned, on_copied, ready0, va_ones = a.sem("on_turned"), a.sem("on_copied"), a.sem("ready0"), a.sem("va_ones")
        a.await_values = lambda eng, b: eng.wait_ge(va_ready, b + 1)
        a.tm = lambda u: tm[:, u, 0:2].rearrange("p k h e -> p (k h) e")
        block = ctx.enter_context(nc.Block())

        token_steps = lambda n: [("x", n), ("qkv0", n), ("qkv1", n), ("qkv2", n)]
        FIRST = token_steps(0) + token_steps(1)[:3] + [("s", m) for m in range(STACKS)] + [("m", 0), ("pen", 0), ("qkv2", 1), ("idle", 0)]
        AT = {1: [("s", 0)], 2: [("x", 2), ("s", 1), ("m", 1)], 3: [("qkv0", 2), ("s", 2)], 4: [("qkv1", 2), ("s", 3)],
              5: [("qkv2", 2), ("s", 4)], 6: [("s", 5), ("m", 2)], 7: [("s", 6)], 8: [("s", 7)],
              10: [("m", 3), ("o", 0)], 14: [("m", 0)]}
        LOOP = [k for n in range(NH) for k in AT.get(n, [])] + [("pen", 0), ("o", 1), ("out", 0)]
        fills = Fillings(a, FIRST, LOOP)

        def tm_ready(eng, n, u):
            if isinstance(n, int):
                for k in range(2):
                    fills.await_taken(eng, (f"qkv{k}", n), None)
            else:
                fills.await_taken(eng, ("qkv1", 2), n - 2)
        a.tm_ready = tm_ready

        @block.sync
        def _(sp):
            for k, n in enumerate("qkvo"):
                sp.dma_start(w_in[:, k], I["L3_xattn_W" + n].rearrange("(t p) d -> p t d", p=P)).then_inc(a.w_loaded, 16)
                sp.dma_start(bias[:, k], row(I["L3_xattn_b" + n])).then_inc(a.w_loaded, 16)
            for b in range(B):
                sp.dma_start(mask[:, U * b:U * b + U, :],
                             I["mask_Bx1xSxS2_bf1"][b, 0].rearrange("(u p) k -> p u k", p=P)).then_inc(mask_loaded, 16)
            if c.load_ahead:
                c.load_ahead(sp)

        WLOADS = 16 * 8

        @block.tensor
        def _(pe):
            pe.wait_ge(a.w_loaded, WLOADS)
            for k in range(4):
                if k >= 2:
                    pe.wait_ge(a.w_copied, k - 1)
                for ot in range(KT):
                    for kt in range(KT):
                        last = pe.transpose(a.sc[k % 2][:, kt, P * ot:P * ot + P], w_in[:, k, ot, P * kt:P * kt + P], c.ident[:])
                last.then_inc(a.w_turned, 1)
            pe.wait_ge(ready0, 1)

            def fill(key, n, s, b):
                kind = key[0]
                if kind == "s":
                    turn_stacks_pe(pe, c, a, fills, key, b, n)
                    return
                bank = fills.claim(pe, key, b)
                if kind == "x":
                    pe.wait_ge(a.xs_ready, n + 1)
                    for u in range(U):
                        for kt in range(KT):
                            last = pe.transpose(bank[:, kt, P * u:P * u + P], a.xs[:, u, P * kt:P * kt + P], c.ident[:])
                if kind[0:3] == "qkv":
                    k = int(kind[3])
                    if k == 0:
                        fills.await_taken(pe, ("x", key[1]), b)
                    else:
                        pe.wait_ge(a.cs_ready, n + 1)
                    src = a.csT if k else a.xsT
                    for u in range(U):
                        for kt in range(KT):
                            last = pe.matmul(bank[:, u, :], src[:, kt, P * u:P * u + P], wT[:, kt, k, :],
                                             start=(kt == 0), stop=(kt == KT - 1))
                if kind == "pen":
                    pe.wait_ge(a.pen_ready, n + 1)
                    for u in range(U):
                        for kt in range(U):
                            last = pe.matmul(bank[:, kt, P * u:P * u + P], a.pen[s][:, u, P * kt:P * kt + P],
                                             c.identb[:], start=True, stop=True)
                last.then_inc(fills.filled(key, b), 1)

            for key in FIRST[:-1]:
                if key[0] == "m":
                    for n in range(AHEAD):
                        max_scores_pe(pe, c, a, fills, 0, n, 0, True, None)
                    turn_maxima_pe(pe, c, a, fills, key, None, 0)
                else:
                    fill(key, 0 if key[0] == "s" else key[1], 0, None)
            idle_fill_pe(pe, c, a, fills)
            with pe.Fori(0, B // 2) as i:
                for s in range(2):
                    b = 2 * i + s

                    def mid(n):
                        for key in AT.get(n, []):
                            if key[0] == "m":
                                turn_maxima_pe(pe, c, a, fills, key, b, 4 * b + n // 4 + 1)
                            elif key[0] == "o":
                                turn_outputs_pe(pe, c, a, fills, 0, b)
                            else:
                                fill(key, b + 1 if key[0] == "s" else b + 2, s, b)
                    core_pe(pe, c, a, fills, b, s, True, mid)
                    fill(("pen", 0), b + 1, 1 - s, b)
                    turn_outputs_pe(pe, c, a, fills, 1, b)
                    fills.await_taken(pe, ("o", 1), b)
                    for u in range(U):
                        for kt in range(KT):
                            last = pe.transpose(a.sc[0][:, kt, P * u:P * u + P],
                                                a.on[:, kt, u].rearrange("p h e -> p (h e)"), c.ident[:])
                    last.then_inc(on_turned, 1)
                    bank = fills.claim(pe, ("out", 0), b)
                    pe.wait_ge(on_copied, b + 1)
                    for u in range(U):
                        for kt in range(KT):
                            last = pe.matmul(bank[:, u, :], onT[:, kt, P * u:P * u + P], wT[:, kt, 3, :],
                                             start=(kt == 0), stop=(kt == KT - 1))
                    last.then_inc(fills.filled(("out", 0), b), 1)

        @block.scalar
        def _(act):
            def take_x(key, b):
                bank = fills.await_filled(act, key, b)
                act.activation(a.xsT[:], bank[:], ACT.Copy).then_inc(fills.taken(key, b), 1)

            def take_pen(key, s, b):
                bank = fills.await_filled(act, key, b)
                act.activation(a.penT[s][:], bank[:], ACT.Copy).then_inc(fills.taken(key, b), 1)

            copy = lambda out, in_: act.activation(out, in_, ACT.Copy)
            act.wait_ge(ready0, 1)
            take_x(("x", 0), None)
            first_parts_act(act, a, 0)
            take_x(("x", 1), None)
            second_parts_act(act, a, 0)
            for m in range(0, STACKS, 2):
                take_stacks(act, a, fills, ("s", m), None, a.qk[0], copy)
            fills.await_filled(act, ("s", STACKS - 1), None)
            first_parts_act(act, a, 1)
            second_parts_act(act, a, 1)
            take_maxima_act(act, a, fills, ("m", 0), None, 0, 0)
            take_pen(("pen", 0), 0, None)
            idle_take_act(act, a, fills)
            with act.Fori(0, B // 2) as i:
                for s in range(2):
                    b = 2 * i + s
                    for n in range(NH):
                        act.wait_ge(a.scored, NH * b + n + 1)
                        act.activation(a.pT[n % 2][:], a.sc[n % 2][:], ACT.Exp, scale=HD ** -0.5).then_inc(a.exp_done, 1)
                        for key in AT.get(n, []):
                            if key[0] == "m":
                                take_maxima_act(act, a, fills, key, b, 4 * b + n // 4 + 1, (n // 4 + 1) % 2)
                            if key[0] == "x":
                                take_x(key, b)
                            if key[0] == "s" and key[1] % 2 == 0:
                                take_stacks(act, a, fills, key, b, a.qk[1 - s], copy)
                        if n == 9:
                            copy_outputs_act(act, a, b, 0)
                            fills.await_filled(act, ("s", STACKS - 1), b)
                            first_parts_act(act, a, b + 2)
                        if n == 11:
                            second_parts_act(act, a, b + 2)
                    copy_outputs_act(act, a, b, 1)
                    take_pen(("pen", 0), 1 - s, b)
                    act.wait_ge(on_turned, b + 1)
                    act.activation(onT[:], a.sc[0][:], ACT.Copy).then_inc(on_copied, 1)

        @block.gpsimd
        def _(pool):
            def context(n):
                pool.tensor_copy(a.csT[:], c.ctxT[:, :, ds(n * S, S)]).then_inc(a.cs_ready, 1)

            def values_and_penalties(n, s):
                pool.tensor_copy(mask_f[:], mask[:, ds(n * U, U), :]).then_inc(mask_wide, 1)
                pool.wait_ge(mask_wide, n + 1)
                pool.tensor_tensor(a.va[s][:, :, :, 0:HD], tm[:, :, 2, :, :],
                                   c.ones[:, 0:1].unsqueeze(2).unsqueeze(3).to_broadcast([P, U, NH, HD]), ALU.mult).then_inc(va_ready, 1)
                pool.tensor_scalar(a.pen[s][:], mask_f[:], MASKED, -MASKED, ALU.mult, ALU.add).then_inc(a.pen_ready, 1)

            context(0)
            fills.await_filled(pool, ("qkv2", 0), None)
            context(1)
            pool.wait_ge(mask_loaded, 16 * B)
            pool.wait_ge(va_ones, 1)
            fills.await_taken(pool, ("qkv2", 0), None)
            values_and_penalties(0, 0)
            fills.await_taken(pool, ("qkv2", 1), None)
            with pool.Fori(0, B // 2) as i:
                for s in range(2):
                    b = 2 * i + s
                    fills.await_before(pool, ("qkv0", 2), b)
                    pool.wait_ge(a.pv_done, NH * b)
                    pool.wait_ge(a.pen_ready, b + 1)
                    context(b + 2)
                    values_and_penalties(b + 1, 1 - s)
                    fills.await_taken(pool, ("qkv2", 2), b)

        @block.vector
        def _(dve):
            link = Chain(dve, a.dve_chain)
            link(dve.memset(mask[:, NT:, :], 0))
            for s in range(2):
                link(dve.memset(a.va[s][:], 1.0))
            dve.sem_inc(va_ones, 1)
            make_pick(dve, link, c, a)
            dve.wait_ge(a.w_loaded, WLOADS)
            for k in range(4):
                dve.wait_ge(a.w_turned, k + 1)
                for kt in range(KT):
                    last = dve.tensor_copy(wT[:, kt, k, :], a.sc[k % 2][:, kt, :])
                last.then_inc(a.w_copied, 1)
            dve.wait_ge(a.w_copied, 4)
            moments(link, dve, c.st[:], a.mean[:], a.rstd[:], a.mt[:])
            rsqrt(link, dve, a.mt[:], a.rstd[:], a.xs[:, 0, 0:NTD])
            dve.sem_inc(ready0, 1)

            def rows_of(n):
                for u in range(U):
                    t = U * n + u
                    last = dve.tensor_scalar(a.xs[:, u, :], c.x[:, t, :], a.mean[:, ds(t, 1)], a.rstd[:, ds(t, 1)],
                                             ALU.subtract, ALU.mult)
                last.then_inc(a.xs_ready, 1)

            def take_qkv(key, n, b):
                k = int(key[0][3])
                bank = fills.await_filled(dve, key, b)
                if b is not None or n > 0:
                    dve.wait_ge(*((va_ready, n) if k == 2 else (a.rest1, U * n)))
                dve.tensor_tensor(tm[:, :, k, :, :].rearrange("p u h e -> p u (h e)"), bank[:],
                                  bias[:, k:k + 1, :].to_broadcast([P, U, D]), ALU.add).then_inc(fills.taken(key, b), 1)

            rows_of(0)
            for k in range(3):
                take_qkv((f"qkv{k}", 0), 0, None)
            fills.await_filled(dve, ("x", 0), None)
            rows_of(1)
            parts_dve(dve, a, 0, 0)
            take_qkv(("qkv0", 1), 1, None)
            parts_dve(dve, a, 0, 1)
            take_qkv(("qkv1", 1), 1, None)
            for m in range(1, STACKS, 2):
                take_stacks(dve, a, fills, ("s", m), None, a.qk[0], dve.tensor_copy)
            parts_dve(dve, a, 1, 0)
            parts_dve(dve, a, 1, 1)
            for n in range(AHEAD):
                reduce_dve(dve, a, 0, n)
                if n == 3:
                    split_maxima_dve(dve, link, a, 0, 0, None)
            take_qkv(("qkv2", 1), 1, None)
            base = link.n
            with dve.Fori(0, B // 2) as i:
                for s in range(2):
                    b = 2 * i + s
                    link = Chain(dve, a.dve_chain, base + b * (4 * SPLIT_LINKS + 2 + 1 + U))
                    for n in range(NH):
                        if n + AHEAD < NH:
                            reduce_dve(dve, a, b, n + AHEAD)
                        else:
                            reduce_dve(dve, a, b + 1, n + AHEAD - NH)
                        if n % 4 == 1:
                            g = n // 4 + 1
                            split_maxima_dve(dve, link, a, b + g // 4, g % 4,
                                             lambda: fills.await_filled(dve, ("m", g - 1), b if g > 1 else b - 1))
                        if n == 0:
                            fills.await_before(dve, ("x", 2), b)
                            rows_of(b + 2)
                        for key in AT.get(n, []):
                            if key[0][0:3] == "qkv":
                                take_qkv(key, b + 2, b)
                            if key[0] == "s" and key[1] % 2:
                                take_stacks(dve, a, fills, key, b, a.qk[1 - s], dve.tensor_copy)
                        if n == 9:
                            parts_dve(dve, a, b + 2, 0)
                        if n == 11:
                            normalise_dve(dve, link, a, fills, 0, b)
                            parts_dve(dve, a, b + 2, 1)
                    normalise_dve(dve, link, a, fills, 1, b)
                    bank = fills.await_filled(dve, ("out", 0), b)
                    dve.tensor_tensor(y[:], bank[:], bias[:, 3:4, :].to_broadcast([P, U, D]), ALU.add).then_inc(fills.taken(("out", 0), b), 1)
                    fills.await_taken(dve, ("out", 0), b)
                    v = c.x[:, ds(b * U, U), :].rearrange("p u d -> p (u d)")
                    link(dve.scalar_tensor_tensor(v, y[:].rearrange("p u d -> p (u d)"), c.tg[:, 3:4], v, ALU.mult, ALU.add))
                    for u in range(U):
                        link(dve.bn_stats(c.st[:, U * b + u, :], c.x[:, U * b + u, :]))


QUADS = 4
NQ = NT // QUADS
QT = QUADS * P
FF0 = 1024 // P


def layer0_ffn_weights(nc, I, c, ctx):
    w = Core()
    sb = lambda n, s: ctx.enter_context(nc.sbuf_tensor("l0f_" + n, s, F32))
    w.w_in, w.wo = sb("w_in", [P, KT, FF0 * P]), sb("wo", [P, FF0, D])
    w.b_in, w.b_out = sb("b_in", [P, FF0]), sb("b_out", [P, D])
    w.w_loaded, w.wo_loaded = c.semaphore("l0f_w_loaded"), c.semaphore("l0f_wo_loaded")

    def load(sp):
        sp.dma_start(w.w_in[:], I["L0_ffn_W_in"].rearrange("(t p) f -> p t f", p=P)).then_inc(w.w_loaded, 16)
        sp.dma_start(w.wo[:], I["L0_ffn_W_out"].rearrange("(t p) d -> p t d", p=P)).then_inc(w.wo_loaded, 16)
        sp.dma_start(w.b_in[:], col(I["L0_ffn_b_in"])).then_inc(w.w_loaded, 16)
        sp.dma_start(w.b_out[:], row(I["L0_ffn_b_out"])).then_inc(w.w_loaded, 16)
    w.load = load
    return w


def layer0_ffn(nc, I, c):
    with ExitStack() as ctx:
        sb = lambda n, s, d=F32: ctx.enter_context(nc.sbuf_tensor("l0f_" + n, s, d))
        ps = lambda n, s, d=F32: ctx.enter_context(nc.psum_tensor("l0f_" + n, s, d))
        sem = lambda n: c.semaphore("l0f_" + n)
        w = c.ahead or layer0_ffn_weights(nc, I, c, ctx)
        w_in, wo, b_in, b_out, w_loaded, wo_loaded = w.w_in, w.wo, w.b_in, w.b_out, w.w_loaded, w.wo_loaded
        wq = sb("wq", [P, KT, FF0 * P], BF16)
        wqT = sb("wqT", [P, FF0, D], BF16)
        wot = sb("wot", [P, FF0, D])
        amax_in, mul_in, dq_in = sb("amax_in", [P, FF0]), sb("mul_in", [P, FF0]), sb("dq_in", [P, FF0])
        amax_out, mul_out = sb("amax_out", [P, FF0]), sb("mul_out", [P, FF0])
        mean, rstd, mt, mt2 = sb("mean", [P, NTD]), sb("rstd", [P, NTD]), sb("mt", [P, NTD]), sb("mt2", [P, NTD])
        xn, xmax, xall = sb("xn", [P, NT + QUADS, D]), sb("xmax", [P, NT]), sb("xall", [P, 4])
        xi = sb("xi", [P, QUADS, D])
        xh, xl = ([sb(f"{n}{i}", [P, KT, QT], BF16) for i in range(2)] for n in ("xh", "xl"))
        hid, hmax, hall = sb("hid", [P, FF0, NT * P]), sb("hmax", [P, NQ * FF0]), sb("hall", [P, 4])
        hq, ht = [sb(f"hq{i}", [P, FF0, S]) for i in range(2)], [sb(f"ht{i}", [P, FF0, S]) for i in range(2)]
        magic = sb("magic", [P, 1])
        y = xi[:, 0:U, :]
        xt = ps("xt", [P, KT, QT])
        hb = [ps(f"hb{i}", [P, QT]) for i in range(3)]
        ob = [ps(f"ob{i}", [P, U, D]) for i in range(2)]
        wb = ps("wb", [P, 4, KT, P], BF16)
        w_turned, w_int, w_back, w_ready = (sem(n) for n in ("w_turned", "w_int", "w_back", "w_ready"))
        chain, pchain, wo_amax, wo_ready, x_amax, x_all = (sem(n) for n in ("chain", "pchain", "wo_amax", "wo_ready", "x_amax", "x_all"))
        xi_ready, x_turned, x_split, h_done, gelu_done, hmax_done = (sem(n) for n in ("xi_ready", "x_turned", "x_split", "h_done", "gelu_done", "hmax_done"))
        h_amax, h_all, hq_ready, out_done, out_added = (sem(n) for n in ("h_amax", "h_all", "hq_ready", "out_done", "out_added"))
        lnc, shifted, steps_ready = sem("lnc"), sem("shifted"), sem("steps_ready")
        w_bank = [xt[:].rearrange("p k (f c) -> p (k f) c", c=D), ob[0][:], ob[1][:]]
        w_tiles = [slice(0, 4), slice(4, 6), slice(6, 8)]
        wt = hq[0]
        block = ctx.enter_context(nc.Block())

        @block.sync
        def _(sp):
            if not c.ahead:
                w.load(sp)

        @block.tensor
        def _(pe):
            pe.wait_ge(w_loaded, 48)
            for bank, tiles in zip(w_bank, w_tiles):
                for f in range(tiles.start, tiles.stop):
                    for kt in range(KT):
                        last = pe.transpose(bank[:, f - tiles.start, P * kt:P * kt + P], w_in[:, kt, P * f:P * f + P], c.ident[:])
                last.then_inc(w_turned, 1)
            for half in range(FF0 // 4):
                pe.wait_ge(w_int, half + 1)
                pe.wait_ge(w_ready, half)
                for f in range(4):
                    for kt in range(KT):
                        last = pe.transpose(wb[:, f, kt, :], wqT[:, 4 * half + f, P * kt:P * kt + P], c.identb[:])
                last.then_inc(w_back, 1)
            pe.wait_ge(w_ready, FF0 // 4)

            def turn_integers(n):
                pe.wait_ge(xi_ready, n + 1)
                pe.wait_ge(x_split, n)
                for t in range(QUADS):
                    for kt in range(KT):
                        last = pe.transpose(xt[:, kt, P * t:P * t + P], xi[:, t, P * kt:P * kt + P], c.ident[:])
                last.then_inc(x_turned, 1)

            turn_integers(0)
            with pe.Fori(0, NQ // 2) as j:
                for s in range(2):
                    i = 2 * j + s
                    pe.wait_ge(x_split, i + 1)
                    for f in range(FF0):
                        if f == 3:
                            turn_integers(i + 1)
                        pe.wait_ge(gelu_done, FF0 * i + max(f - 2, 0))
                        for kt in range(KT):
                            for part in (xh[s], xl[s]):
                                last = pe.matmul(hb[f % 3][:], wq[:, kt, P * f:P * f + P], part[:, kt, :],
                                                 start=(kt == 0 and part is xh[s]), stop=(kt == KT - 1 and part is xl[s]))
                        last.then_inc(h_done, 1)
            pe.wait_ge(wo_ready, 1)
            with pe.Fori(0, B // 2) as i:
                for s in range(2):
                    b = 2 * i + s
                    pe.wait_ge(hq_ready, b + 1)
                    pe.wait_ge(out_added, b)
                    for u in range(U):
                        for f in range(FF0):
                            last = pe.matmul(ob[s][:, u, :], hq[s][:, f, P * u:P * u + P], wo[:, f, :],
                                             start=(f == 0), stop=(f == FF0 - 1))
                    last.then_inc(out_done, 1)

        @block.scalar
        def _(act):
            for half in range(FF0 // 4):
                act.wait_ge(w_back, half + 1)
                act.activation(wq[:, :, 4 * P * half:4 * P * half + 4 * P].rearrange("p k (f c) -> p f k c", c=P), wb[:],
                               ACT.Copy).then_inc(w_ready, 1)
            act.wait_ge(x_all, 2)
            act.wait_ge(w_loaded, 48)
            act.activation(xall[:, 3:4], xall[:, 0:1], ACT.Gelu)
            with act.Fori(0, NQ) as i:
                for f in range(FF0):
                    act.wait_ge(h_done, FF0 * i + f + 1)
                    act.activation(hid[:, f, ds(i * QT, QT)], hb[f % 3][:], ACT.Gelu,
                                   bias=b_in[:, f:f + 1], scale=dq_in[:, f:f + 1]).then_inc(gelu_done, 1)
            act.wait_ge(steps_ready, 1)
            with act.Fori(0, B // 2) as i:
                for s in range(2):
                    b = 2 * i + s
                    act.wait_ge(hq_ready, 2 * i)
                    act.activation(ht[s][:], hid[:, :, ds(b * S, S)], ACT.Identity, bias=magic[:, 0:1],
                                   scale=hall[:, 2:3]).then_inc(shifted, 1)

        @block.gpsimd
        def _(pool):
            link = Chain(pool, pchain)
            pool.wait_ge(wo_loaded, 16)
            pool.wait_ge(wo_amax, 1)
            full = [P, FF0, D]
            link(pool.tensor_tensor(wot[:], wo[:], mul_out[:].unsqueeze(2).to_broadcast(full), ALU.mult))
            link(pool.tensor_scalar(wot[:], wot[:], ROUND, ROUND, ALU.add, ALU.subtract))
            link(pool.tensor_scalar(wot[:], wot[:], 127.0, -128.0, ALU.min, ALU.max))
            pool.tensor_tensor(wo[:], wot[:], amax_out[:].unsqueeze(2).to_broadcast(full), ALU.mult).then_inc(wo_ready, 1)
            pool.wait_ge(x_amax, 1)
            pool.partition_all_reduce(xall[:, 1:2], xall[:, 0:1], P, bass.bass_isa.ReduceOp.max).then_inc(x_all, 1)
            pool.wait_ge(h_amax, 1)
            pool.partition_all_reduce(hall[:, 1:2], hall[:, 0:1], P, bass.bass_isa.ReduceOp.max).then_inc(h_all, 1)

        @block.vector
        def _(dve):
            link = Chain(dve, chain)
            dve.wait_ge(wo_loaded, 16)
            link(dve.tensor_reduce(amax_out[:], wo[:], AX, ALU.max, apply_absolute_value=True))
            link(dve.tensor_scalar(amax_out[:], amax_out[:], 1e-8, None, ALU.max))
            link(dve.reciprocal(mul_out[:], amax_out[:]))
            link(dve.tensor_scalar(mul_out[:], mul_out[:], 127.0, None, ALU.mult))
            link(dve.tensor_scalar(amax_out[:], amax_out[:], 1.0 / 127.0, None, ALU.mult))
            dve.sem_inc(wo_amax, 1)
            for n, (bank, tiles) in enumerate(zip(w_bank, w_tiles)):
                dve.wait_ge(w_turned, n + 1)
                last = dve.tensor_reduce(amax_in[:, tiles], bank, AX, ALU.max, apply_absolute_value=True)
            link(last)
            link(dve.tensor_scalar(amax_in[:], amax_in[:], 1e-8, None, ALU.max))
            link(dve.reciprocal(mul_in[:], amax_in[:]))
            link(dve.tensor_scalar(mul_in[:], mul_in[:], 127.0, None, ALU.mult))
            for bank, tiles in zip(w_bank, w_tiles):
                last = dve.tensor_tensor(wt[:, tiles, :], bank,
                                         mul_in[:, tiles].unsqueeze(2).to_broadcast([P, tiles.stop - tiles.start, D]), ALU.mult)
            link(last)
            link(dve.tensor_scalar(wt[:], wt[:], ROUND, ROUND, ALU.add, ALU.subtract))
            for half in range(FF0 // 4):
                v = slice(4 * half, 4 * half + 4)
                dve.tensor_scalar(wqT[:, v, :], wt[:, v, :], 127.0, -128.0, ALU.min, ALU.max).then_inc(w_int, 1)
            dve.wait_ge(w_int, FF0 // 4)
            moments(link, dve, c.st[:], mean[:], rstd[:], mt[:])
            rsqrt(link, dve, mt[:], rstd[:], mt2[:])
            link(dve.memset(xn[:, NT:, :], 0.0))
            with dve.Fori(0, NQ) as i:
                for q in range(QUADS):
                    t = i * QUADS + q
                    last = dve.tensor_scalar(xn[:, t, :], c.x[:, t, :], mean[:, ds(t, 1)], rstd[:, ds(t, 1)],
                                             ALU.subtract, ALU.mult)
                last.then_inc(lnc, 1)
                dve.wait_ge(lnc, 2 * i + 1)
                dve.tensor_reduce(xmax[:, ds(i * QUADS, QUADS)], xn[:, ds(i * QUADS, QUADS), :], AX, ALU.max,
                                  apply_absolute_value=True).then_inc(lnc, 1)
            dve.wait_ge(lnc, 2 * NQ)
            link(dve.tensor_reduce(xall[:, 0:1], xmax[:], AX, ALU.max))
            dve.sem_inc(x_amax, 1)
            dve.wait_ge(x_all, 1)
            link(dve.tensor_scalar(xall[:, 1:2], xall[:, 1:2], 1e-8, None, ALU.max))
            link(dve.reciprocal(xall[:, 2:3], xall[:, 1:2]))
            link(dve.tensor_scalar(xall[:, 2:3], xall[:, 2:3], 32767.0, None, ALU.mult))
            link(dve.tensor_scalar(dq_in[:], amax_in[:], xall[:, 1:2], 1.0 / (127.0 * 32767.0), ALU.mult, ALU.mult))
            dve.sem_inc(x_all, 1)

            def integers(link, n):
                dve.wait_ge(x_turned, n)
                link(dve.tensor_scalar(xi[:], xn[:, ds(n * QUADS, QUADS), :], xall[:, 2:3], ROUND, ALU.mult, ALU.add))
                link(dve.tensor_scalar(xi[:], xi[:], ROUND, 32767.0, ALU.subtract, ALU.min))
                dve.tensor_scalar(xi[:], xi[:], -32768.0, None, ALU.max).then_inc(xi_ready, 1)

            def split(link, n, s):
                dve.wait_ge(x_turned, n + 1)
                link(dve.tensor_scalar(xh[s][:], xt[:], ROUND256, ROUND256, ALU.add, ALU.subtract))
                dve.tensor_tensor(xl[s][:], xt[:], xh[s][:], ALU.subtract).then_inc(x_split, 1)

            integers(link, 0)
            split(link, 0, 0)
            base = link.n
            with dve.Fori(0, NQ // 2) as j:
                for s in range(2):
                    i = 2 * j + s
                    link = Chain(dve, chain, base + i * 3)
                    integers(link, i + 1)
                    for f in range(FF0):
                        if f == 2:
                            dve.wait_ge(h_done, FF0 * i)
                            split(link, i + 1, 1 - s)
                        dve.wait_ge(gelu_done, FF0 * i + f + 1)
                        dve.tensor_reduce(hmax[:, ds(i * FF0 + f, 1)], hid[:, f, ds(i * QT, QT)], AX, ALU.max,
                                          apply_absolute_value=True).then_inc(hmax_done, 1)
            dve.wait_ge(hmax_done, NQ * FF0)
            link = Chain(dve, chain, base + NQ * 3)
            link(dve.tensor_reduce(hall[:, 0:1], hmax[:], AX, ALU.max))
            dve.sem_inc(h_amax, 1)
            dve.wait_ge(h_all, 1)
            link(dve.tensor_scalar(hall[:, 1:2], hall[:, 1:2], 1e-8, None, ALU.max))
            link(dve.reciprocal(hall[:, 2:3], hall[:, 1:2]))
            link(dve.tensor_scalar(hall[:, 2:3], hall[:, 2:3], 32767.0, None, ALU.mult))
            link(dve.tensor_scalar(hall[:, 3:4], hall[:, 1:2], 1.0 / 32767.0, None, ALU.mult))
            link(dve.memset(magic[:], ROUND))
            dve.sem_inc(steps_ready, 1)
            base = base + NQ * 3 + link.n

            def quantise(link, b, s):
                dve.wait_ge(shifted, b + 1)
                link(dve.tensor_scalar(ht[s][:], ht[s][:], ROUND, 32767.0, ALU.subtract, ALU.min))
                dve.tensor_scalar(hq[s][:], ht[s][:], -32768.0, hall[:, 3:4], ALU.max, ALU.mult).then_inc(hq_ready, 1)
                dve.wait_ge(hq_ready, b + 1)

            def add_out(link, b, s):
                dve.wait_ge(out_done, b + 1)
                dve.tensor_tensor(y, ob[s][:], b_out[:].unsqueeze(1).to_broadcast([P, U, D]), ALU.add).then_inc(out_added, 1)
                dve.wait_ge(out_added, b + 2)
                v = c.x[:, ds(b * U, U), :].rearrange("p u d -> p (u d)")
                link(dve.scalar_tensor_tensor(v, y.rearrange("p u d -> p (u d)"), c.tg[:, 4:5], v, ALU.mult, ALU.add))
                for u in range(U):
                    link(dve.bn_stats(c.st[:, U * b + u, :], c.x[:, U * b + u, :]))

            dve.sem_inc(out_added, 1)
            link = Chain(dve, chain, base)
            for s in range(2):
                quantise(link, s, s)
            base += link.n
            with dve.Fori(0, B // 2 - 1) as i:
                link = Chain(dve, chain, base + i * 8)
                for s in range(2):
                    add_out(link, 2 * i + s, s)
                    quantise(link, 2 * i + s + 2, s)
            link = Chain(dve, chain, base + (B // 2 - 1) * 8)
            for s in range(2):
                add_out(link, B - 2 + s, s)


FF3, FF3W = 6, 704
FF3R = FF3W - (FF3 - 1) * P


def layer3_ffn_weights(nc, I, c, ctx):
    w = Core()
    sb = lambda n, s: ctx.enter_context(nc.sbuf_tensor("l3f_" + n, s, F32))
    w.w_up = sb("w_up", [P, 2, FF3, D])
    w.w_dn = sb("w_dn", [P, KT, FF3W])
    w.clip = sb("clip", [P, 2])
    w.w_loaded = c.semaphore("l3f_w_loaded")

    def load(sp):
        full = (FF3 - 1) * P
        for k, n in enumerate(("gate", "up")):
            v = I["L3_ffn_w_" + n]
            sp.dma_start(w.w_up[:, k, 0:FF3 - 1, :], v[0:full, :].rearrange("(t p) d -> p t d", p=P)).then_inc(w.w_loaded, 16)
            sp.dma_start(w.w_up[0:FF3R, k, FF3 - 1, :], v[full:, :]).then_inc(w.w_loaded, 16)
        for kt in range(KT):
            sp.dma_start(w.w_dn[:, kt, :], I["L3_ffn_w_down"][P * kt:P * kt + P, :]).then_inc(w.w_loaded, 16)
        sp.dma_start(w.clip[:, 0:1], row(I["L3_ffn_clip_x"])).then_inc(w.w_loaded, 16)
        sp.dma_start(w.clip[:, 1:2], row(I["L3_ffn_clip_down"])).then_inc(w.w_loaded, 16)
    w.load = load
    return w


def layer3_ffn(nc, I, c):
    with ExitStack() as ctx:
        sb = lambda n, s, d=F32: ctx.enter_context(nc.sbuf_tensor("l3f_" + n, s, d))
        ps = lambda n, s, d=F32: ctx.enter_context(nc.psum_tensor("l3f_" + n, s, d))
        sem = lambda n: c.semaphore("l3f_" + n)
        w = c.ahead or layer3_ffn_weights(nc, I, c, ctx)
        w_up, w_dn, clip, w_loaded = w.w_up, w.w_dn, w.clip, w.w_loaded
        q_up, q_dn = sb("q_up", [P, 2, FF3, D], BF16), sb("q_dn", [P, KT, FF3W], BF16)
        upT, dnT = sb("upT", [P, KT, 2, FF3W], BF16), sb("dnT", [P, FF3, D], BF16)
        am_up, mul_up, dq_up = (sb(n, [P, 2, FF3]) for n in ("am_up", "mul_up", "dq_up"))
        am_dn, mul_dn = sb("am_dn", [P, KT]), sb("mul_dn", [P, KT])
        diag, dn_row = sb("diag", [P, KT, P]), sb("dn_row", [P, D])
        mean, rstd, mt, mt2 = sb("mean", [P, NTD]), sb("rstd", [P, NTD]), sb("mt", [P, NTD]), sb("mt2", [P, NTD])
        xn, xmax, xall = sb("xn", [P, NT + QUADS, D]), sb("xmax", [P, NT]), sb("xall", [P, 4])
        xt1, xq = sb("xt1", [P, QUADS, D]), sb("xq", [P, QUADS, D], BF16)
        xT = [sb(f"xT{i}", [P, KT, QT], BF16) for i in range(2)]
        sg = [sb(f"sg{i}", [P, QT]) for i in range(2)]
        hid, hmax, hall = sb("hid", [P, FF3, NT * P]), sb("hmax", [P, NQ * FF3]), sb("hall", [P, 4])
        ht, hq = [sb(f"ht{i}", [P, FF3, S]) for i in range(2)], [sb(f"hq{i}", [P, FF3, S], BF16) for i in range(2)]
        magic = sb("magic", [P, 1])
        y = sb("y", [P, U, D])
        xb = ps("xb", [P, KT, QT], BF16)
        gb = [ps(f"gb{i}", [P, QT]) for i in range(2)]
        ub = [ps(f"ub{i}", [P, QT]) for i in range(2)]
        ob = [ps(f"ob{i}", [P, U, D]) for i in range(2)]
        wb = ps("wb", [P, 8 * P], BF16)
        names = ("chain", "zeroed", "w_int", "w_back", "w_ready", "clip_ready", "x_amax", "x_all", "xq_ready",
                 "x_turned", "x_copied", "gate_done", "up_done", "silu_done", "h_ready", "hmax_done", "h_amax", "h_all",
                 "hq_ready", "out_done", "out_taken", "lnc", "row_done", "diag_ready", "scales_ready", "shifted", "steps_ready", "added", "stored")
        (chain, zeroed, w_int, w_back, w_ready, clip_ready, x_amax, x_all, xq_ready, x_turned, x_copied,
         gate_done, up_done, silu_done, h_ready, hmax_done, h_amax, h_all, hq_ready, out_done, out_taken, lnc,
         row_done, diag_ready, scales_ready, shifted, steps_ready, added, stored) = (sem(n) for n in names)
        block = ctx.enter_context(nc.Block())
        rows = lambda t: P if t < FF3 - 1 else FF3R
        WLOADS = 16 * 8

        @block.sync
        def _(sp):
            if not c.ahead:
                w.load(sp)
            for b in range(B):
                sp.wait_ge(added, b + 1)
                sp.dma_start(c.out[b].rearrange("(u p) d -> p u d", p=P), c.x[:, U * b:U * b + U, :]).then_inc(stored, 16)
            sp.wait_ge(stored, 16 * B)

        UP_JOBS = [(k, kt) for k in range(2) for kt in range(KT)]
        DN_JOBS = [(0, 1, 2), (3, 4), (5,)]
        N_JOBS = len(UP_JOBS) + len(DN_JOBS)
        turn_bank = [wb, xb[:].rearrange("p k n -> p (k n)")]

        @block.tensor
        def _(pe):
            pe.wait_ge(w_int, 3)
            for n in range(N_JOBS):
                bank = turn_bank[n % 2]
                if n >= 2:
                    pe.wait_ge(w_ready, n - 1)
                if n < len(UP_JOBS):
                    k, kt = UP_JOBS[n]
                    for t in range(FF3):
                        r = rows(t)
                        last = pe.transpose(bank[:, P * t:P * t + r], q_up[0:r, k, t, P * kt:P * kt + P], c.identb[0:r, 0:r])
                else:
                    for m, t in enumerate(DN_JOBS[n - len(UP_JOBS)]):
                        r = rows(t)
                        for kt in range(KT):
                            last = pe.transpose(bank[0:r, D * m + P * kt:D * m + P * kt + P], q_dn[:, kt, P * t:P * t + r],
                                                c.identb[:])
                last.then_inc(w_back, 1)
            pe.wait_ge(diag_ready, 1)
            for kt in range(KT):
                last = pe.matmul(ob[0][:, 0, P * kt:P * kt + P], c.ones[:], diag[:, kt, :], start=True, stop=True)
            last.then_inc(row_done, 1)
            pe.wait_ge(w_ready, N_JOBS)

            def turn_integers(n):
                pe.wait_ge(xq_ready, n + 1)
                pe.wait_ge(x_copied, n)
                for t in range(QUADS):
                    for kt in range(KT):
                        last = pe.transpose(xb[:, kt, P * t:P * t + P], xq[:, t, P * kt:P * kt + P], c.identb[:])
                last.then_inc(x_turned, 1)

            turn_integers(0)
            with pe.Fori(0, NQ // 2) as j:
                for s in range(2):
                    i = 2 * j + s
                    pe.wait_ge(x_copied, i + 1)
                    for t in range(FF3):
                        if t == 2:
                            turn_integers(i + 1)
                        r = rows(t)
                        pe.wait_ge(h_ready, FF3 * i + max(t - 1, 0))
                        for k, bank, done in ((0, gb, gate_done), (1, ub, up_done)):
                            for kt in range(KT):
                                last = pe.matmul(bank[t % 2][0:r, :], upT[:, kt, k, P * t:P * t + r], xT[s][:, kt, :],
                                                 start=(kt == 0), stop=(kt == KT - 1))
                            last.then_inc(done, 1)
            with pe.Fori(0, B // 2) as i:
                for s in range(2):
                    b = 2 * i + s
                    pe.wait_ge(hq_ready, b + 1)
                    pe.wait_ge(out_taken, b)
                    for u in range(U):
                        for t in range(FF3):
                            r = rows(t)
                            last = pe.matmul(ob[s][:, u, :], hq[s][0:r, t, P * u:P * u + P], dnT[0:r, t, :],
                                             start=(t == 0), stop=(t == FF3 - 1))
                    last.then_inc(out_done, 1)

        @block.scalar
        def _(act):
            act.wait_ge(w_loaded, WLOADS)
            act.activation(clip[:], clip[:], ACT.Sigmoid).then_inc(clip_ready, 1)
            for n in range(N_JOBS):
                act.wait_ge(w_back, n + 1)
                bank = turn_bank[n % 2]
                if n < len(UP_JOBS):
                    k, kt = UP_JOBS[n]
                    act.activation(upT[:, kt, k, :], bank[:, 0:FF3W], ACT.Copy).then_inc(w_ready, 1)
                else:
                    ts = DN_JOBS[n - len(UP_JOBS)]
                    r = rows(ts[-1])
                    act.activation(dnT[0:r, ts[0]:ts[-1] + 1, :], bank[0:r, 0:D * len(ts)], ACT.Copy).then_inc(w_ready, 1)
            act.wait_ge(scales_ready, 1)
            act.activation(xall[:, 3:4], xall[:, 0:1], ACT.Silu)

            def copy_integers(n, s):
                act.wait_ge(x_turned, n + 1)
                act.activation(xT[s][:], xb[:], ACT.Copy).then_inc(x_copied, 1)

            copy_integers(0, 0)
            with act.Fori(0, NQ // 2) as j:
                for s in range(2):
                    i = 2 * j + s
                    for t in range(FF3):
                        if t == 3:
                            act.wait_ge(up_done, FF3 * i)
                            copy_integers(i + 1, 1 - s)
                        r = rows(t)
                        act.wait_ge(gate_done, FF3 * i + t + 1)
                        act.wait_ge(h_ready, FF3 * i + max(t - 1, 0))
                        act.activation(sg[t % 2][0:r, :], gb[t % 2][0:r, :], ACT.Silu,
                                       scale=dq_up[0:r, 0, t:t + 1]).then_inc(silu_done, 1)
            act.wait_ge(steps_ready, 1)
            with act.Fori(0, B // 2) as i:
                for s in range(2):
                    b = 2 * i + s
                    act.wait_ge(hq_ready, 2 * i)
                    act.activation(ht[s][:], hid[:, :, ds(b * S, S)], ACT.Identity, bias=magic[:, 0:1],
                                   scale=hall[:, 2:3]).then_inc(shifted, 1)

        @block.gpsimd
        def _(pool):
            pool.memset(hid[:, FF3 - 1, :], 0.0).then_inc(zeroed, 1)
            pool.memset(hmax[:], 0.0).then_inc(zeroed, 1)
            pool.wait_ge(x_amax, 1)
            pool.partition_all_reduce(xall[:, 1:2], xall[:, 0:1], P, bass.bass_isa.ReduceOp.max).then_inc(x_all, 1)
            pool.wait_ge(h_amax, 1)
            pool.partition_all_reduce(hall[:, 1:2], hall[:, 0:1], P, bass.bass_isa.ReduceOp.max).then_inc(h_all, 1)

        @block.vector
        def _(dve):
            link = Chain(dve, chain)
            link(dve.memset(w_up[FF3R:, :, FF3 - 1, :], 1.0))
            dve.wait_ge(w_loaded, WLOADS)
            link(dve.tensor_reduce(am_up[:], w_up[:], AX, ALU.max, apply_absolute_value=True))
            link(dve.tensor_reduce(am_dn[:], w_dn[:], AX, ALU.max, apply_absolute_value=True))
            for am, mul in ((am_up, mul_up), (am_dn, mul_dn)):
                link(dve.tensor_scalar(am[:], am[:], 1.0 / 127.0, None, ALU.mult))
                link(dve.reciprocal(mul[:], am[:]))
            for v, q, mul in ((w_up[:, 0], q_up[:, 0], mul_up[:, 0]), (w_up[:, 1], q_up[:, 1], mul_up[:, 1]),
                              (w_dn[:], q_dn[:], mul_dn[:])):
                full = list(v.shape)
                link(dve.tensor_tensor(v, v, mul.unsqueeze(2).to_broadcast(full), ALU.mult))
                link(dve.tensor_scalar(v, v, ROUND, ROUND, ALU.add, ALU.subtract))
                link(dve.tensor_scalar(q, v, 127.0, -128.0, ALU.min, ALU.max))
                dve.sem_inc(w_int, 1)
            for kt in range(KT):
                link(dve.tensor_scalar(diag[:, kt, :], c.ident[:], am_dn[:, kt:kt + 1], None, ALU.mult))
            dve.sem_inc(diag_ready, 1)
            moments(link, dve, c.st[:], mean[:], rstd[:], mt[:])
            rsqrt(link, dve, mt[:], rstd[:], mt2[:])
            link(dve.memset(xn[:, NT:, :], 0.0))
            with dve.Fori(0, NQ) as i:
                for q in range(QUADS):
                    t = i * QUADS + q
                    last = dve.tensor_scalar(xn[:, t, :], c.x[:, t, :], mean[:, ds(t, 1)], rstd[:, ds(t, 1)],
                                             ALU.subtract, ALU.mult)
                last.then_inc(lnc, 1)
                dve.wait_ge(lnc, 2 * i + 1)
                dve.tensor_reduce(xmax[:, ds(i * QUADS, QUADS)], xn[:, ds(i * QUADS, QUADS), :], AX, ALU.max,
                                  apply_absolute_value=True).then_inc(lnc, 1)
            dve.wait_ge(lnc, 2 * NQ)
            link(dve.tensor_reduce(xall[:, 0:1], xmax[:], AX, ALU.max))
            dve.sem_inc(x_amax, 1)
            dve.wait_ge(x_all, 1)
            dve.wait_ge(clip_ready, 1)
            link(dve.tensor_scalar(xall[:, 1:2], xall[:, 1:2], clip[:, 0:1], 1.0 / 127.0, ALU.mult, ALU.mult))
            link(dve.reciprocal(xall[:, 2:3], xall[:, 1:2]))
            link(dve.tensor_scalar(dq_up[:], am_up[:], xall[:, 1:2], None, ALU.mult))
            dve.sem_inc(scales_ready, 1)
            dve.wait_ge(row_done, 1)
            link(dve.tensor_copy(dn_row[:], ob[0][:, 0, :]))

            def integers(link, n):
                dve.wait_ge(x_turned, n)
                link(dve.tensor_scalar(xt1[:], xn[:, ds(n * QUADS, QUADS), :], xall[:, 2:3], ROUND, ALU.mult, ALU.add))
                link(dve.tensor_scalar(xt1[:], xt1[:], ROUND, 127.0, ALU.subtract, ALU.min))
                dve.tensor_scalar(xq[:], xt1[:], -128.0, None, ALU.max).then_inc(xq_ready, 1)

            def largest(i, t):
                dve.wait_ge(h_ready, FF3 * i + t + 1)
                dve.tensor_reduce(hmax[0:rows(t), ds(i * FF3 + t, 1)], hid[0:rows(t), t, ds(i * QT, QT)], AX, ALU.max,
                                  apply_absolute_value=True).then_inc(hmax_done, 1)

            dve.wait_ge(zeroed, 2)
            integers(link, 0)
            base = link.n
            with dve.Fori(0, NQ // 2) as j:
                for s in range(2):
                    i = 2 * j + s
                    link = Chain(dve, chain, base + i * 2)
                    for t in range(FF3):
                        r = rows(t)
                        dve.wait_ge(silu_done, FF3 * i + t + 1)
                        dve.wait_ge(up_done, FF3 * i + t + 1)
                        dve.scalar_tensor_tensor(hid[0:r, t, ds(i * QT, QT)], ub[t % 2][0:r, :], dq_up[0:r, 1, t:t + 1],
                                                 sg[t % 2][0:r, :], ALU.mult, ALU.mult).then_inc(h_ready, 1)
                        if t == 0:
                            integers(link, i + 1)
                        else:
                            largest(i, t - 1)
                    largest(i, FF3 - 1)
            dve.wait_ge(hmax_done, NQ * FF3)
            link = Chain(dve, chain, base + NQ * 2)
            link(dve.tensor_reduce(hall[:, 0:1], hmax[:], AX, ALU.max))
            dve.sem_inc(h_amax, 1)
            dve.wait_ge(h_all, 1)
            link(dve.tensor_scalar(hall[:, 1:2], hall[:, 1:2], clip[:, 1:2], 1.0 / 127.0, ALU.mult, ALU.mult))
            link(dve.reciprocal(hall[:, 2:3], hall[:, 1:2]))
            link(dve.memset(magic[:], ROUND))
            dve.sem_inc(steps_ready, 1)
            link(dve.tensor_scalar(dn_row[:], dn_row[:], hall[:, 1:2], c.tg[:, 7:8], ALU.mult, ALU.mult))
            base = base + NQ * 2 + link.n

            def quantise(link, b, s):
                dve.wait_ge(shifted, b + 1)
                link(dve.tensor_scalar(ht[s][:], ht[s][:], ROUND, 127.0, ALU.subtract, ALU.min))
                dve.tensor_scalar(hq[s][:], ht[s][:], -128.0, None, ALU.max).then_inc(hq_ready, 1)
                dve.wait_ge(hq_ready, b + 1)

            def add_out(b, s):
                dve.wait_ge(out_done, b + 1)
                dve.tensor_tensor(y[:], ob[s][:], dn_row[:].unsqueeze(1).to_broadcast([P, U, D]), ALU.mult).then_inc(out_taken, 1)
                dve.wait_ge(out_taken, b + 2)
                v = c.x[:, ds(b * U, U), :]
                dve.tensor_tensor(v, y[:], v, ALU.add).then_inc(added, 1)
                dve.wait_ge(added, b + 1)

            dve.sem_inc(out_taken, 1)
            link = Chain(dve, chain, base)
            for s in range(2):
                quantise(link, s, s)
            base += link.n
            with dve.Fori(0, B // 2 - 1) as i:
                link = Chain(dve, chain, base + i * 2)
                for s in range(2):
                    add_out(2 * i + s, s)
                    quantise(link, 2 * i + s + 2, s)
            for s in range(2):
                add_out(B - 2 + s, s)


FF1 = 1024 // P


def layer1_attention(nc, I, c):
    with ExitStack() as ctx:
        sb = lambda n, s, d=F32: ctx.enter_context(nc.sbuf_tensor("l1a_" + n, s, d))
        ps = lambda n, s, d=F32: ctx.enter_context(nc.psum_tensor("l1a_" + n, s, d))
        sem = lambda n: c.semaphore("l1a_" + n)
        INNER = FF1 * P
        wv, wvT, wout = sb("wv", [P, KT, INNER]), sb("wvT", [P, FF1, D]), sb("wout", [P, FF1, D])
        wf, bout = sb("wf", [P, KT, D]), sb("bout", [P, D])
        csT = [sb(f"csT{i}", [P, KT, S]) for i in range(2)]
        y = sb("y", [P, U, D])
        tb = [ps(f"tb{i}", [P, 2, D]) for i in range(2)]
        fb = ps("fb", [P, KT, D])
        ob = [ps(f"ob{i}", [P, U, D]) for i in range(2)]
        w_loaded, turned, copied, fused, wf_ready, cs_ready, out_done, out_taken, chain = (
            sem(n) for n in ("w_loaded", "turned", "copied", "fused", "wf_ready", "cs_ready", "out_done", "out_taken", "chain"))
        block = ctx.enter_context(nc.Block())

        @block.sync
        def _(sp):
            sp.dma_start(wv[:], I["L1_xattn_Wkv"][:, INNER:].rearrange("(t p) f -> p t f", p=P)).then_inc(w_loaded, 16)
            sp.dma_start(wout[:], I["L1_xattn_Wout"].rearrange("(t p) d -> p t d", p=P)).then_inc(w_loaded, 16)
            sp.dma_start(bout[:], row(I["L1_xattn_bout"])).then_inc(w_loaded, 16)
            if c.load_ahead:
                c.load_ahead(sp)

        @block.tensor
        def _(pe):
            pe.wait_ge(w_loaded, 48)
            for n in range(FF1 // 2):
                if n >= 2:
                    pe.wait_ge(copied, n - 1)
                for m in range(2):
                    for kt in range(KT):
                        last = pe.transpose(tb[n % 2][:, m, P * kt:P * kt + P],
                                            wv[:, kt, P * (2 * n + m):P * (2 * n + m) + P], c.ident[:])
                last.then_inc(turned, 1)
            pe.wait_ge(copied, FF1 // 2)
            for kt in range(KT):
                for f in range(FF1):
                    last = pe.matmul(fb[:, kt, :], wvT[:, f, P * kt:P * kt + P], wout[:, f, :], start=(f == 0), stop=(f == FF1 - 1))
            last.then_inc(fused, 1)
            pe.wait_ge(wf_ready, 1)
            with pe.Fori(0, B // 2) as i:
                for s in range(2):
                    pe.wait_ge(cs_ready, 2 * i + s + 1)
                    pe.wait_ge(out_taken, 2 * i)
                    for u in range(U):
                        for kt in range(KT):
                            last = pe.matmul(ob[s][:, u, :], csT[s][:, kt, P * u:P * u + P], wf[:, kt, :],
                                             start=(kt == 0), stop=(kt == KT - 1))
                    last.then_inc(out_done, 1)

        @block.scalar
        def _(act):
            for n in range(FF1 // 2):
                act.wait_ge(turned, n + 1)
                act.activation(wvT[:, 2 * n:2 * n + 2, :], tb[n % 2][:], ACT.Copy).then_inc(copied, 1)
            act.wait_ge(fused, 1)
            act.activation(wf[:], fb[:], ACT.Copy).then_inc(wf_ready, 1)

        @block.gpsimd
        def _(pool):
            with pool.Fori(0, B // 2) as i:
                for s in range(2):
                    pool.wait_ge(out_done, 2 * i)
                    pool.tensor_copy(csT[s][:], c.ctxT[:, :, ds((2 * i + s) * S, S)]).then_inc(cs_ready, 1)

        @block.vector
        def _(dve):
            dve.wait_ge(w_loaded, 48)
            with dve.Fori(0, B // 2) as i:
                link = Chain(dve, chain, i * 6)
                for s in range(2):
                    b = 2 * i + s
                    dve.wait_ge(out_done, b + 1)
                    dve.tensor_tensor(y[:], ob[s][:], bout[:].unsqueeze(1).to_broadcast([P, U, D]), ALU.add).then_inc(out_taken, 1)
                    dve.wait_ge(out_taken, b + 1)
                    v = c.x[:, ds(b * U, U), :].rearrange("p u d -> p (u d)")
                    link(dve.scalar_tensor_tensor(v, y[:].rearrange("p u d -> p (u d)"), c.tg[:, 1:2], v, ALU.mult, ALU.add))
                    for u in range(U):
                        link(dve.bn_stats(c.st[:, U * b + u, :], c.x[:, U * b + u, :]))


def layer1_ffn_weights(nc, I, c, ctx):
    w = Core()
    sb = lambda n, s: ctx.enter_context(nc.sbuf_tensor("l1f_" + n, s, F32))
    w.w1 = [sb(f"w1_{i}", [P, FF1, D]) for i in range(2)]
    w.w2 = [sb(f"w2_{i}", [P, KT, FF1 * P]) for i in range(2)]
    w.b1_rows, w.b2 = sb("b1_rows", [B * FF1, P]), sb("b2", [P, B, D])
    w.w1_loaded, w.w2_loaded = ([c.semaphore(f"l1f_{n}_loaded{i}") for i in range(2)] for n in ("w1", "w2"))
    w.b_loaded = c.semaphore("l1f_b_loaded")

    def load_batch(sp, b):
        sp.dma_start(w.w2[b % 2][:], I["L1_ffn_W2"][b].rearrange("(t p) f -> p t f", p=P)).then_inc(w.w2_loaded[b % 2], 16)
        sp.dma_start(w.w1[b % 2][:], I["L1_ffn_W1"][b].rearrange("(t p) d -> p t d", p=P)).then_inc(w.w1_loaded[b % 2], 16)

    def load(sp):
        sp.dma_start(w.b1_rows[:], I["L1_ffn_b1"].rearrange("g (t p) -> (g t) p", p=P)).then_inc(w.b_loaded, 16)
        sp.dma_start(w.b2[:], row(I["L1_ffn_b2"])).then_inc(w.b_loaded, 16)
        load_batch(sp, 0)
        load_batch(sp, 1)
    w.load, w.load_batch = load, load_batch
    return w


def layer1_ffn(nc, I, c):
    with ExitStack() as ctx:
        sb = lambda n, s, d=F32: ctx.enter_context(nc.sbuf_tensor("l1f_" + n, s, d))
        ps = lambda n, s, d=F32: ctx.enter_context(nc.psum_tensor("l1f_" + n, s, d))
        sem = lambda n: c.semaphore("l1f_" + n)
        w = c.ahead or layer1_ffn_weights(nc, I, c, ctx)
        w1, w2, b1_rows, b2 = w.w1, w.w2, w.b1_rows, w.b2
        w1_loaded, w2_loaded, b_loaded = w.w1_loaded, w.w2_loaded, w.b_loaded
        w2T = [sb(f"w2T{i}", [P, FF1, D]) for i in range(2)]
        b1_cols = sb("b1_cols", [P, B * FF1])
        b1s = [sb(f"b1s{i}", [P, FF1, P]) for i in range(2)]
        wf, bf = sb("wf", [P, KT, D]), sb("bf", [P, D])
        xs, xsT, y = sb("xs", [P, U, D]), sb("xsT", [P, KT, S]), sb("y", [P, U, D])
        mean, rstd, mt, mt2 = sb("mean", [P, NTD]), sb("rstd", [P, NTD]), sb("mt", [P, NTD]), sb("mt2", [P, NTD])
        tb = [ps(f"tb{i}", [P, 2, D]) for i in range(2)]
        fb, bb, xb, ob = ps("fb", [P, KT, D]), ps("bb", [P, D]), ps("xb", [P, KT, S]), ps("ob", [P, U, D])
        names = ("b1_turned", "b1_ready", "b1s_ready", "turned", "copied", "fused",
                 "wf_ready", "xs_ready", "x_turned", "x_copied", "out_done", "out_taken", "chain")
        (b1_turned, b1_ready, b1s_ready, turned, copied, fused,
         wf_ready, xs_ready, x_turned, x_copied, out_done, out_taken, chain) = (sem(n) for n in names)
        block = ctx.enter_context(nc.Block())
        J = FF1 // 2

        @block.sync
        def _(sp):
            if not c.ahead:
                w.load(sp)
            for b in range(2, B):
                sp.wait_ge(fused, b - 1)
                w.load_batch(sp, b)

        @block.tensor
        def _(pe):
            pe.wait_ge(b_loaded, 32)
            pe.transpose(xb[:, 0, 0:B * FF1], b1_rows[:], c.ident[0:B * FF1, 0:B * FF1]).then_inc(b1_turned, 1)
            pe.wait_ge(b1_ready, 1)
            with pe.Fori(0, B // 2) as i:
                for s in range(2):
                    b = 2 * i + s
                    pe.wait_ge(w2_loaded[s], 16 * i + 16)
                    for n in range(J):
                        pe.wait_ge(copied, J * b + max(n - 1, 0))
                        for m in range(2):
                            for kt in range(KT):
                                last = pe.transpose(tb[n % 2][:, m, P * kt:P * kt + P],
                                                    w2[s][:, kt, P * (2 * n + m):P * (2 * n + m) + P], c.ident[:])
                        last.then_inc(turned, 1)
                    pe.wait_ge(xs_ready, b + 1)
                    pe.wait_ge(x_copied, b)
                    for u in range(U):
                        for kt in range(KT):
                            last = pe.transpose(xb[:, kt, P * u:P * u + P], xs[:, u, P * kt:P * kt + P], c.ident[:])
                    last.then_inc(x_turned, 1)
                    pe.wait_ge(copied, J * b + J)
                    pe.wait_ge(w1_loaded[s], 16 * i + 16)
                    pe.wait_ge(b1s_ready, b + 1)
                    pe.wait_ge(wf_ready, 2 * b)
                    for f in range(FF1):
                        pe.matmul(bb[:], b1s[s][:, f, :], w2T[s][:, f, :], start=(f == 0), stop=(f == FF1 - 1))
                    for kt in range(KT):
                        for f in range(FF1):
                            last = pe.matmul(fb[:, kt, :], w1[s][:, f, P * kt:P * kt + P], w2T[s][:, f, :],
                                             start=(f == 0), stop=(f == FF1 - 1))
                    last.then_inc(fused, 1)
                    pe.wait_ge(wf_ready, 2 * b + 2)
                    pe.wait_ge(x_copied, b + 1)
                    pe.wait_ge(out_taken, b)
                    for u in range(U):
                        for kt in range(KT):
                            last = pe.matmul(ob[:, u, :], xsT[:, kt, P * u:P * u + P], wf[:, kt, :],
                                             start=(kt == 0), stop=(kt == KT - 1))
                    last.then_inc(out_done, 1)

        @block.scalar
        def _(act):
            act.wait_ge(b1_turned, 1)
            act.activation(b1_cols[:], xb[:, 0, 0:B * FF1], ACT.Copy).then_inc(b1_ready, 1)
            with act.Fori(0, B // 2) as i:
                for s in range(2):
                    b = 2 * i + s
                    for n in range(J):
                        act.wait_ge(turned, J * b + n + 1)
                        act.activation(w2T[s][:, 2 * n:2 * n + 2, :], tb[n % 2][:], ACT.Copy).then_inc(copied, 1)
                    act.wait_ge(x_turned, b + 1)
                    act.activation(xsT[:], xb[:], ACT.Copy).then_inc(x_copied, 1)
                    act.wait_ge(fused, b + 1)
                    act.wait_ge(out_done, b)
                    act.activation(wf[:], fb[:], ACT.Copy).then_inc(wf_ready, 1)

        @block.gpsimd
        def _(pool):
            pool.wait_ge(b1_ready, 1)
            with pool.Fori(0, B // 2) as i:
                for s in range(2):
                    b = 2 * i + s
                    pool.wait_ge(fused, 2 * i)
                    pool.tensor_copy(b1s[s][:], b1_cols[:, ds(b * FF1, FF1)].unsqueeze(2).to_broadcast([P, FF1, P])).then_inc(b1s_ready, 1)

        @block.vector
        def _(dve):
            link = Chain(dve, chain)
            moments(link, dve, c.st[:], mean[:], rstd[:], mt[:])
            rsqrt(link, dve, mt[:], rstd[:], mt2[:])
            dve.wait_ge(b_loaded, 32)
            base = link.n

            def rows_of(n):
                for u in range(U):
                    t = U * n + u
                    last = dve.tensor_scalar(xs[:, u, :], c.x[:, t, :], mean[:, ds(t, 1)], rstd[:, ds(t, 1)], ALU.subtract, ALU.mult)
                last.then_inc(xs_ready, 1)
            rows_of(0)
            with dve.Fori(0, B) as b:
                link = Chain(dve, chain, base + b * 3)
                dve.wait_ge(fused, b + 1)
                dve.tensor_tensor(bf[:], bb[:], b2[:, b, :], ALU.add).then_inc(wf_ready, 1)
                dve.wait_ge(wf_ready, 2 * b + 2)
                rows_of(b + 1)
                dve.wait_ge(out_done, b + 1)
                dve.tensor_tensor(y[:], ob[:], bf[:].unsqueeze(1).to_broadcast([P, U, D]), ALU.add).then_inc(out_taken, 1)
                dve.wait_ge(out_taken, b + 1)
                v = c.x[:, ds(b * U, U), :].rearrange("p u d -> p (u d)")
                link(dve.scalar_tensor_tensor(v, y[:].rearrange("p u d -> p (u d)"), c.tg[:, 5:6], v, ALU.mult, ALU.add))
                for u in range(U):
                    link(dve.bn_stats(c.st[:, U * b + u, :], c.x[:, U * b + u, :]))


H2, HD2 = 8, 32


def layer2_attention(nc, I, c):
    with ExitStack() as ctx:
        sb = lambda n, s, d=F32: ctx.enter_context(nc.sbuf_tensor("l2a_" + n, s, d))
        ps = lambda n, s, d=F32: ctx.enter_context(nc.psum_tensor("l2a_" + n, s, d))
        sem = lambda n: c.semaphore("l2a_" + n)
        w_in, wT = sb("w_in", [P, 4, KT, D]), sb("wT", [P, 4, KT, D])
        xs, xsT = sb("xs", [P, U, D]), sb("xsT", [P, KT, S])
        csT = sb("csT", [P, KT, S])
        qT, kT = [sb(f"qT{i}", [P, 2, S]) for i in range(2)], [sb(f"kT{i}", [P, 2, S]) for i in range(2)]
        vs = [sb(f"vs{i}", [P, U, D]) for i in range(2)]
        mx = [sb(f"mx{i}", [P, S]) for i in range(2)]
        low = [sb(f"low{i}", [P, 4, 2, S]) for i in range(2)]
        ex = [sb(f"ex{i}", [P, 4, 2, S]) for i in range(2)]
        den, rden = [sb(f"den{i}", [P, S]) for i in range(2)], [sb(f"rden{i}", [P, S]) for i in range(2)]
        oT = sb("oT", [P, 2, S])
        mean, rstd, mt, mt2 = sb("mean", [P, NTD]), sb("rstd", [P, NTD]), sb("mt", [P, NTD]), sb("mt2", [P, NTD])
        sc = ps("sc", [P, 4, 2, S])
        po = [ps(f"po{i}", [P, S]) for i in range(2)]
        pb = [ps(f"pb{i}", [P, 2, S]) for i in range(2)]
        names = ("w_loaded", "w_turned", "w_copied", "chain", "xs_ready", "cs_ready", "filled", "copied", "scored", "lowered",
                 "exp_done", "rden_ready", "weighted", "pv_done", "o_copied", "out_done", "out_taken", "ready0", "maxed")
        (w_loaded, w_turned, w_copied, chain, xs_ready, cs_ready, filled, copied, scored, lowered,
         exp_done, rden_ready, weighted, pv_done, o_copied, out_done, out_taken, ready0, maxed) = (sem(n) for n in names)
        block = ctx.enter_context(nc.Block())

        @block.sync
        def _(sp):
            for k, n in enumerate("QKVO"):
                sp.dma_start(w_in[:, k], I["L2_xattn_W_" + n].rearrange("(t p) d -> p t d", p=P)).then_inc(w_loaded, 16)
            if c.load_ahead:
                c.load_ahead(sp)

        @block.tensor
        def _(pe):
            pe.wait_ge(w_loaded, 64)
            for k in range(4):
                if k >= 2:
                    pe.wait_ge(w_copied, k - 1)
                for ot in range(KT):
                    for kt in range(KT):
                        last = pe.transpose(pb[k % 2][:, kt, P * ot:P * ot + P], w_in[:, k, ot, P * kt:P * kt + P], c.ident[:])
                last.then_inc(w_turned, 1)
            pe.wait_ge(w_copied, 4)
            pe.wait_ge(ready0, 1)

            def prep(step, n, s, out=None):
                if step == 0:
                    pe.wait_ge(xs_ready, n + 1)
                    if out is not None:
                        pe.wait_ge(out_taken, out)
                    for u in range(U):
                        for kt in range(KT):
                            last = pe.transpose(pb[0][:, kt, P * u:P * u + P], xs[:, u, P * kt:P * kt + P], c.ident[:])
                if step == 1:
                    pe.wait_ge(copied, 4 * n + 1)
                    for g in range(2):
                        for kt in range(KT):
                            last = pe.matmul(pb[1][:, g, :], wT[:, 0, kt, P * g:P * g + P], xsT[:, kt, :],
                                             start=(kt == 0), stop=(kt == KT - 1))
                if step == 2:
                    for g in range(2):
                        for kt in range(KT):
                            last = pe.matmul(pb[0][:, g, :], wT[:, 1, kt, P * g:P * g + P], c.ctxT[:, kt, ds(n * S, S)],
                                             start=(kt == 0), stop=(kt == KT - 1))
                if step == 3:
                    pe.wait_ge(cs_ready, n + 1)
                    pe.wait_ge(copied, 4 * n + 2)
                    for u in range(U):
                        for kt in range(KT):
                            last = pe.matmul(pb[1][:, u, :], csT[:, kt, P * u:P * u + P], wT[:, 2, kt, :],
                                             start=(kt == 0), stop=(kt == KT - 1))
                last.then_inc(filled, 1)

            def scores(b, s, kt):
                pe.wait_ge(copied, 4 * b + 3)
                pe.wait_ge(lowered, U * b + kt)
                for r in range(4):
                    for g in range(2):
                        last = pe.matmul(sc[:, r, g, :], kT[s][HD2 * r:HD2 * r + HD2, g, P * kt:P * kt + P],
                                         qT[s][HD2 * r:HD2 * r + HD2, g, :], start=True, stop=True)
                last.then_inc(scored, 1)

            def values(b, s, kt):
                pe.wait_ge(weighted, U * b + kt + 1)
                if kt == 0:
                    pe.wait_ge(copied, 4 * b + 4)
                    pe.wait_ge(o_copied, b)
                for g in range(2):
                    for r in range(4):
                        h = 4 * g + r
                        last = pe.matmul(po[g][HD2 * r:HD2 * r + HD2, :], vs[s][:, kt, HD2 * h:HD2 * h + HD2],
                                         ex[kt][:, r, g, :], start=(kt == 0), stop=(kt == U - 1))
                last.then_inc(pv_done, 1)

            for step in range(4):
                prep(step, 0, 0)
            scores(0, 0, 0)
            for step in range(3):
                prep(step, 1, 1)
            scores(0, 0, 1)
            scores(1, 1, 0)
            with pe.Fori(0, B // 2) as i:
                for s in range(2):
                    b = 2 * i + s
                    scores(b + 1, 1 - s, 1)
                    values(b, s, 0)
                    prep(3, b + 1, 1 - s)
                    prep(0, b + 2, s, b)
                    prep(1, b + 2, s)
                    prep(2, b + 2, s)
                    values(b, s, 1)
                    scores(b + 2, s, 0)
                    pe.wait_ge(o_copied, b + 1)
                    pe.wait_ge(copied, 4 * b + 11)
                    for u in range(U):
                        for g in range(2):
                            last = pe.matmul(pb[0][:, u, :], oT[:, g, P * u:P * u + P], wT[:, 3, g, :],
                                             start=(g == 0), stop=(g == 1))
                    last.then_inc(out_done, 1)

        @block.scalar
        def _(act):
            for k in range(4):
                act.wait_ge(w_turned, k + 1)
                act.activation(wT[:, k], pb[k % 2][:], ACT.Copy).then_inc(w_copied, 1)

            def prep(step, n, s):
                act.wait_ge(filled, 4 * n + step + 1)
                dst = (xsT, qT[s], kT[s], vs[s])[step]
                act.activation(dst[:], pb[step % 2][:], ACT.Copy).then_inc(copied, 1)

            def exps(n, kt):
                act.wait_ge(lowered, U * n + kt + 1)
                act.activation(ex[kt][:], low[kt][:], ACT.Exp, scale=HD2 ** -0.5).then_inc(exp_done, 1)

            for step in range(4):
                prep(step, 0, 0)
            exps(0, 0)
            for step in range(3):
                prep(step, 1, 1)
            exps(0, 1)
            with act.Fori(0, B // 2) as i:
                for s in range(2):
                    b = 2 * i + s
                    act.wait_ge(pv_done, U * b + 1)
                    exps(b + 1, 0)
                    prep(3, b + 1, 1 - s)
                    for step in range(3):
                        prep(step, b + 2, s)
                    act.wait_ge(pv_done, U * b + U)
                    act.activation(oT[:, 0, :], po[0][:], ACT.Copy)
                    act.activation(oT[:, 1, :], po[1][:], ACT.Copy).then_inc(o_copied, 1)
                    exps(b + 1, 1)

        @block.gpsimd
        def _(pool):
            def weigh(n, kt):
                pool.wait_ge(rden_ready, U * n + kt + 1)
                e = ex[kt][:].rearrange("p r g q -> p (r g) q")
                pool.tensor_tensor(e, e, rden[kt][:].unsqueeze(1).to_broadcast([P, H2, S]), ALU.mult).then_inc(weighted, 1)

            pool.tensor_copy(csT[:], c.ctxT[:, :, 0:S]).then_inc(cs_ready, 1)
            weigh(0, 0)
            pool.wait_ge(filled, 4)
            pool.tensor_copy(csT[:], c.ctxT[:, :, S:2 * S]).then_inc(cs_ready, 1)
            with pool.Fori(0, B) as b:
                weigh(b, 1)
                weigh(b + 1, 0)
                pool.wait_ge(filled, 4 * b + 8)
                pool.tensor_copy(csT[:], c.ctxT[:, :, ds(b * S + 2 * S, S)]).then_inc(cs_ready, 1)

        @block.vector
        def _(dve):
            link = Chain(dve, chain)
            moments(link, dve, c.st[:], mean[:], rstd[:], mt[:])
            rsqrt(link, dve, mt[:], rstd[:], mt2[:])
            dve.sem_inc(ready0, 1)

            def rows_of(n):
                for u in range(U):
                    t = U * n + u
                    last = dve.tensor_scalar(xs[:, u, :], c.x[:, t, :], mean[:, ds(t, 1)], rstd[:, ds(t, 1)], ALU.subtract, ALU.mult)
                last.then_inc(xs_ready, 1)

            def lower(b, kt):
                dve.wait_ge(scored, U * b + kt + 1)
                dve.tensor_reduce(mx[kt][:], sc[:].rearrange("p r g q -> p q (r g)"), AX, ALU.max).then_inc(maxed, 1)
                dve.wait_ge(maxed, U * b + kt + 1)
                dve.tensor_tensor(low[kt][:].rearrange("p r g q -> p (r g) q"), sc[:].rearrange("p r g q -> p (r g) q"),
                                  mx[kt][:].unsqueeze(1).to_broadcast([P, H2, S]), ALU.subtract).then_inc(lowered, 1)

            def divide(link, b, kt, first=False):
                dve.wait_ge(exp_done, U * b + kt + 1)
                if not first:
                    dve.wait_ge(weighted, U * b + kt - 1)
                link(dve.tensor_reduce(den[kt][:], ex[kt][:].rearrange("p r g q -> p q (r g)"), AX, ALU.add))
                dve.reciprocal(rden[kt][:], den[kt][:]).then_inc(rden_ready, 1)

            rows_of(0)
            lower(0, 0)
            dve.wait_ge(filled, 1)
            rows_of(1)
            lower(0, 1)
            divide(link, 0, 0, True)
            lower(1, 0)
            base = link.n
            with dve.Fori(0, B // 2) as i:
                for s in range(2):
                    b = 2 * i + s
                    link = Chain(dve, chain, base + b * (U + U))
                    divide(link, b, 1)
                    lower(b + 1, 1)
                    dve.wait_ge(filled, 4 * b + 5)
                    rows_of(b + 2)
                    divide(link, b + 1, 0)
                    lower(b + 2, 0)
                    dve.wait_ge(out_done, b + 1)
                    v = c.x[:, ds(b * U, U), :].rearrange("p u d -> p (u d)")
                    dve.scalar_tensor_tensor(v, pb[0][:].rearrange("p u d -> p (u d)"), c.tg[:, 2:3], v,
                                             ALU.mult, ALU.add).then_inc(out_taken, 1)
                    dve.wait_ge(out_taken, b + 1)
                    for u in range(U):
                        link(dve.bn_stats(c.st[:, U * b + u, :], c.x[:, U * b + u, :]))


NROT = 4
BASE_SQ = 5
LEVELS = 12
NORM0 = 16.0
TAYLOR0 = (1.0, 1.0, 1 / 2, 1 / 6)
TAYLOR1 = (1 / 24, 1 / 120, 1 / 720, 1 / 5040, 1 / 40320)


def rotation_weights(nc, I, c, ctx):
    w = Core()
    w.tensor = ctx.enter_context(nc.sbuf_tensor("rot_A", [P, NROT, KT, D], F32))
    w.gens = [w.tensor[:, m] for m in range(NROT)]
    w.loaded = c.semaphore("rot_loaded")

    def load(sp):
        for m in range(NROT):
            sp.dma_start(w.gens[m][:], I["L2_ffn_gens"][m].rearrange("(t p) d -> p t d", p=P)).then_inc(w.loaded, 16)
    w.load = load
    return w


def rotation(nc, I, c, w, side):
    with ExitStack() as ctx:
        sb = lambda n, s, d=F32: ctx.enter_context(nc.sbuf_tensor("rot_" + n, s, d))
        sem = lambda n: c.semaphore("rot_" + n)
        mats = lambda n: [sb(f"{n}{m}", [P, KT, D]) for m in range(NROT)]
        A, loaded = w.gens, w.loaded
        L, A2, A3, A4, T0, T1 = (mats(n) for n in ("L", "A2_", "A3_", "A4_", "T0_", "T1_"))
        R = A3
        rowsum, norm = sb("rowsum", [P, NROT, KT]), sb("norm", [P, 2, NROT])
        over, half, scale = sb("over", [P, LEVELS, NROT]), sb("half", [P, LEVELS, NROT]), sb("scale", [P, NROT])
        flag, take, aside = sb("flag", [P, 1], I32), sb("take", [P, NROT]), sb("aside", [P, NROT])
        bank = [ctx.enter_context(nc.psum_tensor(f"rot_bank{m}", [P, KT, D], F32)) for m in range(NROT)]
        names = ("chain", "norm_ready", "norm_all", "scaled", "done", "copied", "poly", "summed",
                 "x_done", "x_taken", "x_turned", "x_copied", "took", "f_done", "f_copied")
        (chain, norm_ready, norm_all, scaled, done, copied, poly, summed,
         x_done, x_taken, x_turned, x_copied, took, f_done, f_copied) = (sem(n) for n in names)

        def turn(pe, out, src):
            for ot in range(KT):
                for kt in range(KT):
                    last = pe.transpose(out[:, kt, P * ot:P * ot + P], src[:, ot, P * kt:P * kt + P], c.ident[:])
            return last

        def product(pe, out, leftT, right):
            for ot in range(KT):
                for kt in range(KT):
                    last = pe.matmul(out[:, ot, :], leftT[:, kt, P * ot:P * ot + P], right[:, kt, :],
                                     start=(kt == 0), stop=(kt == KT - 1))
            return last

        STEPS = [(A, None, L), (L, A, A2), (A2, None, L), (L, A, A3), (L, A2, A4), (A4, None, L), (L, T1, R)]
        POLY = len(STEPS) - 1
        STEPS += [(R, None, L), (L, R, R)] * BASE_SQ + [(R, None, L)]
        BESIDE = {POLY + 1 + 2 * i: i for i in range(B // 2)}

        with nc.Block() as block:
            @block.sync
            def _(sp):
                if not c.ahead:
                    w.load(sp)
                side.sync(sp)

            @block.tensor
            def _(pe):
                for k, (left, right, dst) in enumerate(STEPS):
                    for m in range(NROT):
                        if k == 0:
                            pe.wait_ge(scaled, m + 1)
                        elif k == POLY + 1:
                            pe.wait_ge(summed, m + 1)
                        else:
                            pe.wait_ge(copied, NROT * (k - 1 if k <= POLY else k - 2) + m + 1)
                        if k == POLY:
                            pe.wait_ge(poly, m + 1)
                        last = turn(pe, bank[m], left[m]) if right is None else product(pe, bank[m], left[m], right[m])
                        last.then_inc(done, 1)
                    if k in BESIDE:
                        side.tensor(pe, BESIDE[k])

            @block.scalar
            def _(act):
                for k, (left, right, dst) in enumerate(STEPS):
                    for m in range(NROT if k != POLY else 0):
                        act.wait_ge(done, NROT * k + m + 1)
                        act.activation(dst[m][:], bank[m][:], ACT.Copy).then_inc(copied, 1)
                    if k in BESIDE:
                        side.scalar(act, BESIDE[k])

            @block.gpsimd
            def _(pool):
                pool.wait_ge(norm_ready, 1)
                pool.partition_all_reduce(norm[:, 1, :], norm[:, 0, :], P, bass.bass_isa.ReduceOp.max).then_inc(norm_all, 1)

            @block.vector
            def _(dve):
                link = Chain(dve, chain)
                dve.wait_ge(loaded, 16 * NROT)
                for m in range(NROT):
                    link(dve.tensor_reduce(rowsum[:, m, :], A[m][:], AX, ALU.add, apply_absolute_value=True))
                link(dve.tensor_reduce(norm[:, 0, :], rowsum[:], AX, ALU.max))
                dve.sem_inc(norm_ready, 1)
                dve.wait_ge(norm_all, 1)
                for k in range(LEVELS):
                    link(dve.tensor_scalar(over[:, k, :], norm[:, 1, :], NORM0 * 2.0 ** k, None, ALU.is_gt))
                link(dve.tensor_scalar(half[:], over[:], -0.5, 1.0, ALU.mult, ALU.add))
                link(dve.tensor_reduce(scale[:], half[:].rearrange("p k m -> p m k"), AX, ALU.mult))
                link(dve.tensor_scalar(scale[:], scale[:], 2.0 ** -BASE_SQ, None, ALU.mult))
                link(dve.tensor_reduce(flag[:], over[:, 0, :], AX, ALU.max))
                for m in range(NROT):
                    dve.tensor_scalar(A[m][:], A[m][:], scale[:, m:m + 1], None, ALU.mult).then_inc(scaled, 1)
                dve.wait_ge(scaled, NROT)
                side.vector_first(dve)
                for m in range(NROT):
                    dve.wait_ge(copied, NROT * 4 + m + 1)
                    link(dve.tensor_scalar(T1[m][:], A4[m][:], TAYLOR1[4], None, ALU.mult))
                    for coef, mat in ((TAYLOR1[3], A3), (TAYLOR1[2], A2), (TAYLOR1[1], A)):
                        link(dve.scalar_tensor_tensor(T1[m][:], mat[m][:], coef, T1[m][:], ALU.mult, ALU.add))
                    for kt in range(KT):
                        v = T1[m][:, kt, P * kt:P * kt + P]
                        link(dve.scalar_tensor_tensor(v, c.ident[:], TAYLOR1[0], v, ALU.mult, ALU.add))
                    dve.sem_inc(poly, 1)
                    link(dve.scalar_tensor_tensor(T0[m][:], A2[m][:], TAYLOR0[2], A[m][:], ALU.mult, ALU.add))
                    link(dve.scalar_tensor_tensor(T0[m][:], A3[m][:], TAYLOR0[3], T0[m][:], ALU.mult, ALU.add))
                    for kt in range(KT):
                        v = T0[m][:, kt, P * kt:P * kt + P]
                        link(dve.tensor_tensor(v, v, c.ident[:], ALU.add))
                for m in range(NROT):
                    dve.wait_ge(done, NROT * POLY + m + 1)
                    dve.tensor_tensor(R[m][:], bank[m][:], T0[m][:], ALU.add).then_inc(summed, 1)
                dve.wait_ge(summed, NROT)
                for i in range(B // 2):
                    side.vector(dve, i)

        with nc.Block() as block:
            @block.tensor
            def _(pe):
                with pe.If(pe.value_load(flag[0:1, 0:1], min_val=0, max_val=1) > 0):
                    with pe.Fori(0, LEVELS) as k:
                        for m in range(NROT):
                            pe.wait_ge(x_copied, NROT * k + m)
                            product(pe, bank[m], L[m], R[m]).then_inc(x_done, 1)
                            pe.wait_ge(x_taken, NROT * k + m + 1)
                            turn(pe, bank[m], R[m]).then_inc(x_turned, 1)

            @block.scalar
            def _(act):
                with act.If(act.value_load(flag[0:1, 0:1], min_val=0, max_val=1) > 0):
                    with act.Fori(0, LEVELS) as k:
                        for m in range(NROT):
                            act.wait_ge(x_turned, NROT * k + m + 1)
                            act.activation(L[m][:], bank[m][:], ACT.Copy).then_inc(x_copied, 1)

            @block.vector
            def _(dve):
                with dve.If(dve.value_load(flag[0:1, 0:1], min_val=0, max_val=1) > 0):
                    with dve.Fori(0, LEVELS) as k:
                        dve.tensor_copy(take[:], over[:, k, :]).then_inc(took, 1)
                        for m in range(NROT):
                            dve.wait_ge(x_done, NROT * k + m + 1)
                            dve.wait_ge(took, (NROT + 1) * k + m + 1)
                            dve.tensor_copy(aside[:, m:m + 1], take[:, m:m + 1]).then_inc(took, 1)
                            v = R[m][:].rearrange("p k d -> p (k d)")
                            dve.copy_predicated(v, take[:, m:m + 1].bitcast(I32).to_broadcast([P, KT * D]),
                                                bank[m][:].rearrange("p k d -> p (k d)")).then_inc(x_taken, 1)

        with nc.Block() as block:
            M = [R[0], A[1], A[2], c.rot]

            @block.tensor
            def _(pe):
                for m in range(1, NROT):
                    if m > 1:
                        pe.wait_ge(f_copied, 2 * m - 3)
                        turn(pe, bank[0], M[m - 1]).then_inc(f_done, 1)
                        pe.wait_ge(f_copied, 2 * m - 2)
                    product(pe, bank[1], L[0], R[m]).then_inc(f_done, 1)

            @block.vector
            def _(dve):
                side.vector_last(dve)

            @block.scalar
            def _(act):
                for m in range(1, NROT):
                    if m > 1:
                        act.wait_ge(f_done, 2 * m - 2)
                        act.activation(L[0][:], bank[0][:], ACT.Copy).then_inc(f_copied, 1)
                    act.wait_ge(f_done, 2 * m - 1)
                    act.activation(M[m][:], bank[1][:], ACT.Copy).then_inc(f_copied, 1)
                    if m == 2:
                        side.scalar_last(act)
                act.wait_ge(f_copied, 2 * NROT - 3)


NE = 6
FE = 512 // P
UNITS = FF1 // FE + NE


def layer2_ffn(nc, I, c):
    with ExitStack() as ctx:
        gens = c.ahead or rotation_weights(nc, I, c, ctx)
        sb = lambda n, s, d=F32: ctx.enter_context(nc.sbuf_tensor("l2f_" + n, s, d))
        sem = lambda n: c.semaphore("l2f_" + n)
        znT = sb("znT", [P, KT, NT * P])
        logit, w6, eb2 = sb("logit", [P, NT, 8]), sb("w6", [P, NT, NE]), sb("eb2", [NE, D])
        mean, rstd, mt, mt2 = sb("mean", [P, NTD]), sb("rstd", [P, NTD]), sb("mt", [P, NTD]), sb("mt2", [P, NTD])
        rstd2 = sb("rstd2", [P, NTD])
        aw1, aw2 = sb("aw1", [P, KT, FF1 * P]), sb("aw2", [P, FF1, D])
        ew1, ew2 = sb("ew1", [P, NE, KT, FE * P]), sb("ew2", [P, NE, FE, D])
        ab1, eb1, ab2 = sb("ab1", [P, FF1]), sb("eb1", [P, NE * FE]), sb("ab2", [P, D])
        gc_w, gc_b = sb("gc_w", [P, 2, D]), sb("gc_b", [P, 1])
        a_loaded, e_loaded = sem("a_loaded"), sem("e_loaded")

        with ExitStack() as first:
            fsb = lambda n, s, d=F32: first.enter_context(nc.sbuf_tensor("l2f_" + n, s, d))
            fps = lambda n, s, d=F32: first.enter_context(nc.psum_tensor("l2f_" + n, s, d))
            zs, zsT = [fsb(f"zs{i}", [P, U, D]) for i in range(2)], [fsb(f"zsT{i}", [P, KT, S]) for i in range(2)]
            ln_g, ln_b, gate_w, gate_b = fsb("ln_g", [P, D]), fsb("ln_b", [P, D]), fsb("gate_w", [P, KT, NE]), fsb("gate_b", [P, NE])
            top, idx, idxf = fsb("top", [P, NT, 8]), fsb("idx", [P, NT, 8], U32), fsb("idxf", [P, NT, 8])
            iota, wk, sel = fsb("iota", [P, NE]), fsb("wk", [P, NT, 4]), fsb("sel", [P, NT, NE])
            tb, lb = [fps(f"tb{i}", [P, KT, S]) for i in range(2)], [fps(f"lb{i}", [P, U, 8]) for i in range(2)]
            names = ("loaded", "chain", "zs_ready", "turned", "copied", "logits_done", "logits_taken", "tops", "diff_ready",
                     "exp_ready", "w6_ready")
            (loaded, chain, zs_ready, turned, copied, logits_done, logits_taken, tops, diff_ready, exp_ready,
             w6_ready) = (sem(n) for n in names)
            side = Core()
            link_of = Core()

            def sync(sp):
                sp.dma_start(ln_g[:], row(I["L2_ffn_ln_g"])).then_inc(loaded, 16)
                sp.dma_start(ln_b[:], row(I["L2_ffn_ln_b"])).then_inc(loaded, 16)
                sp.dma_start(gate_w[:], I["L2_ffn_gate_w"].rearrange("(t p) e -> p t e", p=P)).then_inc(loaded, 16)
                sp.dma_start(gate_b[:], row(I["L2_ffn_gate_b"])).then_inc(loaded, 16)
                for e in range(NE):
                    sp.dma_start(ew1[:, e], I["L2_ffn_ew1"][e].rearrange("(t p) f -> p t f", p=P)).then_inc(e_loaded, 16)
                    sp.dma_start(ew2[:, e], I["L2_ffn_ew2"][e].rearrange("(t p) d -> p t d", p=P)).then_inc(e_loaded, 16)
                sp.dma_start(aw1[:], I["L2_ffn_aw1"].rearrange("(t p) f -> p t f", p=P)).then_inc(a_loaded, 16)
                sp.dma_start(ab1[:], col(I["L2_ffn_ab1"])).then_inc(a_loaded, 16)
                sp.dma_start(eb1[:], col(I["L2_ffn_eb1"].rearrange("e f -> (e f)"))).then_inc(a_loaded, 16)
                sp.dma_start(aw2[:], I["L2_ffn_aw2"].rearrange("(t p) d -> p t d", p=P)).then_inc(a_loaded, 16)
                sp.dma_start(ab2[:], row(I["L2_ffn_ab2"])).then_inc(a_loaded, 16)
                sp.dma_start(eb2[:], I["L2_ffn_eb2"]).then_inc(a_loaded, 16)
                v = I["L2_ffn_gc_w"].rearrange("(a d) o -> a (d o)", a=2)
                for k in range(2):
                    sp.dma_start(gc_w[:, k, :], row(v[k])).then_inc(a_loaded, 16)
                sp.dma_start(gc_b[:], row(I["L2_ffn_gc_b"])).then_inc(a_loaded, 16)

            def vector_first(dve):
                link = link_of.link = Chain(dve, chain)
                moments(link, dve, c.st[:], mean[:], rstd[:], mt[:])
                rsqrt(link, dve, mt[:], rstd[:], mt2[:])
                link(dve.memset(logit[:], -3.0e38))
                link(dve.tensor_scalar(mt[:], mt[:], LN_EPS, None, ALU.subtract))
                link(dve.tensor_tensor(mt[:], mt[:], rstd[:], ALU.mult))
                link(dve.tensor_tensor(mt[:], mt[:], rstd[:], ALU.mult))
                link(dve.tensor_scalar(mt[:], mt[:], LN_EPS, None, ALU.add))
                rsqrt(link, dve, mt[:], rstd2[:], mt2[:])
                link(dve.tensor_tensor(rstd2[:], rstd2[:], rstd[:], ALU.mult))
                dve.wait_ge(loaded, 64)

            def vector(dve, i):
                link = link_of.link
                dve.wait_ge(turned, 2 * i)
                for s in range(2):
                    for u in range(U):
                        t = U * (2 * i + s) + u
                        ins = dve.tensor_scalar(zs[s][:, u, :], c.x[:, t, :], mean[:, t:t + 1], rstd2[:, t:t + 1],
                                                ALU.subtract, ALU.mult)
                    link(ins)
                    link(dve.tensor_tensor(zs[s][:], zs[s][:], ln_g[:].unsqueeze(1).to_broadcast([P, U, D]), ALU.mult))
                    dve.tensor_tensor(zs[s][:], zs[s][:], ln_b[:].unsqueeze(1).to_broadcast([P, U, D]), ALU.add).then_inc(zs_ready, 1)
                for s in range(2):
                    b = 2 * i + s
                    dve.wait_ge(logits_done, b + 1)
                    dve.tensor_tensor(logit[:, b * U:b * U + U, 0:NE], lb[s][:, :, 0:NE],
                                      gate_b[:].unsqueeze(1).to_broadcast([P, U, NE]), ALU.add).then_inc(logits_taken, 1)

            def tensor(pe, i):
                pe.wait_ge(loaded, 64)
                for s in range(2):
                    b = 2 * i + s
                    pe.wait_ge(zs_ready, b + 1)
                    pe.wait_ge(copied, 4 * i)
                    for u in range(U):
                        for kt in range(KT):
                            last = pe.transpose(tb[s][:, kt, P * u:P * u + P], zs[s][:, u, P * kt:P * kt + P], c.ident[:])
                    last.then_inc(turned, 1)
                for s in range(2):
                    b = 2 * i + s
                    pe.wait_ge(copied, 4 * i + 2 * s + 1)
                    pe.wait_ge(logits_taken, 2 * i)
                    for u in range(U):
                        for kt in range(KT):
                            last = pe.matmul(lb[s][:, u, 0:NE], zsT[s][:, kt, P * u:P * u + P], gate_w[:, kt, :],
                                             start=(kt == 0), stop=(kt == KT - 1))
                    last.then_inc(logits_done, 1)

            def scalar(act, i):
                for s in range(2):
                    b = 2 * i + s
                    act.wait_ge(turned, b + 1)
                    act.wait_ge(logits_done, 2 * i)
                    act.activation(zsT[s][:], tb[s][:], ACT.Copy).then_inc(copied, 1)
                    act.activation(znT[:, :, b * S:b * S + S], tb[s][:], ACT.Copy).then_inc(copied, 1)

            def vector_last(dve):
                link = link_of.link
                dve.wait_ge(logits_taken, B)
                for e in range(NE):
                    last = dve.memset(iota[:, e:e + 1], float(e))
                link(last)
                for t in range(NT):
                    dve.max(top[:, t, :], logit[:, t, :]).then_inc(tops, 1)
                for t in range(NT):
                    dve.wait_ge(tops, t + 1)
                    last = dve.max_index(idx[:, t, :], top[:, t, :], logit[:, t, :])
                link(last)
                link(dve.tensor_copy(idxf[:], idx[:]))
                dve.tensor_tensor(wk[:, :, 0], top[:, :, 1], top[:, :, 0], ALU.subtract).then_inc(diff_ready, 1)
                dve.wait_ge(exp_ready, 1)
                link(dve.tensor_scalar(wk[:, :, 2], wk[:, :, 1], 1.0, None, ALU.add))
                link(dve.reciprocal(wk[:, :, 2], wk[:, :, 2]))
                link(dve.tensor_tensor(wk[:, :, 3], wk[:, :, 1], wk[:, :, 2], ALU.mult))
                full = [P, NT, NE]
                for k, out in ((0, w6), (1, sel)):
                    link(dve.tensor_tensor(out[:], iota[:].unsqueeze(1).to_broadcast(full),
                                           idxf[:, :, k:k + 1].to_broadcast(full), ALU.is_equal))
                    link(dve.tensor_tensor(out[:], out[:], wk[:, :, 2 + k:3 + k].to_broadcast(full), ALU.mult))
                dve.tensor_tensor(w6[:], w6[:], sel[:], ALU.add).then_inc(w6_ready, 1)
                dve.wait_ge(w6_ready, 1)

            def scalar_last(act):
                act.wait_ge(diff_ready, 1)
                act.activation(wk[:, :, 1], wk[:, :, 0], ACT.Exp).then_inc(exp_ready, 1)

            side.sync, side.vector_first, side.vector, side.tensor, side.scalar = sync, vector_first, vector, tensor, scalar
            side.vector_last, side.scalar_last = vector_last, scalar_last
            rotation(nc, I, c, gens, side)

        dense, moe = sb("dense", [P, NT, D]), sb("moe", [P, NT, D])
        gate, gdot = sb("gate", [P, QUADS + NT]), sb("gdot", [P, QUADS + NT])

        with ExitStack() as third:
            fsb = lambda n, s, d=F32: third.enter_context(nc.sbuf_tensor("l2f_" + n, s, d))
            fps = lambda n, s, d=F32: third.enter_context(nc.psum_tensor("l2f_" + n, s, d))
            hs = [fsb(f"hs{i}", [P, FE, QT]) for i in range(2)]
            acc, accT = fsb("acc", [P, QUADS, D]), fsb("accT", [P, KT, QT])
            work = gens.tensor[:].rearrange("p m k d -> p (m k) d")
            wa, wb = work[:, 0:QUADS], work[:, QUADS:2 * QUADS]
            hb = [fps(f"hb{i}", [P, QT]) for i in range(2)]
            ob = [[fps(f"ob{i}{j}", [P, 2, D]) for j in range(2)] for i in range(2)]
            rb = [fps(f"rb{i}", [P, 2, D]) for i in range(2)]
            w6T = fsb("w6T", [NE, NT * P])
            w6_turned, w6T_ready = sem("w6_turned"), sem("w6T_ready")
            names = ("chain3", "h_done", "gelu_done", "o_done", "o_taken", "acc_turned", "accT_ready", "rot_done",
                     "rot_taken", "gates", "chain4")
            (chain, h_done, gelu_done, o_done, o_taken, acc_turned, accT_ready, rot_done, rot_taken, gates, chain4) = (sem(n) for n in names)
            block = third.enter_context(nc.Block())
            ALL = 16 * 9
            DOT_LINKS = 4 + 3

            @block.tensor
            def _(pe):
                for t in range(NT):
                    j, m = divmod(t, QUADS)
                    last = pe.transpose(ob[j // 2][j % 2][0:NE, m // 2, P * (m % 2):P * (m % 2) + P], w6[:, t, :], c.ident[:])
                    if m == QUADS - 1:
                        last.then_inc(w6_turned, 1)
                pe.wait_ge(a_loaded, ALL)
                pe.wait_ge(e_loaded, 32 * NE)
                with pe.Fori(0, NQ) as i:
                    def up(k):
                        for f in range(FE):
                            n = FE * k + f
                            pe.wait_ge(gelu_done, FE * UNITS * i + max(n - 1, 0))
                            for kt in range(KT):
                                m = P * (n - FE * NE)
                                w = ew1[:, k, kt, P * f:P * f + P] if k < NE else aw1[:, kt, m:m + P]
                                last = pe.matmul(hb[n % 2][:], w, znT[:, kt, ds(i * QT, QT)], start=(kt == 0), stop=(kt == KT - 1))
                            last.then_inc(h_done, 1)

                    def down(k):
                        pe.wait_ge(gelu_done, FE * UNITS * i + FE * (k + 1))
                        pe.wait_ge(o_taken, UNITS * i + max(k - 1, 0))
                        if k == 0:
                            pe.wait_ge(w6T_ready, NQ)
                        for t in range(QUADS):
                            for f in range(FE):
                                w = ew2[:, k, f, :] if k < NE else aw2[:, FE * (k - NE) + f, :]
                                last = pe.matmul(ob[k % 2][t // 2][:, t % 2, :], hs[k % 2][:, f, P * t:P * t + P], w,
                                                 start=(f == 0), stop=(f == FE - 1))
                        last.then_inc(o_done, 1)

                    up(0)
                    for k in range(UNITS):
                        if k + 1 < UNITS:
                            up(k + 1)
                        if k == UNITS - 1:
                            pe.wait_ge(o_taken, UNITS * i + NE)
                            pe.wait_ge(rot_taken, i)
                            for kt in range(KT):
                                pe.matmul(rb[kt][:].rearrange("p a n -> p (a n)"), eb2[:, P * kt:P * kt + P],
                                          w6T[:, ds(i * QT, QT)], start=True, stop=False)
                                for t in range(QUADS):
                                    last = pe.matmul(rb[kt][:, t // 2, P * (t % 2):P * (t % 2) + P],
                                                     acc[:, t, P * kt:P * kt + P], c.ident[:], start=False, stop=(t == QUADS - 1))
                            last.then_inc(acc_turned, 1)
                        down(k)
                    pe.wait_ge(accT_ready, i + 1)
                    for t in range(QUADS):
                        for kt in range(KT):
                            last = pe.matmul(rb[t // 2][:, t % 2, :], accT[:, kt, P * t:P * t + P], c.rot[:, kt, :],
                                             start=(kt == 0), stop=(kt == KT - 1))
                    last.then_inc(rot_done, 1)

            @block.scalar
            def _(act):
                for j in range(NQ):
                    act.wait_ge(w6_turned, j + 1)
                    act.activation(w6T[:, QT * j:QT * j + QT], ob[j // 2][j % 2][0:NE].rearrange("p a n -> p (a n)"),
                                   ACT.Copy).then_inc(w6T_ready, 1)
                act.wait_ge(a_loaded, ALL)
                act.activation(mt[:, 0:1], ab1[:, 0:1], ACT.Gelu)
                with act.Fori(0, NQ) as i:
                    for k in range(UNITS):
                        act.wait_ge(o_done, UNITS * i + max(k - 1, 0))
                        if k == 4:
                            act.wait_ge(chain, DOT_LINKS * i + 1)
                            act.activation(gate[:, ds(i * QUADS, QUADS)], gdot[:, ds(i * QUADS, QUADS)], ACT.Sigmoid,
                                           bias=gc_b[:, 0:1]).then_inc(gates, 1)
                        for f in range(FE):
                            n = FE * k + f
                            bias = eb1[:, n:n + 1] if k < NE else ab1[:, n - FE * NE:n - FE * NE + 1]
                            act.wait_ge(h_done, FE * UNITS * i + n + 1)
                            act.activation(hs[k % 2][:, f, :], hb[n % 2][:], ACT.Gelu, bias=bias).then_inc(gelu_done, 1)
                    act.wait_ge(acc_turned, i + 1)
                    for kt in range(KT):
                        ins = act.activation(accT[:, kt, :], rb[kt][:], ACT.Copy)
                    ins.then_inc(accT_ready, 1)
                    act.wait_ge(rot_done, i + 1)
                    for j in range(2):
                        ins = act.activation(moe[:, ds(i * QUADS + 2 * j, 2), :], rb[j][:], ACT.Copy)
                    ins.then_inc(rot_taken, 1)
                act.wait_ge(chain, DOT_LINKS * NQ + 1)
                act.activation(gate[:, NT:], gdot[:, NT:], ACT.Sigmoid, bias=gc_b[:, 0:1]).then_inc(gates, 1)

            @block.vector
            def _(dve):
                dve.wait_ge(a_loaded, ALL)
                wide = lambda k: gc_w[:, k:k + 1, :].to_broadcast([P, QUADS, D])
                Chain(dve, chain)(dve.memset(gdot[:, 0:QUADS], 0.0))

                def unit(i, k):
                    dve.wait_ge(o_done, UNITS * i + k + 1)
                    if k >= 1:
                        dve.wait_ge(o_taken, UNITS * i + k)
                    if k == 0:
                        dve.wait_ge(acc_turned, i)
                    for j in range(2):
                        if k >= NE:
                            d = dense[:, ds(i * QUADS + 2 * j, 2), :]
                            other = ab2[:].unsqueeze(1).to_broadcast([P, 2, D]) if k == NE else d
                            last = dve.tensor_tensor(d, ob[k % 2][j][:], other, ALU.add)
                        else:
                            for m in range(2):
                                t = 2 * j + m
                                share = w6[:, i * QUADS + t, k:k + 1]
                                if k == 0:
                                    last = dve.tensor_scalar(acc[:, t, :], ob[k % 2][j][:, m, :], share, None, ALU.mult)
                                else:
                                    last = dve.scalar_tensor_tensor(acc[:, t, :], ob[k % 2][j][:, m, :], share,
                                                                    acc[:, t, :], ALU.mult, ALU.add)
                    last.then_inc(o_taken, 1)

                def logits(i):
                    link = Chain(dve, chain, DOT_LINKS * i + 1)
                    d, m = dense[:, ds(i * QUADS, QUADS), :], moe[:, ds(i * QUADS, QUADS), :]
                    dve.wait_ge(o_taken, UNITS * (i + 1))
                    link(dve.tensor_tensor(wa[:], d, wide(0), ALU.mult))
                    dve.wait_ge(rot_taken, i + 1)
                    link(dve.tensor_tensor(wb[:], m, wide(1), ALU.mult))
                    link(dve.tensor_tensor(wb[:], wa[:], wb[:], ALU.add))
                    link(dve.tensor_reduce(gdot[:, ds(i * QUADS + QUADS, QUADS)], wb[:], AX, ALU.add))
                    link(dve.tensor_tensor(m, m, d, ALU.subtract))
                    for t in range(QUADS):
                        n = i * QUADS + t
                        last = dve.tensor_scalar(wa[:, t, :], c.x[:, n, :],
                                                 mean[:, ds(n, 1)], rstd[:, ds(n, 1)], ALU.subtract, ALU.mult)
                    link(last)
                    link(dve.tensor_tensor(d, d, wa[:], ALU.add))

                def mix(i):
                    link = Chain(dve, chain4, i * 3)
                    dve.wait_ge(gates, i + 2)
                    for t in range(QUADS):
                        n = i * QUADS + t
                        last = dve.scalar_tensor_tensor(wa[:, t, :], moe[:, n, :], gate[:, ds(n + QUADS, 1)], dense[:, n, :],
                                                        ALU.mult, ALU.add)
                    link(last)
                    v = c.x[:, ds(i * QUADS, QUADS), :].rearrange("p u d -> p (u d)")
                    link(dve.scalar_tensor_tensor(v, wa[:].rearrange("p u d -> p (u d)"), c.tg[:, 6:7], v, ALU.mult, ALU.add))
                    for t in range(QUADS):
                        last = dve.bn_stats(c.st[:, i * QUADS + t, :], c.x[:, i * QUADS + t, :])
                    link(last)

                for k in range(UNITS):
                    unit(0, k)
                logits(0)
                with dve.Fori(1, NQ) as i:
                    for k in range(UNITS):
                        unit(i, k)
                        if k == 5:
                            mix(i - 1)
                    logits(i)
                mix(NQ - 1)


def store(nc, c, out):
    with ExitStack() as ctx:
        stored = c.semaphore("stored")
        block = ctx.enter_context(nc.Block())

        @block.sync
        def _(sp):
            for b in range(B):
                sp.dma_start(out[b].rearrange("(u p) d -> p u d", p=P), c.x[:, U * b:U * b + U, :]).then_inc(stored, 16)
            sp.wait_ge(stored, 16 * B)


STAGES = (layer0_attention, layer0_ffn, layer1_attention, layer1_ffn, layer2_attention, layer2_ffn,
          layer3_attention, layer3_ffn)


AHEAD_OF = {layer0_attention: layer0_ffn_weights, layer1_attention: layer1_ffn_weights, layer2_attention: rotation_weights, layer3_attention: layer3_ffn_weights}


def program(nc, I, out, stages=STAGES):
    with ExitStack() as ctx:
        ctx.enter_context(nc.allow_non_contiguous_dma(reason="a few short bias columns"))
        c = Core()
        c.nc, c.sems, c.out = nc, [], out
        sb = lambda n, s, d=F32: ctx.enter_context(nc.sbuf_tensor(n, s, d))
        c.x = sb("x", [P, NTD, D])
        c.st = sb("st", [P, NTD, 6])
        c.ctxT = sb("ctxT", [P, KT, TD])
        c.ident = sb("ident", [P, P])
        c.identb = sb("identb", [P, P], BF16)
        c.ones = sb("ones", [P, P])
        c.g = sb("g", [P, 8])
        c.tg = sb("tg", [P, 8])
        c.rot = sb("rot", [P, KT, D])
        setup(nc, I, c)
        c.ahead = c.load_ahead = None
        for n, s in enumerate(stages):
            if s in AHEAD_OF and n + 1 < len(stages):
                pair = ctx.enter_context(ExitStack())
                weights = AHEAD_OF[s](nc, I, c, pair)
                c.load_ahead = weights.load
                s(nc, I, c)
                c.ahead, c.load_ahead = weights, None
            else:
                s(nc, I, c)
                if c.ahead:
                    pair.close()
                c.ahead = None
            if n == 3:
                nc.clear_and_free_semaphores(c.sems)
                c.sems = []
                nc.all_engine_barrier()
        if stages[-1] is not layer3_ffn:
            store(nc, c, out)


_INS = [
    "x", "ctx_1024", "mask_Bx1xSxS2_bf1", "g_xattn", "g_ffn", "L0_xattn_Wq", "L0_xattn_bq", "L0_xattn_Wk",
    "L0_xattn_bk", "L0_xattn_Wv", "L0_xattn_bv", "L0_xattn_q_scale", "L0_xattn_q_bias", "L0_xattn_k_scale",
    "L0_xattn_k_bias", "L0_ffn_W_in", "L0_ffn_b_in", "L0_ffn_W_out", "L0_ffn_b_out", "L1_xattn_Wq", "L1_xattn_Wkv",
    "L1_xattn_Wout", "L1_xattn_bout", "L1_ffn_W1", "L1_ffn_b1", "L1_ffn_W2", "L1_ffn_b2", "L2_xattn_W_Q",
    "L2_xattn_W_K", "L2_xattn_W_V", "L2_xattn_W_O", "L2_ffn_ln_g", "L2_ffn_ln_b", "L2_ffn_aw1", "L2_ffn_ab1",
    "L2_ffn_aw2", "L2_ffn_ab2", "L2_ffn_gate_w", "L2_ffn_gate_b", "L2_ffn_ew1", "L2_ffn_eb1", "L2_ffn_ew2",
    "L2_ffn_eb2", "L2_ffn_gens", "L2_ffn_gc_w", "L2_ffn_gc_b", "L3_xattn_Wq", "L3_xattn_bq", "L3_xattn_Wk",
    "L3_xattn_bk", "L3_xattn_Wv", "L3_xattn_bv", "L3_xattn_Wo", "L3_xattn_bo", "L3_ffn_clip_x", "L3_ffn_clip_down",
    "L3_ffn_w_gate", "L3_ffn_w_up", "L3_ffn_w_down",
]


def kernel(**inputs):
    import numpy as np
    import concourse.bacc as bacc
    from concourse.bass_utils import run_bass_kernel_spmd

    nc = bacc.Bacc("TRN2", target_bir_lowering=False, num_devices=1)
    arrays, drams = {}, {}
    for name in _INS:
        a = np.ascontiguousarray(inputs[name])
        if a.dtype == np.bool_:
            a = a.view(np.uint8)
        arrays["in_" + name] = a
        drams[name] = nc.dram_tensor("in_" + name, a.shape, mybir.dt.from_np(a.dtype), kind="ExternalInput").ap()
    out = nc.dram_tensor("out_0", (B, S, D), F32, kind="ExternalOutput").ap()
    program(nc, drams, out)
    r = run_bass_kernel_spmd(nc, [arrays], core_ids=[0])
    return r.results[0]["out_0"]
```
